# Optimizing a Trainium2 kernel written in Bass

```python
import numpy as np
import jax
import jax.numpy as jnp

def _softmax(x, axis=-1):
    return jax.nn.softmax(x, axis=axis)

def _gelu(x):
    return jax.nn.gelu(x, approximate=True)

def _silu(x):
    return jax.nn.silu(x)

def _sigmoid(x):
    return jax.nn.sigmoid(x)

def _layernorm(x, axis=-1, eps=1e-05):
    m = jnp.mean(x, axis=axis, keepdims=True)
    v = jnp.var(x, axis=axis, keepdims=True)
    return (x - m) / jnp.sqrt(v + eps)

def _scatter_add(tgt, idx, src, axis=0):
    return tgt.at[idx].add(src)

def _segment_sum(src, seg, n):
    return jax.ops.segment_sum(src, seg, n)
kernel_name = 'mk_gnn_resnorm_d4_gnn_r64_3ea19b'

def setup_inputs(seed: int=0):
    np.random.seed(seed)
    _w = jnp.asarray

    def _rec_inputs():
        import jax
        import jax.numpy as jnp
        _gk = jax.random.key(seed)
        x = -0.000202 + 1 * jax.random.normal(jax.random.fold_in(_gk, 1), (100000, 64), jnp.float32)
        src = jax.random.randint(jax.random.fold_in(_gk, 2), (50000,), 0, 100000, jnp.int32)
        dst = jnp.minimum((100000 * jax.random.uniform(jax.random.fold_in(_gk, 3), (50000,)) ** 2.0).astype(jnp.int32), 99999)
        _o = jnp.argsort(dst, stable=True)
        src = src[_o]
        dst = dst[_o]
        edge_attr_16 = 0.000254156 + 0.999948 * jax.random.normal(jax.random.fold_in(_gk, 13), (50000, 16), jnp.float32)
        return (x, src, dst, edge_attr_16)
    x, src, dst, edge_attr_16 = _rec_inputs()

    def _L0_gnn_setup():
        import jax, jax.numpy as jnp
        import numpy as np
        EPS = 1e-15
        CLIP = 0.98
        N_NODES = 100000
        N_EDGES = 25000
        D_IN = 64
        D_OUT = 64

        def _norm(x):
            return jnp.sqrt(jnp.sum(x * x, axis=1, keepdims=True))

        def _forward(h, W, c, edge_index):
            N = h.shape[0]
            f = h + EPS
            f = f * CLIP / jnp.maximum(CLIP, _norm(f))
            fn = _norm(f)
            p = jnp.tanh(fn) * f / fn
            sqrt_c = jnp.sqrt(c)
            p = p + EPS
            p = p * CLIP / jnp.maximum(CLIP, _norm(p))
            Mp = p @ W
            pn = _norm(p)
            atan_norm = jnp.arctanh(jnp.clip(sqrt_c * pn, -0.9, 0.9))
            t = Mp * atan_norm / pn / sqrt_c
            clip2 = CLIP / sqrt_c
            t = t * clip2 / jnp.maximum(clip2, _norm(t))
            tn = _norm(t)
            hh = jnp.tanh(sqrt_c * tn) / sqrt_c / tn * t
            row, col = (edge_index[0], edge_index[1])
            u = -hh[row]
            v = hh[col]
            c0 = c[0]
            sqrt_c0 = jnp.sqrt(c0)
            nu = jnp.sum(u * u, axis=1)
            nv = jnp.sum(v * v, axis=1)
            duv = jnp.sum(u * v, axis=1)
            coef1 = 1.0 + 2.0 * c0 * duv + c0 * nv
            coef2 = 1.0 - c0 * nu
            den = 1.0 + 2.0 * c0 * duv + c0 * c0 * nu * nv
            ma = (coef1[:, None] * u + coef2[:, None] * v) / den[:, None]
            rn = jnp.sqrt(jnp.sum(ma * ma, axis=1))
            e = -2.0 / sqrt_c0 * jnp.arctanh(jnp.clip(sqrt_c0 * rn, 1e-08, CLIP))
            e_max = jax.ops.segment_max(e, row, num_segments=N)
            e_max = jnp.where(jnp.isfinite(e_max), e_max, 0.0)
            ex = jnp.exp(e - e_max[row])
            denom = jax.ops.segment_sum(ex, row, num_segments=N)
            attention = ex / (denom[row] + 1e-16)
            g = hh + EPS
            g = g * CLIP / jnp.maximum(CLIP, _norm(g))
            gn = _norm(g)
            log_h = jnp.arctanh(jnp.clip(sqrt_c * gn, -0.9, 0.9)) * g / gn
            weighted = sqrt_c0 * attention[:, None] * log_h[col]
            att_log_h = jax.ops.segment_sum(weighted, row, num_segments=N)
            z = jax.nn.elu(att_log_h) + EPS
            clip3 = CLIP / sqrt_c
            z = z * clip3 / jnp.maximum(clip3, _norm(z))
            zn = _norm(z)
            h_prime = jnp.tanh(sqrt_c * zn) * z / sqrt_c / zn
            return h_prime
        key = jax.random.key(seed)
        k1, k2, k3 = jax.random.split(key, 3)
        h = jax.random.normal(k1, (N_NODES, D_IN), dtype=jnp.float32)
        limit = 1.414 * np.sqrt(6.0 / (D_IN + D_OUT))
        W = jax.random.uniform(k2, (D_IN, D_OUT), dtype=jnp.float32, minval=-limit, maxval=limit)
        c = jnp.array([1.0], dtype=jnp.float32)
        edge_index = jax.random.randint(k3, (2, N_EDGES), 0, N_NODES, dtype=jnp.int32)
        return {'h': h, 'W': W, 'c': c, 'edge_index': edge_index}
    _L0_gnn_all = _L0_gnn_setup()
    _L0_gnn_in = {k: v for k, v in _L0_gnn_all.items() if k in ('W', 'c')}
    del _L0_gnn_all

    def _L1_gnn_setup():
        import jax, jax.numpy as jnp
        import numpy as np
        N_NODES = 100000
        N_EDGES = 25000
        D = 64

        def _ngcf_conv(x, W1, W2, src, dst, n_nodes):
            ones = jnp.ones(src.shape[0], dtype=x.dtype)
            deg_out = jnp.clip(jax.ops.segment_sum(ones, src, num_segments=n_nodes), 1.0)
            deg_in = jnp.clip(jax.ops.segment_sum(ones, dst, num_segments=n_nodes), 1.0)
            norm = jax.lax.rsqrt(deg_out[src] * deg_in[dst])
            h_src = x[src]
            h_dst = x[dst]
            msg = (h_src @ W1 + h_src * h_dst @ W2) * norm[:, None]
            agg = jax.ops.segment_sum(msg, dst, num_segments=n_nodes)
            return x @ W1 + agg
        key = jax.random.key(seed)
        ks = jax.random.split(key, 8)
        s = 1.0 / np.sqrt(D)
        return {'x': jax.random.normal(ks[0], (N_NODES, D), dtype=jnp.float32), 'edge_src': jax.random.randint(ks[1], (N_EDGES,), 0, N_NODES, dtype=jnp.int32), 'edge_dst': jax.random.randint(ks[2], (N_EDGES,), 0, N_NODES, dtype=jnp.int32), 'W1_1': jax.random.normal(ks[3], (D, D), dtype=jnp.float32) * s, 'W2_1': jax.random.normal(ks[4], (D, D), dtype=jnp.float32) * s, 'W1_2': jax.random.normal(ks[5], (D, D), dtype=jnp.float32) * s, 'W2_2': jax.random.normal(ks[6], (D, D), dtype=jnp.float32) * s}
    _L1_gnn_all = _L1_gnn_setup()
    _L1_gnn_in = {k: v for k, v in _L1_gnn_all.items() if k in ('W1_1', 'W2_1', 'W1_2', 'W2_2')}
    del _L1_gnn_all

    def _L2_gnn_setup():
        import jax, jax.numpy as jnp
        import numpy as np
        DIM = 64
        HEADS = 4
        N_NODES = 50000
        N_EDGES = 12500
        NEG_SLOPE = 0.2
        key = jax.random.key(seed)
        k1, k2, k3, k4, k5 = jax.random.split(key, 5)
        meta_x = jax.random.normal(k1, (N_NODES, DIM), dtype=jnp.float32)
        meta_edge_index = jax.random.randint(k2, (2, N_EDGES), 0, N_NODES, dtype=jnp.int64)
        glorot = float(np.sqrt(2.0 / (DIM + HEADS * DIM)))
        W = jax.random.normal(k3, (DIM, HEADS * DIM), dtype=jnp.float32) * glorot
        att_src = jax.random.normal(k4, (1, HEADS, DIM), dtype=jnp.float32) * glorot
        att_dst = jax.random.normal(k5, (1, HEADS, DIM), dtype=jnp.float32) * glorot
        bias = jnp.zeros((DIM,), dtype=jnp.float32)
        return {'meta_x': meta_x, 'meta_edge_index': meta_edge_index, 'W': W, 'att_src': att_src, 'att_dst': att_dst, 'bias': bias}
    _L2_gnn_all = _L2_gnn_setup()
    _L2_gnn_in = {k: v for k, v in _L2_gnn_all.items() if k in ('W', 'att_src', 'att_dst', 'bias')}
    del _L2_gnn_all

    def _L3_gnn_setup():
        import jax, jax.numpy as jnp
        import numpy as np
        NUM_NODES = 50000
        NUM_EDGES = 12500
        IN_F = 64
        OUT_F = 64
        EDGE_DIM = 16
        NUM_GRAPHS = 64
        T = 1.0
        NEG_SLOPE = 0.2
        key = jax.random.key(seed)
        k = jax.random.split(key, 6)
        x = jax.random.normal(k[0], (NUM_NODES, IN_F), dtype=jnp.float32)
        edge_index = jax.random.randint(k[1], (2, NUM_EDGES), 0, NUM_NODES, dtype=jnp.int32)
        edge_attr = jax.random.normal(k[2], (NUM_EDGES, EDGE_DIM), dtype=jnp.float32)
        batch_id = jnp.sort(jax.random.randint(k[3], (NUM_NODES,), 0, NUM_GRAPHS, dtype=jnp.int32))
        W = jax.random.normal(k[4], (IN_F, OUT_F), dtype=jnp.float32) * (1.0 / np.sqrt(IN_F))
        a = jax.random.normal(k[5], (2 * OUT_F + EDGE_DIM, 1), dtype=jnp.float32) * 0.1
        return {'x': x, 'edge_index': edge_index, 'edge_attr': edge_attr, 'batch_id': batch_id, 'W': W, 'a': a}
    _L3_gnn_all = _L3_gnn_setup()
    _L3_gnn_in = {k: v for k, v in _L3_gnn_all.items() if k in ('W', 'a')}
    del _L3_gnn_all
    return {'x': x, 'src': src, 'dst': dst, 'edge_attr_16': edge_attr_16, 'L0_gnn_W': _L0_gnn_in['W'], 'L0_gnn_c': _L0_gnn_in['c'], 'L1_gnn_W1_1': _L1_gnn_in['W1_1'], 'L1_gnn_W2_1': _L1_gnn_in['W2_1'], 'L1_gnn_W1_2': _L1_gnn_in['W1_2'], 'L1_gnn_W2_2': _L1_gnn_in['W2_2'], 'L2_gnn_W': _L2_gnn_in['W'], 'L2_gnn_att_src': _L2_gnn_in['att_src'], 'L2_gnn_att_dst': _L2_gnn_in['att_dst'], 'L2_gnn_bias': _L2_gnn_in['bias'], 'L3_gnn_W': _L3_gnn_in['W'], 'L3_gnn_a': _L3_gnn_in['a']}

def reference(x, src, dst, edge_attr_16, L0_gnn_W, L0_gnn_c, L1_gnn_W1_1, L1_gnn_W2_1, L1_gnn_W1_2, L1_gnn_W2_2, L2_gnn_W, L2_gnn_att_src, L2_gnn_att_dst, L2_gnn_bias, L3_gnn_W, L3_gnn_a):
    import jax
    import jax.numpy as jnp

    def _L0_gnn_ref(h, W, c, edge_index):
        import jax, jax.numpy as jnp
        import numpy as np
        EPS = 1e-15
        CLIP = 0.98
        N_NODES = 100000
        N_EDGES = 25000
        D_IN = 64
        D_OUT = 64

        def _norm(x):
            return jnp.sqrt(jnp.sum(x * x, axis=1, keepdims=True))

        def _forward(h, W, c, edge_index):
            N = h.shape[0]
            f = h + EPS
            f = f * CLIP / jnp.maximum(CLIP, _norm(f))
            fn = _norm(f)
            p = jnp.tanh(fn) * f / fn
            sqrt_c = jnp.sqrt(c)
            p = p + EPS
            p = p * CLIP / jnp.maximum(CLIP, _norm(p))
            Mp = p @ W
            pn = _norm(p)
            atan_norm = jnp.arctanh(jnp.clip(sqrt_c * pn, -0.9, 0.9))
            t = Mp * atan_norm / pn / sqrt_c
            clip2 = CLIP / sqrt_c
            t = t * clip2 / jnp.maximum(clip2, _norm(t))
            tn = _norm(t)
            hh = jnp.tanh(sqrt_c * tn) / sqrt_c / tn * t
            row, col = (edge_index[0], edge_index[1])
            u = -hh[row]
            v = hh[col]
            c0 = c[0]
            sqrt_c0 = jnp.sqrt(c0)
            nu = jnp.sum(u * u, axis=1)
            nv = jnp.sum(v * v, axis=1)
            duv = jnp.sum(u * v, axis=1)
            coef1 = 1.0 + 2.0 * c0 * duv + c0 * nv
            coef2 = 1.0 - c0 * nu
            den = 1.0 + 2.0 * c0 * duv + c0 * c0 * nu * nv
            ma = (coef1[:, None] * u + coef2[:, None] * v) / den[:, None]
            rn = jnp.sqrt(jnp.sum(ma * ma, axis=1))
            e = -2.0 / sqrt_c0 * jnp.arctanh(jnp.clip(sqrt_c0 * rn, 1e-08, CLIP))
            e_max = jax.ops.segment_max(e, row, num_segments=N)
            e_max = jnp.where(jnp.isfinite(e_max), e_max, 0.0)
            ex = jnp.exp(e - e_max[row])
            denom = jax.ops.segment_sum(ex, row, num_segments=N)
            attention = ex / (denom[row] + 1e-16)
            g = hh + EPS
            g = g * CLIP / jnp.maximum(CLIP, _norm(g))
            gn = _norm(g)
            log_h = jnp.arctanh(jnp.clip(sqrt_c * gn, -0.9, 0.9)) * g / gn
            weighted = sqrt_c0 * attention[:, None] * log_h[col]
            att_log_h = jax.ops.segment_sum(weighted, row, num_segments=N)
            z = jax.nn.elu(att_log_h) + EPS
            clip3 = CLIP / sqrt_c
            z = z * clip3 / jnp.maximum(clip3, _norm(z))
            zn = _norm(z)
            h_prime = jnp.tanh(sqrt_c * zn) * z / sqrt_c / zn
            return h_prime
        return _forward(h, W, c, edge_index)

    def _L1_gnn_ref(x, edge_src, edge_dst, W1_1, W2_1, W1_2, W2_2):
        import jax, jax.numpy as jnp
        import numpy as np
        N_NODES = 100000
        N_EDGES = 25000
        D = 64

        def _ngcf_conv(x, W1, W2, src, dst, n_nodes):
            ones = jnp.ones(src.shape[0], dtype=x.dtype)
            deg_out = jnp.clip(jax.ops.segment_sum(ones, src, num_segments=n_nodes), 1.0)
            deg_in = jnp.clip(jax.ops.segment_sum(ones, dst, num_segments=n_nodes), 1.0)
            norm = jax.lax.rsqrt(deg_out[src] * deg_in[dst])
            h_src = x[src]
            h_dst = x[dst]
            msg = (h_src @ W1 + h_src * h_dst @ W2) * norm[:, None]
            agg = jax.ops.segment_sum(msg, dst, num_segments=n_nodes)
            return x @ W1 + agg
        n = x.shape[0]
        h = _ngcf_conv(x, W1_1, W2_1, edge_src, edge_dst, n)
        h = jax.nn.relu(h)
        h = _ngcf_conv(h, W1_2, W2_2, edge_src, edge_dst, n)
        return h

    def _L2_gnn_ref(meta_x, meta_edge_index, W, att_src, att_dst, bias):
        import jax, jax.numpy as jnp
        import numpy as np
        DIM = 64
        HEADS = 4
        N_NODES = 50000
        N_EDGES = 12500
        NEG_SLOPE = 0.2
        N = meta_x.shape[0]
        loops = jnp.arange(N, dtype=meta_edge_index.dtype)
        edge = jnp.concatenate([meta_edge_index, jnp.stack([loops, loops])], axis=1)
        src, dst = (edge[0], edge[1])
        x = (meta_x @ W).reshape(N, HEADS, DIM)
        a_src = jnp.sum(x * att_src, axis=-1)
        a_dst = jnp.sum(x * att_dst, axis=-1)
        logits = a_src[src] + a_dst[dst]
        logits = jax.nn.leaky_relu(logits, NEG_SLOPE)
        seg_max = jax.ops.segment_max(logits, dst, num_segments=N)
        ex = jnp.exp(logits - seg_max[dst])
        seg_sum = jax.ops.segment_sum(ex, dst, num_segments=N)
        alpha = ex / (seg_sum[dst] + 1e-16)
        msg = x[src] * alpha[:, :, None]
        out = jax.ops.segment_sum(msg, dst, num_segments=N)
        return out.mean(axis=1) + bias

    def _L3_gnn_ref(x, edge_index, edge_attr, batch_id, W, a):
        import jax, jax.numpy as jnp
        import numpy as np
        NUM_NODES = 50000
        NUM_EDGES = 12500
        IN_F = 64
        OUT_F = 64
        EDGE_DIM = 16
        NUM_GRAPHS = 64
        T = 1.0
        NEG_SLOPE = 0.2
        num_nodes = x.shape[0]
        src0, dst0 = (edge_index[0], edge_index[1])
        loop = jnp.arange(num_nodes, dtype=src0.dtype)
        src = jnp.concatenate([src0, dst0, loop])
        dst = jnp.concatenate([dst0, src0, loop])
        xt = x @ W
        a_src = a[:OUT_F, 0]
        a_dst = a[OUT_F:2 * OUT_F, 0]
        a_edge = a[2 * OUT_F:, 0]
        s_node = xt @ a_src
        d_node = xt @ a_dst
        e_contrib = edge_attr @ a_edge
        e_all = jnp.concatenate([e_contrib, e_contrib, jnp.zeros((num_nodes,), xt.dtype)])
        logits = jax.nn.leaky_relu(s_node[src] + d_node[dst] + e_all, NEG_SLOPE) / T
        m = jax.ops.segment_max(logits, dst, num_segments=num_nodes)
        z = jnp.exp(logits - m[dst])
        denom = jax.ops.segment_sum(z, dst, num_segments=num_nodes)
        att = z / denom[dst]
        h_src = xt[src]
        out = jax.ops.segment_sum(att[:, None] * h_src, dst, num_segments=num_nodes)
        return out
    edge_index = jnp.stack([src, dst])
    batch0 = jnp.zeros((100000,), jnp.int32)
    x = _layernorm(x + _L0_gnn_ref(x, L0_gnn_W, L0_gnn_c, edge_index), axis=-1)
    x = _layernorm(x + _L1_gnn_ref(x, src, dst, L1_gnn_W1_1, L1_gnn_W2_1, L1_gnn_W1_2, L1_gnn_W2_2), axis=-1)
    x = _layernorm(x + _L2_gnn_ref(x, edge_index, L2_gnn_W, L2_gnn_att_src, L2_gnn_att_dst, L2_gnn_bias), axis=-1)
    x = _layernorm(x + _L3_gnn_ref(x, edge_index, edge_attr_16, batch0, L3_gnn_W, L3_gnn_a), axis=-1)
    return x

_drawn_inputs = setup_inputs


def setup_inputs(seed=0):
    import zlib

    import numpy as np

    out = dict(_drawn_inputs(seed))
    spreads = {'L2_gnn_bias': (0.0, 0.1)}
    factors = {'L2_gnn_att_src': 4.69, 'L2_gnn_att_dst': 23.132}
    for name, (base, spread) in spreads.items():
        noise = np.random.default_rng([zlib.crc32(name.encode()), seed]).standard_normal(out[name].shape)
        drawn = base * np.exp(spread * noise) if base else spread * noise
        out[name] = jnp.asarray(drawn.astype(out[name].dtype))
    for name, factor in factors.items():
        out[name] = (out[name] * factor).astype(out[name].dtype)
    return out
```

```python
import math
from contextlib import ExitStack

import concourse.bass as bass
from concourse import mybir

F32 = mybir.dt.float32
I32 = mybir.dt.int32
BF16 = mybir.dt.bfloat16
F16 = mybir.dt.float16
ALU = mybir.AluOpType
ACT = mybir.ActivationFunctionType
AX = mybir.AxisListType

P = 128
D = 64
HEADS = 4
N = 100000
E = 50000
GROUP = 8
NODES = P * GROUP
CH = -(-N // NODES)
NP = CH * NODES
TAIL = (N - (CH - 1) * NODES) // GROUP
JT = 4
EDGES = P * JT
EC = -(-E // EDGES)
EP = EC * EDGES
TILES = EP // P
PAD_KEY = NP - 1
SKIP = 1 << 20
LOW = 256
HIGH = NP // LOW
LAST_E = E - (P - 1) * TILES
EPS, CLIP, LN_EPS, SLOPE = 1e-15, 0.98, 1e-5, 0.2
NEG = -1e30
ORDERS = 2

assert (N - (CH - 1) * NODES) % GROUP == 0 and EC == CH and HIGH <= 512


class Chunk:

    def __init__(self, i, r, unroll):
        self.n = i * unroll + r
        self.slot = r % unroll
        self.k = i + r // unroll


def stages(eng, count, unroll, skew, body, tail=0):
    def single(n):
        body(*[Chunk(0, n - s, unroll) if 0 <= n - s < count else None for s in range(skew + 1)])

    for n in range(skew):
        single(n)
    loops = (count - skew - tail) // unroll
    with eng.Fori(0, loops) as i:
        for u in range(unroll):
            body(*[Chunk(i, skew + u - s, unroll) for s in range(skew + 1)])
    for n in range(skew + loops * unroll, count + skew):
        single(n)


class Engine:

    def __init__(self, sem, names):
        self.sem, self.names, self.next = sem, names.split(), 0

    def done(self, instruction, name):
        assert self.names[self.next % len(self.names)] == name, (name, self.names[self.next % len(self.names)])
        self.next += 1
        instruction.then_inc(self.sem, 1)

    def after(self, n, name):
        return n * len(self.names) + self.names.index(name) + 1


class Semaphores:

    def __init__(self, nc):
        self.nc, self.held, self.n = nc, [], 0

    def __call__(self, name):
        s = self.nc.alloc_semaphore(name)
        self.held.append(s)
        return s

    def pair(self, name):
        return [self(f"{name}{h}") for h in range(2)]

    def quad(self, name):
        return [self(f"{name}{h}") for h in range(4)]

    def clear(self):
        self.nc.clear_and_free_semaphores(self.held)
        self.held = []
        self.nc.all_engine_barrier()


def lay_out_edges(nc, g, sem):
    for s in range(ORDERS):
        ctx = ExitStack()
        with ctx:
            def sb(name, shape, dt):
                return ctx.enter_context(nc.sbuf_tensor(name, shape, dt))

            rows = [sb(f"lay_rows{s}{q}", [EC, EDGES, 4], I32) for q in range(3)]
            key = [sb(f"lay_key{s}{q}", [EC, EDGES], F32) for q in range(3)]
            other = sb(f"lay_other{s}", [EC, EDGES], F32)
            contrib = sb(f"lay_contrib{s}", [EC, EDGES], F32)
            same = sb(f"lay_same{s}", [EC, EDGES], F32)
            more = sb(f"lay_more{s}", [EC, EDGES], F32)
            scat = sb(f"lay_scat{s}", [EC, EDGES], F32)
            pen = sb(f"lay_pen{s}", [EC, EDGES], F32)
            flat = [key[1], other, scat, pen, contrib, same]
            turned = [ctx.enter_context(nc.psum_tensor(f"lay_turned{s}{a}", [P, JT * EC], F32)) for a in range(6)]
            loaded, split, turn, stored = (sem(f"lay_{x}{s}") for x in ("loaded", "split", "turn", "stored"))
            with nc.Block() as block:
                @block.sync
                def _(sp):
                    for q in range(3):
                        sp.dma_start(rows[q][:, :, :].rearrange("p t k -> p (t k)"),
                                     g.sorted[s][q:q + EP, :].rearrange("(p t) k -> p (t k)", p=EC)).then_inc(loaded, 16)
                    sp.wait_ge(split, 3)
                    sp.dma_start(g.same_row[s][:, :].rearrange("a (p t) -> (a p) t", p=EC), same[:, :]).then_inc(stored, 16)
                    sp.dma_start(g.pen_row[s][:, :].rearrange("a (p t) -> (a p) t", p=EC), pen[:, :]).then_inc(stored, 16)
                    sp.wait_ge(stored, 32)

                @block.vector
                def _(v):
                    v.wait_ge(loaded, 48)
                    for q in range(3):
                        v.tensor_copy(key[q][:, :], rows[q][:, :, 0])
                    v.tensor_copy(other[:, :], rows[1][:, :, 1])
                    v.tensor_copy(contrib[:, :], rows[1][:, :, 2].bitcast(F32)).then_inc(split, 1)
                    v.wait_ge(split, 1)
                    v.tensor_tensor(same[:, :], key[1][:, :], key[0][:, :], ALU.is_equal)
                    v.tensor_tensor(more[:, :], key[1][:, :], key[2][:, :], ALU.is_equal).then_inc(split, 1)
                    v.wait_ge(split, 2)
                    v.tensor_scalar(pen[:, :], same[:, :], -1.0, -NEG, ALU.add, ALU.mult)
                    v.scalar_tensor_tensor(out=scat[:, :], in0=more[:, :], scalar=float(SKIP), in1=key[1][:, :],
                                           op0=ALU.mult, op1=ALU.add).then_inc(split, 1)
                    v.wait_ge(turn, 1)
                    for a in range(3):
                        v.tensor_copy(g.rows[s][:, :, a * JT:(a + 1) * JT],
                                      turned[a][:, :].rearrange("p (j c) -> p c j", j=JT))
                    for a, out in ((3, g.pen[s]), (4, g.contrib[s]), (5, g.same[s])):
                        last = v.tensor_copy(out[:, :, :], turned[a][:, :].rearrange("p (j c) -> p c j", j=JT))
                    last.then_inc(split, 1)

                @block.tensor
                def _(pe):
                    pe.wait_ge(split, 3)
                    for a in range(6):
                        for j in range(JT):
                            last = pe.matmul(turned[a][:, j * EC:(j + 1) * EC], lhsT=flat[a][:, j * P:(j + 1) * P],
                                             rhs=g.ident[0:EC, 0:EC], start=True, stop=True)
                    last.then_inc(turn, 1)
        sem.clear()


def sum_edges(nc, g, name, table, sums, sem):
    W = D + 1
    s = 1
    ctx = ExitStack()
    with ctx:
        def sb(label, shape, dt=F32):
            return ctx.enter_context(nc.sbuf_tensor(f"{name}_{label}", shape, dt))

        def ps(label, shape):
            return ctx.enter_context(nc.psum_tensor(f"{name}_{label}", shape, F32))

        from_rows = sb("from_rows", [P, 2, JT], I32)
        to_rows = sb("to_rows", [P, 2, JT], I32)
        got = sb("got", [P, 2, JT, W])
        same = sb("same_b", [W, 2, EDGES])
        run = sb("run", [W, 2, EDGES])
        out = sb("out", [P, 2, JT, W])
        turned = [ps(f"turned{h}", [W, EDGES]) for h in range(2)]
        back = [ps(f"back{h}", [P, JT * W]) for h in range(2)]
        from_ready, gathered, same_loaded, flipped, scanned, unflipped, out_ready, to_ready, filed = (
            sem.pair(f"{name}_{x}") for x in ("from_ready", "gathered", "same_loaded", "flipped", "scanned",
                                             "unflipped", "out_ready", "to_ready", "filed"))
        set_up = sem(f"{name}_set_up")
        with nc.Block() as block:
            @block.sync
            def _(sp):
                def body(c0, c1, c2):
                    if c0:
                        h, k = c0.slot, c0.k
                        sp.wait_ge(scanned[h], k)
                        sp.dma_start(same[:, h, :], g.same_row[s][:, bass.ds(c0.n * EDGES, EDGES)]
                                     .to_broadcast([W, EDGES])).then_inc(same_loaded[h], 16)
                stages(sp, EC, 2, 2, body)

            @block.vector
            def _(v):
                v.memset(got[:, :, :, D:W], 1.0)
                v.memset(run[:, 1, :], 0.0).then_inc(set_up, 1)
                v.wait_ge(set_up, 1)

                def body(c0, c1, c2):
                    if c0:
                        h, k = c0.slot, c0.k
                        v.wait_ge(gathered[h], k * 16 * JT)
                        v.tensor_copy(from_rows[:, h, :], g.rows[s][:, bass.ds(c0.n, 1), JT:2 * JT]
                                      .rearrange("p a j -> p (a j)")).then_inc(from_ready[h], 1)
                    if c1:
                        h, k = c1.slot, c1.k
                        v.wait_ge(filed[h], k * 16 * JT)
                        v.tensor_copy(to_rows[:, h, :], g.rows[s][:, bass.ds(c1.n, 1), 2 * JT:3 * JT]
                                      .rearrange("p a j -> p (a j)")).then_inc(to_ready[h], 1)
                        v.wait_ge(same_loaded[h], (k + 1) * 16)
                        v.wait_ge(flipped[h], k + 1)
                        v.wait_ge(unflipped[h], k)
                        v.wait_ge(scanned[1 - h], k + h)
                        v.tensor_tensor_scan(run[:, h, :], same[:, h, :], turned[h][:, :],
                                             run[:, 1 - h, EDGES - 1:EDGES], ALU.mult, ALU.add).then_inc(scanned[h], 1)
                stages(v, EC, 2, 2, body)

            @block.tensor
            def _(pe):
                pe.wait_ge(set_up, 1)

                def body(c0, c1, c2):
                    if c1:
                        h, k = c1.slot, c1.k
                        pe.wait_ge(gathered[h], (k + 1) * 16 * JT)
                        pe.wait_ge(scanned[h], k)
                        for j in range(JT):
                            last = pe.matmul(turned[h][:, j * P:(j + 1) * P], lhsT=got[:, h, j, :], rhs=g.ident[:, :],
                                             start=True, stop=True)
                        last.then_inc(flipped[h], 1)
                        pe.wait_ge(scanned[h], k + 1)
                        pe.wait_ge(out_ready[h], k)
                        for j in range(JT):
                            last = pe.matmul(back[h][:, j * W:(j + 1) * W], lhsT=run[:, h, j * P:(j + 1) * P],
                                             rhs=g.ident[0:W, 0:W], start=True, stop=True)
                        last.then_inc(unflipped[h], 1)
                stages(pe, EC, 2, 2, body)

            @block.scalar
            def _(a):
                def body(c0, c1, c2):
                    if c1:
                        h, k = c1.slot, c1.k
                        a.wait_ge(unflipped[h], k + 1)
                        a.wait_ge(filed[h], k * 16 * JT)
                        a.activation(out[:, h, :, :].rearrange("p j w -> p (j w)"), back[h][:, :],
                                     ACT.Copy).then_inc(out_ready[h], 1)
                stages(a, EC, 2, 2, body)

            @block.gpsimd
            def _(gp):
                gp.wait_ge(set_up, 1)

                def body(c0, c1, c2):
                    if c0:
                        h, k = c0.slot, c0.k
                        gp.wait_ge(from_ready[h], k + 1)
                        gp.wait_ge(flipped[h], k)
                        gp.nop(nofuse=True)
                        for j in range(JT):
                            gp.indirect_dma_start(out=got[:, h, j, 0:D], out_offset=None, in_=table[:, :],
                                                  in_offset=bass.IndirectOffsetOnAxis(ap=from_rows[:, h, j:j + 1], axis=0)
                                                  ).then_inc(gathered[h], 16)
                    if c2:
                        h, k = c2.slot, c2.k
                        gp.wait_ge(out_ready[h], k + 1)
                        gp.wait_ge(to_ready[h], k + 1)
                        gp.nop(nofuse=True)
                        for j in range(JT):
                            gp.indirect_dma_start(out=sums[:, :],
                                                  out_offset=bass.IndirectOffsetOnAxis(ap=to_rows[:, h, j:j + 1], axis=0),
                                                  in_=out[:, h, j, :], in_offset=None,
                                                  bounds_check=NP - 1, oob_is_err=False).then_inc(filed[h], 16)
                stages(gp, EC, 2, 2, body)
                for h in range(2):
                    gp.wait_ge(filed[h], EC // 2 * 16 * JT)
    sem.clear()


def chunk_rows(table, n, width):
    return table[bass.ds(n * NODES, NODES), :].rearrange("(p j) k -> p (j k)", p=P)


def flat(tile):
    return tile.rearrange("p j k -> p (j k)")


def set_up(nc, g, w, sem):
    ctx = ExitStack()
    with ctx:
        def sb(label, shape, dt=F32):
            return ctx.enter_context(nc.sbuf_tensor(f"su_{label}", shape, dt))

        ones = sb("ones", [D, P])
        w0 = sb("w0", [P, D])
        w_att = sb("w_att", [P, HEADS, D])
        att = sb("att", [P, 2, HEADS, D])
        prod = sb("prod", [P, 2, HEADS, D])
        summed = sb("summed", [P, 2, HEADS])
        mean = sb("mean", [P, D])
        w3 = sb("w3", [P, D])
        a3 = sb("a3", [P, 2, D])
        prod3 = sb("prod3", [P, 2, D])
        sum3 = sb("sum3", [P, 2])
        prod0 = sb("prod0", [P, 2, D])
        sum0 = sb("sum0", [P, 2])
        colsum = ctx.enter_context(nc.psum_tensor("su_colsum", [P, D], F32))
        const, loaded, pe_done, act_done, dve, pooled = (sem(f"su_{x}") for x in (
            "const", "loaded", "pe", "act", "dve", "pooled"))
        with nc.Block() as block:
            @block.gpsimd
            def _(gp):
                gp.memset(g.ident[:, :], 0.0)
                gp.memset(g.zeros_bf[:, :], 0.0)
                gp.memset(g.zero_rows[:, :], 0.0)
                gp.memset(g.half[:, :], 0.5)
                gp.memset(g.minus_half[:, :], -0.5)
                gp.memset(ones[:, :], 1.0)
                gp.memset(g.w0_pair[:, :, :], 0.0)
                gp.memset(g.w2_pair[:, :, :], 0.0)
                gp.memset(g.a3_pair[:, :, :], 0.0)
                gp.memset(g.w3_pair[:, :, :], 0.0)
                gp.memset(g.pick[:, :, :, :], 0.0).then_inc(const, 1)
                gp.wait_ge(const, 1)
                gp.affine_select(out=g.ident[:, :], in_=g.ident[:, :], compare_op=ALU.not_equal, fill=1.0,
                                 base=0, pattern=[[-1, P]], channel_multiplier=1)
                picked = g.pick[:, :, :, :].rearrange("r w q (a d) -> r (w q a) d", d=D)
                gp.affine_select(out=picked, in_=picked, compare_op=ALU.not_equal, fill=1.0,
                                 base=0, pattern=[[-1, 8], [0, D]], channel_multiplier=1).then_inc(const, 1)
                gp.wait_ge(loaded, 16 * w.loads)
                gp.tensor_tensor(g.c_cols[:, 1:2], g.c_cols[:, 0:1], g.half[:, 0:1], ALU.pow).then_inc(pooled, 1)

            @block.sync
            def _(sp):
                n = 0

                def load(out, in_):
                    nonlocal n
                    n += 1
                    sp.dma_start(out, in_).then_inc(loaded, 16)

                for a in range(2):
                    half = slice(a * D, (a + 1) * D)
                    load(w0[half, :], w.L0_W[:, :])
                    load(w3[half, :], w.L3_W[:, :])
                    load(w_att[half, :, :], w.L2_W.rearrange("k (h d) -> k h d", h=HEADS))
                    for q in range(2):
                        load(g.w_heads[half, q, :], w.L2_W[:, (2 * q + a) * D:(2 * q + a + 1) * D])
                    load(g.w_conv1[half, :], (w.L1_W1_1, w.L1_W2_1)[a][:, :])
                    load(g.w_conv2[half, :], (w.L1_W1_2, w.L1_W2_2)[a][:, :])
                for a, x in enumerate((w.L2_att_dst, w.L2_att_src)):
                    load(att[:, a, :, :].rearrange("p h d -> p (h d)"), x.rearrange("a h d -> a (h d)").to_broadcast([P, HEADS * D]))
                load(a3[:, 0, :], w.L3_a[D:2 * D, :].rearrange("k a -> a k").to_broadcast([P, D]))
                load(a3[:, 1, :], w.L3_a[0:D, :].rearrange("k a -> a k").to_broadcast([P, D]))
                load(g.bias[:, :], w.L2_bias.rearrange("(a d) -> a d", a=1).to_broadcast([P, D]))
                load(g.c_cols[:, 0:1], w.L0_c.rearrange("(a d) -> a d", a=1).to_broadcast([P, 1]))
                assert n == w.loads, n

            @block.tensor
            def _(pe):
                pe.wait_ge(const, 2)
                pe.wait_ge(loaded, 16 * w.loads)
                pe.matmul(colsum[:, :], lhsT=ones[:, :], rhs=w0[0:D, :], start=True, stop=True).then_inc(pe_done, 1)

            @block.vector
            def _(v):
                n = 0

                def step(instruction):
                    nonlocal n
                    n += 1
                    instruction.then_inc(dve, 1)
                    v.wait_ge(dve, n)

                v.wait_ge(loaded, 16 * w.loads)
                v.wait_ge(const, 2)
                v.wait_ge(pe_done, 1)
                v.tensor_copy(g.k_row[:, :], colsum[:, :])
                step(v.tensor_copy(prod0[:, 1, :], w0[:, :]))
                step(v.tensor_tensor(prod0[:, 0, :], w0[:, :], g.k_row[:, :], ALU.mult))
                step(v.tensor_reduce(sum0[:, :], prod0[:, :, :], AX.X, ALU.add))
                for a in range(2):
                    half = slice(a * D, (a + 1) * D)
                    v.tensor_copy(g.w0_pair[half, a, 0:D], w0[half, :])
                    v.tensor_copy(g.w0_pair[half, a, D:D + 2], sum0[half, :])
                    v.tensor_copy(g.w3_pair[half, a, :], w3[half, :])
                step(v.tensor_reduce(g.k_cols[:, 0:1], g.k_row[:, :], AX.X, ALU.add))
                step(v.tensor_tensor(prod0[:, 0, :], g.k_row[:, :], g.k_row[:, :], ALU.mult))
                step(v.tensor_reduce(g.k_cols[:, 1:2], prod0[:, 0, :], AX.X, ALU.add))
                step(v.tensor_scalar(g.k_cols[:, 0:1], g.k_cols[:, 0:1], EPS, None, ALU.mult))
                step(v.tensor_scalar(g.k_cols[:, 1:2], g.k_cols[:, 1:2], EPS * EPS, None, ALU.mult))
                step(v.tensor_tensor(prod[:, :, :, :].rearrange("p a h d -> p a (h d)"), att[:, :, :, :].rearrange("p a h d -> p a (h d)"),
                                     w_att[:, :, :].rearrange("p h d -> p (h d)").unsqueeze(1).to_broadcast([P, 2, HEADS * D]), ALU.mult))
                step(v.tensor_reduce(summed[:, :, :], prod[:, :, :, :], AX.X, ALU.add))
                step(v.tensor_reduce(mean[:, :], w_att[:, :, :].rearrange("p h d -> p d h"), AX.X, ALU.add))
                step(v.tensor_scalar(mean[:, :], mean[:, :], 1.0 / HEADS, None, ALU.mult))
                step(v.tensor_scalar(g.w_heads[:, :, :], g.w_heads[:, :, :], 1.0 / HEADS, None, ALU.mult))
                step(v.tensor_tensor(prod3[:, :, :], a3[:, :, :], w3[:, :].unsqueeze(1).to_broadcast([P, 2, D]), ALU.mult))
                step(v.tensor_reduce(sum3[:, :], prod3[:, :, :], AX.X, ALU.add))
                for a in range(2):
                    half = slice(a * D, (a + 1) * D)
                    v.tensor_copy(g.w2_pair[half, a, 0:8], summed[half, :, :].rearrange("p a h -> p (a h)"))
                    v.tensor_copy(g.w2_pair[half, a, 8:], mean[half, :])
                    v.tensor_copy(g.a3_pair[half, a, :], sum3[half, :])
                c = g.cs
                v.wait_ge(pooled, 1)
                step(v.reciprocal(c["1/sqrt"], c["sqrt"]))
                step(v.tensor_scalar(c["clip"], c["1/sqrt"], CLIP, None, ALU.mult))
                step(v.tensor_scalar(c["-2c"], c["c"], -2.0, None, ALU.mult))
                step(v.tensor_tensor(c["c*c"], c["c"], c["c"], ALU.mult))
    sem.clear()


def project(nc, g, x, sem):
    ctx = ExitStack()
    with ctx:
        def sb(label, shape, dt=F32):
            return ctx.enter_context(nc.sbuf_tensor(f"pr_{label}", shape, dt))

        def ps(label, shape):
            return ctx.enter_context(nc.psum_tensor(f"pr_{label}", shape, F32))

        xin = sb("x", [P, 4, GROUP, D])
        f0 = sb("f0", [P, 2, GROUP, D])
        xt = sb("xt", [P, 2, GROUP // 2, P])
        y = sb("y", [P, 4, GROUP, D])
        squares = sb("squares", [P, 2, 2, GROUP, D])
        turned = [ps(f"turned{h}", [P, GROUP // 2 * P]) for h in range(2)]
        W2 = 2 * (D + 2)
        prod = [[ps(f"prod{h}{b}", [P, 2, 2, D + 2]) for b in range(2)] for h in range(2)]
        loaded, stored = sem.quad("pr_loaded"), sem.quad("pr_stored")
        dve = Engine(sem("pr_dve"), "f0 sum more n2 y2")
        act = Engine(sem("pr_act"), "sqx xt y0 y1 sqy0 sqy1")
        pe = Engine(sem("pr_pe"), "turn prod")
        with nc.Block() as block:
            @block.sync
            def _(sp):
                def body(c0, c1, c2):
                    if c0:
                        h, k = c0.slot, c0.k
                        sp.wait_ge(stored[h], k * 16)
                        if isinstance(c0.n, int) and c0.n == CH - 1:
                            sp.dma_start(flat(xin[0:TAIL, h, :, :]), x[(CH - 1) * NODES:N, :]
                                         .rearrange("(p j) k -> p (j k)", j=GROUP)).then_inc(loaded[h], 16)
                        else:
                            sp.dma_start(flat(xin[:, h, :, :]), chunk_rows(x, c0.n, D)).then_inc(loaded[h], 16)
                    if c2:
                        sp.wait_ge(act.sem, act.after(c2.n, "y1"))
                        sp.dma_start(chunk_rows(g.Y, c2.n, D), flat(y[:, c2.slot, :, :])).then_inc(stored[c2.slot], 16)
                stages(sp, CH, 4, 2, body, tail=1)
                for h in range(4):
                    sp.wait_ge(stored[h], len(range(h, CH, 4)) * 16)

            @block.vector
            def _(v):
                def body(c0, c1, c2):
                    if c1:
                        n, h, b = c1.n, c1.slot, c1.slot % 2
                        v.wait_ge(loaded[h], (c1.k + 1) * 16)
                        dve.done(v.tensor_scalar(f0[:, b, :, :], xin[:, h, :, :], EPS, None, ALU.add), "f0")
                        v.wait_ge(dve.sem, dve.after(n, "f0"))
                        dve.done(v.tensor_reduce(g.node["sf"][:, bass.ds(n, 1), :].rearrange("p a j -> p (a j)"),
                                                 f0[:, b, :, :], AX.X, ALU.add), "sum")
                        v.wait_ge(act.sem, act.after(n, "sqy1"))
                        for i in range(2):
                            for which, name in enumerate(("yk", "sy")):
                                at = g.node[name][:, bass.ds(n, 1), 4 * i:4 * i + 4]
                                last = v.tensor_copy(at, prod[b][i][:, :, :, D + which].rearrange("p q a -> p (q a)").unsqueeze(1))
                        dve.done(last, "more")
                        for which, name, after in ((0, "n2", "sqx"), (1, "y2", "sqy1")):
                            v.wait_ge(act.sem, act.after(n, after))
                            dve.done(v.tensor_reduce(g.node[name][:, bass.ds(n, 1), :].rearrange("p a j -> p (a j)"),
                                                     squares[:, b, which, :, :], AX.X, ALU.add), name)
                stages(v, CH, 4, 2, body)

            @block.tensor
            def _(t):
                def body(c0, c1, c2):
                    if c1:
                        n, b = c1.n, c1.slot % 2
                        t.wait_ge(dve.sem, dve.after(n, "f0"))
                        for q in range(GROUP // 2):
                            last = t.matmul(turned[b][:, q * P:(q + 1) * P],
                                            lhsT=f0[:, b, 2 * q:2 * q + 2, :].rearrange("p a d -> p (a d)"),
                                            rhs=g.ident[:, :], start=True, stop=True)
                        pe.done(last, "turn")
                        t.wait_ge(act.sem, act.after(n, "xt"))
                        for q in range(GROUP // 2):
                            last = t.matmul(prod[b][q // 2][:, q % 2, :, :].rearrange("p a k -> p (a k)"),
                                            lhsT=xt[:, b, q, :], rhs=g.w0_pair[:, :, :].rearrange("p a k -> p (a k)"),
                                            start=True, stop=True)
                        pe.done(last, "prod")
                stages(t, CH, 4, 2, body)

            @block.scalar
            def _(a):
                def body(c0, c1, c2):
                    if c1:
                        n, h, b = c1.n, c1.slot, c1.slot % 2
                        a.wait_ge(dve.sem, dve.after(n, "f0"))
                        act.done(a.activation(squares[:, b, 0, :, :], f0[:, b, :, :], ACT.Square), "sqx")
                        a.wait_ge(pe.sem, pe.after(n, "turn"))
                        act.done(a.activation(xt[:, b, :, :].rearrange("p q m -> p (q m)"), turned[b][:, :], ACT.Copy), "xt")
                        a.wait_ge(pe.sem, pe.after(n, "prod"))
                        a.wait_ge(stored[h], c1.k * 16)
                        for i in range(2):
                            act.done(a.activation(y[:, h, 4 * i:4 * i + 4, :], prod[b][i][:, :, :, 0:D]
                                                  .rearrange("p q a k -> p (q a) k"), ACT.Copy), f"y{i}")
                        for i in range(2):
                            act.done(a.activation(squares[:, b, 1, 4 * i:4 * i + 4, :], prod[b][i][:, :, :, 0:D]
                                                  .rearrange("p q a k -> p (q a) k"), ACT.Square), f"sqy{i}")
                stages(a, CH, 4, 2, body)
    sem.clear()


def factors(nc, g, sem):
    ctx = ExitStack()
    with ctx:
        node, c = g.node, g.cs
        names = "n fs a pn pc yn sp b t t2 m u s sg".split()
        tile = {x: ctx.enter_context(nc.sbuf_tensor(f"fa_{x}", [P, CH * GROUP], F32)) for x in names}
        A = {x: tile[x][:, :] for x in names}
        for x in ("n2", "sf", "y2", "yk", "sy", "nh2", "zeta", "s1", "s2"):
            A[x] = node[x][:, :, :].rearrange("p c j -> p (c j)")
        to_act, from_act, dve = sem("fa_to_act"), sem("fa_from_act"), sem("fa_dve")
        asked = []

        with nc.Block() as block:
            @block.vector
            def _(v):
                n = 0

                def step(instruction):
                    nonlocal n
                    n += 1
                    instruction.then_inc(dve, 1)
                    v.wait_ge(dve, n)

                def ts(out, x, a, op, b=None, op2=None):
                    if op2 is None:
                        step(v.tensor_scalar(A[out], A[x], a, None, op))
                    else:
                        step(v.tensor_scalar(A[out], A[x], a, b, op, op2))

                def tt(out, x, y, op):
                    step(v.tensor_tensor(A[out], A[x], A[y], op))

                def stt(out, x, a, y, op, op2):
                    step(v.scalar_tensor_tensor(out=A[out], in0=A[x], scalar=a, in1=A[y], op0=op, op1=op2))

                def inv(out, x):
                    step(v.reciprocal(A[out], A[x]))

                def on_act(out, x, f, scale=1.0, bias=0.0):
                    asked.append((out, x, f, scale, bias))
                    v.sem_inc(to_act, 1)
                    v.wait_ge(from_act, len(asked))

                def clip_factor(out, norm, limit):
                    ts("t", norm, limit, ALU.max)
                    inv("t", "t")
                    ts(out, "t", limit, ALU.mult)

                def artanh(out, x):
                    tt("t", x, x, ALU.mult)
                    ts("t2", "t", 1 / 15, ALU.mult, 1 / 13, ALU.add)
                    for d in (11, 9, 7, 5, 3, 1):
                        tt("t2", "t2", "t", ALU.mult)
                        ts("t2", "t2", 1 / d, ALU.add)
                    tt("t2", "t2", x, ALU.mult)
                    on_act("t", x, ACT.Ln, 1.0, 1.0)
                    on_act("u", x, ACT.Ln, -1.0, 1.0)
                    tt("t", "t", "u", ALU.subtract)
                    ts("t", "t", 0.5, ALU.mult)
                    ts("m", x, 0.25, ALU.is_lt)
                    tt("t2", "t2", "m", ALU.mult)
                    ts("m", x, 0.25, ALU.is_ge)
                    tt("t", "t", "m", ALU.mult)
                    tt(out, "t", "t2", ALU.add)

                on_act("n", "n2", ACT.Sqrt)
                clip_factor("fs", "n", CLIP)
                tt("n", "n", "fs", ALU.mult)
                inv("s", "n")
                on_act("n", "n", ACT.Tanh)
                tt("a", "n", "s", ALU.mult)
                tt("a", "a", "fs", ALU.mult)
                tt("s", "a", "a", ALU.mult)
                tt("t", "s", "n2", ALU.mult)
                tt("u", "a", "sf", ALU.mult)
                stt("t", "u", 2 * EPS, "t", ALU.mult, ALU.add)
                ts("t", "t", D * EPS * EPS, ALU.add, 0.0, ALU.max)
                on_act("pn", "t", ACT.Sqrt)
                clip_factor("pc", "pn", CLIP)
                tt("pn", "pn", "pc", ALU.mult)
                tt("t", "s", "y2", ALU.mult)
                tt("u", "a", "yk", ALU.mult)
                stt("t", "u", 2 * EPS, "t", ALU.mult, ALU.add)
                ts("t", "t", g.k_cols[:, 1:2], ALU.add)
                ts("t", "t", 0.0, ALU.max)
                on_act("yn", "t", ACT.Sqrt)
                tt("sp", "a", "sy", ALU.mult)
                ts("sp", "sp", g.k_cols[:, 0:1], ALU.add)
                ts("s", "pn", c["sqrt"], ALU.mult, 0.9, ALU.min)
                artanh("b", "s")
                inv("s", "pn")
                tt("b", "b", "s", ALU.mult)
                tt("b", "b", "pc", ALU.mult)
                ts("b", "b", c["1/sqrt"], ALU.mult)
                tt("n", "b", "yn", ALU.mult)
                clip_factor("fs", "n", c["clip"])
                tt("n", "n", "fs", ALU.mult)
                inv("s", "n")
                on_act("n", "n", ACT.Tanh, "sqrt")
                tt("n", "n", "s", ALU.mult)
                tt("n", "n", "fs", ALU.mult)
                tt("n", "n", "b", ALU.mult)
                ts("sg", "n", c["1/sqrt"], ALU.mult)
                tt("s1", "sg", "a", ALU.mult)
                ts("s2", "sg", EPS, ALU.mult)
                tt("t", "sg", "yn", ALU.mult)
                tt("nh2", "t", "t", ALU.mult)
                tt("u", "sg", "sp", ALU.mult)
                stt("t", "u", 2 * EPS, "nh2", ALU.mult, ALU.add)
                ts("t", "t", D * EPS * EPS, ALU.add, 0.0, ALU.max)
                on_act("n", "t", ACT.Sqrt)
                clip_factor("fs", "n", CLIP)
                tt("n", "n", "fs", ALU.mult)
                ts("s", "n", c["sqrt"], ALU.mult, 0.9, ALU.min)
                artanh("b", "s")
                inv("s", "n")
                tt("b", "b", "s", ALU.mult)
                tt("zeta", "b", "fs", ALU.mult)

            @block.scalar
            def _(a):
                for i, (out, x, f, scale, bias) in enumerate(asked):
                    a.wait_ge(to_act, i + 1)
                    a.activation(A[out], A[x], f, bias=bias, scale=c["sqrt"] if scale == "sqrt" else scale).then_inc(from_act, 1)
    sem.clear()


def place(nc, g, sem):
    ctx = ExitStack()
    with ctx:
        def sb(label, shape, dt=F32):
            return ctx.enter_context(nc.sbuf_tensor(f"pl_{label}", shape, dt))

        y = sb("y", [P, 4, GROUP, D])
        t1 = sb("t1", [P, 2, GROUP, D])
        t2 = sb("t2", [P, 2, GROUP, D])
        row = sb("row", [P, 4, GROUP, D + 2])
        loaded, stored, ready = (sem.quad(f"pl_{x}") for x in ("loaded", "stored", "ready"))
        made = Engine(sem("pl_dve"), "t1 t2")
        with nc.Block() as block:
            @block.sync
            def _(sp):
                def body(c0, c1, c2):
                    if c0:
                        sp.wait_ge(stored[c0.slot], c0.k * 16)
                        sp.dma_start(flat(y[:, c0.slot, :, :]), chunk_rows(g.Y, c0.n, D)).then_inc(loaded[c0.slot], 16)
                    if c2:
                        sp.wait_ge(ready[c2.slot], c2.k + 1)
                        sp.dma_start(chunk_rows(g.T0, c2.n, D + 2), flat(row[:, c2.slot, :, :])).then_inc(stored[c2.slot], 16)
                stages(sp, CH, 4, 2, body)
                for h in range(4):
                    sp.wait_ge(stored[h], len(range(h, CH, 4)) * 16)

            @block.vector
            def _(v):
                def body(c0, c1, c2):
                    if c1:
                        n, h, b = c1.n, c1.slot, c1.slot % 2

                        def per_node(name):
                            return g.node[name][:, bass.ds(n, 1), :].rearrange("p a j -> p j a")

                        v.wait_ge(loaded[h], (c1.k + 1) * 16)
                        made.done(v.tensor_tensor(t1[:, b, :, :], y[:, h, :, :], per_node("s1").to_broadcast([P, GROUP, D]), ALU.mult), "t1")
                        made.done(v.tensor_tensor(t2[:, b, :, :], g.k_row[:, :].unsqueeze(1).to_broadcast([P, GROUP, D]),
                                                  per_node("s2").to_broadcast([P, GROUP, D]), ALU.mult), "t2")
                        v.wait_ge(stored[h], c1.k * 16)
                        v.tensor_copy(row[:, h, :, 0:1], per_node("nh2"))
                        v.tensor_copy(row[:, h, :, 1:2], per_node("zeta"))
                        v.wait_ge(made.sem, made.after(n, "t2"))
                        v.tensor_tensor(row[:, h, :, 2:], t1[:, b, :, :], t2[:, b, :, :], ALU.add).then_inc(ready[h], 1)
                stages(v, CH, 4, 2, body)
    sem.clear()


def sort_edges(nc, g, src, dst, l3_a, attr, sem):
    ctx = ExitStack()
    with ctx:
        def sb(name, shape, dt):
            return ctx.enter_context(nc.sbuf_tensor(name, shape, dt))

        keys = sb("sort_keys", [P, ORDERS, TILES], I32)
        digit_i = sb("sort_digit_i", [P, TILES], I32)
        digits = sb("sort_digits", [P, ORDERS, 2, TILES], F32)
        attrs = sb("sort_attrs", [P, TILES, 16], F32)
        a_edge = sb("sort_a_edge", [P, 16], F32)
        contrib = sb("sort_contrib", [P, TILES], F32)
        record = sb("sort_record", [P, ORDERS, TILES, 4], I32)
        hot = sb("sort_hot", [P, 8, 2 * LOW + 2 * HIGH], BF16)
        buckets = sb("sort_buckets", [P, 512], F16)
        ones_row = sb("sort_ones_row", [P, 512], F32)
        total = sb("sort_total", [P, 2 * LOW + 2 * HIGH], F32)
        upto = sb("sort_upto", [P, 2 * LOW + 2 * HIGH], F32)
        base = sb("sort_base", [P, 2 * LOW + 2 * HIGH], F32)
        before = sb("sort_before", [P, P], BF16)
        notbefore = sb("sort_notbefore", [P, P], BF16)
        ones_bf = sb("sort_ones", [P, P], BF16)
        stage = sb("sort_stage", [P, 2, ORDERS, JT, 4], I32)
        half_i = sb("sort_half_i", [P, 2, ORDERS * JT], I32)
        half_d = sb("sort_half_d", [P, 2, ORDERS * JT], F32)
        place_f = sb("sort_place_f", [P, 2, ORDERS * JT], F32)
        place_i = sb("sort_place_i", [P, 2, ORDERS * JT], I32)
        junk = sb("sort_junk", [P, 2, 512], F32)
        edge_row = sb("sort_edge_row", [1, 8], I32)
        count_lo = ctx.enter_context(nc.psum_tensor("sort_count_lo", [P, 512], F32))
        count_hi = [ctx.enter_context(nc.psum_tensor(f"sort_count_hi{s}", [P, 512], F32)) for s in range(2)]
        ranks = [ctx.enter_context(nc.psum_tensor(f"sort_ranks{s}", [P, 512], F32)) for s in range(2)]

        def cols(s, high):
            at = 2 * LOW + s * HIGH if high else s * LOW
            return slice(at, at + (HIGH if high else LOW))

        mid0, mid1, final = g.mid0, g.mid1, g.sorted

        loaded, const, made, dve, counted = (sem(x) for x in (
            "sort_loaded", "sort_const", "sort_made", "sort_dve", "sort_counted"))
        cleared = sem("sort_cleared")
        hot_ready, hot_used, mid_stored = sem("sort_hot_ready"), sem("sort_hot_used"), sem("sort_mid_stored")
        with nc.Block() as block:
            @block.sync
            def _(sp):
                sp.wait_ge(const, 3)
                for s, key in enumerate((src, dst)):
                    whole = key[0:(P - 1) * TILES].rearrange("(p t) -> p t", t=TILES)
                    sp.dma_start(keys[0:P - 1, s, :], whole).then_inc(loaded, 16)
                    sp.dma_start(keys[P - 1:P, s, 0:LAST_E],
                                 key[(P - 1) * TILES:E].rearrange("(a t) -> a t", a=1)).then_inc(loaded, 16)
                sp.dma_start(attrs[0:P - 1, :, :].rearrange("p t k -> p (t k)"),
                             attr[0:(P - 1) * TILES, :].rearrange("(p t) k -> p (t k)", t=TILES)).then_inc(loaded, 16)
                sp.dma_start(attrs[P - 1:P, 0:LAST_E, :].rearrange("p t k -> p (t k)"),
                             attr[(P - 1) * TILES:E, :].rearrange("(a t) k -> a (t k)", a=1)).then_inc(loaded, 16)
                sp.dma_start(a_edge[:, :], l3_a[2 * D:2 * D + 16, :].rearrange("k a -> a k").to_broadcast([P, 16])).then_inc(loaded, 16)
                sp.wait_ge(made, 1)
                for s in range(ORDERS):
                    sp.dma_start(mid0[s][:, :].rearrange("(p t) k -> p (t k)", p=P),
                                 record[:, s, :, :].rearrange("p t k -> p (t k)")).then_inc(mid_stored, 16)
                    sp.dma_start(final[s][0:1, :], edge_row[0:1, 0:4]).then_inc(mid_stored, 16)
                    sp.dma_start(final[s][EP + 1:EP + 2, :], edge_row[0:1, 4:8]).then_inc(mid_stored, 16)
                sp.wait_ge(mid_stored, 16 * 6)

            @block.gpsimd
            def _(gp):
                gp.memset(keys[:, :, :], PAD_KEY).then_inc(const, 1)
                gp.memset(attrs[:, :, :], 0.0).then_inc(const, 1)
                gp.memset(edge_row[:, :], -1).then_inc(const, 1)
                gp.iota(buckets[:, :], pattern=[[1, 512]], base=0, channel_multiplier=0,
                        allow_small_or_imprecise_dtypes=True).then_inc(const, 1)
                gp.memset(ones_bf[:, :], 1.0).then_inc(const, 1)
                gp.memset(ones_row[:, :], 1.0).then_inc(const, 1)
                gp.wait_ge(const, 6)
                gp.affine_select(out=before[:, :], in_=ones_bf[:, :], compare_op=ALU.is_gt, fill=0.0,
                                 base=0, pattern=[[1, P]], channel_multiplier=-1).then_inc(const, 1)
                gp.affine_select(out=notbefore[:, :], in_=ones_bf[:, :], compare_op=ALU.is_ge, fill=0.0,
                                 base=0, pattern=[[-1, P]], channel_multiplier=1).then_inc(const, 1)

            @block.vector
            def _(v):
                n = 0
                v.wait_ge(loaded, 16 * 7)
                for s in range(ORDERS):
                    for high in range(2):
                        if high:
                            i = v.tensor_scalar(digit_i[:, :], keys[:, s, :], 8, None, ALU.arith_shift_right)
                        else:
                            i = v.tensor_scalar(digit_i[:, :], keys[:, s, :], LOW - 1, None, ALU.bitwise_and)
                        i.then_inc(dve, 1)
                        n += 1
                        v.wait_ge(dve, n)
                        v.tensor_copy(digits[:, s, high, :], digit_i[:, :]).then_inc(dve, 1)
                        n += 1
                        v.wait_ge(dve, n)
                v.wait_ge(const, 8)
                v.tensor_tensor(attrs[:, :, :], attrs[:, :, :],
                                a_edge[:, :].unsqueeze(1).to_broadcast([P, TILES, 16]), ALU.mult).then_inc(dve, 1)
                n += 1
                v.wait_ge(dve, n)
                v.tensor_reduce(contrib[:, :], attrs[:, :, :], AX.X, ALU.add).then_inc(dve, 1)
                n += 1
                v.wait_ge(dve, n)
                for s in range(ORDERS):
                    v.tensor_copy(record[:, s, :, 0], keys[:, s, :])
                    v.tensor_copy(record[:, s, :, 1], keys[:, 1 - s, :])
                    v.tensor_copy(record[:, s, :, 3], keys[:, s, :])
                    last = v.tensor_copy(record[:, s, :, 2].bitcast(F32), contrib[:, :])
                    if s == 0:
                        last.then_inc(dve, 1)
                n += 1
                last.then_inc(made, 1)
                with v.Fori(0, TILES // 8) as i:
                    for k in range(8):
                        t = i * 8 + k
                        v.wait_ge(hot_used, i * 8)
                        for s in range(ORDERS):
                            for high in range(2):
                                c = cols(s, high)
                                last = v.tensor_scalar(hot[:, k, c], buckets[:, 0:c.stop - c.start],
                                                       digits[:, s, high, bass.ds(t, 1)], None, ALU.is_equal)
                        last.then_inc(hot_ready, 1)
                v.wait_ge(counted, 1)
                v.tensor_copy(total[:, 0:512], count_lo[:, :])
                v.tensor_copy(total[:, cols(0, 1)], count_hi[0][:, 0:HIGH])
                v.tensor_copy(total[:, cols(1, 1)], count_hi[1][:, 0:HIGH]).then_inc(dve, 1)
                n += 1
                v.wait_ge(dve, n)
                for s in range(ORDERS):
                    for high in range(2):
                        c = cols(s, high)
                        last = v.tensor_tensor_scan(upto[:, c], ones_row[:, 0:c.stop - c.start], total[:, c],
                                                    0.0, ALU.mult, ALU.add)
                last.then_inc(dve, 1)
                n += 1
                v.wait_ge(dve, n)
                v.tensor_tensor(base[:, :], upto[:, :], total[:, :], ALU.subtract).then_inc(dve, 1)
                n += 1
                v.wait_ge(dve, n)
                v.tensor_scalar(base[:, 2 * LOW:], base[:, 2 * LOW:], 1.0, None, ALU.add).then_inc(dve, 1)

            @block.scalar
            def _(a):
                with a.Fori(0, CH) as n:
                    for table, width in g.zeroed_tables:
                        a.dma_start(chunk_rows(table, n, width), g.zero_rows[:, 0:GROUP * width]).then_inc(cleared, 16)
                a.wait_ge(cleared, CH * 16 * len(g.zeroed_tables))

            @block.tensor
            def _(pe):
                pe.wait_ge(const, 8)
                pe.matmul(count_lo[:, :], lhsT=g.zeros_bf[:, 0:P], rhs=g.zeros_bf[:, :], start=True, stop=False)
                pe.matmul(count_hi[0][:, 0:HIGH], lhsT=g.zeros_bf[:, 0:P], rhs=g.zeros_bf[:, 0:HIGH], start=True, stop=False)
                pe.matmul(count_hi[1][:, 0:HIGH], lhsT=g.zeros_bf[:, 0:P], rhs=g.zeros_bf[:, 0:HIGH], start=True, stop=False)
                with pe.Fori(0, TILES // 8) as i:
                    for k in range(8):
                        pe.wait_ge(hot_ready, i * 8 + k + 1)
                        pe.matmul(count_lo[:, :], lhsT=ones_bf[:, :], rhs=hot[:, k, 0:512], start=False, stop=False)
                        pe.matmul(count_hi[0][:, 0:HIGH], lhsT=ones_bf[:, :], rhs=hot[:, k, cols(0, 1)], start=False, stop=False)
                        pe.matmul(count_hi[1][:, 0:HIGH], lhsT=ones_bf[:, :], rhs=hot[:, k, cols(1, 1)],
                                  start=False, stop=False).then_inc(hot_used, 1)
                pe.matmul(count_lo[:, :], lhsT=g.zeros_bf[:, 0:P], rhs=g.zeros_bf[:, :], start=False, stop=True)
                pe.matmul(count_hi[0][:, 0:HIGH], lhsT=g.zeros_bf[:, 0:P], rhs=g.zeros_bf[:, 0:HIGH], start=False, stop=True)
                pe.matmul(count_hi[1][:, 0:HIGH], lhsT=g.zeros_bf[:, 0:P], rhs=g.zeros_bf[:, 0:HIGH],
                          start=False, stop=True).then_inc(counted, 1)

        for high in range(2):
            source, target = ((mid0, mid1), (mid1, final))[high]
            width = HIGH if high else LOW
            read, split, hot_made, ranked, placed, filed = (
                [sem(f"pass{high}_{x}{h}") for h in range(2)] for x in
                ("read", "split", "hot_made", "ranked", "placed", "filed"))
            summed, taken = sem(f"pass{high}_summed"), sem(f"pass{high}_taken")
            PAIRS = ORDERS * JT
            with nc.Block() as block:
                @block.sync
                def _(sp):
                    with sp.Fori(0, TILES // (2 * JT)) as i:
                        for h in range(2):
                            sp.wait_ge(filed[h], i * (16 * PAIRS))
                            for s in range(ORDERS):
                                rows = source[s][bass.ds((i * 2 + h) * EDGES, EDGES), :]
                                sp.dma_start(stage[:, h, s, :, :],
                                             rows.rearrange("(t p) k -> p t k", p=P)).then_inc(read[h], 16)

                @block.vector
                def _(v):
                    with v.Fori(0, TILES // (2 * JT)) as i:
                        for h in range(2):
                            v.wait_ge(read[h], (i + 1) * 32)
                            keys_h = stage[:, h, :, :, 0].rearrange("p s t -> p (s t)")
                            if high:
                                ins = v.tensor_scalar(half_i[:, h, :], keys_h, 8, None, ALU.arith_shift_right)
                            else:
                                ins = v.tensor_scalar(half_i[:, h, :], keys_h, LOW - 1, None, ALU.bitwise_and)
                            ins.then_inc(split[h], 1)
                            v.wait_ge(split[h], i * 2 + 1)
                            v.tensor_copy(half_d[:, h, :], half_i[:, h, :]).then_inc(split[h], 1)
                            v.wait_ge(split[h], i * 2 + 2)
                            for k in range(PAIRS):
                                if k == 0:
                                    v.wait_ge(taken, (i * 2 + h) * PAIRS)
                                tile, s = k // 2, k % 2
                                v.tensor_scalar(hot[:, k, 0:width], buckets[:, 0:width],
                                                half_d[:, h, s * JT + tile:s * JT + tile + 1],
                                                None, ALU.is_equal).then_inc(hot_made[h], 1)
                            for k in range(PAIRS):
                                tile, s = k // 2, k % 2
                                v.wait_ge(summed, (i * 2 + h) * PAIRS + k + 1)
                                v.tensor_tensor_reduce(
                                    out=junk[:, s, 0:width], in0=ranks[s][:, 0:width], in1=hot[:, k, 0:width],
                                    scale=1.0, scalar=0.0, op0=ALU.mult, op1=ALU.add,
                                    accum_out=place_f[:, h, s * JT + tile:s * JT + tile + 1]).then_inc(ranked[h], 1)
                            v.wait_ge(ranked[h], (i + 1) * PAIRS)
                            v.tensor_copy(place_i[:, h, :], place_f[:, h, :]).then_inc(placed[h], 1)

                @block.tensor
                def _(pe):
                    for s in range(ORDERS):
                        pe.matmul(ranks[s][:, 0:width], lhsT=g.ident[:, :], rhs=base[:, cols(s, high)],
                                  start=True, stop=False, skip_group_check=True)
                    with pe.Fori(0, TILES // (2 * JT)) as i:
                        for h in range(2):
                            def add(k):
                                pe.wait_ge(hot_made[h], i * PAIRS + k + 1)
                                pe.matmul(ranks[k % 2][:, 0:width], lhsT=before[:, :], rhs=hot[:, k, 0:width],
                                          start=False, stop=False, skip_group_check=True).then_inc(summed, 1)

                            def rest(k):
                                pe.wait_ge(ranked[h], i * PAIRS + k + 1)
                                pe.matmul(ranks[k % 2][:, 0:width], lhsT=notbefore[:, :], rhs=hot[:, k, 0:width],
                                          start=False, stop=False, skip_group_check=True).then_inc(taken, 1)

                            add(0)
                            add(1)
                            for k in range(PAIRS):
                                rest(k)
                                if k + 2 < PAIRS:
                                    add(k + 2)

                @block.gpsimd
                def _(gp):
                    with gp.Fori(0, TILES // (2 * JT)) as i:
                        for h in range(2):
                            gp.wait_ge(placed[h], i + 1)
                            gp.nop(nofuse=True)
                            for s in range(ORDERS):
                                for t in range(JT):
                                    k = s * JT + t
                                    gp.indirect_dma_start(
                                        out=target[s][:, :],
                                        out_offset=bass.IndirectOffsetOnAxis(ap=place_i[:, h, k:k + 1], axis=0),
                                        in_=stage[:, h, s, t, :], in_offset=None).then_inc(filed[h], 16)
                    for h in range(2):
                        gp.wait_ge(filed[h], TILES // (2 * JT) * 16 * PAIRS)
    sem.clear()


def attend_edges(nc, g, name, s, kind, own, others, target, sem):
    H = HEADS if kind == "heads" else 1
    WOWN = {"hyper": D + 2, "heads": D + 8, "edge": 2}[kind]
    WOTHER = {"hyper": D + 2, "heads": D + 8, "edge": D + 2}[kind]
    WRUN = {"hyper": D + 2, "heads": P, "edge": D + 1}[kind]
    WOUT = D if kind == "heads" else D + 2
    Q = 2 if kind == "heads" else 1
    ctx = ExitStack()
    with ctx:
        def sb(label, shape, dt=F32):
            return ctx.enter_context(nc.sbuf_tensor(f"{name}_{label}", shape, dt))

        def ps(label, shape):
            return ctx.enter_context(nc.psum_tensor(f"{name}_{label}", shape, F32))

        from_rows = sb("from_rows", [P, 2, 2 * JT], I32)
        to_rows = sb("to_rows", [P, 2, JT], I32)
        mine = sb("mine", [P, 2, JT, WOWN])
        other = sb("other", [P, 2, JT, WOTHER])
        pen = sb("pen_b", [H, 2, EDGES])
        score = sb("score", [P, JT, H])
        loop = sb("loop", [P, JT, H])
        tmp = sb("tmp", [P, 12, JT, H])
        top = sb("top", [H, 2, EDGES + 1])
        cols = sb("cols", [P, 2, JT, H])
        lows = sb("lows", [P, 2, JT, H])
        ex = sb("ex", [P, 2, JT, H])
        pay = sb("pay", [P, JT, Q * WRUN])
        decay = sb("decay", [P, Q, EDGES])
        run = sb("run", [P, 2, Q, EDGES])
        out = sb("out", [P, 2, JT, WOUT])
        score_row, top_col, pay_row, spread = ps("score_row", [H, EDGES]), ps("top_col", [P, 2 * JT * H + JT * H]), \
            ps("pay_row0", [P, EDGES]), [ps("spread0", [P, EDGES])]
        back = ps("back", [P, JT * WOUT])
        pay_rows = [pay_row]
        if kind == "hyper":
            big = sb("big", [P, 4, JT, D])
            log_h = sb("log_h", [P, JT, D])
            decays = sb("decays", [P, JT, WRUN])
        if kind == "heads":
            pay_rows.append(ps("pay_row1", [P, EDGES]))
            spread.append(ps("spread1", [P, EDGES]))
            decay_row = ps("decay_row", [2 * H, EDGES])
            decay_row_s = sb("decay_row_s", [H, EDGES])
            weights = sb("weights", [H, 2, EDGES])
            wcol = sb("wcol", [P, JT, H])
            fin = sb("fin", [P, 2, JT, H])
            share = sb("share", [P, JT, 2, H])
            share_row = sb("share_row", [2 * H, EDGES])
            twice = sb("twice", [P, JT, 2, D])
            own_row = sb("own_row", [P, EDGES])
            z = sb("z", [P, 4, EDGES])
        cs = g.cs

        dve = Engine(sem(f"{name}_dve"), {
            "hyper": "prod dot a c1 c2 nn den rden t1 t2 ma ma2 rn2 low clip lndiff score "
                     "keep top cols fall fallen rise log pay payw decays decay1 run",
            "edge": "s1 s2 score keep top cols fall fallen rise pay run",
            "heads": "sadd score qadd loop keep top cols fall fallen rise pay weights run0 run1 "
                     "wcol most f1 f2 g1 g2 g3 beta al0 alpha z0 z1 z2 z3"}[kind])
        act = Engine(sem(f"{name}_act"), {
            "hyper": "square root ln1 ln2 ex decay out", "edge": "ex decay out",
            "heads": "twice ex decay_row decay0 decay1 own exf share_row out"}[kind])
        pe = Engine(sem(f"{name}_pe"), {
            "hyper": "score_row top_col decay pay back", "edge": "score_row top_col decay pay back",
            "heads": "score_row top_col weight_row decay_row decay0 decay1 pay own wcol share_row "
                     "beta0 beta1 alpha0 alpha1 back"}[kind])
        from_ready, gathered, pen_loaded, to_ready, filed = (
            sem.pair(f"{name}_{x}") for x in ("from_ready", "gathered", "pen_loaded", "to_ready", "filed"))
        set_up = sem(f"{name}_set_up")

        with nc.Block() as block:
            @block.sync
            def _(sp):
                def body(c0, c1, c2):
                    if c0:
                        h = c0.slot
                        if not (isinstance(c0.n, int) and c0.n < 2):
                            sp.wait_ge(dve.sem, dve.after(c0.n - 2, "top"))
                        sp.dma_start(pen[:, h, :], g.pen_row[s][:, bass.ds(c0.n * EDGES, EDGES)]
                                     .to_broadcast([H, EDGES])).then_inc(pen_loaded[h], 16)
                stages(sp, EC, 2, 2, body)

            @block.gpsimd
            def _(gp):
                gp.wait_ge(set_up, 1)

                def body(c0, c1, c2):
                    if c0:
                        h, k = c0.slot, c0.k
                        gp.wait_ge(from_ready[h], k + 1)
                        if not (isinstance(c0.n, int) and c0.n < 2):
                            gp.wait_ge(dve.sem, dve.after(c0.n - 2, dve.names[-1]))
                        gp.nop(nofuse=True)
                        for j in range(JT):
                            gp.indirect_dma_start(out=mine[:, h, j, :], out_offset=None, in_=own[:, :],
                                                  in_offset=bass.IndirectOffsetOnAxis(ap=from_rows[:, h, j:j + 1], axis=0)
                                                  ).then_inc(gathered[h], 16)
                            gp.indirect_dma_start(out=other[:, h, j, :], out_offset=None, in_=others[:, :],
                                                  in_offset=bass.IndirectOffsetOnAxis(ap=from_rows[:, h, JT + j:JT + j + 1], axis=0)
                                                  ).then_inc(gathered[h], 16)
                    if c2:
                        h, k = c2.slot, c2.k
                        gp.wait_ge(act.sem, act.after(c2.n, "out"))
                        gp.wait_ge(to_ready[h], k + 1)
                        gp.nop(nofuse=True)
                        for j in range(JT):
                            gp.indirect_dma_start(out=target[:, :],
                                                  out_offset=bass.IndirectOffsetOnAxis(ap=to_rows[:, h, j:j + 1], axis=0),
                                                  in_=out[:, h, j, :], in_offset=None,
                                                  bounds_check=NP - 1, oob_is_err=False).then_inc(filed[h], 16)
                stages(gp, EC, 2, 2, body)
                for h in range(2):
                    gp.wait_ge(filed[h], EC // 2 * 16 * JT)

            @block.vector
            def _(v):
                v.memset(top[:, 1, :], NEG)
                if kind == "hyper":
                    v.memset(pay[:, :, D + 1:D + 2], 1.0)
                if kind == "heads":
                    v.memset(weights[:, 1, :], 0.0)
                v.memset(run[:, 1, :, :], 0.0).then_inc(set_up, 1)
                v.wait_ge(set_up, 1)

                def body(c0, c1, c2):
                    if c0:
                        h, k = c0.slot, c0.k
                        v.wait_ge(gathered[h], k * 32 * JT)
                        v.tensor_copy(from_rows[:, h, :], g.rows[s][:, bass.ds(c0.n, 1), 0:2 * JT]
                                      .rearrange("p a j -> p (a j)")).then_inc(from_ready[h], 1)
                    if c1:
                        attend(c1)

                def attend(c):
                    n, h, k = c.n, c.slot, c.k

                    def need(engine, step):
                        v.wait_ge(engine.sem, engine.after(n, step))

                    v.wait_ge(filed[h], k * 16 * JT)
                    v.tensor_copy(to_rows[:, h, :], g.rows[s][:, bass.ds(n, 1), 2 * JT:3 * JT]
                                  .rearrange("p a j -> p (a j)")).then_inc(to_ready[h], 1)
                    v.wait_ge(gathered[h], (k + 1) * 32 * JT)
                    mi, ot = mine[:, h, :, :], other[:, h, :, :]
                    if kind == "hyper":
                        dve.done(v.tensor_tensor(big[:, 0, :, :], mi[:, :, 2:], ot[:, :, 2:], ALU.mult), "prod")
                        need(dve, "prod")
                        dve.done(v.tensor_reduce(tmp[:, 0, :, 0], big[:, 0, :, :], AX.X, ALU.add), "dot")
                        need(dve, "dot")
                        nu, nv = mi[:, :, 0], ot[:, :, 0]
                        dve.done(v.tensor_scalar(tmp[:, 1, :, 0], tmp[:, 0, :, 0], cs["-2c"], 1.0, ALU.mult, ALU.add), "a")
                        need(dve, "a")
                        dve.done(v.scalar_tensor_tensor(out=tmp[:, 2, :, 0], in0=nv, scalar=cs["c"], in1=tmp[:, 1, :, 0],
                                                        op0=ALU.mult, op1=ALU.add), "c1")
                        dve.done(v.tensor_scalar(tmp[:, 3, :, 0], nu, cs["c"], -1.0, ALU.mult, ALU.add), "c2")
                        dve.done(v.scalar_tensor_tensor(out=tmp[:, 4, :, 0], in0=nu, scalar=cs["c*c"], in1=nv,
                                                        op0=ALU.mult, op1=ALU.mult), "nn")
                        need(dve, "nn")
                        dve.done(v.tensor_tensor(tmp[:, 5, :, 0], tmp[:, 4, :, 0], tmp[:, 1, :, 0], ALU.add), "den")
                        need(dve, "den")
                        dve.done(v.reciprocal(tmp[:, 6, :, 0], tmp[:, 5, :, 0]), "rden")
                        dve.done(v.tensor_tensor(big[:, 1, :, :], mi[:, :, 2:], tmp[:, 2, :, :].to_broadcast([P, JT, D]), ALU.mult), "t1")
                        dve.done(v.tensor_tensor(big[:, 2, :, :], ot[:, :, 2:], tmp[:, 3, :, :].to_broadcast([P, JT, D]), ALU.mult), "t2")
                        need(dve, "t2")
                        dve.done(v.tensor_tensor(big[:, 1, :, :], big[:, 1, :, :], big[:, 2, :, :], ALU.add), "ma")
                        need(dve, "ma")
                        dve.done(v.tensor_tensor(big[:, 3, :, :], big[:, 1, :, :], tmp[:, 6, :, :].to_broadcast([P, JT, D]), ALU.mult), "ma2")
                        need(act, "square")
                        dve.done(v.tensor_reduce(tmp[:, 7, :, 0], big[:, 0, :, :], AX.X, ALU.add), "rn2")
                        need(dve, "rn2")
                        dve.done(v.tensor_scalar(tmp[:, 8, :, 0], tmp[:, 7, :, 0], cs["c"], 1e-16, ALU.mult, ALU.max), "low")
                        need(act, "root")
                        dve.done(v.tensor_scalar(tmp[:, 9, :, 0], tmp[:, 9, :, 0], CLIP, None, ALU.min), "clip")
                        need(act, "ln2")
                        dve.done(v.tensor_tensor(tmp[:, 0, :, 0], tmp[:, 11, :, 0], tmp[:, 10, :, 0], ALU.subtract), "lndiff")
                        need(dve, "lndiff")
                        dve.done(v.tensor_scalar(score[:, :, 0], tmp[:, 0, :, 0], cs["1/sqrt"], None, ALU.mult), "score")
                    elif kind == "edge":
                        dve.done(v.tensor_tensor(tmp[:, 0, :, 0], ot[:, :, 0], mi[:, :, 0], ALU.add), "s1")
                        need(dve, "s1")
                        dve.done(v.tensor_tensor(tmp[:, 1, :, 0], tmp[:, 0, :, 0],
                                                 g.contrib[s][:, bass.ds(n, 1), :].rearrange("p a j -> p (a j)"), ALU.add), "s2")
                        need(dve, "s2")
                        dve.done(v.scalar_tensor_tensor(out=score[:, :, 0], in0=tmp[:, 1, :, 0], scalar=SLOPE, in1=tmp[:, 1, :, 0],
                                                        op0=ALU.mult, op1=ALU.max), "score")
                    else:
                        dve.done(v.tensor_tensor(tmp[:, 0, :, :], ot[:, :, 4:8], mi[:, :, 0:4], ALU.add), "sadd")
                        need(dve, "sadd")
                        dve.done(v.scalar_tensor_tensor(out=score[:, :, :], in0=tmp[:, 0, :, :], scalar=SLOPE, in1=tmp[:, 0, :, :],
                                                        op0=ALU.mult, op1=ALU.max), "score")
                        dve.done(v.tensor_tensor(tmp[:, 1, :, :], mi[:, :, 4:8], mi[:, :, 0:4], ALU.add), "qadd")
                        need(dve, "qadd")
                        dve.done(v.scalar_tensor_tensor(out=loop[:, :, :], in0=tmp[:, 1, :, :], scalar=SLOPE, in1=tmp[:, 1, :, :],
                                                        op0=ALU.mult, op1=ALU.max), "loop")
                    dve.done(v.tensor_copy(top[:, h, 0:1], top[:, 1 - h, EDGES:EDGES + 1]), "keep")
                    v.wait_ge(pen_loaded[h], (k + 1) * 16)
                    need(pe, "score_row")
                    dve.done(v.tensor_tensor_scan(top[:, h, 1:], pen[:, h, :], score_row[:, :],
                                                  top[:, 1 - h, EDGES:EDGES + 1], ALU.add, ALU.max), "top")
                    need(pe, "top_col")
                    dve.done(v.tensor_copy(cols[:, :, :, :], top_col[:, 0:2 * JT * H]
                                           .rearrange("p (a j q) -> p a j q", a=2, j=JT)), "cols")
                    need(dve, "cols")
                    dve.done(v.tensor_tensor(lows[:, 0, :, :], cols[:, 1, :, :], cols[:, 0, :, :], ALU.subtract), "fall")
                    need(dve, "fall")
                    dve.done(v.tensor_tensor(lows[:, 0, :, :], lows[:, 0, :, :],
                                             g.pen[s][:, bass.ds(n, 1), :].rearrange("p a j -> p j a")
                                             .to_broadcast([P, JT, H]), ALU.min), "fallen")
                    dve.done(v.tensor_tensor(lows[:, 1, :, :], score[:, :, :], cols[:, 0, :, :], ALU.subtract), "rise")
                    if kind == "hyper":
                        dve.done(v.scalar_tensor_tensor(out=log_h[:, :, :], in0=ot[:, :, 2:], scalar=EPS,
                                                        in1=ot[:, :, 1:2].to_broadcast([P, JT, D]),
                                                        op0=ALU.add, op1=ALU.mult), "log")
                        need(dve, "log")
                    need(act, "ex")
                    if kind == "hyper":
                        dve.done(v.tensor_tensor(pay[:, :, 0:D], log_h[:, :, :], ex[:, 1, :, :].to_broadcast([P, JT, D]), ALU.mult), "pay")
                        dve.done(v.tensor_copy(pay[:, :, D:D + 1], ex[:, 1, :, :]), "payw")
                        dve.done(v.tensor_copy(decays[:, :, 0:D + 1], ex[:, 0, :, :].to_broadcast([P, JT, D + 1])), "decays")
                        dve.done(v.tensor_copy(decays[:, :, D + 1:D + 2], g.same[s][:, bass.ds(n, 1), :]
                                               .rearrange("p a j -> p j a")), "decay1")
                    elif kind == "edge":
                        dve.done(v.tensor_tensor(pay[:, :, :], ot[:, :, 1:], ex[:, 1, :, :].to_broadcast([P, JT, D + 1]), ALU.mult), "pay")
                    else:
                        dve.done(v.tensor_tensor(pay[:, :, :].rearrange("p j (q d) -> p j q d", d=D),
                                                 ot[:, :, 8:].unsqueeze(2).to_broadcast([P, JT, H, D]),
                                                 ex[:, 1, :, :].unsqueeze(3).to_broadcast([P, JT, H, D]), ALU.mult), "pay")
                    if kind != "heads":
                        need(pe, "pay")
                        need(act, "decay")
                        dve.done(v.tensor_tensor_scan(run[0:WRUN, h, 0, :], decay[0:WRUN, 0, :], pay_rows[0][0:WRUN, :],
                                                      run[0:WRUN, 1 - h, 0, EDGES - 1:EDGES], ALU.mult, ALU.add), "run")
                        return
                    need(act, "decay_row")
                    need(pe, "decay_row")
                    dve.done(v.tensor_tensor_scan(weights[:, h, :], decay_row_s[:, :], score_row[:, :],
                                                  weights[:, 1 - h, EDGES - 1:EDGES], ALU.mult, ALU.add), "weights")
                    need(pe, "pay")
                    for q in range(2):
                        need(act, f"decay{q}")
                        dve.done(v.tensor_tensor_scan(run[:, h, q, :], decay[:, q, :], pay_rows[q][:, :],
                                                      run[:, 1 - h, q, EDGES - 1:EDGES], ALU.mult, ALU.add), f"run{q}")
                    need(pe, "wcol")
                    dve.done(v.tensor_copy(wcol[:, :, :], top_col[:, 2 * JT * H:].rearrange("p (j q) -> p j q", j=JT)), "wcol")
                    dve.done(v.tensor_tensor(tmp[:, 2, :, :], cols[:, 0, :, :], loop[:, :, :], ALU.max), "most")
                    need(dve, "most")
                    dve.done(v.tensor_tensor(fin[:, 0, :, :], cols[:, 0, :, :], tmp[:, 2, :, :], ALU.subtract), "f1")
                    dve.done(v.tensor_tensor(fin[:, 1, :, :], loop[:, :, :], tmp[:, 2, :, :], ALU.subtract), "f2")
                    need(act, "exf")
                    dve.done(v.tensor_tensor(tmp[:, 3, :, :], wcol[:, :, :], fin[:, 0, :, :], ALU.mult), "g1")
                    need(dve, "g1")
                    dve.done(v.scalar_tensor_tensor(out=tmp[:, 4, :, :], in0=fin[:, 1, :, :], scalar=1e-16, in1=tmp[:, 3, :, :],
                                                    op0=ALU.add, op1=ALU.add), "g2")
                    need(dve, "g2")
                    dve.done(v.reciprocal(tmp[:, 5, :, :], tmp[:, 4, :, :]), "g3")
                    need(dve, "g3")
                    dve.done(v.tensor_tensor(share[:, :, 0, :], fin[:, 0, :, :], tmp[:, 5, :, :], ALU.mult), "beta")
                    dve.done(v.tensor_tensor(tmp[:, 6, :, :], fin[:, 1, :, :], tmp[:, 5, :, :], ALU.mult), "al0")
                    need(dve, "al0")
                    dve.done(v.tensor_scalar(share[:, :, 1, :], tmp[:, 6, :, :], -1.0, None, ALU.add), "alpha")
                    for q in range(2):
                        need(pe, f"beta{q}")
                        dve.done(v.tensor_tensor(z[:, q, :], run[:, h, q, :], spread[1 - q][:, :], ALU.mult), f"z{q}")
                    need(act, "own")
                    for q in range(2):
                        need(pe, f"alpha{q}")
                        dve.done(v.tensor_tensor(z[:, 2 + q, :], own_row[:, :], spread[1 - q][:, :], ALU.mult), f"z{2 + q}")
                stages(v, EC, 2, 2, body)

            @block.scalar
            def _(a):
                def body(c0, c1, c2):
                    if not c1:
                        return
                    n, h, k = c1.n, c1.slot, c1.k

                    def need(engine, step):
                        a.wait_ge(engine.sem, engine.after(n, step))

                    if kind == "hyper":
                        need(dve, "ma2")
                        act.done(a.activation(big[:, 0, :, :], big[:, 3, :, :], ACT.Square), "square")
                        need(dve, "low")
                        act.done(a.activation(tmp[:, 9, :, :], tmp[:, 8, :, :], ACT.Sqrt), "root")
                        need(dve, "clip")
                        act.done(a.activation(tmp[:, 10, :, :], tmp[:, 9, :, :], ACT.Ln, bias=1.0, scale=1.0), "ln1")
                        act.done(a.activation(tmp[:, 11, :, :], tmp[:, 9, :, :], ACT.Ln, bias=1.0, scale=-1.0), "ln2")
                    if kind == "heads":
                        a.wait_ge(gathered[h], (k + 1) * 32 * JT)
                        act.done(a.activation(twice[:, :, :, :], mine[:, h, :, 8:].unsqueeze(2).to_broadcast([P, JT, 2, D]),
                                              ACT.Copy), "twice")
                    need(dve, "rise")
                    act.done(a.activation(ex[:, :, :, :], lows[:, :, :, :], ACT.Exp), "ex")
                    if kind != "heads":
                        need(pe, "decay")
                        act.done(a.activation(decay[0:WRUN, 0, :], spread[0][0:WRUN, :], ACT.Copy), "decay")
                    else:
                        need(pe, "decay_row")
                        act.done(a.activation(decay_row_s[:, :], decay_row[0:H, :], ACT.Copy), "decay_row")
                        for q in range(2):
                            need(pe, f"decay{q}")
                            act.done(a.activation(decay[:, q, :], spread[q][:, :], ACT.Copy), f"decay{q}")
                        need(pe, "own")
                        act.done(a.activation(own_row[:, :], spread[0][:, :], ACT.Copy), "own")
                        need(dve, "f2")
                        act.done(a.activation(fin[:, :, :, :], fin[:, :, :, :], ACT.Exp), "exf")
                        need(pe, "share_row")
                        act.done(a.activation(share_row[:, :], decay_row[:, :], ACT.Copy), "share_row")
                    need(pe, "back")
                    a.wait_ge(filed[h], k * 16 * JT)
                    act.done(a.activation(out[:, h, :, :].rearrange("p j w -> p (j w)"), back[:, :], ACT.Copy), "out")
                stages(a, EC, 2, 2, body)

            @block.tensor
            def _(t):
                t.wait_ge(set_up, 1)
                ident = g.ident

                def body(c0, c1, c2):
                    if not c1:
                        return
                    n, h, k = c1.n, c1.slot, c1.k

                    def need(engine, step):
                        t.wait_ge(engine.sem, engine.after(n, step))

                    def mm(out, lhsT, rhs, start=True, stop=True):
                        return t.matmul(out, lhsT=lhsT, rhs=rhs, start=start, stop=stop)

                    def tile(j):
                        return slice(j * P, (j + 1) * P)

                    need(dve, "score")
                    for j in range(JT):
                        last = mm(score_row[:, tile(j)], score[:, j, :], ident[:, :])
                    pe.done(last, "score_row")
                    need(dve, "top")
                    for m in range(2):
                        for j in range(JT):
                            last = mm(top_col[:, (m * JT + j) * H:(m * JT + j + 1) * H],
                                      top[:, h, 1 - m + j * P:1 - m + (j + 1) * P], ident[0:H, 0:H])
                    pe.done(last, "top_col")
                    if kind != "heads":
                        need(act, "ex")
                        if kind == "hyper":
                            need(dve, "decay1")
                        for j in range(JT):
                            last = mm(spread[0][0:WRUN, tile(j)], decays[:, j, :] if kind == "hyper"
                                      else ex[:, 0, j, :].to_broadcast([P, WRUN]), ident[:, :])
                        pe.done(last, "decay")
                        need(dve, "payw" if kind == "hyper" else "pay")
                        for j in range(JT):
                            last = mm(pay_rows[0][0:WRUN, tile(j)], pay[:, j, :], ident[:, :])
                        pe.done(last, "pay")
                        need(dve, "run")
                        for j in range(JT):
                            last = mm(back[:, j * WOUT:j * WOUT + WRUN], run[0:WRUN, h, 0, tile(j)], ident[0:WRUN, 0:WRUN])
                            if kind == "edge":
                                last = mm(back[:, j * WOUT + WRUN:(j + 1) * WOUT],
                                          top[:, h, 1 + j * P:1 + (j + 1) * P], ident[0:1, 0:1])
                        pe.done(last, "back")
                        return
                    need(act, "ex")
                    for what, row in ((1, score_row), (0, decay_row)):
                        for j in range(JT):
                            last = mm(row[0:H, tile(j)], ex[:, what, j, :], ident[:, :])
                        pe.done(last, ("decay_row", "weight_row")[what])

                    def broadcast(rows, what, q, to, step):
                        k = 4 if rows is decay_row_s else 8
                        pe.done(mm(spread[to][:, :], g.pick[0:k, what, q, :], rows[:, :]), step)

                    need(act, "decay_row")
                    broadcast(decay_row_s, 0, 0, 0, "decay0")
                    broadcast(decay_row_s, 0, 1, 1, "decay1")
                    need(dve, "pay")
                    for q in range(2):
                        for j in range(JT):
                            last = mm(pay_rows[q][:, tile(j)], pay[:, j, q * P:(q + 1) * P], ident[:, :])
                    pe.done(last, "pay")
                    need(act, "decay0")
                    for j in range(JT):
                        last = mm(spread[0][:, tile(j)], twice[:, j, :, :].rearrange("p a d -> p (a d)"), ident[:, :])
                    pe.done(last, "own")
                    need(dve, "weights")
                    for j in range(JT):
                        last = mm(top_col[:, (2 * JT + j) * H:(2 * JT + j + 1) * H], weights[:, h, tile(j)], ident[0:H, 0:H])
                    pe.done(last, "wcol")
                    need(dve, "alpha")
                    for j in range(JT):
                        last = mm(decay_row[:, tile(j)], share[:, j, :, :].rearrange("p a q -> p (a q)"), ident[:, :])
                    pe.done(last, "share_row")
                    need(act, "share_row")
                    broadcast(share_row, 0, 0, 1, "beta0")
                    broadcast(share_row, 0, 1, 0, "beta1")
                    need(dve, "z0")
                    broadcast(share_row, 1, 0, 1, "alpha0")
                    need(dve, "z1")
                    broadcast(share_row, 1, 1, 0, "alpha1")
                    need(dve, "z3")
                    for j in range(JT):
                        for m in range(4):
                            last = mm(back[:, j * D:(j + 1) * D], z[:, m, tile(j)], g.w_heads[:, m % 2, :],
                                      start=(m == 0), stop=(m == 3))
                    pe.done(last, "back")
                stages(t, EC, 2, 2, body)
    sem.clear()


LN1 = "total mean centre"
LN2 = "spread var"


class Norm:

    def __init__(self, g, x, squares, small, v_steps, a_steps, p_steps):
        self.g, self.x, self.squares, self.small = g, x, squares, small
        self.v, self.a, self.p = v_steps, a_steps, p_steps

    def centre(self, v, n, b, before):
        steps, x, s = self.v, self.x[:, b, :, :], self.small[:, b]
        v.wait_ge(steps.sem, steps.after(n, before))
        steps.done(v.tensor_reduce(s[:, 0, :], x, AX.X, ALU.add), "total")
        v.wait_ge(steps.sem, steps.after(n, "total"))
        steps.done(v.tensor_scalar(s[:, 1, :], s[:, 0, :], 1.0 / D, None, ALU.mult), "mean")
        v.wait_ge(steps.sem, steps.after(n, "mean"))
        steps.done(v.tensor_tensor(x, x, s[:, 1, :].unsqueeze(2).to_broadcast([P, GROUP, D]), ALU.subtract), "centre")

    def square(self, a, n, b):
        a.wait_ge(self.v.sem, self.v.after(n, "centre"))
        self.a.done(a.activation(self.squares[:, b, :, :], self.x[:, b, :, :], ACT.Square), "lnsq")

    def spread(self, v, n, b):
        steps, s = self.v, self.small[:, b]
        v.wait_ge(self.a.sem, self.a.after(n, "lnsq"))
        steps.done(v.tensor_reduce(s[:, 2, :], self.squares[:, b, :, :], AX.X, ALU.add), "spread")
        v.wait_ge(steps.sem, steps.after(n, "spread"))
        steps.done(v.tensor_scalar(s[:, 3, :], s[:, 2, :], 1.0 / D, LN_EPS, ALU.mult, ALU.add), "var")

    def rstd(self, gp, n, b):
        gp.wait_ge(self.v.sem, self.v.after(n, "var"))
        self.p.done(gp.tensor_tensor(self.small[:, b, 4, :], self.small[:, b, 3, :], self.g.minus_half[:, :], ALU.pow), "rstd")

    def scaled(self, v, out, b):
        return v.tensor_tensor(out, self.x[:, b, :, :],
                               self.small[:, b, 4, :].unsqueeze(2).to_broadcast([P, GROUP, D]), ALU.mult)


def of_node(g, name, n):
    return g.node[name][:, bass.ds(n, 1), :].rearrange("p a j -> p j a")


def close_layer0(nc, g, x, sem):
    ctx = ExitStack()
    with ctx:
        def sb(label, shape, dt=F32):
            return ctx.enter_context(nc.sbuf_tensor(f"c0_{label}", shape, dt))

        xin, att = sb("x", [P, 4, GROUP, D]), sb("att", [P, 4, GROUP, D + 2])
        z1, z2, z3, y = (sb(q, [P, 2, GROUP, D]) for q in ("z1", "z2", "z3", "y"))
        squares = sb("squares", [P, 2, GROUP, D])
        small, t = sb("small", [P, 2, 5, GROUP]), sb("t", [P, 2, 14, GROUP])
        x1, g1 = sb("x1", [P, 4, GROUP, D]), sb("g1", [P, 4, GROUP, D])
        loaded, stored, ready = (sem.quad(f"c0_{q}") for q in ("loaded", "stored", "ready"))
        c = g.cs
        dve = Engine(sem("c0_dve"), "den rden rc att neg elu z z2 zm zr zf zn zi s1 s2 s3 hp y " + LN1)
        act = Engine(sem("c0_act"), "exp relu sq tanh lnsq")
        root, gps = Engine(sem("c0_root"), "zn0"), Engine(sem("c0_gps"), "rstd rso")
        late = Engine(sem("c0_late"), LN2 + " dmax x1 rso")
        norm1 = Norm(g, y, squares, small, dve, act, gps)
        norm2 = Norm(g, y, squares, small, late, act, gps)
        with nc.Block() as block:
            @block.sync
            def _(sp):
                def body(c0, c1, c2):
                    if c0:
                        h, k = c0.slot, c0.k
                        sp.wait_ge(stored[h], k * 32)
                        if isinstance(c0.n, int) and c0.n == CH - 1:
                            sp.dma_start(flat(xin[0:TAIL, h, :, :]), x[(CH - 1) * NODES:N, :]
                                         .rearrange("(p j) k -> p (j k)", j=GROUP)).then_inc(loaded[h], 16)
                        else:
                            sp.dma_start(flat(xin[:, h, :, :]), chunk_rows(x, c0.n, D)).then_inc(loaded[h], 16)
                        sp.dma_start(flat(att[:, h, :, :]), chunk_rows(g.A0, c0.n, D + 2)).then_inc(loaded[h], 16)
                    if c2:
                        n, h = c2.n, c2.slot
                        sp.wait_ge(ready[h], c2.k + 1)
                        sp.dma_start(chunk_rows(g.X1, n, D), flat(x1[:, h, :, :])).then_inc(stored[h], 16)
                        sp.dma_start(chunk_rows(g.G1, n, D), flat(g1[:, h, :, :])).then_inc(stored[h], 16)
                stages(sp, CH, 4, 2, body, tail=1)
                for h in range(4):
                    sp.wait_ge(stored[h], len(range(h, CH, 4)) * 32)

            @block.vector
            def _(v):
                def body(c0, c1, c2):
                    if c1:
                        early(c1)
                    if c2:
                        after(c2)

                def early(ch):
                    n, h, b = ch.n, ch.slot, ch.slot % 2
                    q = [t[:, b, i, :] for i in range(14)]

                    def need(steps, name):
                        v.wait_ge(steps.sem, steps.after(n, name))

                    def per(a):
                        return a.unsqueeze(2).to_broadcast([P, GROUP, D])

                    v.wait_ge(loaded[h], (ch.k + 1) * 32)
                    dve.done(v.tensor_scalar(q[0], att[:, h, :, D], 1e-16, None, ALU.add), "den")
                    need(dve, "den")
                    dve.done(v.reciprocal(q[1], q[0]), "rden")
                    need(dve, "rden")
                    dve.done(v.tensor_scalar(q[2], q[1], c["sqrt"], None, ALU.mult), "rc")
                    need(dve, "rc")
                    dve.done(v.tensor_tensor(z1[:, b, :, :], att[:, h, :, 0:D], per(q[2]), ALU.mult), "att")
                    need(dve, "att")
                    dve.done(v.tensor_scalar(z2[:, b, :, :], z1[:, b, :, :], 0.0, None, ALU.min), "neg")
                    need(act, "relu")
                    dve.done(v.scalar_tensor_tensor(out=z1[:, b, :, :], in0=z2[:, b, :, :], scalar=-1.0, in1=z3[:, b, :, :],
                                                    op0=ALU.add, op1=ALU.add), "elu")
                    need(dve, "elu")
                    dve.done(v.tensor_scalar(z1[:, b, :, :], z1[:, b, :, :], EPS, None, ALU.add), "z")
                    need(act, "sq")
                    dve.done(v.tensor_reduce(q[3], z2[:, b, :, :], AX.X, ALU.add), "z2")
                    need(root, "zn0")
                    dve.done(v.tensor_scalar(q[5], q[4], c["clip"], None, ALU.max), "zm")
                    need(dve, "zm")
                    dve.done(v.reciprocal(q[6], q[5]), "zr")
                    need(dve, "zr")
                    dve.done(v.tensor_scalar(q[7], q[6], c["clip"], None, ALU.mult), "zf")
                    need(dve, "zf")
                    dve.done(v.tensor_tensor(q[8], q[4], q[7], ALU.mult), "zn")
                    need(dve, "zn")
                    dve.done(v.reciprocal(q[9], q[8]), "zi")
                    need(dve, "zi")
                    need(act, "tanh")
                    dve.done(v.tensor_tensor(q[11], q[10], q[9], ALU.mult), "s1")
                    need(dve, "s1")
                    dve.done(v.tensor_tensor(q[12], q[11], q[7], ALU.mult), "s2")
                    need(dve, "s2")
                    dve.done(v.tensor_scalar(q[13], q[12], c["1/sqrt"], None, ALU.mult), "s3")
                    need(dve, "s3")
                    dve.done(v.tensor_tensor(z3[:, b, :, :], z1[:, b, :, :], per(q[13]), ALU.mult), "hp")
                    need(dve, "hp")
                    dve.done(v.tensor_tensor(y[:, b, :, :], z3[:, b, :, :], xin[:, h, :, :], ALU.add), "y")
                    norm1.centre(v, n, b, "y")

                def after(ch):
                    n, h, b = ch.n, ch.slot, ch.slot % 2
                    norm2.spread(v, n, b)
                    late.done(v.tensor_scalar(t[:, b, 0, :], att[:, h, :, D + 1], 1.0, None, ALU.max), "dmax")
                    v.wait_ge(gps.sem, gps.after(n, "rso"))
                    v.wait_ge(stored[h], ch.k * 32)
                    late.done(norm2.scaled(v, x1[:, h, :, :], b), "x1")
                    late.done(v.tensor_copy(of_node(g, "rso", n), t[:, b, 1, :].unsqueeze(2)), "rso")
                    v.wait_ge(late.sem, late.after(n, "x1"))
                    v.tensor_tensor(g1[:, h, :, :], x1[:, h, :, :],
                                    t[:, b, 1, :].unsqueeze(2).to_broadcast([P, GROUP, D]), ALU.mult).then_inc(ready[h], 1)
                stages(v, CH, 4, 2, body)

            @block.scalar
            def _(a):
                def body(c0, c1, c2):
                    if c1:
                        n, b = c1.n, c1.slot % 2
                        a.wait_ge(dve.sem, dve.after(n, "neg"))
                        act.done(a.activation(z2[:, b, :, :], z2[:, b, :, :], ACT.Exp), "exp")
                        act.done(a.activation(z3[:, b, :, :], z1[:, b, :, :], ACT.Relu), "relu")
                        a.wait_ge(dve.sem, dve.after(n, "z"))
                        act.done(a.activation(z2[:, b, :, :], z1[:, b, :, :], ACT.Square), "sq")
                        a.wait_ge(dve.sem, dve.after(n, "zn"))
                        act.done(a.activation(t[:, b, 10, :], t[:, b, 8, :], ACT.Tanh, scale=c["sqrt"]), "tanh")
                        norm1.square(a, n, b)
                stages(a, CH, 4, 2, body)

            @block.gpsimd
            def _(gp):
                def body(c0, c1, c2):
                    if c1:
                        n, b = c1.n, c1.slot % 2
                        gp.wait_ge(dve.sem, dve.after(n, "z2"))
                        root.done(gp.tensor_tensor(t[:, b, 4, :], t[:, b, 3, :], g.half[:, :], ALU.pow), "zn0")
                    if c2:
                        n, h, b = c2.n, c2.slot, c2.slot % 2
                        norm2.rstd(gp, n, b)
                        gp.wait_ge(late.sem, late.after(n, "dmax"))
                        gps.done(gp.tensor_tensor(t[:, b, 1, :], t[:, b, 0, :], g.minus_half[:, :], ALU.pow), "rso")
                stages(gp, CH, 4, 2, body)
    sem.clear()


def convolve(nc, g, last, sem):
    name = "v2" if last else "v1"
    own, sums, weight = (g.H1, g.A2, g.w_conv2) if last else (g.X1, g.A1, g.w_conv1)
    LOADS = 48 if last else 32
    ctx = ExitStack()
    with ctx:
        def sb(label, shape, dt=F32):
            return ctx.enter_context(nc.sbuf_tensor(f"{name}_{label}", shape, dt))

        def ps(label, shape):
            return ctx.enter_context(nc.psum_tensor(f"{name}_{label}", shape, F32))

        x, a_in = sb("x", [P, 4, GROUP, D]), sb("a", [P, 4, GROUP, D + 1])
        s = sb("s", [P, 2, GROUP, D])
        both = sb("both", [P, 2, GROUP, 2 * D])
        small, t = sb("small", [P, 2, 5, GROUP]), sb("t", [P, 2, 2, GROUP])
        both_t = sb("both_t", [P, 2, 2, 4 * P])
        turned = [ps(f"turned{i}", [P, 4 * P]) for i in range(2)]
        result = ps("result", [P, GROUP, D])
        out = sb("out", [P, 4, GROUP, D])
        if last:
            x1 = sb("x1", [P, 4, GROUP, D])
            y, x2, squares = (sb(q, [P, 2, GROUP, D]) for q in ("y", "x2", "squares"))
            x2_t = sb("x2_t", [P, 4 * P])
            turned2 = ps("turned2", [P, 4 * P])
            W2 = D + 8
            heads = [ps(f"heads{i}", [P, 2, 2, W2]) for i in range(2)]
            out2 = sb("out2", [P, 4, GROUP, W2])
        else:
            out2 = sb("out2", [P, 4, GROUP, D])
        loaded, stored, ready = (sem.quad(f"{name}_{q}") for q in ("loaded", "stored", "ready"))
        dve = Engine(sem(f"{name}_dve"), ("dm " if not last else "") + "s u0 u1" + (" y " + LN1 if last else ""))
        act = Engine(sem(f"{name}_act"), "t0 t1" + (" lnsq" if last else " relu"))
        pe = Engine(sem(f"{name}_pe"), "turn result")
        gps = Engine(sem(f"{name}_gps"), "rsi")
        if last:
            late = Engine(sem(f"{name}_late"), LN2 + " x2 row b")
            lact = Engine(sem(f"{name}_lact"), "x2t")
            lpe = Engine(sem(f"{name}_lpe"), "turn2 heads")
            lgps = Engine(sem(f"{name}_lgps"), "rstd")
            norm1 = Norm(g, y, squares, small, dve, act, lgps)
            norm2 = Norm(g, y, squares, small, late, act, lgps)
        with nc.Block() as block:
            @block.sync
            def _(sp):
                def body(c0, c1, c2):
                    if c0:
                        n, h = c0.n, c0.slot
                        sp.wait_ge(stored[h], c0.k * 32)
                        sp.dma_start(flat(x[:, h, :, :]), chunk_rows(own, n, D)).then_inc(loaded[h], 16)
                        sp.dma_start(flat(a_in[:, h, :, :]), chunk_rows(sums, n, D + 1)).then_inc(loaded[h], 16)
                        if last:
                            sp.dma_start(flat(x1[:, h, :, :]), chunk_rows(g.X1, n, D)).then_inc(loaded[h], 16)
                    if c2:
                        n, h = c2.n, c2.slot
                        sp.wait_ge(ready[h], c2.k + 1)
                        first, second = (g.B2, g.X2) if last else (g.H1, g.G2)
                        sp.dma_start(chunk_rows(first, n, D), flat(out[:, h, :, :])).then_inc(stored[h], 16)
                        sp.dma_start(chunk_rows(second, n, D + 8 if last else D), flat(out2[:, h, :, :])).then_inc(stored[h], 16)
                stages(sp, CH, 4, 2, body)
                for h in range(4):
                    sp.wait_ge(stored[h], len(range(h, CH, 4)) * 32)

            @block.vector
            def _(v):
                def body(c0, c1, c2):
                    if c1:
                        n, h, b = c1.n, c1.slot, c1.slot % 2
                        v.wait_ge(loaded[h], (c1.k + 1) * LOADS)
                        if last:
                            rsi = of_node(g, "rsi", n)
                        else:
                            dve.done(v.tensor_scalar(t[:, b, 0, :], a_in[:, h, :, D], 1.0, None, ALU.max), "dm")
                            v.wait_ge(gps.sem, gps.after(n, "rsi"))
                            v.tensor_copy(of_node(g, "rsi", n), t[:, b, 1, :].unsqueeze(2))
                            rsi = t[:, b, 1, :].unsqueeze(2)
                        dve.done(v.tensor_tensor(s[:, b, :, :], a_in[:, h, :, 0:D], rsi.to_broadcast([P, GROUP, D]), ALU.mult), "s")
                        v.wait_ge(dve.sem, dve.after(n, "s"))
                        dve.done(v.tensor_tensor(both[:, b, :, 0:D], s[:, b, :, :], x[:, h, :, :], ALU.add), "u0")
                        dve.done(v.tensor_tensor(both[:, b, :, D:], s[:, b, :, :], x[:, h, :, :], ALU.mult), "u1")
                        if last:
                            v.wait_ge(pe.sem, pe.after(n, "result"))
                            dve.done(v.tensor_tensor(y[:, b, :, :], result[:, :, :], x1[:, h, :, :], ALU.add), "y")
                            norm1.centre(v, n, b, "y")
                        else:
                            v.wait_ge(act.sem, act.after(n, "relu"))
                            v.tensor_tensor(out2[:, h, :, :], out[:, h, :, :],
                                            of_node(g, "rso", n).to_broadcast([P, GROUP, D]), ALU.mult).then_inc(ready[h], 1)
                    if c2 and last:
                        n, h, b = c2.n, c2.slot, c2.slot % 2
                        norm2.spread(v, n, b)
                        v.wait_ge(lgps.sem, lgps.after(n, "rstd"))
                        late.done(norm2.scaled(v, x2[:, b, :, :], b), "x2")
                        v.wait_ge(stored[h], c2.k * 32)
                        v.wait_ge(late.sem, late.after(n, "x2"))
                        late.done(v.tensor_copy(out2[:, h, :, 8:], x2[:, b, :, :]), "row")
                        v.wait_ge(lpe.sem, lpe.after(n, "heads"))
                        v.wait_ge(late.sem, late.after(n, "row"))
                        for i in range(2):
                            part = heads[i][:, :, :, :].rearrange("p q a k -> p (q a) k")
                            v.tensor_copy(out2[:, h, 4 * i:4 * i + 4, 0:8], part[:, :, 0:8])
                            step = v.tensor_tensor(x2[:, b, 4 * i:4 * i + 4, :], x2[:, b, 4 * i:4 * i + 4, :], part[:, :, 8:], ALU.add)
                        late.done(step, "b")
                        v.wait_ge(late.sem, late.after(n, "b"))
                        v.tensor_tensor(out[:, h, :, :], x2[:, b, :, :],
                                        g.bias[:, :].unsqueeze(1).to_broadcast([P, GROUP, D]), ALU.add).then_inc(ready[h], 1)
                stages(v, CH, 4, 2, body)

            @block.tensor
            def _(te):
                def body(c0, c1, c2):
                    if c1:
                        n, b = c1.n, c1.slot % 2
                        te.wait_ge(dve.sem, dve.after(n, "u1"))
                        for j in range(GROUP):
                            step = te.matmul(turned[j // 4][:, (j % 4) * P:(j % 4 + 1) * P], lhsT=both[:, b, j, :],
                                             rhs=g.ident[:, :], start=True, stop=True)
                        pe.done(step, "turn")
                        te.wait_ge(act.sem, act.after(n, "t1"))
                        for j in range(GROUP):
                            step = te.matmul(result[:, j, :], lhsT=both_t[:, b, j // 4, (j % 4) * P:(j % 4 + 1) * P],
                                             rhs=weight[:, :], start=True, stop=True)
                        pe.done(step, "result")
                    if c2 and last:
                        n, b = c2.n, c2.slot % 2
                        te.wait_ge(late.sem, late.after(n, "x2"))
                        for q in range(GROUP // 2):
                            step = te.matmul(turned2[:, q * P:(q + 1) * P],
                                             lhsT=x2[:, b, 2 * q:2 * q + 2, :].rearrange("p a d -> p (a d)"),
                                             rhs=g.ident[:, :], start=True, stop=True)
                        lpe.done(step, "turn2")
                        te.wait_ge(lact.sem, lact.after(n, "x2t"))
                        for q in range(GROUP // 2):
                            step = te.matmul(heads[q // 2][:, q % 2, :, :].rearrange("p a k -> p (a k)"),
                                             lhsT=x2_t[:, q * P:(q + 1) * P],
                                             rhs=g.w2_pair[:, :, :].rearrange("p a k -> p (a k)"), start=True, stop=True)
                        lpe.done(step, "heads")
                stages(te, CH, 4, 2, body)

            @block.scalar
            def _(a):
                def body(c0, c1, c2):
                    if c1:
                        n, h, b = c1.n, c1.slot, c1.slot % 2
                        a.wait_ge(pe.sem, pe.after(n, "turn"))
                        for i in range(2):
                            act.done(a.activation(both_t[:, b, i, :], turned[i][:, :], ACT.Copy), f"t{i}")
                        if last:
                            norm1.square(a, n, b)
                        else:
                            a.wait_ge(stored[h], c1.k * 32)
                            a.wait_ge(pe.sem, pe.after(n, "result"))
                            act.done(a.activation(out[:, h, :, :], result[:, :, :], ACT.Relu), "relu")
                    if c2 and last:
                        n = c2.n
                        a.wait_ge(lpe.sem, lpe.after(n, "turn2"))
                        lact.done(a.activation(x2_t[:, :], turned2[:, :], ACT.Copy), "x2t")
                stages(a, CH, 4, 2, body)

            @block.gpsimd
            def _(gp):
                def body(c0, c1, c2):
                    if c1 and not last:
                        n, b = c1.n, c1.slot % 2
                        gp.wait_ge(dve.sem, dve.after(n, "dm"))
                        gps.done(gp.tensor_tensor(t[:, b, 1, :], t[:, b, 0, :], g.minus_half[:, :], ALU.pow), "rsi")
                    if c2 and last:
                        norm2.rstd(gp, c2.n, c2.slot % 2)
                stages(gp, CH, 4, 2, body)
    sem.clear()


def close_layer2(nc, g, sem):
    ctx = ExitStack()
    with ctx:
        def sb(label, shape, dt=F32):
            return ctx.enter_context(nc.sbuf_tensor(f"c2_{label}", shape, dt))

        def ps(label, shape):
            return ctx.enter_context(nc.psum_tensor(f"c2_{label}", shape, F32))

        base, more = sb("base", [P, 4, GROUP, D]), sb("more", [P, 4, GROUP, D])
        y, x3, squares = (sb(q, [P, 2, GROUP, D]) for q in ("y", "x3", "squares"))
        small = sb("small", [P, 2, 5, GROUP])
        x3_t = sb("x3_t", [P, 4 * P])
        turned = ps("turned", [P, 4 * P])
        scores = ps("scores", [P, GROUP, 2])
        row, pair = sb("row", [P, 4, GROUP, D + 2]), sb("pair", [P, 4, GROUP, 2])
        loaded, stored, ready = (sem.quad(f"c2_{q}") for q in ("loaded", "stored", "ready"))
        dve, act = Engine(sem("c2_dve"), "y " + LN1), Engine(sem("c2_act"), "lnsq")
        late = Engine(sem("c2_late"), LN2 + " x3")
        lact, lpe, gps = Engine(sem("c2_lact"), "x3t"), Engine(sem("c2_lpe"), "turn scores"), Engine(sem("c2_gps"), "rstd")
        norm1 = Norm(g, y, squares, small, dve, act, gps)
        norm2 = Norm(g, y, squares, small, late, act, gps)
        ones_set = sem("c2_ones")
        with nc.Block() as block:
            @block.sync
            def _(sp):
                def body(c0, c1, c2):
                    if c0:
                        n, h = c0.n, c0.slot
                        sp.wait_ge(stored[h], c0.k * 32)
                        sp.dma_start(flat(base[:, h, :, :]), chunk_rows(g.B2, n, D)).then_inc(loaded[h], 16)
                        sp.dma_start(flat(more[:, h, :, :]), chunk_rows(g.A3, n, D)).then_inc(loaded[h], 16)
                    if c2:
                        n, h = c2.n, c2.slot
                        sp.wait_ge(ready[h], c2.k + 1)
                        sp.dma_start(chunk_rows(g.X3, n, D + 2), flat(row[:, h, :, :])).then_inc(stored[h], 16)
                        sp.dma_start(chunk_rows(g.S3, n, 2), flat(pair[:, h, :, :])).then_inc(stored[h], 16)
                stages(sp, CH, 4, 2, body)
                for h in range(4):
                    sp.wait_ge(stored[h], len(range(h, CH, 4)) * 32)

            @block.vector
            def _(v):
                v.memset(row[:, :, :, D + 1:], 1.0).then_inc(ones_set, 1)
                v.wait_ge(ones_set, 1)

                def body(c0, c1, c2):
                    if c1:
                        n, h, b = c1.n, c1.slot, c1.slot % 2
                        v.wait_ge(loaded[h], (c1.k + 1) * 32)
                        dve.done(v.tensor_tensor(y[:, b, :, :], base[:, h, :, :], more[:, h, :, :], ALU.add), "y")
                        norm1.centre(v, n, b, "y")
                    if c2:
                        n, h, b = c2.n, c2.slot, c2.slot % 2
                        norm2.spread(v, n, b)
                        v.wait_ge(gps.sem, gps.after(n, "rstd"))
                        late.done(norm2.scaled(v, x3[:, b, :, :], b), "x3")
                        v.wait_ge(stored[h], c2.k * 32)
                        v.wait_ge(late.sem, late.after(n, "x3"))
                        v.tensor_copy(row[:, h, :, 1:D + 1], x3[:, b, :, :])
                        v.wait_ge(lpe.sem, lpe.after(n, "scores"))
                        v.tensor_copy(row[:, h, :, 0:1], scores[:, :, 1:2])
                        v.tensor_copy(pair[:, h, :, :], scores[:, :, :]).then_inc(ready[h], 1)
                stages(v, CH, 4, 2, body)

            @block.tensor
            def _(te):
                def body(c0, c1, c2):
                    if c2:
                        n, b = c2.n, c2.slot % 2
                        te.wait_ge(late.sem, late.after(n, "x3"))
                        for q in range(GROUP // 2):
                            step = te.matmul(turned[:, q * P:(q + 1) * P],
                                             lhsT=x3[:, b, 2 * q:2 * q + 2, :].rearrange("p a d -> p (a d)"),
                                             rhs=g.ident[:, :], start=True, stop=True)
                        lpe.done(step, "turn")
                        te.wait_ge(lact.sem, lact.after(n, "x3t"))
                        for q in range(GROUP // 2):
                            step = te.matmul(scores[:, 2 * q:2 * q + 2, :].rearrange("p a k -> p (a k)"),
                                             lhsT=x3_t[:, q * P:(q + 1) * P],
                                             rhs=g.a3_pair[:, :, :].rearrange("p a k -> p (a k)"), start=True, stop=True)
                        lpe.done(step, "scores")
                stages(te, CH, 4, 2, body)

            @block.scalar
            def _(a):
                def body(c0, c1, c2):
                    if c1:
                        norm1.square(a, c1.n, c1.slot % 2)
                    if c2:
                        a.wait_ge(lpe.sem, lpe.after(c2.n, "turn"))
                        lact.done(a.activation(x3_t[:, :], turned[:, :], ACT.Copy), "x3t")
                stages(a, CH, 4, 2, body)

            @block.gpsimd
            def _(gp):
                def body(c0, c1, c2):
                    if c2:
                        norm2.rstd(gp, c2.n, c2.slot % 2)
                stages(gp, CH, 4, 2, body)
    sem.clear()


def close_layer3(nc, g, out_rows, sem):
    ctx = ExitStack()
    with ctx:
        def sb(label, shape, dt=F32):
            return ctx.enter_context(nc.sbuf_tensor(f"c3_{label}", shape, dt))

        def ps(label, shape):
            return ctx.enter_context(nc.psum_tensor(f"c3_{label}", shape, F32))

        x3, pair = sb("x3", [P, 4, GROUP, D + 2]), sb("pair", [P, 4, GROUP, 2])
        part = sb("part", [P, 4, 2, GROUP, D + 2])
        t = sb("t", [P, 2, 16, GROUP])
        logs = sb("logs", [P, 2, 3, GROUP])
        share = sb("share", [P, 2, 3, GROUP])
        p0, p1, y, squares = (sb(q, [P, 2, GROUP, D]) for q in ("p0", "p1", "y", "squares"))
        small = sb("small", [P, 2, 5, GROUP])
        pt = sb("pt", [P, 2, 4 * P])
        turned = [ps(f"turned{i}", [P, 4 * P]) for i in range(2)]
        result = [ps(f"result{i}", [P, GROUP, D]) for i in range(2)]
        out = sb("out", [P, 4, GROUP, D])
        loaded, stored, ready = (sem.quad(f"c3_{q}") for q in ("loaded", "stored", "ready"))
        dve = Engine(sem("c3_dve"), "l0 loop has none m0 m1 top0 top rise w0 d0 d1 d2 den shares q0 q1 q2 r0 r1")
        act = Engine(sem("c3_act"), "ex pt")
        pe = Engine(sem("c3_pe"), "turn result")
        late = Engine(sem("c3_late"), "y " + LN1 + " " + LN2)
        lact, gps = Engine(sem("c3_lact"), "lnsq"), Engine(sem("c3_gps"), "rstd")
        norm = Norm(g, y, squares, small, late, lact, gps)
        with nc.Block() as block:
            @block.sync
            def _(sp):
                def body(c0, c1, c2):
                    if c0:
                        n, h = c0.n, c0.slot
                        sp.wait_ge(stored[h], c0.k * 16)
                        sp.dma_start(flat(x3[:, h, :, :]), chunk_rows(g.X3, n, D + 2)).then_inc(loaded[h], 16)
                        sp.dma_start(flat(pair[:, h, :, :]), chunk_rows(g.S3, n, 2)).then_inc(loaded[h], 16)
                        sp.dma_start(flat(part[:, h, 0, :, :]), chunk_rows(g.A4[1], n, D + 2)).then_inc(loaded[h], 16)
                        sp.dma_start(flat(part[:, h, 1, :, :]), chunk_rows(g.A4[0], n, D + 2)).then_inc(loaded[h], 16)
                    if c2:
                        n, h = c2.n, c2.slot
                        sp.wait_ge(ready[h], c2.k + 1)
                        if isinstance(n, int) and n == CH - 1:
                            sp.dma_start(out_rows[(CH - 1) * NODES:N, :].rearrange("(p j) k -> p (j k)", j=GROUP),
                                         flat(out[0:TAIL, h, :, :])).then_inc(stored[h], 16)
                        else:
                            sp.dma_start(chunk_rows(out_rows, n, D), flat(out[:, h, :, :])).then_inc(stored[h], 16)
                stages(sp, CH, 4, 2, body)
                for h in range(4):
                    sp.wait_ge(stored[h], len(range(h, CH, 4)) * 16)

            @block.vector
            def _(v):
                def body(c0, c1, c2):
                    if c1:
                        early(c1)
                    if c2:
                        n, h, b = c2.n, c2.slot, c2.slot % 2
                        v.wait_ge(pe.sem, pe.after(n, "result"))
                        late.done(v.tensor_tensor(y[:, b, :, :], result[b][:, :, :], x3[:, h, :, 1:D + 1], ALU.add), "y")
                        norm.centre(v, n, b, "y")
                        norm.spread(v, n, b)
                        v.wait_ge(gps.sem, gps.after(n, "rstd"))
                        v.wait_ge(stored[h], c2.k * 16)
                        norm.scaled(v, out[:, h, :, :], b).then_inc(ready[h], 1)

                def early(ch):
                    n, h, b = ch.n, ch.slot, ch.slot % 2
                    q = [t[:, b, i, :] for i in range(16)]
                    pt2 = part[:, h, :, :, :]

                    def need(steps, name):
                        v.wait_ge(steps.sem, steps.after(n, name))

                    def two(i):
                        return t[:, b, i:i + 2, :]

                    v.wait_ge(loaded[h], (ch.k + 1) * 64)
                    dve.done(v.tensor_tensor(q[0], pair[:, h, :, 0], pair[:, h, :, 1], ALU.add), "l0")
                    need(dve, "l0")
                    dve.done(v.scalar_tensor_tensor(out=logs[:, b, 2, :], in0=q[0], scalar=SLOPE, in1=q[0], op0=ALU.mult, op1=ALU.max), "loop")
                    dve.done(v.tensor_scalar(two(2), pt2[:, :, :, D], 0.0, None, ALU.is_gt), "has")
                    need(dve, "has")
                    dve.done(v.tensor_scalar(two(4), two(2), -1.0, -NEG, ALU.add, ALU.mult), "none")
                    dve.done(v.tensor_tensor(two(6), pt2[:, :, :, D + 1], two(2), ALU.mult), "m0")
                    need(dve, "m0")
                    dve.done(v.tensor_tensor(logs[:, b, 0:2, :], two(6), two(4), ALU.add), "m1")
                    need(dve, "m1")
                    dve.done(v.tensor_tensor(q[8], logs[:, b, 0, :], logs[:, b, 1, :], ALU.max), "top0")
                    need(dve, "top0")
                    dve.done(v.tensor_tensor(q[9], q[8], logs[:, b, 2, :], ALU.max), "top")
                    need(dve, "top")
                    dve.done(v.tensor_tensor(logs[:, b, :, :], logs[:, b, :, :], q[9].unsqueeze(1).to_broadcast([P, 3, GROUP]), ALU.subtract), "rise")
                    need(act, "ex")
                    dve.done(v.tensor_tensor(two(10), pt2[:, :, :, D], logs[:, b, 0:2, :], ALU.mult), "w0")
                    need(dve, "w0")
                    dve.done(v.tensor_tensor(q[12], q[10], q[11], ALU.add), "d0")
                    need(dve, "d0")
                    dve.done(v.tensor_tensor(q[13], q[12], logs[:, b, 2, :], ALU.add), "d1")
                    need(dve, "d1")
                    dve.done(v.reciprocal(q[14], q[13]), "d2")
                    need(dve, "d2")
                    dve.done(v.tensor_copy(q[15], q[14]), "den")
                    dve.done(v.tensor_tensor(share[:, b, :, :], logs[:, b, :, :], q[14].unsqueeze(1).to_broadcast([P, 3, GROUP]), ALU.mult), "shares")
                    need(dve, "shares")

                    def of(i):
                        return share[:, b, i, :].unsqueeze(2).to_broadcast([P, GROUP, D])

                    dve.done(v.tensor_tensor(p0[:, b, :, :], pt2[:, 0, :, 0:D], of(0), ALU.mult), "q0")
                    dve.done(v.tensor_tensor(p1[:, b, :, :], pt2[:, 1, :, 0:D], of(1), ALU.mult), "q1")
                    need(dve, "q1")
                    dve.done(v.tensor_tensor(p0[:, b, :, :], p0[:, b, :, :], p1[:, b, :, :], ALU.add), "q2")
                    need(dve, "q2")
                    dve.done(v.tensor_tensor(p1[:, b, :, :], x3[:, h, :, 1:D + 1], of(2), ALU.mult), "r0")
                    need(dve, "r0")
                    dve.done(v.tensor_tensor(p0[:, b, :, :], p0[:, b, :, :], p1[:, b, :, :], ALU.add), "r1")
                stages(v, CH, 4, 2, body)

            @block.tensor
            def _(te):
                def body(c0, c1, c2):
                    if c1:
                        n, b = c1.n, c1.slot % 2
                        te.wait_ge(dve.sem, dve.after(n, "r1"))
                        for q in range(GROUP // 2):
                            step = te.matmul(turned[b][:, q * P:(q + 1) * P],
                                             lhsT=p0[:, b, 2 * q:2 * q + 2, :].rearrange("p a d -> p (a d)"),
                                             rhs=g.ident[:, :], start=True, stop=True)
                        pe.done(step, "turn")
                        te.wait_ge(act.sem, act.after(n, "pt"))
                        for q in range(GROUP // 2):
                            step = te.matmul(result[b][:, 2 * q:2 * q + 2, :].rearrange("p a k -> p (a k)"),
                                             lhsT=pt[:, b, q * P:(q + 1) * P],
                                             rhs=g.w3_pair[:, :, :].rearrange("p a k -> p (a k)"), start=True, stop=True)
                        pe.done(step, "result")
                stages(te, CH, 4, 2, body)

            @block.scalar
            def _(a):
                def body(c0, c1, c2):
                    if c1:
                        n, b = c1.n, c1.slot % 2
                        a.wait_ge(dve.sem, dve.after(n, "rise"))
                        act.done(a.activation(logs[:, b, :, :], logs[:, b, :, :], ACT.Exp), "ex")
                        a.wait_ge(pe.sem, pe.after(n, "turn"))
                        act.done(a.activation(pt[:, b, :], turned[b][:, :], ACT.Copy), "pt")
                    if c2:
                        norm.square(a, c2.n, c2.slot % 2)
                stages(a, CH, 4, 2, body)

            @block.gpsimd
            def _(gp):
                def body(c0, c1, c2):
                    if c2:
                        norm.rstd(gp, c2.n, c2.slot % 2)
                stages(gp, CH, 4, 2, body)
    sem.clear()


class Bag:
    pass


def gnn_kernel(nc, x, src, dst, edge_attr_16, L0_gnn_W, L0_gnn_c, L1_gnn_W1_1, L1_gnn_W2_1, L1_gnn_W1_2,
               L1_gnn_W2_2, L2_gnn_W, L2_gnn_att_src, L2_gnn_att_dst, L2_gnn_bias, L3_gnn_W, L3_gnn_a, out,
               table=None):
    def dram(name, rows, width, dt=F32):
        if table:
            return table(name, rows, width, dt)
        return nc.dram_tensor(name, (rows, width), dt).ap()

    g, w = Bag(), Bag()
    w.L0_W, w.L0_c, w.L2_W, w.L2_bias, w.L3_W, w.L3_a = L0_gnn_W, L0_gnn_c, L2_gnn_W, L2_gnn_bias, L3_gnn_W, L3_gnn_a
    w.L2_att_dst, w.L2_att_src = L2_gnn_att_dst, L2_gnn_att_src
    w.L1_W1_1, w.L1_W2_1, w.L1_W1_2, w.L1_W2_2 = L1_gnn_W1_1, L1_gnn_W2_1, L1_gnn_W1_2, L1_gnn_W2_2
    w.loads = 20
    g.mid0 = [dram(f"mid0_{s}", EP, 4, I32) for s in range(ORDERS)]
    g.mid1 = [dram(f"mid1_{s}", EP, 4, I32) for s in range(ORDERS)]
    g.sorted = [dram(f"sorted_{s}", EP + 2, 4, I32) for s in range(ORDERS)]
    g.same_row = [dram(f"same_row{s}", 1, EP) for s in range(ORDERS)]
    g.pen_row = [dram(f"pen_row{s}", 1, EP) for s in range(ORDERS)]
    g.Y, g.T0 = dram("Y", NP, D), dram("T0", NP, D + 2)
    g.X1, g.G1, g.H1, g.G2 = (dram(q, NP, D) for q in ("X1", "G1", "H1", "G2"))
    g.X2, g.B2, g.X3, g.S3 = dram("X2", NP, D + 8), dram("B2", NP, D), dram("X3", NP, D + 2), dram("S3", NP, 2)
    g.A0, g.A1, g.A2, g.A3 = dram("A0", NP, D + 2), dram("A1", NP, D + 1), dram("A2", NP, D + 1), dram("A3", NP, D)
    g.A4 = [dram(f"A4_{s}", NP, D + 2) for s in range(ORDERS)]
    g.zeroed_tables = [(g.A0, D + 2), (g.A1, D + 1), (g.A2, D + 1), (g.A3, D), (g.A4[0], D + 2), (g.A4[1], D + 2)]

    ctx = ExitStack()
    with ctx:
        def sb(name, shape, dt=F32):
            return ctx.enter_context(nc.sbuf_tensor(name, shape, dt))

        g.ident = sb("ident", [P, P])
        g.zeros_bf = sb("zeros_bf", [P, 512], BF16)
        g.zero_rows = sb("zero_rows", [P, GROUP * (D + 2)])
        g.half, g.minus_half = sb("half", [P, GROUP]), sb("minus_half", [P, GROUP])
        g.pick = sb("pick", [8, 2, 2, P])
        g.w0_pair, g.w2_pair = sb("w0_pair", [P, 2, D + 2]), sb("w2_pair", [P, 2, D + 8])
        g.a3_pair, g.w3_pair = sb("a3_pair", [P, 2, 2]), sb("w3_pair", [P, 2, D])
        g.w_heads = sb("w_heads", [P, 2, D])
        g.w_conv1, g.w_conv2 = sb("w_conv1", [P, D]), sb("w_conv2", [P, D])
        g.bias, g.k_row, g.k_cols = sb("bias", [P, D]), sb("k_row", [P, D]), sb("k_cols", [P, 2])
        g.c_cols = sb("c_cols", [P, 8])
        g.cs = {q: g.c_cols[:, i:i + 1] for i, q in enumerate(("c", "sqrt", "1/sqrt", "clip", "-2c", "c*c"))}
        g.rows = [sb(f"rows{s}", [P, EC, 3 * JT], I32) for s in range(ORDERS)]
        g.pen = [sb(f"pen{s}", [P, EC, JT]) for s in range(ORDERS)]
        g.contrib = [sb(f"contrib{s}", [P, EC, JT]) for s in range(ORDERS)]
        g.same = [sb(f"same{s}", [P, EC, JT]) for s in range(ORDERS)]
        g.node = {q: sb(f"node_{q}", [P, CH, GROUP]) for q in
                  "n2 sf y2 yk sy nh2 zeta s1 s2 rso rsi".split()}
        sem = Semaphores(nc)
        set_up(nc, g, w, sem)
        sort_edges(nc, g, src, dst, L3_gnn_a, edge_attr_16, sem)
        lay_out_edges(nc, g, sem)
        project(nc, g, x, sem)
        factors(nc, g, sem)
        place(nc, g, sem)
        attend_edges(nc, g, "e0", 0, "hyper", g.T0, g.T0, g.A0, sem)
        close_layer0(nc, g, x, sem)
        sum_edges(nc, g, "e1", g.G1, g.A1, sem)
        convolve(nc, g, False, sem)
        sum_edges(nc, g, "e2", g.G2, g.A2, sem)
        convolve(nc, g, True, sem)
        attend_edges(nc, g, "e3", 1, "heads", g.X2, g.X2, g.A3, sem)
        close_layer2(nc, g, sem)
        attend_edges(nc, g, "e4d", 1, "edge", g.S3, g.X3, g.A4[1], sem)
        attend_edges(nc, g, "e4s", 0, "edge", g.S3, g.X3, g.A4[0], sem)
        close_layer3(nc, g, out, sem)


_INS = ["x", "src", "dst", "edge_attr_16", "L0_gnn_W", "L0_gnn_c", "L1_gnn_W1_1", "L1_gnn_W2_1", "L1_gnn_W1_2",
        "L1_gnn_W2_2", "L2_gnn_W", "L2_gnn_att_src", "L2_gnn_att_dst", "L2_gnn_bias", "L3_gnn_W", "L3_gnn_a"]
_OUT = ((N, D), "float32")


def kernel(**inputs):
    import numpy as np
    import concourse.bacc as bacc
    from concourse.bass_utils import run_bass_kernel_spmd

    nc = bacc.Bacc("TRN2", target_bir_lowering=False, num_devices=1)
    arrays, args = {}, []
    for name in _INS:
        a = np.ascontiguousarray(inputs[name])
        arrays[f"in_{name}"] = a
        args.append(nc.dram_tensor(f"in_{name}", a.shape, mybir.dt.from_np(a.dtype), kind="ExternalInput").ap())
    result = nc.dram_tensor("out_rows", _OUT[0], mybir.dt.from_np(np.dtype(_OUT[1])), kind="ExternalOutput").ap()
    gnn_kernel(nc, *args, result)
    return run_bass_kernel_spmd(nc, [arrays], core_ids=[0]).results[0]["out_rows"]
```

```python
import math
from contextlib import ExitStack

import concourse.bass as bass
from concourse import mybir

F32 = mybir.dt.float32
I32 = mybir.dt.int32
BF16 = mybir.dt.bfloat16
F16 = mybir.dt.float16
ALU = mybir.AluOpType
ACT = mybir.ActivationFunctionType
AX = mybir.AxisListType

P = 128
D = 64
HEADS = 4
N = 100000
E = 50000
GROUP = 8
NODES = P * GROUP
CH = -(-N // NODES)
NP = CH * NODES
TAIL = (N - (CH - 1) * NODES) // GROUP
JT = 4
EDGES = P * JT
EC = -(-E // EDGES)
EP = EC * EDGES
TILES = EP // P
PAD_KEY = NP - 1
SKIP = 1 << 20
LOW = 256
HIGH = NP // LOW
LAST_E = E - (P - 1) * TILES
EPS, CLIP, LN_EPS, SLOPE = 1e-15, 0.98, 1e-5, 0.2
NEG = -1e30
ORDERS = 2

assert (N - (CH - 1) * NODES) % GROUP == 0 and EC == CH and HIGH <= 512


class Chunk:

    def __init__(self, i, r, unroll):
        self.n = i * unroll + r
        self.slot = r % unroll
        self.k = i + r // unroll


def stages(eng, count, unroll, skew, body, tail=0):
    def single(n):
        body(*[Chunk(0, n - s, unroll) if 0 <= n - s < count else None for s in range(skew + 1)])

    first = skew + unroll
    for n in range(first):
        single(n)
    loops = (count - first - tail) // unroll
    with eng.Fori(0, loops) as i:
        for u in range(unroll):
            body(*[Chunk(i, first + u - s, unroll) for s in range(skew + 1)])
    for n in range(first + loops * unroll, count + skew):
        single(n)


class Engine:

    def __init__(self, sem, names):
        self.sem, self.names, self.next = sem, names.split(), 0

    def done(self, instruction, name):
        assert self.names[self.next % len(self.names)] == name, (name, self.names[self.next % len(self.names)])
        self.next += 1
        instruction.then_inc(self.sem, 1)

    def after(self, n, name):
        return n * len(self.names) + self.names.index(name) + 1


class Semaphores:

    def __init__(self, nc):
        self.nc, self.held, self.n = nc, [], 0

    def __call__(self, name):
        s = self.nc.alloc_semaphore(name)
        self.held.append(s)
        return s

    def pair(self, name):
        return [self(f"{name}{h}") for h in range(2)]

    def quad(self, name):
        return [self(f"{name}{h}") for h in range(4)]

    def clear(self):
        self.nc.clear_and_free_semaphores(self.held)
        self.held = []
        self.nc.all_engine_barrier()


def lay_out_edges(nc, g, sem):
    for s in range(ORDERS):
        ctx = ExitStack()
        with ctx:
            def sb(name, shape, dt):
                return ctx.enter_context(nc.sbuf_tensor(name, shape, dt))

            rows = [sb(f"lay_rows{s}{q}", [EC, EDGES, 4], I32) for q in range(3)]
            key = [sb(f"lay_key{s}{q}", [EC, EDGES], F32) for q in range(3)]
            other = sb(f"lay_other{s}", [EC, EDGES], F32)
            contrib = sb(f"lay_contrib{s}", [EC, EDGES], F32)
            same = sb(f"lay_same{s}", [EC, EDGES], F32)
            more = sb(f"lay_more{s}", [EC, EDGES], F32)
            scat = sb(f"lay_scat{s}", [EC, EDGES], F32)
            pen = sb(f"lay_pen{s}", [EC, EDGES], F32)
            flat = [key[1], other, scat, pen, contrib, same]
            turned = [ctx.enter_context(nc.psum_tensor(f"lay_turned{s}{a}", [P, JT * EC], F32)) for a in range(6)]
            loaded, split, turn, stored = (sem(f"lay_{x}{s}") for x in ("loaded", "split", "turn", "stored"))
            with nc.Block() as block:
                @block.sync
                def _(sp):
                    for q in range(3):
                        sp.dma_start(rows[q][:, :, :].rearrange("p t k -> p (t k)"),
                                     g.sorted[s][q:q + EP, :].rearrange("(p t) k -> p (t k)", p=EC)).then_inc(loaded, 16)
                    sp.wait_ge(split, 3)
                    sp.dma_start(g.same_row[s][:, :].rearrange("a (p t) -> (a p) t", p=EC), same[:, :]).then_inc(stored, 16)
                    sp.dma_start(g.pen_row[s][:, :].rearrange("a (p t) -> (a p) t", p=EC), pen[:, :]).then_inc(stored, 16)
                    sp.wait_ge(stored, 32)

                @block.vector
                def _(v):
                    v.wait_ge(loaded, 48)
                    for q in range(3):
                        v.tensor_copy(key[q][:, :], rows[q][:, :, 0])
                    v.tensor_copy(other[:, :], rows[1][:, :, 1])
                    v.tensor_copy(contrib[:, :], rows[1][:, :, 2].bitcast(F32)).then_inc(split, 1)
                    v.wait_ge(split, 1)
                    v.tensor_tensor(same[:, :], key[1][:, :], key[0][:, :], ALU.is_equal)
                    v.tensor_tensor(more[:, :], key[1][:, :], key[2][:, :], ALU.is_equal).then_inc(split, 1)
                    v.wait_ge(split, 2)
                    v.tensor_scalar(pen[:, :], same[:, :], -1.0, -NEG, ALU.add, ALU.mult)
                    v.scalar_tensor_tensor(out=scat[:, :], in0=more[:, :], scalar=float(SKIP), in1=key[1][:, :],
                                           op0=ALU.mult, op1=ALU.add).then_inc(split, 1)
                    v.wait_ge(turn, 1)
                    for a in range(3):
                        v.tensor_copy(g.rows[s][:, :, a * JT:(a + 1) * JT],
                                      turned[a][:, :].rearrange("p (j c) -> p c j", j=JT))
                    for a, out in ((3, g.pen[s]), (4, g.contrib[s]), (5, g.same[s])):
                        last = v.tensor_copy(out[:, :, :], turned[a][:, :].rearrange("p (j c) -> p c j", j=JT))
                    last.then_inc(split, 1)

                @block.tensor
                def _(pe):
                    pe.wait_ge(split, 3)
                    for a in range(6):
                        for j in range(JT):
                            last = pe.transpose(turned[a][:, j * EC:(j + 1) * EC], flat[a][:, j * P:(j + 1) * P], g.ident[0:EC, 0:EC])
                    last.then_inc(turn, 1)
        sem.clear()


def sum_edges(nc, g, name, table, sums, sem):
    W = D + 1
    s = 1
    ctx = ExitStack()
    with ctx:
        def sb(label, shape, dt=F32):
            return ctx.enter_context(nc.sbuf_tensor(f"{name}_{label}", shape, dt))

        def ps(label, shape):
            return ctx.enter_context(nc.psum_tensor(f"{name}_{label}", shape, F32))

        from_rows = sb("from_rows", [P, 2, JT], I32)
        to_rows = sb("to_rows", [P, 2, JT], I32)
        got = sb("got", [P, 2, JT, W])
        same = sb("same_b", [W, 2, EDGES])
        run = sb("run", [W, 2, EDGES])
        out = sb("out", [P, 2, JT, W])
        turned = [ps(f"turned{h}", [W, EDGES]) for h in range(2)]
        back = [ps(f"back{h}", [P, JT * W]) for h in range(2)]
        from_ready, gathered, same_loaded, flipped, scanned, unflipped, out_ready, to_ready, filed = (
            sem.pair(f"{name}_{x}") for x in ("from_ready", "gathered", "same_loaded", "flipped", "scanned",
                                             "unflipped", "out_ready", "to_ready", "filed"))
        set_up = sem(f"{name}_set_up")
        with nc.Block() as block:
            @block.sync
            def _(sp):
                def body(c0, c1, c2):
                    if c0:
                        h, k = c0.slot, c0.k
                        sp.wait_ge(scanned[h], k)
                        sp.dma_start(same[:, h, :], g.same_row[s][:, bass.ds(c0.n * EDGES, EDGES)]
                                     .to_broadcast([W, EDGES])).then_inc(same_loaded[h], 16)
                stages(sp, EC, 2, 2, body)

            @block.vector
            def _(v):
                v.memset(got[:, :, :, D:W], 1.0)
                v.memset(run[:, 1, :], 0.0).then_inc(set_up, 1)
                v.wait_ge(set_up, 1)

                def body(c0, c1, c2):
                    if c0:
                        h, k = c0.slot, c0.k
                        v.wait_ge(gathered[h], k * 16 * JT)
                        v.tensor_copy(from_rows[:, h, :], g.rows[s][:, bass.ds(c0.n, 1), JT:2 * JT]
                                      .rearrange("p a j -> p (a j)")).then_inc(from_ready[h], 1)
                    if c1:
                        h, k = c1.slot, c1.k
                        v.wait_ge(filed[h], k * 16 * JT)
                        v.tensor_copy(to_rows[:, h, :], g.rows[s][:, bass.ds(c1.n, 1), 2 * JT:3 * JT]
                                      .rearrange("p a j -> p (a j)")).then_inc(to_ready[h], 1)
                        v.wait_ge(same_loaded[h], (k + 1) * 16)
                        v.wait_ge(flipped[h], k + 1)
                        v.wait_ge(unflipped[h], k)
                        v.wait_ge(scanned[1 - h], k + h)
                        v.tensor_tensor_scan(run[:, h, :], same[:, h, :], turned[h][:, :],
                                             run[:, 1 - h, EDGES - 1:EDGES], ALU.mult, ALU.add).then_inc(scanned[h], 1)
                stages(v, EC, 2, 2, body)

            @block.tensor
            def _(pe):
                pe.wait_ge(set_up, 1)

                def body(c0, c1, c2):
                    if c1:
                        h, k = c1.slot, c1.k
                        pe.wait_ge(gathered[h], (k + 1) * 16 * JT)
                        pe.wait_ge(scanned[h], k)
                        for j in range(JT):
                            last = pe.transpose(turned[h][:, j * P:(j + 1) * P], got[:, h, j, :], g.ident[:, :])
                        last.then_inc(flipped[h], 1)
                        pe.wait_ge(scanned[h], k + 1)
                        pe.wait_ge(out_ready[h], k)
                        for j in range(JT):
                            last = pe.transpose(back[h][:, j * W:(j + 1) * W], run[:, h, j * P:(j + 1) * P], g.ident[0:W, 0:W])
                        last.then_inc(unflipped[h], 1)
                stages(pe, EC, 2, 2, body)

            @block.scalar
            def _(a):
                def body(c0, c1, c2):
                    if c1:
                        h, k = c1.slot, c1.k
                        a.wait_ge(unflipped[h], k + 1)
                        a.wait_ge(filed[h], k * 16 * JT)
                        a.activation(out[:, h, :, :].rearrange("p j w -> p (j w)"), back[h][:, :],
                                     ACT.Copy).then_inc(out_ready[h], 1)
                stages(a, EC, 2, 2, body)

            @block.gpsimd
            def _(gp):
                gp.wait_ge(set_up, 1)

                def body(c0, c1, c2):
                    if c0:
                        h, k = c0.slot, c0.k
                        gp.wait_ge(from_ready[h], k + 1)
                        gp.wait_ge(flipped[h], k)
                        gp.nop(nofuse=True)
                        for j in range(JT):
                            gp.indirect_dma_start(out=got[:, h, j, 0:D], out_offset=None, in_=table[:, :],
                                                  in_offset=bass.IndirectOffsetOnAxis(ap=from_rows[:, h, j:j + 1], axis=0)
                                                  ).then_inc(gathered[h], 16)
                    if c2:
                        h, k = c2.slot, c2.k
                        gp.wait_ge(out_ready[h], k + 1)
                        gp.wait_ge(to_ready[h], k + 1)
                        gp.nop(nofuse=True)
                        for j in range(JT):
                            gp.indirect_dma_start(out=sums[:, :],
                                                  out_offset=bass.IndirectOffsetOnAxis(ap=to_rows[:, h, j:j + 1], axis=0),
                                                  in_=out[:, h, j, :], in_offset=None,
                                                  bounds_check=NP - 1, oob_is_err=False).then_inc(filed[h], 16)
                stages(gp, EC, 2, 2, body)
                for h in range(2):
                    gp.wait_ge(filed[h], EC // 2 * 16 * JT)
    sem.clear()


def chunk_rows(table, n, width):
    return table[bass.ds(n * NODES, NODES), :].rearrange("(p j) k -> p (j k)", p=P)


def flat(tile):
    return tile.rearrange("p j k -> p (j k)")


def set_up(nc, g, w, sem):
    ctx = ExitStack()
    with ctx:
        def sb(label, shape, dt=F32):
            return ctx.enter_context(nc.sbuf_tensor(f"su_{label}", shape, dt))

        ones = sb("ones", [D, P])
        w0 = sb("w0", [P, D])
        w_att = sb("w_att", [P, HEADS, D])
        att = sb("att", [P, 2, HEADS, D])
        prod = sb("prod", [P, 2, HEADS, D])
        summed = sb("summed", [P, 2, HEADS])
        mean = sb("mean", [P, D])
        w3 = sb("w3", [P, D])
        a3 = sb("a3", [P, 2, D])
        prod3 = sb("prod3", [P, 2, D])
        sum3 = sb("sum3", [P, 2])
        prod0 = sb("prod0", [P, 2, D])
        sum0 = sb("sum0", [P, 2])
        colsum = ctx.enter_context(nc.psum_tensor("su_colsum", [P, D], F32))
        const, loaded, pe_done, act_done, dve, pooled = (sem(f"su_{x}") for x in (
            "const", "loaded", "pe", "act", "dve", "pooled"))
        with nc.Block() as block:
            @block.gpsimd
            def _(gp):
                gp.memset(g.ident[:, :], 0.0)
                gp.memset(g.zeros_bf[:, :], 0.0)
                gp.memset(g.zero_rows[:, :], 0.0)
                gp.memset(g.half[:, :], 0.5)
                gp.memset(g.minus_half[:, :], -0.5)
                gp.memset(ones[:, :], 1.0)
                gp.memset(g.w0_pair[:, :, :], 0.0)
                gp.memset(g.w2_pair[:, :, :], 0.0)
                gp.memset(g.a3_pair[:, :, :], 0.0)
                gp.memset(g.w3_pair[:, :, :], 0.0)
                gp.memset(g.pick[:, :, :, :], 0.0).then_inc(const, 1)
                gp.wait_ge(const, 1)
                gp.affine_select(out=g.ident[:, :], in_=g.ident[:, :], compare_op=ALU.not_equal, fill=1.0,
                                 base=0, pattern=[[-1, P]], channel_multiplier=1)
                picked = g.pick[:, :, :, :].rearrange("r w q (a d) -> r (w q a) d", d=D)
                gp.affine_select(out=picked, in_=picked, compare_op=ALU.not_equal, fill=1.0,
                                 base=0, pattern=[[-1, 8], [0, D]], channel_multiplier=1).then_inc(const, 1)
                gp.wait_ge(loaded, 16 * w.loads)
                gp.tensor_tensor(g.c_cols[:, 1:2], g.c_cols[:, 0:1], g.half[:, 0:1], ALU.pow).then_inc(pooled, 1)

            @block.sync
            def _(sp):
                n = 0

                def load(out, in_):
                    nonlocal n
                    n += 1
                    sp.dma_start(out, in_).then_inc(loaded, 16)

                for a in range(2):
                    half = slice(a * D, (a + 1) * D)
                    load(w0[half, :], w.L0_W[:, :])
                    load(w3[half, :], w.L3_W[:, :])
                    load(w_att[half, :, :], w.L2_W.rearrange("k (h d) -> k h d", h=HEADS))
                    for q in range(2):
                        load(g.w_heads[half, q, :], w.L2_W[:, (2 * q + a) * D:(2 * q + a + 1) * D])
                    load(g.w_conv1[half, :], (w.L1_W1_1, w.L1_W2_1)[a][:, :])
                    load(g.w_conv2[half, :], (w.L1_W1_2, w.L1_W2_2)[a][:, :])
                for a, x in enumerate((w.L2_att_dst, w.L2_att_src)):
                    load(att[:, a, :, :].rearrange("p h d -> p (h d)"), x.rearrange("a h d -> a (h d)").to_broadcast([P, HEADS * D]))
                load(a3[:, 0, :], w.L3_a[D:2 * D, :].rearrange("k a -> a k").to_broadcast([P, D]))
                load(a3[:, 1, :], w.L3_a[0:D, :].rearrange("k a -> a k").to_broadcast([P, D]))
                load(g.bias[:, :], w.L2_bias.rearrange("(a d) -> a d", a=1).to_broadcast([P, D]))
                load(g.c_cols[:, 0:1], w.L0_c.rearrange("(a d) -> a d", a=1).to_broadcast([P, 1]))
                assert n == w.loads, n

            @block.tensor
            def _(pe):
                pe.wait_ge(const, 2)
                pe.wait_ge(loaded, 16 * w.loads)
                pe.matmul(colsum[:, :], lhsT=ones[:, :], rhs=w0[0:D, :], start=True, stop=True).then_inc(pe_done, 1)

            @block.vector
            def _(v):
                n = 0

                def step(instruction):
                    nonlocal n
                    n += 1
                    instruction.then_inc(dve, 1)
                    v.wait_ge(dve, n)

                v.wait_ge(loaded, 16 * w.loads)
                v.wait_ge(const, 2)
                v.wait_ge(pe_done, 1)
                v.tensor_copy(g.k_row[:, :], colsum[:, :])
                step(v.tensor_copy(prod0[:, 1, :], w0[:, :]))
                step(v.tensor_tensor(prod0[:, 0, :], w0[:, :], g.k_row[:, :], ALU.mult))
                step(v.tensor_reduce(sum0[:, :], prod0[:, :, :], AX.X, ALU.add))
                for a in range(2):
                    half = slice(a * D, (a + 1) * D)
                    v.tensor_copy(g.w0_pair[half, a, 0:D], w0[half, :])
                    v.tensor_copy(g.w0_pair[half, a, D:D + 2], sum0[half, :])
                    v.tensor_copy(g.w3_pair[half, a, :], w3[half, :])
                step(v.tensor_reduce(g.k_cols[:, 0:1], g.k_row[:, :], AX.X, ALU.add))
                step(v.tensor_tensor(prod0[:, 0, :], g.k_row[:, :], g.k_row[:, :], ALU.mult))
                step(v.tensor_reduce(g.k_cols[:, 1:2], prod0[:, 0, :], AX.X, ALU.add))
                step(v.tensor_scalar(g.k_cols[:, 0:1], g.k_cols[:, 0:1], EPS, None, ALU.mult))
                step(v.tensor_scalar(g.k_cols[:, 1:2], g.k_cols[:, 1:2], EPS * EPS, None, ALU.mult))
                step(v.tensor_tensor(prod[:, :, :, :].rearrange("p a h d -> p a (h d)"), att[:, :, :, :].rearrange("p a h d -> p a (h d)"),
                                     w_att[:, :, :].rearrange("p h d -> p (h d)").unsqueeze(1).to_broadcast([P, 2, HEADS * D]), ALU.mult))
                step(v.tensor_reduce(summed[:, :, :], prod[:, :, :, :], AX.X, ALU.add))
                step(v.tensor_reduce(mean[:, :], w_att[:, :, :].rearrange("p h d -> p d h"), AX.X, ALU.add))
                step(v.tensor_scalar(mean[:, :], mean[:, :], 1.0 / HEADS, None, ALU.mult))
                step(v.tensor_scalar(g.w_heads[:, :, :], g.w_heads[:, :, :], 1.0 / HEADS, None, ALU.mult))
                step(v.tensor_tensor(prod3[:, :, :], a3[:, :, :], w3[:, :].unsqueeze(1).to_broadcast([P, 2, D]), ALU.mult))
                step(v.tensor_reduce(sum3[:, :], prod3[:, :, :], AX.X, ALU.add))
                for a in range(2):
                    half = slice(a * D, (a + 1) * D)
                    v.tensor_copy(g.w2_pair[half, a, 0:8], summed[half, :, :].rearrange("p a h -> p (a h)"))
                    v.tensor_copy(g.w2_pair[half, a, 8:], mean[half, :])
                    v.tensor_copy(g.a3_pair[half, a, :], sum3[half, :])
                c = g.cs
                v.wait_ge(pooled, 1)
                step(v.reciprocal(c["1/sqrt"], c["sqrt"]))
                step(v.tensor_scalar(c["clip"], c["1/sqrt"], CLIP, None, ALU.mult))
                step(v.tensor_scalar(c["-2c"], c["c"], -2.0, None, ALU.mult))
                step(v.tensor_tensor(c["c*c"], c["c"], c["c"], ALU.mult))
    sem.clear()


def project(nc, g, x, sem):
    ctx = ExitStack()
    with ctx:
        def sb(label, shape, dt=F32):
            return ctx.enter_context(nc.sbuf_tensor(f"pr_{label}", shape, dt))

        def ps(label, shape):
            return ctx.enter_context(nc.psum_tensor(f"pr_{label}", shape, F32))

        xin = sb("x", [P, 4, GROUP, D])
        f0 = sb("f0", [P, 2, GROUP, D])
        xt = sb("xt", [P, 2, GROUP // 2, P])
        y = sb("y", [P, 4, GROUP, D])
        squares = sb("squares", [P, 2, 2, GROUP, D])
        turned = [ps(f"turned{h}", [P, GROUP // 2 * P]) for h in range(2)]
        prod = [[ps(f"prod{h}{b}", [P, 2, 2, D + 2]) for b in range(2)] for h in range(2)]
        loaded, stored = sem.quad("pr_loaded"), sem.quad("pr_stored")
        turn_dve, turn_act, turn_pe = Engine(sem("pr_dve"), "f0 sum"), Engine(sem("pr_act"), "sqx xt"), Engine(sem("pr_pe"), "turn")
        prod_act, prod_pe = Engine(sem("pr_prod_act"), "y0 y1 sqy0 sqy1"), Engine(sem("pr_prod_pe"), "prod")
        with nc.Block() as block:
            @block.sync
            def _(sp):
                def body(c0, c1, c2, c3):
                    if c0:
                        h, k = c0.slot, c0.k
                        if not (isinstance(c0.n, int) and c0.n < 4):
                            sp.wait_ge(turn_dve.sem, turn_dve.after(c0.n - 4, "f0"))
                        if isinstance(c0.n, int) and c0.n == CH - 1:
                            sp.dma_start(flat(xin[0:TAIL, h, :, :]), x[(CH - 1) * NODES:N, :]
                                         .rearrange("(p j) k -> p (j k)", j=GROUP)).then_inc(loaded[h], 16)
                        else:
                            sp.dma_start(flat(xin[:, h, :, :]), chunk_rows(x, c0.n, D)).then_inc(loaded[h], 16)
                    if c3:
                        sp.wait_ge(prod_act.sem, prod_act.after(c3.n, "y1"))
                        sp.dma_start(chunk_rows(g.Y, c3.n, D), flat(y[:, c3.slot, :, :])).then_inc(stored[c3.slot], 16)
                stages(sp, CH, 4, 3, body, tail=1)
                for h in range(4):
                    sp.wait_ge(stored[h], len(range(h, CH, 4)) * 16)

            @block.vector
            def _(v):
                def reduce(name, n, of):
                    return v.tensor_reduce(g.node[name][:, bass.ds(n, 1), :].rearrange("p a j -> p (a j)"), of, AX.X, ALU.add)

                def body(c0, c1, c2, c3):
                    if c3:
                        n, b = c3.n, c3.slot % 2
                        v.wait_ge(prod_act.sem, prod_act.after(n, "sqy1"))
                        for i in range(2):
                            for which, name in enumerate(("yk", "sy")):
                                at = g.node[name][:, bass.ds(n, 1), 4 * i:4 * i + 4]
                                v.tensor_copy(at, prod[b][i][:, :, :, D + which].rearrange("p q a -> p (q a)").unsqueeze(1))
                        reduce("y2", n, squares[:, b, 1, :, :])
                    if c1:
                        n, h, b = c1.n, c1.slot, c1.slot % 2
                        v.wait_ge(loaded[h], (c1.k + 1) * 16)
                        turn_dve.done(v.tensor_scalar(f0[:, b, :, :], xin[:, h, :, :], EPS, None, ALU.add), "f0")
                        v.wait_ge(turn_dve.sem, turn_dve.after(n, "f0"))
                        turn_dve.done(reduce("sf", n, f0[:, b, :, :]), "sum")
                    if c2:
                        n, b = c2.n, c2.slot % 2
                        v.wait_ge(turn_act.sem, turn_act.after(n, "sqx"))
                        reduce("n2", n, squares[:, b, 0, :, :])
                stages(v, CH, 4, 3, body)

            @block.tensor
            def _(t):
                def body(c0, c1, c2, c3):
                    if c2:
                        n, b = c2.n, c2.slot % 2
                        t.wait_ge(turn_act.sem, turn_act.after(n, "xt"))
                        for q in range(GROUP // 2):
                            last = t.matmul(prod[b][q // 2][:, q % 2, :, :].rearrange("p a k -> p (a k)"),
                                            lhsT=xt[:, b, q, :], rhs=g.w0_pair[:, :, :].rearrange("p a k -> p (a k)"),
                                            start=True, stop=True)
                        prod_pe.done(last, "prod")
                    if c1:
                        n, b = c1.n, c1.slot % 2
                        t.wait_ge(turn_dve.sem, turn_dve.after(n, "f0"))
                        for q in range(GROUP // 2):
                            last = t.transpose(turned[b][:, q * P:(q + 1) * P],
                                               f0[:, b, 2 * q:2 * q + 2, :].rearrange("p a d -> p (a d)"), g.ident[:, :])
                        turn_pe.done(last, "turn")
                stages(t, CH, 4, 3, body)

            @block.scalar
            def _(a):
                def body(c0, c1, c2, c3):
                    if c1:
                        n, b = c1.n, c1.slot % 2
                        a.wait_ge(turn_dve.sem, turn_dve.after(n, "f0"))
                        turn_act.done(a.activation(squares[:, b, 0, :, :], f0[:, b, :, :], ACT.Square), "sqx")
                        a.wait_ge(turn_pe.sem, turn_pe.after(n, "turn"))
                        turn_act.done(a.activation(xt[:, b, :, :].rearrange("p q m -> p (q m)"), turned[b][:, :], ACT.Copy), "xt")
                    if c2:
                        n, h, b = c2.n, c2.slot, c2.slot % 2
                        a.wait_ge(prod_pe.sem, prod_pe.after(n, "prod"))
                        a.wait_ge(stored[h], c2.k * 16)
                        for i in range(2):
                            prod_act.done(a.activation(y[:, h, 4 * i:4 * i + 4, :], prod[b][i][:, :, :, 0:D]
                                                       .rearrange("p q a k -> p (q a) k"), ACT.Copy), f"y{i}")
                        for i in range(2):
                            prod_act.done(a.activation(squares[:, b, 1, 4 * i:4 * i + 4, :], prod[b][i][:, :, :, 0:D]
                                                       .rearrange("p q a k -> p (q a) k"), ACT.Square), f"sqy{i}")
                stages(a, CH, 4, 3, body)
    sem.clear()


def factors(nc, g, sem):
    ctx = ExitStack()
    with ctx:
        node, c = g.node, g.cs
        names = "n fs a pn pc yn sp b t t2 m u s sg".split()
        tile = {x: ctx.enter_context(nc.sbuf_tensor(f"fa_{x}", [P, CH * GROUP], F32)) for x in names}
        A = {x: tile[x][:, :] for x in names}
        for x in ("n2", "sf", "y2", "yk", "sy", "nh2", "zeta", "s1", "s2"):
            A[x] = node[x][:, :, :].rearrange("p c j -> p (c j)")
        to_act, from_act, dve = sem("fa_to_act"), sem("fa_from_act"), sem("fa_dve")
        asked = []

        with nc.Block() as block:
            @block.vector
            def _(v):
                n = 0

                def step(instruction):
                    nonlocal n
                    n += 1
                    instruction.then_inc(dve, 1)
                    v.wait_ge(dve, n)

                def ts(out, x, a, op, b=None, op2=None):
                    if op2 is None:
                        step(v.tensor_scalar(A[out], A[x], a, None, op))
                    else:
                        step(v.tensor_scalar(A[out], A[x], a, b, op, op2))

                def tt(out, x, y, op):
                    step(v.tensor_tensor(A[out], A[x], A[y], op))

                def stt(out, x, a, y, op, op2):
                    step(v.scalar_tensor_tensor(out=A[out], in0=A[x], scalar=a, in1=A[y], op0=op, op1=op2))

                def inv(out, x):
                    step(v.reciprocal(A[out], A[x]))

                def on_act(out, x, f, scale=1.0, bias=0.0):
                    asked.append((out, x, f, scale, bias))
                    v.sem_inc(to_act, 1)
                    v.wait_ge(from_act, len(asked))

                def clip_factor(out, norm, limit):
                    ts("t", norm, limit, ALU.max)
                    inv("t", "t")
                    ts(out, "t", limit, ALU.mult)

                def artanh(out, x):
                    tt("t", x, x, ALU.mult)
                    ts("t2", "t", 1 / 15, ALU.mult, 1 / 13, ALU.add)
                    for d in (11, 9, 7, 5, 3, 1):
                        tt("t2", "t2", "t", ALU.mult)
                        ts("t2", "t2", 1 / d, ALU.add)
                    tt("t2", "t2", x, ALU.mult)
                    on_act("t", x, ACT.Ln, 1.0, 1.0)
                    on_act("u", x, ACT.Ln, -1.0, 1.0)
                    tt("t", "t", "u", ALU.subtract)
                    ts("t", "t", 0.5, ALU.mult)
                    ts("m", x, 0.25, ALU.is_lt)
                    tt("t2", "t2", "m", ALU.mult)
                    ts("m", x, 0.25, ALU.is_ge)
                    tt("t", "t", "m", ALU.mult)
                    tt(out, "t", "t2", ALU.add)

                on_act("n", "n2", ACT.Sqrt)
                clip_factor("fs", "n", CLIP)
                tt("n", "n", "fs", ALU.mult)
                inv("s", "n")
                on_act("n", "n", ACT.Tanh)
                tt("a", "n", "s", ALU.mult)
                tt("a", "a", "fs", ALU.mult)
                tt("s", "a", "a", ALU.mult)
                tt("t", "s", "n2", ALU.mult)
                tt("u", "a", "sf", ALU.mult)
                stt("t", "u", 2 * EPS, "t", ALU.mult, ALU.add)
                ts("t", "t", D * EPS * EPS, ALU.add, 0.0, ALU.max)
                on_act("pn", "t", ACT.Sqrt)
                clip_factor("pc", "pn", CLIP)
                tt("pn", "pn", "pc", ALU.mult)
                tt("t", "s", "y2", ALU.mult)
                tt("u", "a", "yk", ALU.mult)
                stt("t", "u", 2 * EPS, "t", ALU.mult, ALU.add)
                ts("t", "t", g.k_cols[:, 1:2], ALU.add)
                ts("t", "t", 0.0, ALU.max)
                on_act("yn", "t", ACT.Sqrt)
                tt("sp", "a", "sy", ALU.mult)
                ts("sp", "sp", g.k_cols[:, 0:1], ALU.add)
                ts("s", "pn", c["sqrt"], ALU.mult, 0.9, ALU.min)
                artanh("b", "s")
                inv("s", "pn")
                tt("b", "b", "s", ALU.mult)
                tt("b", "b", "pc", ALU.mult)
                ts("b", "b", c["1/sqrt"], ALU.mult)
                tt("n", "b", "yn", ALU.mult)
                clip_factor("fs", "n", c["clip"])
                tt("n", "n", "fs", ALU.mult)
                inv("s", "n")
                on_act("n", "n", ACT.Tanh, "sqrt")
                tt("n", "n", "s", ALU.mult)
                tt("n", "n", "fs", ALU.mult)
                tt("n", "n", "b", ALU.mult)
                ts("sg", "n", c["1/sqrt"], ALU.mult)
                tt("s1", "sg", "a", ALU.mult)
                ts("s2", "sg", EPS, ALU.mult)
                tt("t", "sg", "yn", ALU.mult)
                tt("nh2", "t", "t", ALU.mult)
                tt("u", "sg", "sp", ALU.mult)
                stt("t", "u", 2 * EPS, "nh2", ALU.mult, ALU.add)
                ts("t", "t", D * EPS * EPS, ALU.add, 0.0, ALU.max)
                on_act("n", "t", ACT.Sqrt)
                clip_factor("fs", "n", CLIP)
                tt("n", "n", "fs", ALU.mult)
                ts("s", "n", c["sqrt"], ALU.mult, 0.9, ALU.min)
                artanh("b", "s")
                inv("s", "n")
                tt("b", "b", "s", ALU.mult)
                tt("zeta", "b", "fs", ALU.mult)

            @block.scalar
            def _(a):
                for i, (out, x, f, scale, bias) in enumerate(asked):
                    a.wait_ge(to_act, i + 1)
                    a.activation(A[out], A[x], f, bias=bias, scale=c["sqrt"] if scale == "sqrt" else scale).then_inc(from_act, 1)
    sem.clear()


def place(nc, g, sem):
    ctx = ExitStack()
    with ctx:
        def sb(label, shape, dt=F32):
            return ctx.enter_context(nc.sbuf_tensor(f"pl_{label}", shape, dt))

        y = sb("y", [P, 4, GROUP, D])
        t1 = sb("t1", [P, 2, GROUP, D])
        t2 = sb("t2", [P, 2, GROUP, D])
        row = sb("row", [P, 4, GROUP, D + 2])
        loaded, stored, ready = (sem.quad(f"pl_{x}") for x in ("loaded", "stored", "ready"))
        made = Engine(sem("pl_dve"), "t1 t2")
        with nc.Block() as block:
            @block.sync
            def _(sp):
                def body(c0, c1, c2):
                    if c0:
                        sp.wait_ge(stored[c0.slot], c0.k * 16)
                        sp.dma_start(flat(y[:, c0.slot, :, :]), chunk_rows(g.Y, c0.n, D)).then_inc(loaded[c0.slot], 16)
                    if c2:
                        sp.wait_ge(ready[c2.slot], c2.k + 1)
                        sp.dma_start(chunk_rows(g.T0, c2.n, D + 2), flat(row[:, c2.slot, :, :])).then_inc(stored[c2.slot], 16)
                stages(sp, CH, 4, 2, body)
                for h in range(4):
                    sp.wait_ge(stored[h], len(range(h, CH, 4)) * 16)

            @block.vector
            def _(v):
                def body(c0, c1, c2):
                    if c1:
                        n, h, b = c1.n, c1.slot, c1.slot % 2

                        def per_node(name):
                            return g.node[name][:, bass.ds(n, 1), :].rearrange("p a j -> p j a")

                        v.wait_ge(loaded[h], (c1.k + 1) * 16)
                        made.done(v.tensor_tensor(t1[:, b, :, :], y[:, h, :, :], per_node("s1").to_broadcast([P, GROUP, D]), ALU.mult), "t1")
                        made.done(v.tensor_tensor(t2[:, b, :, :], g.k_row[:, :].unsqueeze(1).to_broadcast([P, GROUP, D]),
                                                  per_node("s2").to_broadcast([P, GROUP, D]), ALU.mult), "t2")
                        v.wait_ge(stored[h], c1.k * 16)
                        v.tensor_copy(row[:, h, :, 0:1], per_node("nh2"))
                        v.tensor_copy(row[:, h, :, 1:2], per_node("zeta"))
                        v.wait_ge(made.sem, made.after(n, "t2"))
                        v.tensor_tensor(row[:, h, :, 2:], t1[:, b, :, :], t2[:, b, :, :], ALU.add).then_inc(ready[h], 1)
                stages(v, CH, 4, 2, body)
    sem.clear()


def sort_edges(nc, g, src, dst, l3_a, attr, sem):
    ctx = ExitStack()
    with ctx:
        def sb(name, shape, dt):
            return ctx.enter_context(nc.sbuf_tensor(name, shape, dt))

        keys = sb("sort_keys", [P, ORDERS, TILES], I32)
        digit_i = sb("sort_digit_i", [P, TILES], I32)
        digits = sb("sort_digits", [P, ORDERS, 2, TILES], F32)
        attrs = sb("sort_attrs", [P, TILES, 16], F32)
        a_edge = sb("sort_a_edge", [P, 16], F32)
        contrib = sb("sort_contrib", [P, TILES], F32)
        record = sb("sort_record", [P, ORDERS, TILES, 4], I32)
        hot = sb("sort_hot", [P, 8, 2 * LOW + 2 * HIGH], BF16)
        buckets = sb("sort_buckets", [P, 512], F16)
        ones_row = sb("sort_ones_row", [P, 512], F32)
        total = sb("sort_total", [P, 2 * LOW + 2 * HIGH], F32)
        upto = sb("sort_upto", [P, 2 * LOW + 2 * HIGH], F32)
        base = sb("sort_base", [P, 2 * LOW + 2 * HIGH], F32)
        before = sb("sort_before", [P, P], BF16)
        notbefore = sb("sort_notbefore", [P, P], BF16)
        ones_bf = sb("sort_ones", [P, P], BF16)
        stage = sb("sort_stage", [P, 4, ORDERS, JT, 4], I32)
        half_i = sb("sort_half_i", [P, 4, ORDERS * JT], I32)
        half_d = sb("sort_half_d", [P, 4, ORDERS * JT], F32)
        place_f = sb("sort_place_f", [P, 4, ORDERS * JT], F32)
        place_i = sb("sort_place_i", [P, 4, ORDERS * JT], I32)
        junk = sb("sort_junk", [P, 2, 512], F32)
        edge_row = sb("sort_edge_row", [1, 8], I32)
        count_lo = ctx.enter_context(nc.psum_tensor("sort_count_lo", [P, 512], F32))
        count_hi = [ctx.enter_context(nc.psum_tensor(f"sort_count_hi{s}", [P, 512], F32)) for s in range(2)]
        ranks = [ctx.enter_context(nc.psum_tensor(f"sort_ranks{s}", [P, 512], F32)) for s in range(2)]

        def cols(s, high):
            at = 2 * LOW + s * HIGH if high else s * LOW
            return slice(at, at + (HIGH if high else LOW))

        mid0, mid1, final = g.mid0, g.mid1, g.sorted

        loaded, const, made, dve, counted = (sem(x) for x in (
            "sort_loaded", "sort_const", "sort_made", "sort_dve", "sort_counted"))
        cleared = sem("sort_cleared")
        hot_ready, hot_used, mid_stored = sem("sort_hot_ready"), sem("sort_hot_used"), sem("sort_mid_stored")
        with nc.Block() as block:
            @block.sync
            def _(sp):
                sp.wait_ge(const, 3)
                for s, key in enumerate((src, dst)):
                    whole = key[0:(P - 1) * TILES].rearrange("(p t) -> p t", t=TILES)
                    sp.dma_start(keys[0:P - 1, s, :], whole).then_inc(loaded, 16)
                    sp.dma_start(keys[P - 1:P, s, 0:LAST_E],
                                 key[(P - 1) * TILES:E].rearrange("(a t) -> a t", a=1)).then_inc(loaded, 16)
                sp.dma_start(attrs[0:P - 1, :, :].rearrange("p t k -> p (t k)"),
                             attr[0:(P - 1) * TILES, :].rearrange("(p t) k -> p (t k)", t=TILES)).then_inc(loaded, 16)
                sp.dma_start(attrs[P - 1:P, 0:LAST_E, :].rearrange("p t k -> p (t k)"),
                             attr[(P - 1) * TILES:E, :].rearrange("(a t) k -> a (t k)", a=1)).then_inc(loaded, 16)
                sp.dma_start(a_edge[:, :], l3_a[2 * D:2 * D + 16, :].rearrange("k a -> a k").to_broadcast([P, 16])).then_inc(loaded, 16)
                sp.wait_ge(made, 1)
                for s in range(ORDERS):
                    sp.dma_start(mid0[s][:, :].rearrange("(p t) k -> p (t k)", p=P),
                                 record[:, s, :, :].rearrange("p t k -> p (t k)")).then_inc(mid_stored, 16)
                    sp.dma_start(final[s][0:1, :], edge_row[0:1, 0:4]).then_inc(mid_stored, 16)
                    sp.dma_start(final[s][EP + 1:EP + 2, :], edge_row[0:1, 4:8]).then_inc(mid_stored, 16)
                sp.wait_ge(mid_stored, 16 * 6)

            @block.gpsimd
            def _(gp):
                gp.memset(keys[:, :, :], PAD_KEY).then_inc(const, 1)
                gp.memset(attrs[:, :, :], 0.0).then_inc(const, 1)
                gp.memset(edge_row[:, :], -1).then_inc(const, 1)
                gp.iota(buckets[:, :], pattern=[[1, 512]], base=0, channel_multiplier=0,
                        allow_small_or_imprecise_dtypes=True).then_inc(const, 1)
                gp.memset(ones_bf[:, :], 1.0).then_inc(const, 1)
                gp.memset(ones_row[:, :], 1.0).then_inc(const, 1)
                gp.wait_ge(const, 6)
                gp.affine_select(out=before[:, :], in_=ones_bf[:, :], compare_op=ALU.is_gt, fill=0.0,
                                 base=0, pattern=[[1, P]], channel_multiplier=-1).then_inc(const, 1)
                gp.affine_select(out=notbefore[:, :], in_=ones_bf[:, :], compare_op=ALU.is_ge, fill=0.0,
                                 base=0, pattern=[[-1, P]], channel_multiplier=1).then_inc(const, 1)

            @block.vector
            def _(v):
                n = 0
                v.wait_ge(loaded, 16 * 7)
                for s in range(ORDERS):
                    for high in range(2):
                        if high:
                            i = v.tensor_scalar(digit_i[:, :], keys[:, s, :], 8, None, ALU.arith_shift_right)
                        else:
                            i = v.tensor_scalar(digit_i[:, :], keys[:, s, :], LOW - 1, None, ALU.bitwise_and)
                        i.then_inc(dve, 1)
                        n += 1
                        v.wait_ge(dve, n)
                        v.tensor_copy(digits[:, s, high, :], digit_i[:, :]).then_inc(dve, 1)
                        n += 1
                        v.wait_ge(dve, n)
                v.wait_ge(const, 8)
                v.tensor_tensor(attrs[:, :, :], attrs[:, :, :],
                                a_edge[:, :].unsqueeze(1).to_broadcast([P, TILES, 16]), ALU.mult).then_inc(dve, 1)
                n += 1
                v.wait_ge(dve, n)
                v.tensor_reduce(contrib[:, :], attrs[:, :, :], AX.X, ALU.add).then_inc(dve, 1)
                n += 1
                v.wait_ge(dve, n)
                for s in range(ORDERS):
                    v.tensor_copy(record[:, s, :, 0], keys[:, s, :])
                    v.tensor_copy(record[:, s, :, 1], keys[:, 1 - s, :])
                    v.tensor_copy(record[:, s, :, 3], keys[:, s, :])
                    last = v.tensor_copy(record[:, s, :, 2].bitcast(F32), contrib[:, :])
                    if s == 0:
                        last.then_inc(dve, 1)
                n += 1
                last.then_inc(made, 1)
                def one_hot(t, k, first):
                    if not first:
                        v.wait_ge(hot_used, t - k)
                    for s in range(ORDERS):
                        for high in range(2):
                            c = cols(s, high)
                            last = v.tensor_scalar(hot[:, k, c], buckets[:, 0:c.stop - c.start],
                                                   digits[:, s, high, bass.ds(t, 1)], None, ALU.is_equal)
                    last.then_inc(hot_ready, 1)

                for k in range(8):
                    one_hot(k, k, True)
                with v.Fori(1, TILES // 8) as i:
                    for k in range(8):
                        one_hot(i * 8 + k, k, False)
                v.wait_ge(counted, 1)
                v.tensor_copy(total[:, 0:512], count_lo[:, :])
                v.tensor_copy(total[:, cols(0, 1)], count_hi[0][:, 0:HIGH])
                v.tensor_copy(total[:, cols(1, 1)], count_hi[1][:, 0:HIGH]).then_inc(dve, 1)
                n += 1
                v.wait_ge(dve, n)
                for s in range(ORDERS):
                    for high in range(2):
                        c = cols(s, high)
                        last = v.tensor_tensor_scan(upto[:, c], ones_row[:, 0:c.stop - c.start], total[:, c],
                                                    0.0, ALU.mult, ALU.add)
                last.then_inc(dve, 1)
                n += 1
                v.wait_ge(dve, n)
                v.tensor_tensor(base[:, :], upto[:, :], total[:, :], ALU.subtract).then_inc(dve, 1)
                n += 1
                v.wait_ge(dve, n)
                v.tensor_scalar(base[:, 2 * LOW:], base[:, 2 * LOW:], 1.0, None, ALU.add).then_inc(dve, 1)

            @block.scalar
            def _(a):
                with a.Fori(0, CH) as n:
                    for table, width in g.zeroed_tables:
                        a.dma_start(chunk_rows(table, n, width), g.zero_rows[:, 0:GROUP * width]).then_inc(cleared, 16)
                a.wait_ge(cleared, CH * 16 * len(g.zeroed_tables))

            @block.tensor
            def _(pe):
                pe.wait_ge(const, 8)
                pe.matmul(count_lo[:, :], lhsT=g.zeros_bf[:, 0:P], rhs=g.zeros_bf[:, :], start=True, stop=False)
                pe.matmul(count_hi[0][:, 0:HIGH], lhsT=g.zeros_bf[:, 0:P], rhs=g.zeros_bf[:, 0:HIGH], start=True, stop=False)
                pe.matmul(count_hi[1][:, 0:HIGH], lhsT=g.zeros_bf[:, 0:P], rhs=g.zeros_bf[:, 0:HIGH], start=True, stop=False)
                with pe.Fori(0, TILES // 8) as i:
                    for k in range(8):
                        pe.wait_ge(hot_ready, i * 8 + k + 1)
                        pe.matmul(count_lo[:, :], lhsT=ones_bf[:, :], rhs=hot[:, k, 0:512], start=False, stop=False)
                        pe.matmul(count_hi[0][:, 0:HIGH], lhsT=ones_bf[:, :], rhs=hot[:, k, cols(0, 1)], start=False, stop=False)
                        pe.matmul(count_hi[1][:, 0:HIGH], lhsT=ones_bf[:, :], rhs=hot[:, k, cols(1, 1)],
                                  start=False, stop=False).then_inc(hot_used, 1)
                pe.matmul(count_lo[:, :], lhsT=g.zeros_bf[:, 0:P], rhs=g.zeros_bf[:, :], start=False, stop=True)
                pe.matmul(count_hi[0][:, 0:HIGH], lhsT=g.zeros_bf[:, 0:P], rhs=g.zeros_bf[:, 0:HIGH], start=False, stop=True)
                pe.matmul(count_hi[1][:, 0:HIGH], lhsT=g.zeros_bf[:, 0:P], rhs=g.zeros_bf[:, 0:HIGH],
                          start=False, stop=True).then_inc(counted, 1)

        for high in range(2):
            source, target = ((mid0, mid1), (mid1, final))[high]
            width = HIGH if high else LOW
            read, split, hot_made, ranked, placed, filed = (
                sem.quad(f"pass{high}_{x}") for x in
                ("read", "split", "hot_made", "ranked", "placed", "filed"))
            summed, taken = sem(f"pass{high}_summed"), sem(f"pass{high}_taken")
            PAIRS = ORDERS * JT

            def hot_rows(c, k):
                return hot[:, k, c.slot % 2 * HIGH:c.slot % 2 * HIGH + width]

            with nc.Block() as block:
                @block.sync
                def _(sp):
                    def body(c0, c1, c2):
                        if c0:
                            h = c0.slot
                            sp.wait_ge(filed[h], c0.k * (16 * PAIRS))
                            for s in range(ORDERS):
                                rows = source[s][bass.ds(c0.n * EDGES, EDGES), :]
                                sp.dma_start(stage[:, h, s, :, :],
                                             rows.rearrange("(t p) k -> p t k", p=P)).then_inc(read[h], 16)
                    stages(sp, EC, 4, 2, body)

                @block.vector
                def _(v):
                    def body(c0, c1, c2):
                        if c1:
                            h, i = c1.slot, c1.k
                            v.wait_ge(read[h], (i + 1) * 32)
                            keys_h = stage[:, h, :, :, 0].rearrange("p s t -> p (s t)")
                            if high:
                                ins = v.tensor_scalar(half_i[:, h, :], keys_h, 8, None, ALU.arith_shift_right)
                            else:
                                ins = v.tensor_scalar(half_i[:, h, :], keys_h, LOW - 1, None, ALU.bitwise_and)
                            ins.then_inc(split[h], 1)
                            v.wait_ge(split[h], i * 2 + 1)
                            v.tensor_copy(half_d[:, h, :], half_i[:, h, :]).then_inc(split[h], 1)
                            v.wait_ge(split[h], i * 2 + 2)
                        for k in range(PAIRS):
                            tile, s = k // 2, k % 2
                            if c2:
                                h = c2.slot
                                v.wait_ge(summed, c2.n * PAIRS + k + 1)
                                v.tensor_tensor_reduce(
                                    out=junk[:, s, 0:width], in0=ranks[s][:, 0:width], in1=hot_rows(c2, k),
                                    scale=1.0, scalar=0.0, op0=ALU.mult, op1=ALU.add,
                                    accum_out=place_f[:, h, s * JT + tile:s * JT + tile + 1]).then_inc(ranked[h], 1)
                            if c1:
                                h = c1.slot
                                if k == 0 and not (isinstance(c1.n, int) and c1.n < 2):
                                    v.wait_ge(taken, (c1.n - 1) * PAIRS)
                                v.tensor_scalar(hot_rows(c1, k), buckets[:, 0:width],
                                                half_d[:, h, s * JT + tile:s * JT + tile + 1],
                                                None, ALU.is_equal).then_inc(hot_made[h], 1)
                        if c2:
                            h = c2.slot
                            v.wait_ge(ranked[h], (c2.k + 1) * PAIRS)
                            v.tensor_copy(place_i[:, h, :], place_f[:, h, :]).then_inc(placed[h], 1)
                    stages(v, EC, 4, 2, body)

                @block.tensor
                def _(pe):
                    for s in range(ORDERS):
                        pe.matmul(ranks[s][:, 0:width], lhsT=g.ident[:, :], rhs=base[:, cols(s, high)],
                                  start=True, stop=False, skip_group_check=True)

                    def body(c0, c1, c2):
                        def add(k):
                            pe.wait_ge(hot_made[c2.slot], c2.k * PAIRS + k + 1)
                            pe.matmul(ranks[k % 2][:, 0:width], lhsT=before[:, :], rhs=hot_rows(c2, k),
                                      start=False, stop=False, skip_group_check=True).then_inc(summed, 1)

                        def rest(k):
                            pe.wait_ge(ranked[c2.slot], c2.k * PAIRS + k + 1)
                            pe.matmul(ranks[k % 2][:, 0:width], lhsT=notbefore[:, :], rhs=hot_rows(c2, k),
                                      start=False, stop=False, skip_group_check=True).then_inc(taken, 1)

                        if c2:
                            add(0)
                            add(1)
                            for k in range(PAIRS):
                                rest(k)
                                if k + 2 < PAIRS:
                                    add(k + 2)
                    stages(pe, EC, 4, 2, body)

                @block.gpsimd
                def _(gp):
                    def body(c0, c1, c2):
                        if c2:
                            h = c2.slot
                            gp.wait_ge(placed[h], c2.k + 1)
                            gp.nop(nofuse=True)
                            for s in range(ORDERS):
                                for t in range(JT):
                                    k = s * JT + t
                                    gp.indirect_dma_start(
                                        out=target[s][:, :],
                                        out_offset=bass.IndirectOffsetOnAxis(ap=place_i[:, h, k:k + 1], axis=0),
                                        in_=stage[:, h, s, t, :], in_offset=None).then_inc(filed[h], 16)
                    stages(gp, EC, 4, 2, body)
                    for h in range(4):
                        gp.wait_ge(filed[h], len(range(h, EC, 4)) * 16 * PAIRS)
    sem.clear()


def attend_edges(nc, g, name, s, kind, own, others, target, sem):
    H = HEADS if kind == "heads" else 1
    WOWN = {"hyper": D + 2, "heads": D + 8, "edge": 2}[kind]
    WOTHER = {"hyper": D + 2, "heads": D + 8, "edge": D + 2}[kind]
    WRUN = {"hyper": D + 2, "heads": P, "edge": D + 1}[kind]
    WOUT = D if kind == "heads" else D + 2
    Q = 2 if kind == "heads" else 1
    RING = 4
    ctx = ExitStack()
    with ctx:
        def sb(label, shape, dt=F32):
            return ctx.enter_context(nc.sbuf_tensor(f"{name}_{label}", shape, dt))

        def ps(label, shape):
            return ctx.enter_context(nc.psum_tensor(f"{name}_{label}", shape, F32))

        from_rows = sb("from_rows", [P, RING, 2 * JT], I32)
        to_rows = sb("to_rows", [P, RING, JT], I32)
        mine = sb("mine", [P, RING, JT, WOWN])
        other = sb("other", [P, RING, JT, WOTHER])
        pen = sb("pen_b", [H, RING, EDGES])
        score = sb("score", [P, JT, H])
        loop = sb("loop", [P, 2, JT, H])
        tmp = sb("tmp", [P, 12, JT, H])
        top = sb("top", [H, 2, EDGES + 1])
        cols = sb("cols", [P, 2, 2, JT, H])
        lows = sb("lows", [P, 2, 2, JT, H])
        ex = sb("ex", [P, 2, 2, JT, H])
        pay = sb("pay", [P, JT, Q * WRUN])
        decay = sb("decay", [P, Q, EDGES])
        run = sb("run", [P, 2, Q, EDGES])
        out = sb("out", [P, RING, JT, WOUT])
        score_row, top_col, pay_row, spread = ps("score_row", [H, EDGES]), ps("top_col", [P, 2 * JT * H + JT * H]), \
            ps("pay_row0", [P, EDGES]), [ps("spread0", [P, EDGES])]
        back = ps("back", [P, JT * WOUT])
        pay_rows = [pay_row]
        if kind == "hyper":
            big = sb("big", [P, 4, JT, D])
            log_h = sb("log_h", [P, 2, JT, D])
            decays = sb("decays", [P, JT, WRUN])
        if kind == "heads":
            pay_rows.append(ps("pay_row1", [P, EDGES]))
            spread.append(ps("spread1", [P, EDGES]))
            decay_row = ps("decay_row", [2 * H, EDGES])
            decay_row_s = sb("decay_row_s", [P, EDGES])
            weights = sb("weights", [H, 2, EDGES])
            wcol = sb("wcol", [P, JT, H])
            fin = sb("fin", [P, 2, JT, H])
            share = sb("share", [P, JT, 2, H])
            share_row = sb("share_row", [P, EDGES])
            twice = sb("twice", [P, JT, 2, D])
            own_row = sb("own_row", [P, 2, EDGES])
            z = sb("z", [P, 4, EDGES])
        cs = g.cs

        SKEW = 4 if kind == "heads" else 3
        dve, act, pe = Engine(sem(f"{name}_dve"), {
            "hyper": "prod dot a c1 c2 nn den rden t1 t2 ma ma2 rn2 low clip lndiff score "
                     "keep top cols fall fallen rise log",
            "edge": "s1 s2 score keep top cols fall fallen rise",
            "heads": "sadd score qadd loop keep top cols fall fallen rise"}[kind]), \
            Engine(sem(f"{name}_act"), "square root ln1 ln2 ex" if kind == "hyper" else "ex"), \
            Engine(sem(f"{name}_pe"), "score_row top_col")
        acc_dve = Engine(sem(f"{name}_acc_dve"), {
            "hyper": "pay payw decays decay1 run", "edge": "pay run",
            "heads": "pay weights run0 run1 wcol most f1 f2"}[kind])
        acc_act = Engine(sem(f"{name}_acc_act"), "twice decay_row decay0 decay1 own" if kind == "heads" else "decay out")
        acc_pe = Engine(sem(f"{name}_acc_pe"), "weight_row decay_row decay0 decay1 pay own wcol" if kind == "heads"
                        else "decay pay back")
        end_dve, end_act, end_pe = acc_dve, acc_act, acc_pe
        if kind == "heads":
            end_dve = Engine(sem(f"{name}_end_dve"), "g1 g2 g3 beta al0 alpha z0 z1 z2 z3")
            end_act = Engine(sem(f"{name}_end_act"), "exf share_row out")
            end_pe = Engine(sem(f"{name}_end_pe"), "share_row beta0 beta1 alpha0 alpha1 back")
        from_ready, gathered, pen_loaded, to_ready, filed = (
            sem.quad(f"{name}_{x}") for x in ("from_ready", "gathered", "pen_loaded", "to_ready", "filed"))
        set_up = sem(f"{name}_set_up")

        with nc.Block() as block:
            @block.sync
            def _(sp):
                def body(*c):
                    gather, attending, adding, end, scatter = c[0], c[1], c[2], c[-2], c[-1]
                    if gather:
                        n, h = gather.n, gather.slot
                        if not (isinstance(n, int) and n < RING):
                            sp.wait_ge(dve.sem, dve.after(n - RING, "top"))
                        sp.dma_start(pen[:, h, :], g.pen_row[s][:, bass.ds(n * EDGES, EDGES)]
                                     .to_broadcast([H, EDGES])).then_inc(pen_loaded[h], 16)
                stages(sp, EC, RING, SKEW, body)

            @block.gpsimd
            def _(gp):
                gp.wait_ge(set_up, 1)

                def body(*c):
                    gather, attending, adding, end, scatter = c[0], c[1], c[2], c[-2], c[-1]
                    if gather:
                        n, h, k = gather.n, gather.slot, gather.k
                        gp.wait_ge(from_ready[h], k + 1)
                        if not (isinstance(n, int) and n < RING):
                            gp.wait_ge(acc_dve.sem, acc_dve.after(n - RING, acc_dve.names[-1]))
                        gp.nop(nofuse=True)
                        for j in range(JT):
                            gp.indirect_dma_start(out=mine[:, h, j, :], out_offset=None, in_=own[:, :],
                                                  in_offset=bass.IndirectOffsetOnAxis(ap=from_rows[:, h, j:j + 1], axis=0)
                                                  ).then_inc(gathered[h], 16)
                            gp.indirect_dma_start(out=other[:, h, j, :], out_offset=None, in_=others[:, :],
                                                  in_offset=bass.IndirectOffsetOnAxis(ap=from_rows[:, h, JT + j:JT + j + 1], axis=0)
                                                  ).then_inc(gathered[h], 16)
                    if scatter:
                        h, k = scatter.slot, scatter.k
                        gp.wait_ge(end_act.sem, end_act.after(scatter.n, "out"))
                        gp.wait_ge(to_ready[h], k + 1)
                        gp.nop(nofuse=True)
                        for j in range(JT):
                            gp.indirect_dma_start(out=target[:, :],
                                                  out_offset=bass.IndirectOffsetOnAxis(ap=to_rows[:, h, j:j + 1], axis=0),
                                                  in_=out[:, h, j, :], in_offset=None,
                                                  bounds_check=NP - 1, oob_is_err=False).then_inc(filed[h], 16)
                stages(gp, EC, RING, SKEW, body)
                for h in range(RING):
                    gp.wait_ge(filed[h], len(range(h, EC, RING)) * 16 * JT)

            @block.vector
            def _(v):
                v.memset(top[:, 1, :], NEG)
                if kind == "hyper":
                    v.memset(pay[:, :, D + 1:D + 2], 1.0)
                if kind == "heads":
                    v.memset(weights[:, 1, :], 0.0)
                    v.memset(decay_row_s[:, :], 0.0)
                    v.memset(share_row[:, :], 0.0)
                v.memset(run[:, 1, :, :], 0.0).then_inc(set_up, 1)
                v.wait_ge(set_up, 1)

                def body(*c):
                    gather, attending, adding, end, scatter = c[0], c[1], c[2], c[-2], c[-1]
                    if gather:
                        h, k = gather.slot, gather.k
                        v.wait_ge(gathered[h], k * 32 * JT)
                        v.tensor_copy(from_rows[:, h, :], g.rows[s][:, bass.ds(gather.n, 1), 0:2 * JT]
                                      .rearrange("p a j -> p (a j)")).then_inc(from_ready[h], 1)
                    if adding:
                        pay_out(adding)
                    if end:
                        row_numbers(end)
                        if kind == "heads":
                            shares(end)
                    if attending:
                        scores(attending)
                    if adding:
                        running_sums(adding)
                    if attending:
                        if kind == "hyper":
                            distances(attending)
                        maximum(attending)
                    if end and kind == "heads":
                        scaled_runs(end)
                    if attending:
                        weigh(attending)
                    if end and kind == "heads":
                        scaled_own(end)
                    if adding and kind == "heads":
                        join_loop(adding)

                def row_numbers(c):
                    n, h, k, b = c.n, c.slot, c.k, c.slot % 2
                    v.wait_ge(filed[h], k * 16 * JT)
                    v.tensor_copy(to_rows[:, h, :], g.rows[s][:, bass.ds(n, 1), 2 * JT:3 * JT]
                                  .rearrange("p a j -> p (a j)")).then_inc(to_ready[h], 1)

                def scores(c):
                    n, h, k, b = c.n, c.slot, c.k, c.slot % 2

                    def need(engine, step):
                        v.wait_ge(engine.sem, engine.after(n, step))

                    v.wait_ge(gathered[h], (k + 1) * 32 * JT)
                    mi, ot = mine[:, h, :, :], other[:, h, :, :]
                    if kind == "hyper":
                        dve.done(v.tensor_tensor(big[:, 0, :, :], mi[:, :, 2:], ot[:, :, 2:], ALU.mult), "prod")
                        need(dve, "prod")
                        dve.done(v.tensor_reduce(tmp[:, 0, :, 0], big[:, 0, :, :], AX.X, ALU.add), "dot")
                        need(dve, "dot")
                        nu, nv = mi[:, :, 0], ot[:, :, 0]
                        dve.done(v.tensor_scalar(tmp[:, 1, :, 0], tmp[:, 0, :, 0], cs["-2c"], 1.0, ALU.mult, ALU.add), "a")
                        need(dve, "a")
                        dve.done(v.scalar_tensor_tensor(out=tmp[:, 2, :, 0], in0=nv, scalar=cs["c"], in1=tmp[:, 1, :, 0],
                                                        op0=ALU.mult, op1=ALU.add), "c1")
                        dve.done(v.tensor_scalar(tmp[:, 3, :, 0], nu, cs["c"], -1.0, ALU.mult, ALU.add), "c2")
                        dve.done(v.scalar_tensor_tensor(out=tmp[:, 4, :, 0], in0=nu, scalar=cs["c*c"], in1=nv,
                                                        op0=ALU.mult, op1=ALU.mult), "nn")
                        need(dve, "nn")
                        dve.done(v.tensor_tensor(tmp[:, 5, :, 0], tmp[:, 4, :, 0], tmp[:, 1, :, 0], ALU.add), "den")
                        need(dve, "den")
                        dve.done(v.reciprocal(tmp[:, 6, :, 0], tmp[:, 5, :, 0]), "rden")
                        dve.done(v.tensor_tensor(big[:, 1, :, :], mi[:, :, 2:], tmp[:, 2, :, :].to_broadcast([P, JT, D]), ALU.mult), "t1")
                        dve.done(v.tensor_tensor(big[:, 2, :, :], ot[:, :, 2:], tmp[:, 3, :, :].to_broadcast([P, JT, D]), ALU.mult), "t2")
                        need(dve, "t2")
                        dve.done(v.tensor_tensor(big[:, 1, :, :], big[:, 1, :, :], big[:, 2, :, :], ALU.add), "ma")
                        need(dve, "ma")
                        dve.done(v.tensor_tensor(big[:, 3, :, :], big[:, 1, :, :], tmp[:, 6, :, :].to_broadcast([P, JT, D]), ALU.mult), "ma2")
                    elif kind == "edge":
                        dve.done(v.tensor_tensor(tmp[:, 0, :, 0], ot[:, :, 0], mi[:, :, 0], ALU.add), "s1")
                        need(dve, "s1")
                        dve.done(v.tensor_tensor(tmp[:, 1, :, 0], tmp[:, 0, :, 0],
                                                 g.contrib[s][:, bass.ds(n, 1), :].rearrange("p a j -> p (a j)"), ALU.add), "s2")
                        need(dve, "s2")
                        dve.done(v.scalar_tensor_tensor(out=score[:, :, 0], in0=tmp[:, 1, :, 0], scalar=SLOPE, in1=tmp[:, 1, :, 0],
                                                        op0=ALU.mult, op1=ALU.max), "score")
                    else:
                        dve.done(v.tensor_tensor(tmp[:, 0, :, :], ot[:, :, 4:8], mi[:, :, 0:4], ALU.add), "sadd")
                        need(dve, "sadd")
                        dve.done(v.scalar_tensor_tensor(out=score[:, :, :], in0=tmp[:, 0, :, :], scalar=SLOPE, in1=tmp[:, 0, :, :],
                                                        op0=ALU.mult, op1=ALU.max), "score")
                        dve.done(v.tensor_tensor(tmp[:, 1, :, :], mi[:, :, 4:8], mi[:, :, 0:4], ALU.add), "qadd")
                        need(dve, "qadd")
                        dve.done(v.scalar_tensor_tensor(out=loop[:, b, :, :], in0=tmp[:, 1, :, :], scalar=SLOPE, in1=tmp[:, 1, :, :],
                                                        op0=ALU.mult, op1=ALU.max), "loop")

                def distances(c):
                    n, h, k, b = c.n, c.slot, c.k, c.slot % 2

                    def need(engine, step):
                        v.wait_ge(engine.sem, engine.after(n, step))

                    need(act, "square")
                    dve.done(v.tensor_reduce(tmp[:, 7, :, 0], big[:, 0, :, :], AX.X, ALU.add), "rn2")
                    need(dve, "rn2")
                    dve.done(v.tensor_scalar(tmp[:, 8, :, 0], tmp[:, 7, :, 0], cs["c"], 1e-16, ALU.mult, ALU.max), "low")
                    need(act, "root")
                    dve.done(v.tensor_scalar(tmp[:, 9, :, 0], tmp[:, 9, :, 0], CLIP, None, ALU.min), "clip")
                    need(act, "ln2")
                    dve.done(v.tensor_tensor(tmp[:, 0, :, 0], tmp[:, 11, :, 0], tmp[:, 10, :, 0], ALU.subtract), "lndiff")
                    need(dve, "lndiff")
                    dve.done(v.tensor_scalar(score[:, :, 0], tmp[:, 0, :, 0], cs["1/sqrt"], None, ALU.mult), "score")

                def maximum(c):
                    n, h, k, b = c.n, c.slot, c.k, c.slot % 2

                    def need(engine, step):
                        v.wait_ge(engine.sem, engine.after(n, step))

                    dve.done(v.tensor_copy(top[:, b, 0:1], top[:, 1 - b, EDGES:EDGES + 1]), "keep")
                    v.wait_ge(pen_loaded[h], (k + 1) * 16)
                    need(pe, "score_row")
                    dve.done(v.tensor_tensor_scan(top[:, b, 1:], pen[:, h, :], score_row[:, :],
                                                  top[:, 1 - b, EDGES:EDGES + 1], ALU.add, ALU.max), "top")

                def weigh(c):
                    n, h, k, b = c.n, c.slot, c.k, c.slot % 2
                    ot = other[:, h, :, :]

                    def need(engine, step):
                        v.wait_ge(engine.sem, engine.after(n, step))

                    need(pe, "top_col")
                    dve.done(v.tensor_copy(cols[:, b, :, :, :], top_col[:, 0:2 * JT * H]
                                           .rearrange("p (a j q) -> p a j q", a=2, j=JT)), "cols")
                    need(dve, "cols")
                    dve.done(v.tensor_tensor(lows[:, b, 0, :, :], cols[:, b, 1, :, :], cols[:, b, 0, :, :], ALU.subtract), "fall")
                    need(dve, "fall")
                    dve.done(v.tensor_tensor(lows[:, b, 0, :, :], lows[:, b, 0, :, :],
                                             g.pen[s][:, bass.ds(n, 1), :].rearrange("p a j -> p j a")
                                             .to_broadcast([P, JT, H]), ALU.min), "fallen")
                    dve.done(v.tensor_tensor(lows[:, b, 1, :, :], score[:, :, :], cols[:, b, 0, :, :], ALU.subtract), "rise")
                    if kind == "hyper":
                        dve.done(v.scalar_tensor_tensor(out=log_h[:, b, :, :], in0=ot[:, :, 2:], scalar=EPS,
                                                        in1=ot[:, :, 1:2].to_broadcast([P, JT, D]),
                                                        op0=ALU.add, op1=ALU.mult), "log")
                        need(dve, "log")

                def pay_out(c):
                    n, h, k, b = c.n, c.slot, c.k, c.slot % 2
                    ot = other[:, h, :, :]

                    def need(engine, step):
                        v.wait_ge(engine.sem, engine.after(n, step))

                    need(act, "ex")
                    if kind == "hyper":
                        acc_dve.done(v.tensor_tensor(pay[:, :, 0:D], log_h[:, b, :, :], ex[:, b, 1, :, :].to_broadcast([P, JT, D]), ALU.mult), "pay")
                        acc_dve.done(v.tensor_copy(pay[:, :, D:D + 1], ex[:, b, 1, :, :]), "payw")
                        acc_dve.done(v.tensor_copy(decays[:, :, 0:D + 1], ex[:, b, 0, :, :].to_broadcast([P, JT, D + 1])), "decays")
                        acc_dve.done(v.tensor_copy(decays[:, :, D + 1:D + 2], g.same[s][:, bass.ds(n, 1), :]
                                               .rearrange("p a j -> p j a")), "decay1")
                    elif kind == "edge":
                        acc_dve.done(v.tensor_tensor(pay[:, :, :], ot[:, :, 1:], ex[:, b, 1, :, :].to_broadcast([P, JT, D + 1]), ALU.mult), "pay")
                    else:
                        acc_dve.done(v.tensor_tensor(pay[:, :, :].rearrange("p j (q d) -> p j q d", d=D),
                                                 ot[:, :, 8:].unsqueeze(2).to_broadcast([P, JT, H, D]),
                                                 ex[:, b, 1, :, :].unsqueeze(3).to_broadcast([P, JT, H, D]), ALU.mult), "pay")

                def running_sums(c):
                    n, h, k, b = c.n, c.slot, c.k, c.slot % 2

                    def need(engine, step):
                        v.wait_ge(engine.sem, engine.after(n, step))

                    if kind != "heads":
                        need(acc_pe, "pay")
                        need(acc_act, "decay")
                        acc_dve.done(v.tensor_tensor_scan(run[0:WRUN, b, 0, :], decay[0:WRUN, 0, :], pay_rows[0][0:WRUN, :],
                                                      run[0:WRUN, 1 - b, 0, EDGES - 1:EDGES], ALU.mult, ALU.add), "run")
                        return
                    need(acc_act, "decay_row")
                    need(acc_pe, "decay_row")
                    acc_dve.done(v.tensor_tensor_scan(weights[:, b, :], decay_row_s[0:H, :], score_row[:, :],
                                                  weights[:, 1 - b, EDGES - 1:EDGES], ALU.mult, ALU.add), "weights")
                    need(acc_pe, "pay")
                    for q in range(2):
                        need(acc_act, f"decay{q}")
                        acc_dve.done(v.tensor_tensor_scan(run[:, b, q, :], decay[:, q, :], pay_rows[q][:, :],
                                                      run[:, 1 - b, q, EDGES - 1:EDGES], ALU.mult, ALU.add), f"run{q}")

                def join_loop(c):
                    n, h, k, b = c.n, c.slot, c.k, c.slot % 2

                    def need(engine, step):
                        v.wait_ge(engine.sem, engine.after(n, step))

                    need(acc_pe, "wcol")
                    acc_dve.done(v.tensor_copy(wcol[:, :, :], top_col[:, 2 * JT * H:].rearrange("p (j q) -> p j q", j=JT)), "wcol")
                    acc_dve.done(v.tensor_tensor(tmp[:, 2, :, :], cols[:, b, 0, :, :], loop[:, b, :, :], ALU.max), "most")
                    need(acc_dve, "most")
                    acc_dve.done(v.tensor_tensor(fin[:, 0, :, :], cols[:, b, 0, :, :], tmp[:, 2, :, :], ALU.subtract), "f1")
                    acc_dve.done(v.tensor_tensor(fin[:, 1, :, :], loop[:, b, :, :], tmp[:, 2, :, :], ALU.subtract), "f2")

                def shares(c):
                    n = c.n

                    def need(engine, step):
                        v.wait_ge(engine.sem, engine.after(n, step))

                    need(end_act, "exf")
                    end_dve.done(v.tensor_tensor(tmp[:, 3, :, :], wcol[:, :, :], fin[:, 0, :, :], ALU.mult), "g1")
                    need(end_dve, "g1")
                    end_dve.done(v.scalar_tensor_tensor(out=tmp[:, 4, :, :], in0=fin[:, 1, :, :], scalar=1e-16, in1=tmp[:, 3, :, :],
                                                        op0=ALU.add, op1=ALU.add), "g2")
                    need(end_dve, "g2")
                    end_dve.done(v.reciprocal(tmp[:, 5, :, :], tmp[:, 4, :, :]), "g3")
                    need(end_dve, "g3")
                    end_dve.done(v.tensor_tensor(share[:, :, 0, :], fin[:, 0, :, :], tmp[:, 5, :, :], ALU.mult), "beta")
                    end_dve.done(v.tensor_tensor(tmp[:, 6, :, :], fin[:, 1, :, :], tmp[:, 5, :, :], ALU.mult), "al0")
                    need(end_dve, "al0")
                    end_dve.done(v.tensor_scalar(share[:, :, 1, :], tmp[:, 6, :, :], -1.0, None, ALU.add), "alpha")

                def scaled_runs(c):
                    for q in range(2):
                        v.wait_ge(end_pe.sem, end_pe.after(c.n, f"beta{q}"))
                        end_dve.done(v.tensor_tensor(z[:, q, :], run[:, c.slot % 2, q, :], spread[1 - q][:, :], ALU.mult), f"z{q}")

                def scaled_own(c):
                    v.wait_ge(acc_act.sem, acc_act.after(c.n, "own"))
                    for q in range(2):
                        v.wait_ge(end_pe.sem, end_pe.after(c.n, f"alpha{q}"))
                        end_dve.done(v.tensor_tensor(z[:, 2 + q, :], own_row[:, c.slot % 2, :], spread[1 - q][:, :], ALU.mult), f"z{2 + q}")
                stages(v, EC, RING, SKEW, body)

            @block.scalar
            def _(a):
                a.wait_ge(set_up, 1)

                def body(*c):
                    gather, attending, adding, end, scatter = c[0], c[1], c[2], c[-2], c[-1]
                    if kind == "heads" and end:
                        a.wait_ge(acc_dve.sem, acc_dve.after(end.n, "f2"))
                        end_act.done(a.activation(fin[:, :, :, :], fin[:, :, :, :], ACT.Exp), "exf")
                    if kind == "heads" and adding:
                        a.wait_ge(gathered[adding.slot], (adding.k + 1) * 32 * JT)
                        acc_act.done(a.activation(twice[:, :, :, :], mine[:, adding.slot, :, 8:].unsqueeze(2)
                                                  .to_broadcast([P, JT, 2, D]), ACT.Copy), "twice")
                    if adding:
                        accumulate(adding)
                    if kind == "heads" and end:
                        a.wait_ge(end_pe.sem, end_pe.after(end.n, "share_row"))
                        end_act.done(a.activation(share_row[0:2 * H, :], decay_row[:, :], ACT.Copy), "share_row")
                    if attending:
                        attend(attending)
                    if end:
                        n, h, k = end.n, end.slot, end.k
                        a.wait_ge(end_pe.sem, end_pe.after(n, "back"))
                        a.wait_ge(filed[h], k * 16 * JT)
                        end_act.done(a.activation(out[:, h, :, :].rearrange("p j w -> p (j w)"), back[:, :], ACT.Copy), "out")

                def attend(c):
                    n, h, k, b = c.n, c.slot, c.k, c.slot % 2

                    def need(engine, step):
                        a.wait_ge(engine.sem, engine.after(n, step))

                    if kind == "hyper":
                        need(dve, "ma2")
                        act.done(a.activation(big[:, 0, :, :], big[:, 3, :, :], ACT.Square), "square")
                        need(dve, "low")
                        act.done(a.activation(tmp[:, 9, :, :], tmp[:, 8, :, :], ACT.Sqrt), "root")
                        need(dve, "clip")
                        act.done(a.activation(tmp[:, 10, :, :], tmp[:, 9, :, :], ACT.Ln, bias=1.0, scale=1.0), "ln1")
                        act.done(a.activation(tmp[:, 11, :, :], tmp[:, 9, :, :], ACT.Ln, bias=1.0, scale=-1.0), "ln2")
                    need(dve, "rise")
                    act.done(a.activation(ex[:, b, :, :, :], lows[:, b, :, :, :], ACT.Exp), "ex")

                def accumulate(c):
                    n = c.n

                    def need(engine, step):
                        a.wait_ge(engine.sem, engine.after(n, step))

                    if kind != "heads":
                        need(acc_pe, "decay")
                        acc_act.done(a.activation(decay[0:WRUN, 0, :], spread[0][0:WRUN, :], ACT.Copy), "decay")
                    else:
                        need(acc_pe, "decay_row")
                        acc_act.done(a.activation(decay_row_s[0:H, :], decay_row[0:H, :], ACT.Copy), "decay_row")
                        for q in range(2):
                            need(acc_pe, f"decay{q}")
                            acc_act.done(a.activation(decay[:, q, :], spread[q][:, :], ACT.Copy), f"decay{q}")
                        need(acc_pe, "own")
                        acc_act.done(a.activation(own_row[:, c.slot % 2, :], spread[0][:, :], ACT.Copy), "own")
                stages(a, EC, RING, SKEW, body)

            @block.tensor
            def _(t):
                t.wait_ge(set_up, 1)
                ident = g.ident

                def body(*c):
                    gather, attending, adding, end, scatter = c[0], c[1], c[2], c[-2], c[-1]
                    if adding:
                        if kind == "heads":
                            weight_rows(adding)
                            turn(adding)
                        else:
                            turn_and_back(adding)
                    if attending:
                        score_rows(attending)
                    if kind == "heads":
                        if end:
                            share_rows(end)
                        if adding:
                            turn_own(adding)
                    if attending:
                        maxima(attending)
                    if kind == "heads" and end:
                        spread_shares(end)
                        products(end)

                def mm(out, lhsT, rhs, start=True, stop=True):
                    return t.matmul(out, lhsT=lhsT, rhs=rhs, start=start, stop=stop)

                def tile(j):
                    return slice(j * P, (j + 1) * P)

                def need_of(c):
                    def need(engine, step):
                        t.wait_ge(engine.sem, engine.after(c.n, step))
                    return need

                def score_rows(c):
                    need_of(c)(dve, "score")
                    if kind == "heads" and not (isinstance(c.n, int) and c.n < 1):
                        t.wait_ge(acc_dve.sem, acc_dve.after(c.n - 1, "weights"))
                    for j in range(JT):
                        last = t.transpose(score_row[:, tile(j)], score[:, j, :], ident[:, :])
                    pe.done(last, "score_row")

                def maxima(c):
                    need_of(c)(dve, "top")
                    t.nop(nofuse=True)
                    for m in range(2):
                        for j in range(JT):
                            last = t.transpose(top_col[:, (m * JT + j) * H:(m * JT + j + 1) * H],
                                               top[:, c.slot % 2, 1 - m + j * P:1 - m + (j + 1) * P], ident[0:H, 0:H])
                    pe.done(last, "top_col")

                def turn_and_back(c):
                    b, need = c.slot % 2, need_of(c)
                    need(act, "ex")
                    if kind == "hyper":
                        need(acc_dve, "decay1")
                    for j in range(JT):
                        last = t.transpose(spread[0][0:WRUN, tile(j)], decays[:, j, :] if kind == "hyper"
                                  else ex[:, b, 0, j, :].to_broadcast([P, WRUN]), ident[:, :])
                    acc_pe.done(last, "decay")
                    need(acc_dve, "payw" if kind == "hyper" else "pay")
                    for j in range(JT):
                        last = t.transpose(pay_rows[0][0:WRUN, tile(j)], pay[:, j, :], ident[:, :])
                    acc_pe.done(last, "pay")
                    need(acc_dve, "run")
                    for j in range(JT):
                        last = t.transpose(back[:, j * WOUT:j * WOUT + WRUN], run[0:WRUN, b, 0, tile(j)], ident[0:WRUN, 0:WRUN])
                        if kind == "edge":
                            last = t.transpose(back[:, j * WOUT + WRUN:(j + 1) * WOUT],
                                      top[:, b, 1 + j * P:1 + (j + 1) * P], ident[0:1, 0:1])
                    acc_pe.done(last, "back")

                def broadcast(rows, what, q, to):
                    return mm(spread[to][:, :], g.pick[:, what, q, :], rows[:, :])

                def weight_rows(c):
                    need_of(c)(act, "ex")
                    for what, row in ((1, score_row), (0, decay_row)):
                        for j in range(JT):
                            last = t.transpose(row[0:H, tile(j)], ex[:, c.slot % 2, what, j, :], ident[:, :])
                        acc_pe.done(last, ("decay_row", "weight_row")[what])

                def turn(c):
                    b, need = c.slot % 2, need_of(c)
                    need(acc_act, "decay_row")
                    acc_pe.done(broadcast(decay_row_s, 0, 0, 0), "decay0")
                    acc_pe.done(broadcast(decay_row_s, 0, 1, 1), "decay1")
                    need(acc_dve, "pay")
                    for q in range(2):
                        for j in range(JT):
                            last = t.transpose(pay_rows[q][:, tile(j)], pay[:, j, q * P:(q + 1) * P], ident[:, :])
                    acc_pe.done(last, "pay")

                def turn_own(c):
                    b, need = c.slot % 2, need_of(c)
                    need(acc_act, "decay0")
                    for j in range(JT):
                        last = t.transpose(spread[0][:, tile(j)], twice[:, j, :, :].rearrange("p a d -> p (a d)"), ident[:, :])
                    acc_pe.done(last, "own")
                    need(acc_dve, "weights")
                    t.nop(nofuse=True)
                    for j in range(JT):
                        last = t.transpose(top_col[:, (2 * JT + j) * H:(2 * JT + j + 1) * H], weights[:, b, tile(j)], ident[0:H, 0:H])
                    acc_pe.done(last, "wcol")

                def share_rows(c):
                    need_of(c)(end_dve, "alpha")
                    for j in range(JT):
                        last = t.transpose(decay_row[:, tile(j)], share[:, j, :, :].rearrange("p a q -> p (a q)"), ident[:, :])
                    end_pe.done(last, "share_row")

                def spread_shares(c):
                    need = need_of(c)
                    need(end_act, "share_row")
                    end_pe.done(broadcast(share_row, 0, 0, 1), "beta0")
                    end_pe.done(broadcast(share_row, 0, 1, 0), "beta1")
                    need(end_dve, "z0")
                    end_pe.done(broadcast(share_row, 1, 0, 1), "alpha0")
                    need(end_dve, "z1")
                    end_pe.done(broadcast(share_row, 1, 1, 0), "alpha1")

                def products(c):
                    need_of(c)(end_dve, "z3")
                    for j in range(JT):
                        for m in range(4):
                            last = mm(back[:, j * D:(j + 1) * D], z[:, m, tile(j)], g.w_heads[:, m % 2, :],
                                      start=(m == 0), stop=(m == 3))
                    end_pe.done(last, "back")
                stages(t, EC, RING, SKEW, body)
    sem.clear()


LN1 = "total mean centre"
LN2 = "spread var"


class Norm:

    def __init__(self, g, x, squares, small, v_steps, a_steps, p_steps):
        self.g, self.x, self.squares, self.small = g, x, squares, small
        self.v, self.a, self.p = v_steps, a_steps, p_steps

    def centre(self, v, n, b, before):
        steps, x, s = self.v, self.x[:, b, :, :], self.small[:, b]
        v.wait_ge(steps.sem, steps.after(n, before))
        steps.done(v.tensor_reduce(s[:, 0, :], x, AX.X, ALU.add), "total")
        v.wait_ge(steps.sem, steps.after(n, "total"))
        steps.done(v.tensor_scalar(s[:, 1, :], s[:, 0, :], 1.0 / D, None, ALU.mult), "mean")
        v.wait_ge(steps.sem, steps.after(n, "mean"))
        steps.done(v.tensor_tensor(x, x, s[:, 1, :].unsqueeze(2).to_broadcast([P, GROUP, D]), ALU.subtract), "centre")

    def square(self, a, n, b):
        a.wait_ge(self.v.sem, self.v.after(n, "centre"))
        self.a.done(a.activation(self.squares[:, b, :, :], self.x[:, b, :, :], ACT.Square), "lnsq")

    def spread(self, v, n, b):
        steps, s = self.v, self.small[:, b]
        v.wait_ge(self.a.sem, self.a.after(n, "lnsq"))
        steps.done(v.tensor_reduce(s[:, 2, :], self.squares[:, b, :, :], AX.X, ALU.add), "spread")
        v.wait_ge(steps.sem, steps.after(n, "spread"))
        steps.done(v.tensor_scalar(s[:, 3, :], s[:, 2, :], 1.0 / D, LN_EPS, ALU.mult, ALU.add), "var")

    def rstd(self, gp, n, b):
        gp.wait_ge(self.v.sem, self.v.after(n, "var"))
        self.p.done(gp.tensor_tensor(self.small[:, b, 4, :], self.small[:, b, 3, :], self.g.minus_half[:, :], ALU.pow), "rstd")

    def scaled(self, v, out, b):
        return v.tensor_tensor(out, self.x[:, b, :, :],
                               self.small[:, b, 4, :].unsqueeze(2).to_broadcast([P, GROUP, D]), ALU.mult)


def of_node(g, name, n):
    return g.node[name][:, bass.ds(n, 1), :].rearrange("p a j -> p j a")


def close_layer0(nc, g, x, sem):
    ctx = ExitStack()
    with ctx:
        def sb(label, shape, dt=F32):
            return ctx.enter_context(nc.sbuf_tensor(f"c0_{label}", shape, dt))

        xin, att = sb("x", [P, 4, GROUP, D]), sb("att", [P, 4, GROUP, D + 2])
        z1, z2, z3, y = (sb(q, [P, 4, GROUP, D]) for q in ("z1", "z2", "z3", "y"))
        squares = sb("squares", [P, 4, GROUP, D])
        small, t = sb("small", [P, 4, 5, GROUP]), sb("t", [P, 4, 14, GROUP])
        rso = sb("rso", [P, 4, GROUP])
        x1, g1 = sb("x1", [P, 4, GROUP, D]), sb("g1", [P, 4, GROUP, D])
        loaded, stored, ready = (sem.quad(f"c0_{q}") for q in ("loaded", "stored", "ready"))
        c = g.cs
        dve, ball = Engine(sem("c0_dve"), "den rden rc att elu z dmax"), Engine(sem("c0_ball"), "z2 zm zr zf zn zi")
        late = Engine(sem("c0_late"), "s1 s2 s3 hp y " + LN1 + " " + LN2 + " rso")
        act, ball_act = Engine(sem("c0_act"), "low exp relu sq"), Engine(sem("c0_ball_act"), "tanh")
        degree_pool, root_pool = Engine(sem("c0_degree_pool"), "rso"), Engine(sem("c0_root_pool"), "zn0")
        lact, lgps = Engine(sem("c0_lact"), "lnsq"), Engine(sem("c0_lgps"), "rstd x1")
        norm = Norm(g, y, squares, small, late, lact, lgps)
        with nc.Block() as block:
            @block.sync
            def _(sp):
                def body(c0, c1, c2, c3, c4):
                    if c0:
                        h, k = c0.slot, c0.k
                        if not (isinstance(c0.n, int) and c0.n < 4):
                            sp.wait_ge(late.sem, late.after(c0.n - 4, "y"))
                        if isinstance(c0.n, int) and c0.n == CH - 1:
                            sp.dma_start(flat(xin[0:TAIL, h, :, :]), x[(CH - 1) * NODES:N, :]
                                         .rearrange("(p j) k -> p (j k)", j=GROUP)).then_inc(loaded[h], 16)
                        else:
                            sp.dma_start(flat(xin[:, h, :, :]), chunk_rows(x, c0.n, D)).then_inc(loaded[h], 16)
                        sp.dma_start(flat(att[:, h, :, :]), chunk_rows(g.A0, c0.n, D + 2)).then_inc(loaded[h], 16)
                    if c4:
                        n, h = c4.n, c4.slot
                        sp.wait_ge(ready[h], c4.k + 1)
                        sp.dma_start(chunk_rows(g.X1, n, D), flat(x1[:, h, :, :])).then_inc(stored[h], 16)
                        sp.dma_start(chunk_rows(g.G1, n, D), flat(g1[:, h, :, :])).then_inc(stored[h], 16)
                stages(sp, CH, 4, 4, body, tail=1)
                for h in range(4):
                    sp.wait_ge(stored[h], len(range(h, CH, 4)) * 32)

            @block.vector
            def _(v):
                def tiles(ch):
                    b = ch.slot
                    return ch.n, ch.slot, b, [t[:, b, i, :] for i in range(14)]

                def per(a):
                    return a.unsqueeze(2).to_broadcast([P, GROUP, D])

                def attention(ch):
                    n, h, b, q = tiles(ch)
                    v.wait_ge(loaded[h], (ch.k + 1) * 32)
                    dve.done(v.tensor_scalar(q[0], att[:, h, :, D], 1e-16, None, ALU.add), "den")
                    v.wait_ge(dve.sem, dve.after(n, "den"))
                    dve.done(v.reciprocal(q[1], q[0]), "rden")
                    v.wait_ge(dve.sem, dve.after(n, "rden"))
                    dve.done(v.tensor_scalar(q[2], q[1], c["sqrt"], None, ALU.mult), "rc")
                    v.wait_ge(dve.sem, dve.after(n, "rc"))
                    dve.done(v.tensor_tensor(z1[:, b, :, :], att[:, h, :, 0:D], per(q[2]), ALU.mult), "att")

                def elu(ch):
                    n, h, b, q = tiles(ch)
                    v.wait_ge(act.sem, act.after(n, "relu"))
                    dve.done(v.scalar_tensor_tensor(out=z1[:, b, :, :], in0=z2[:, b, :, :], scalar=-1.0, in1=z3[:, b, :, :],
                                                    op0=ALU.add, op1=ALU.add), "elu")
                    v.wait_ge(dve.sem, dve.after(n, "elu"))
                    dve.done(v.tensor_scalar(z1[:, b, :, :], z1[:, b, :, :], EPS, None, ALU.add), "z")
                    dve.done(v.tensor_scalar(q[3], att[:, h, :, D + 1], 1.0, None, ALU.max), "dmax")

                def norm_of_z(ch):
                    n, h, b, q = tiles(ch)
                    v.wait_ge(act.sem, act.after(n, "sq"))
                    ball.done(v.tensor_reduce(q[4], z2[:, b, :, :], AX.X, ALU.add), "z2")

                def on_ball(ch):
                    n, h, b, q = tiles(ch)

                    def need(steps, name):
                        v.wait_ge(steps.sem, steps.after(n, name))

                    need(root_pool, "zn0")
                    ball.done(v.tensor_scalar(q[6], q[5], c["clip"], None, ALU.max), "zm")
                    need(ball, "zm")
                    ball.done(v.reciprocal(q[7], q[6]), "zr")
                    need(ball, "zr")
                    ball.done(v.tensor_scalar(q[8], q[7], c["clip"], None, ALU.mult), "zf")
                    need(ball, "zf")
                    ball.done(v.tensor_tensor(q[9], q[5], q[8], ALU.mult), "zn")
                    need(ball, "zn")
                    ball.done(v.reciprocal(q[10], q[9]), "zi")

                def residual(ch):
                    n, h, b, q = tiles(ch)

                    def need(steps, name):
                        v.wait_ge(steps.sem, steps.after(n, name))

                    need(ball, "zi")
                    late.done(v.tensor_tensor(q[12], q[8], q[10], ALU.mult), "s1")
                    need(ball_act, "tanh")
                    need(late, "s1")
                    late.done(v.tensor_tensor(q[13], q[11], q[12], ALU.mult), "s2")
                    need(late, "s2")
                    late.done(v.tensor_scalar(q[0], q[13], c["1/sqrt"], None, ALU.mult), "s3")
                    need(late, "s3")
                    late.done(v.tensor_tensor(z3[:, b, :, :], z1[:, b, :, :], per(q[0]), ALU.mult), "hp")
                    need(late, "hp")
                    late.done(v.tensor_tensor(y[:, b, :, :], z3[:, b, :, :], xin[:, h, :, :], ALU.add), "y")
                    norm.centre(v, n, b, "y")

                def close(ch):
                    n, h, b, q = tiles(ch)
                    norm.spread(v, n, b)
                    v.wait_ge(degree_pool.sem, degree_pool.after(n, "rso"))
                    late.done(v.tensor_copy(of_node(g, "rso", n), rso[:, h, :].unsqueeze(2)), "rso")

                def body(c0, c1, c2, c3, c4):
                    if c1:
                        attention(c1)
                    if c2:
                        norm_of_z(c2)
                    if c3:
                        residual(c3)
                    if c1:
                        elu(c1)
                    if c3:
                        close(c3)
                    if c2:
                        on_ball(c2)
                stages(v, CH, 4, 4, body)

            @block.scalar
            def _(a):
                def body(c0, c1, c2, c3, c4):
                    if c1:
                        n, b = c1.n, c1.slot
                        a.wait_ge(dve.sem, dve.after(n, "att"))
                        act.done(a.activation(z3[:, b, :, :], z1[:, b, :, :], ACT.Relu, scale=-1.0), "low")
                        a.wait_ge(act.sem, act.after(n, "low"))
                        act.done(a.activation(z2[:, b, :, :], z3[:, b, :, :], ACT.Exp, scale=-1.0), "exp")
                        a.wait_ge(act.sem, act.after(n, "exp"))
                        act.done(a.activation(z3[:, b, :, :], z1[:, b, :, :], ACT.Relu), "relu")
                    if c3:
                        norm.square(a, c3.n, c3.slot)
                    if c1:
                        n, b = c1.n, c1.slot
                        a.wait_ge(dve.sem, dve.after(n, "z"))
                        act.done(a.activation(z2[:, b, :, :], z1[:, b, :, :], ACT.Square), "sq")
                    if c2:
                        n, b = c2.n, c2.slot
                        a.wait_ge(ball.sem, ball.after(n, "zn"))
                        ball_act.done(a.activation(t[:, b, 11, :], t[:, b, 9, :], ACT.Tanh, scale=c["sqrt"]), "tanh")
                stages(a, CH, 4, 4, body)

            @block.gpsimd
            def _(gp):
                def body(c0, c1, c2, c3, c4):
                    if c2:
                        n, b = c2.n, c2.slot
                        gp.wait_ge(ball.sem, ball.after(n, "z2"))
                        root_pool.done(gp.tensor_tensor(t[:, b, 5, :], t[:, b, 4, :], g.half[:, :], ALU.pow), "zn0")
                    if c3:
                        n, h, k = c3.n, c3.slot, c3.k
                        norm.rstd(gp, n, h)
                        gp.wait_ge(lgps.sem, lgps.after(n, "rstd"))
                        gp.wait_ge(stored[h], k * 32)
                        lgps.done(norm.scaled(gp, x1[:, h, :, :], h), "x1")
                        gp.wait_ge(lgps.sem, lgps.after(n, "x1"))
                        gp.tensor_tensor(g1[:, h, :, :], x1[:, h, :, :],
                                         rso[:, h, :].unsqueeze(2).to_broadcast([P, GROUP, D]), ALU.mult).then_inc(ready[h], 1)
                    if c1:
                        n, b = c1.n, c1.slot
                        gp.wait_ge(dve.sem, dve.after(n, "dmax"))
                        degree_pool.done(gp.tensor_tensor(rso[:, b, :], t[:, b, 3, :], g.minus_half[:, :], ALU.pow), "rso")
                stages(gp, CH, 4, 4, body)
    sem.clear()


def convolve(nc, g, last, sem):
    name = "v2" if last else "v1"
    own, sums, weight = (g.H1, g.A2, g.w_conv2) if last else (g.X1, g.A1, g.w_conv1)
    LOADS = 48 if last else 32
    ctx = ExitStack()
    with ctx:
        def sb(label, shape, dt=F32):
            return ctx.enter_context(nc.sbuf_tensor(f"{name}_{label}", shape, dt))

        def ps(label, shape):
            return ctx.enter_context(nc.psum_tensor(f"{name}_{label}", shape, F32))

        x, a_in = sb("x", [P, 4, GROUP, D]), sb("a", [P, 4, GROUP, D + 1])
        s = sb("s", [P, 2, GROUP, D])
        both = sb("both", [P, 2, GROUP, 2 * D])
        both_t = sb("both_t", [P, 2, 2, 4 * P])
        turned = [ps(f"turned{i}", [P, 4 * P]) for i in range(2)]
        result = [ps(f"result{b}", [P, GROUP, D]) for b in range(2)]
        out = sb("out", [P, 4, GROUP, D])
        loaded, stored, ready = (sem.quad(f"{name}_{q}") for q in ("loaded", "stored", "ready"))
        sums_dve, turn_act = Engine(sem(f"{name}_sums"), "s u0 u1"), Engine(sem(f"{name}_turn_act"), "t0 t1")
        turn_pe, product_pe = Engine(sem(f"{name}_turn_pe"), "turn"), Engine(sem(f"{name}_product_pe"), "result")
        if last:
            x1 = sb("x1", [P, 4, GROUP, D])
            y, x2, squares = (sb(q, [P, 2, GROUP, D]) for q in ("y", "x2", "squares"))
            small = sb("small", [P, 2, 5, GROUP])
            x2_t = sb("x2_t", [P, 4 * P])
            turned2 = ps("turned2", [P, 4 * P])
            heads = [ps(f"heads{i}", [P, 2, 2, D + 8]) for i in range(2)]
            out2 = sb("out2", [P, 4, GROUP, D + 8])
            centre_dve, centre_act = Engine(sem(f"{name}_centre"), "y " + LN1), Engine(sem(f"{name}_square"), "lnsq")
            norm_dve, rstd_pool = Engine(sem(f"{name}_norm"), LN2 + " x2"), Engine(sem(f"{name}_rstd"), "rstd")
            row_act, heads_pe = Engine(sem(f"{name}_row"), "row x2t"), Engine(sem(f"{name}_heads_pe"), "turn2 heads")
            close_dve = Engine(sem(f"{name}_close"), "b")
            norm1 = Norm(g, y, squares, small, centre_dve, centre_act, rstd_pool)
            norm2 = Norm(g, y, squares, small, norm_dve, centre_act, rstd_pool)
        else:
            degree, rsi = sb("degree", [P, 2, GROUP]), sb("rsi", [P, 4, GROUP])
            out2 = sb("out2", [P, 4, GROUP, D])
            degree_dve, relu_act = Engine(sem(f"{name}_degree"), "dm"), Engine(sem(f"{name}_relu"), "relu")
            rsi_pool = Engine(sem(f"{name}_rsi"), "rsi")

        SKEW = 5 if last else 4

        def roles(c):
            return (None, c[1], c[2], c[3], c[4]) if last else (c[1], c[2], c[3], None, None)

        with nc.Block() as block:
            @block.sync
            def _(sp):
                def body(*c):
                    if c[0]:
                        n, h = c[0].n, c[0].slot
                        if not (isinstance(n, int) and n < 4):
                            if last:
                                sp.wait_ge(centre_dve.sem, centre_dve.after(n - 4, "y"))
                            else:
                                sp.wait_ge(sums_dve.sem, sums_dve.after(n - 4, "u1"))
                        sp.dma_start(flat(x[:, h, :, :]), chunk_rows(own, n, D)).then_inc(loaded[h], 16)
                        sp.dma_start(flat(a_in[:, h, :, :]), chunk_rows(sums, n, D + 1)).then_inc(loaded[h], 16)
                        if last:
                            sp.dma_start(flat(x1[:, h, :, :]), chunk_rows(g.X1, n, D)).then_inc(loaded[h], 16)
                    if c[-1]:
                        n, h = c[-1].n, c[-1].slot
                        sp.wait_ge(ready[h], c[-1].k + 1)
                        first, second = (g.B2, g.X2) if last else (g.H1, g.G2)
                        sp.dma_start(chunk_rows(first, n, D), flat(out[:, h, :, :])).then_inc(stored[h], 16)
                        sp.dma_start(chunk_rows(second, n, D + 8 if last else D), flat(out2[:, h, :, :])).then_inc(stored[h], 16)
                stages(sp, CH, 4, SKEW, body)
                for h in range(4):
                    sp.wait_ge(stored[h], len(range(h, CH, 4)) * 32)

            @block.vector
            def _(v):
                def body(*c):
                    for_degree, for_sums, for_products, for_norm, for_heads = roles(c)
                    if for_norm:
                        norm2.spread(v, for_norm.n, for_norm.slot % 2)
                    if for_degree:
                        n, h, b = for_degree.n, for_degree.slot, for_degree.slot % 2
                        v.wait_ge(loaded[h], (for_degree.k + 1) * LOADS)
                        degree_dve.done(v.tensor_scalar(degree[:, b, :], a_in[:, h, :, D], 1.0, None, ALU.max), "dm")
                    if for_sums:
                        n, h, b = for_sums.n, for_sums.slot, for_sums.slot % 2
                        if last:
                            v.wait_ge(loaded[h], (for_sums.k + 1) * LOADS)
                            factor = of_node(g, "rsi", n)
                        else:
                            v.wait_ge(rsi_pool.sem, rsi_pool.after(n, "rsi"))
                            v.tensor_copy(of_node(g, "rsi", n), rsi[:, h, :].unsqueeze(2))
                            factor = rsi[:, h, :].unsqueeze(2)
                        sums_dve.done(v.tensor_tensor(s[:, b, :, :], a_in[:, h, :, 0:D], factor.to_broadcast([P, GROUP, D]), ALU.mult), "s")
                        v.wait_ge(sums_dve.sem, sums_dve.after(n, "s"))
                        if not (isinstance(n, int) and n < 2):
                            v.wait_ge(turn_pe.sem, turn_pe.after(n - 2, "turn"))
                        sums_dve.done(v.tensor_tensor(both[:, b, :, 0:D], s[:, b, :, :], x[:, h, :, :], ALU.add), "u0")
                        sums_dve.done(v.tensor_tensor(both[:, b, :, D:], s[:, b, :, :], x[:, h, :, :], ALU.mult), "u1")
                    if for_heads:
                        n, h, b = for_heads.n, for_heads.slot, for_heads.slot % 2
                        v.wait_ge(heads_pe.sem, heads_pe.after(n, "heads"))
                        for i in range(2):
                            part = heads[i][:, :, :, :].rearrange("p q a k -> p (q a) k")
                            v.tensor_copy(out2[:, h, 4 * i:4 * i + 4, 0:8], part[:, :, 0:8])
                            step = v.tensor_tensor(x2[:, b, 4 * i:4 * i + 4, :], x2[:, b, 4 * i:4 * i + 4, :], part[:, :, 8:], ALU.add)
                        close_dve.done(step, "b")
                    if for_norm:
                        n, b = for_norm.n, for_norm.slot % 2
                        v.wait_ge(rstd_pool.sem, rstd_pool.after(n, "rstd"))
                        norm_dve.done(norm2.scaled(v, x2[:, b, :, :], b), "x2")
                    if for_products and last:
                        n, h, b = for_products.n, for_products.slot, for_products.slot % 2
                        v.wait_ge(product_pe.sem, product_pe.after(n, "result"))
                        centre_dve.done(v.tensor_tensor(y[:, b, :, :], result[b][:, :, :], x1[:, h, :, :], ALU.add), "y")
                        norm1.centre(v, n, b, "y")
                stages(v, CH, 4, SKEW, body)

            @block.tensor
            def _(te):
                def body(*c):
                    _, for_sums, for_products, for_norm, _ = roles(c)
                    if for_products:
                        n, b = for_products.n, for_products.slot % 2
                        te.wait_ge(turn_act.sem, turn_act.after(n, "t1"))
                        if not last and not (isinstance(n, int) and n < 2):
                            te.wait_ge(relu_act.sem, relu_act.after(n - 2, "relu"))
                        for j in range(GROUP):
                            step = te.matmul(result[b][:, j, :], lhsT=both_t[:, b, j // 4, (j % 4) * P:(j % 4 + 1) * P],
                                             rhs=weight[:, :], start=True, stop=True)
                        product_pe.done(step, "result")
                    if for_sums:
                        n, b = for_sums.n, for_sums.slot % 2
                        te.wait_ge(sums_dve.sem, sums_dve.after(n, "u1"))
                        for j in range(GROUP):
                            step = te.transpose(turned[j // 4][:, (j % 4) * P:(j % 4 + 1) * P], both[:, b, j, :], g.ident[:, :])
                        turn_pe.done(step, "turn")
                    if for_norm:
                        n, b = for_norm.n, for_norm.slot % 2
                        te.wait_ge(norm_dve.sem, norm_dve.after(n, "x2"))
                        for q in range(GROUP // 2):
                            step = te.transpose(turned2[:, q * P:(q + 1) * P],
                                                x2[:, b, 2 * q:2 * q + 2, :].rearrange("p a d -> p (a d)"), g.ident[:, :])
                        heads_pe.done(step, "turn2")
                        te.wait_ge(row_act.sem, row_act.after(n, "x2t"))
                        if not (isinstance(n, int) and n < 1):
                            te.wait_ge(close_dve.sem, close_dve.after(n - 1, "b"))
                        for q in range(GROUP // 2):
                            step = te.matmul(heads[q // 2][:, q % 2, :, :].rearrange("p a k -> p (a k)"),
                                             lhsT=x2_t[:, q * P:(q + 1) * P],
                                             rhs=g.w2_pair[:, :, :].rearrange("p a k -> p (a k)"), start=True, stop=True)
                        heads_pe.done(step, "heads")
                stages(te, CH, 4, SKEW, body)

            @block.scalar
            def _(a):
                def body(*c):
                    _, for_sums, for_products, for_norm, _ = roles(c)
                    if for_products and not last:
                        n, h, b = for_products.n, for_products.slot, for_products.slot % 2
                        a.wait_ge(product_pe.sem, product_pe.after(n, "result"))
                        a.wait_ge(stored[h], for_products.k * 32)
                        relu_act.done(a.activation(out[:, h, :, :], result[b][:, :, :], ACT.Relu), "relu")
                    if for_sums:
                        n, b = for_sums.n, for_sums.slot % 2
                        a.wait_ge(turn_pe.sem, turn_pe.after(n, "turn"))
                        for i in range(2):
                            turn_act.done(a.activation(both_t[:, b, i, :], turned[i][:, :], ACT.Copy), f"t{i}")
                    if for_norm:
                        n, h, b = for_norm.n, for_norm.slot, for_norm.slot % 2
                        a.wait_ge(norm_dve.sem, norm_dve.after(n, "x2"))
                        a.wait_ge(stored[h], for_norm.k * 32)
                        row_act.done(a.activation(out2[:, h, :, 8:], x2[:, b, :, :], ACT.Copy), "row")
                        a.wait_ge(heads_pe.sem, heads_pe.after(n, "turn2"))
                        row_act.done(a.activation(x2_t[:, :], turned2[:, :], ACT.Copy), "x2t")
                    if for_products and last:
                        norm1.square(a, for_products.n, for_products.slot % 2)
                stages(a, CH, 4, SKEW, body)

            @block.gpsimd
            def _(gp):
                def body(*c):
                    for_degree, _, for_products, for_norm, for_heads = roles(c)
                    if for_degree:
                        n, h, b = for_degree.n, for_degree.slot, for_degree.slot % 2
                        gp.wait_ge(degree_dve.sem, degree_dve.after(n, "dm"))
                        rsi_pool.done(gp.tensor_tensor(rsi[:, h, :], degree[:, b, :], g.minus_half[:, :], ALU.pow), "rsi")
                    if for_products and not last:
                        n, h, b = for_products.n, for_products.slot, for_products.slot % 2
                        gp.wait_ge(relu_act.sem, relu_act.after(n, "relu"))
                        gp.tensor_tensor(out2[:, h, :, :], out[:, h, :, :],
                                         of_node(g, "rso", n).to_broadcast([P, GROUP, D]), ALU.mult).then_inc(ready[h], 1)
                    if for_norm:
                        norm2.rstd(gp, for_norm.n, for_norm.slot % 2)
                    if for_heads:
                        n, h, b = for_heads.n, for_heads.slot, for_heads.slot % 2
                        gp.wait_ge(close_dve.sem, close_dve.after(n, "b"))
                        gp.wait_ge(stored[h], for_heads.k * 32)
                        gp.tensor_tensor(out[:, h, :, :], x2[:, b, :, :],
                                         g.bias[:, :].unsqueeze(1).to_broadcast([P, GROUP, D]), ALU.add).then_inc(ready[h], 1)
                stages(gp, CH, 4, SKEW, body)
    sem.clear()


def close_layer2(nc, g, sem):
    ctx = ExitStack()
    with ctx:
        def sb(label, shape, dt=F32):
            return ctx.enter_context(nc.sbuf_tensor(f"c2_{label}", shape, dt))

        def ps(label, shape):
            return ctx.enter_context(nc.psum_tensor(f"c2_{label}", shape, F32))

        base, more = sb("base", [P, 4, GROUP, D]), sb("more", [P, 4, GROUP, D])
        y, x3, squares = (sb(q, [P, 2, GROUP, D]) for q in ("y", "x3", "squares"))
        small = sb("small", [P, 2, 5, GROUP])
        x3_t = sb("x3_t", [P, 4 * P])
        turned = ps("turned", [P, 4 * P])
        scores = ps("scores", [P, GROUP, 2])
        row, pair = sb("row", [P, 4, GROUP, D + 2]), sb("pair", [P, 4, GROUP, 2])
        loaded, stored, ready = (sem.quad(f"c2_{q}") for q in ("loaded", "stored", "ready"))
        centre_dve, square_act = Engine(sem("c2_centre"), "y " + LN1), Engine(sem("c2_square"), "lnsq")
        norm_dve, rstd_pool = Engine(sem("c2_norm"), LN2 + " x3"), Engine(sem("c2_rstd"), "rstd")
        row_act, scores_pe = Engine(sem("c2_row"), "row x3t"), Engine(sem("c2_scores_pe"), "turn scores")
        close_dve = Engine(sem("c2_close"), "pair")
        norm1 = Norm(g, y, squares, small, centre_dve, square_act, rstd_pool)
        norm2 = Norm(g, y, squares, small, norm_dve, square_act, rstd_pool)
        ones_set = sem("c2_ones")
        with nc.Block() as block:
            @block.sync
            def _(sp):
                def body(c0, c1, c2, c3, c4):
                    if c0:
                        n, h = c0.n, c0.slot
                        if not (isinstance(n, int) and n < 4):
                            sp.wait_ge(centre_dve.sem, centre_dve.after(n - 4, "y"))
                        sp.dma_start(flat(base[:, h, :, :]), chunk_rows(g.B2, n, D)).then_inc(loaded[h], 16)
                        sp.dma_start(flat(more[:, h, :, :]), chunk_rows(g.A3, n, D)).then_inc(loaded[h], 16)
                    if c4:
                        n, h = c4.n, c4.slot
                        sp.wait_ge(ready[h], c4.k + 1)
                        sp.dma_start(chunk_rows(g.X3, n, D + 2), flat(row[:, h, :, :])).then_inc(stored[h], 16)
                        sp.dma_start(chunk_rows(g.S3, n, 2), flat(pair[:, h, :, :])).then_inc(stored[h], 16)
                stages(sp, CH, 4, 4, body)
                for h in range(4):
                    sp.wait_ge(stored[h], len(range(h, CH, 4)) * 32)

            @block.vector
            def _(v):
                v.memset(row[:, :, :, D + 1:], 1.0).then_inc(ones_set, 1)
                v.wait_ge(ones_set, 1)

                def body(c0, c1, c2, c3, c4):
                    if c2:
                        norm2.spread(v, c2.n, c2.slot % 2)
                    if c1:
                        n, h, b = c1.n, c1.slot, c1.slot % 2
                        v.wait_ge(loaded[h], (c1.k + 1) * 32)
                        centre_dve.done(v.tensor_tensor(y[:, b, :, :], base[:, h, :, :], more[:, h, :, :], ALU.add), "y")
                        norm1.centre(v, n, b, "y")
                    if c3:
                        n, h = c3.n, c3.slot
                        v.wait_ge(scores_pe.sem, scores_pe.after(n, "scores"))
                        v.wait_ge(stored[h], c3.k * 32)
                        v.tensor_copy(row[:, h, :, 0:1], scores[:, :, 1:2])
                        close_dve.done(v.tensor_copy(pair[:, h, :, :], scores[:, :, :]), "pair")
                        v.wait_ge(close_dve.sem, close_dve.after(n, "pair"))
                        v.sem_inc(ready[h], 1)
                    if c2:
                        n, b = c2.n, c2.slot % 2
                        v.wait_ge(rstd_pool.sem, rstd_pool.after(n, "rstd"))
                        norm_dve.done(norm2.scaled(v, x3[:, b, :, :], b), "x3")
                stages(v, CH, 4, 4, body)

            @block.tensor
            def _(te):
                def body(c0, c1, c2, c3, c4):
                    if c2:
                        n, b = c2.n, c2.slot % 2
                        te.wait_ge(norm_dve.sem, norm_dve.after(n, "x3"))
                        for q in range(GROUP // 2):
                            step = te.transpose(turned[:, q * P:(q + 1) * P],
                                                x3[:, b, 2 * q:2 * q + 2, :].rearrange("p a d -> p (a d)"), g.ident[:, :])
                        scores_pe.done(step, "turn")
                        te.wait_ge(row_act.sem, row_act.after(n, "x3t"))
                        if not (isinstance(n, int) and n < 1):
                            te.wait_ge(close_dve.sem, close_dve.after(n - 1, "pair"))
                        for q in range(GROUP // 2):
                            step = te.matmul(scores[:, 2 * q:2 * q + 2, :].rearrange("p a k -> p (a k)"),
                                             lhsT=x3_t[:, q * P:(q + 1) * P],
                                             rhs=g.a3_pair[:, :, :].rearrange("p a k -> p (a k)"), start=True, stop=True)
                        scores_pe.done(step, "scores")
                stages(te, CH, 4, 4, body)

            @block.scalar
            def _(a):
                a.wait_ge(ones_set, 1)

                def body(c0, c1, c2, c3, c4):
                    if c1:
                        norm1.square(a, c1.n, c1.slot % 2)
                    if c2:
                        n, h, b = c2.n, c2.slot, c2.slot % 2
                        a.wait_ge(norm_dve.sem, norm_dve.after(n, "x3"))
                        a.wait_ge(stored[h], c2.k * 32)
                        row_act.done(a.activation(row[:, h, :, 1:D + 1], x3[:, b, :, :], ACT.Copy), "row")
                        a.wait_ge(scores_pe.sem, scores_pe.after(n, "turn"))
                        row_act.done(a.activation(x3_t[:, :], turned[:, :], ACT.Copy), "x3t")
                stages(a, CH, 4, 4, body)

            @block.gpsimd
            def _(gp):
                def body(c0, c1, c2, c3, c4):
                    if c2:
                        norm2.rstd(gp, c2.n, c2.slot % 2)
                stages(gp, CH, 4, 4, body)
    sem.clear()


def close_layer3(nc, g, out_rows, sem):
    ctx = ExitStack()
    with ctx:
        def sb(label, shape, dt=F32):
            return ctx.enter_context(nc.sbuf_tensor(f"c3_{label}", shape, dt))

        def ps(label, shape):
            return ctx.enter_context(nc.psum_tensor(f"c3_{label}", shape, F32))

        x3, pair = sb("x3", [P, 4, GROUP, D + 2]), sb("pair", [P, 4, GROUP, 2])
        part = sb("part", [P, 4, 2, GROUP, D + 2])
        t = sb("t", [P, 2, 16, GROUP])
        logs = sb("logs", [P, 2, 3, GROUP])
        share = sb("share", [P, 2, 3, GROUP])
        p0, p1, p2 = (sb(q, [P, 2, GROUP, D]) for q in ("p0", "p1", "p2"))
        y, squares = (sb(q, [P, 4, GROUP, D]) for q in ("y", "squares"))
        small = sb("small", [P, 4, 5, GROUP])
        pt = sb("pt", [P, 2, 4 * P])
        turned = [ps(f"turned{i}", [P, 4 * P]) for i in range(2)]
        result = [ps(f"result{i}", [P, GROUP, D]) for i in range(2)]
        out = sb("out", [P, 4, GROUP, D])
        loaded, stored, ready = (sem.quad(f"c3_{q}") for q in ("loaded", "stored", "ready"))
        logs_dve, ex_act = Engine(sem("c3_logs"), "l0 loop has none m0 m1 top0 top rise"), Engine(sem("c3_ex"), "ex")
        sum_dve, own_pool = Engine(sem("c3_sum"), "w0 d0 d1 d2 shares q0 q1 q2 r1"), Engine(sem("c3_own"), "own")
        turn_pe, turn_act = Engine(sem("c3_turn_pe"), "turn"), Engine(sem("c3_turn_act"), "pt")
        result_pe, square_act = Engine(sem("c3_result_pe"), "result"), Engine(sem("c3_square"), "lnsq")
        centre_dve, norm_dve = Engine(sem("c3_centre"), "y " + LN1), Engine(sem("c3_norm"), LN2)
        rstd_pool = Engine(sem("c3_rstd"), "rstd")
        norm1 = Norm(g, y, squares, small, centre_dve, square_act, rstd_pool)
        norm2 = Norm(g, y, squares, small, norm_dve, square_act, rstd_pool)
        with nc.Block() as block:
            @block.sync
            def _(sp):
                def body(c0, c1, c2, c3, c4, c5):
                    if c0:
                        n, h = c0.n, c0.slot
                        if not (isinstance(n, int) and n < 4):
                            sp.wait_ge(centre_dve.sem, centre_dve.after(n - 4, "y"))
                        sp.dma_start(flat(x3[:, h, :, :]), chunk_rows(g.X3, n, D + 2)).then_inc(loaded[h], 16)
                        sp.dma_start(flat(pair[:, h, :, :]), chunk_rows(g.S3, n, 2)).then_inc(loaded[h], 16)
                        sp.dma_start(flat(part[:, h, 0, :, :]), chunk_rows(g.A4[1], n, D + 2)).then_inc(loaded[h], 16)
                        sp.dma_start(flat(part[:, h, 1, :, :]), chunk_rows(g.A4[0], n, D + 2)).then_inc(loaded[h], 16)
                    if c5:
                        n, h = c5.n, c5.slot
                        sp.wait_ge(ready[h], c5.k + 1)
                        if isinstance(n, int) and n == CH - 1:
                            sp.dma_start(out_rows[(CH - 1) * NODES:N, :].rearrange("(p j) k -> p (j k)", j=GROUP),
                                         flat(out[0:TAIL, h, :, :])).then_inc(stored[h], 16)
                        else:
                            sp.dma_start(chunk_rows(out_rows, n, D), flat(out[:, h, :, :])).then_inc(stored[h], 16)
                stages(sp, CH, 4, 5, body)
                for h in range(4):
                    sp.wait_ge(stored[h], len(range(h, CH, 4)) * 16)

            @block.vector
            def _(v):
                def scores(ch):
                    n, h, b = ch.n, ch.slot, ch.slot % 2
                    q = [t[:, b, i, :] for i in range(16)]
                    both = part[:, h, :, :, :]

                    def need(steps, name):
                        v.wait_ge(steps.sem, steps.after(n, name))

                    v.wait_ge(loaded[h], (ch.k + 1) * 64)
                    logs_dve.done(v.tensor_tensor(q[0], pair[:, h, :, 0], pair[:, h, :, 1], ALU.add), "l0")
                    need(logs_dve, "l0")
                    logs_dve.done(v.scalar_tensor_tensor(out=logs[:, b, 2, :], in0=q[0], scalar=SLOPE, in1=q[0], op0=ALU.mult, op1=ALU.max), "loop")
                    logs_dve.done(v.tensor_scalar(t[:, b, 2:4, :], both[:, :, :, D], 0.0, None, ALU.is_gt), "has")
                    need(logs_dve, "has")
                    logs_dve.done(v.tensor_scalar(t[:, b, 4:6, :], t[:, b, 2:4, :], -1.0, -NEG, ALU.add, ALU.mult), "none")
                    logs_dve.done(v.tensor_tensor(t[:, b, 6:8, :], both[:, :, :, D + 1], t[:, b, 2:4, :], ALU.mult), "m0")
                    need(logs_dve, "m0")
                    logs_dve.done(v.tensor_tensor(logs[:, b, 0:2, :], t[:, b, 6:8, :], t[:, b, 4:6, :], ALU.add), "m1")
                    need(logs_dve, "m1")
                    logs_dve.done(v.tensor_tensor(q[8], logs[:, b, 0, :], logs[:, b, 1, :], ALU.max), "top0")
                    need(logs_dve, "top0")
                    logs_dve.done(v.tensor_tensor(q[9], q[8], logs[:, b, 2, :], ALU.max), "top")
                    need(logs_dve, "top")
                    logs_dve.done(v.tensor_tensor(logs[:, b, :, :], logs[:, b, :, :], q[9].unsqueeze(1).to_broadcast([P, 3, GROUP]), ALU.subtract), "rise")

                def centre(ch):
                    n, h, b = ch.n, ch.slot, ch.slot % 2
                    v.wait_ge(result_pe.sem, result_pe.after(n, "result"))
                    centre_dve.done(v.tensor_tensor(y[:, h, :, :], result[b][:, :, :], x3[:, h, :, 1:D + 1], ALU.add), "y")
                    norm1.centre(v, n, h, "y")

                def sums(ch):
                    n, h, b = ch.n, ch.slot, ch.slot % 2
                    q = [t[:, b, i, :] for i in range(16)]
                    both = part[:, h, :, :, :]

                    def need(steps, name):
                        v.wait_ge(steps.sem, steps.after(n, name))

                    def of(i):
                        return share[:, b, i, :].unsqueeze(2).to_broadcast([P, GROUP, D])

                    need(ex_act, "ex")
                    sum_dve.done(v.tensor_tensor(t[:, b, 10:12, :], both[:, :, :, D], logs[:, b, 0:2, :], ALU.mult), "w0")
                    need(sum_dve, "w0")
                    sum_dve.done(v.tensor_tensor(q[12], q[10], q[11], ALU.add), "d0")
                    need(sum_dve, "d0")
                    sum_dve.done(v.tensor_tensor(q[13], q[12], logs[:, b, 2, :], ALU.add), "d1")
                    need(sum_dve, "d1")
                    sum_dve.done(v.reciprocal(q[14], q[13]), "d2")
                    need(sum_dve, "d2")
                    sum_dve.done(v.tensor_tensor(share[:, b, :, :], logs[:, b, :, :], q[14].unsqueeze(1).to_broadcast([P, 3, GROUP]), ALU.mult), "shares")
                    need(sum_dve, "shares")
                    sum_dve.done(v.tensor_tensor(p0[:, b, :, :], both[:, 0, :, 0:D], of(0), ALU.mult), "q0")
                    sum_dve.done(v.tensor_tensor(p1[:, b, :, :], both[:, 1, :, 0:D], of(1), ALU.mult), "q1")
                    need(sum_dve, "q1")
                    sum_dve.done(v.tensor_tensor(p0[:, b, :, :], p0[:, b, :, :], p1[:, b, :, :], ALU.add), "q2")
                    need(sum_dve, "q2")
                    need(own_pool, "own")
                    sum_dve.done(v.tensor_tensor(p0[:, b, :, :], p0[:, b, :, :], p2[:, b, :, :], ALU.add), "r1")

                def body(c0, c1, c2, c3, c4, c5):
                    if c2:
                        sums(c2)
                    if c4:
                        norm2.spread(v, c4.n, c4.slot)
                    if c1:
                        scores(c1)
                    if c3:
                        centre(c3)
                stages(v, CH, 4, 5, body)

            @block.tensor
            def _(te):
                def body(c0, c1, c2, c3, c4, c5):
                    if c3:
                        n, b = c3.n, c3.slot % 2
                        te.wait_ge(turn_act.sem, turn_act.after(n, "pt"))
                        for q in range(GROUP // 2):
                            step = te.matmul(result[b][:, 2 * q:2 * q + 2, :].rearrange("p a k -> p (a k)"),
                                             lhsT=pt[:, b, q * P:(q + 1) * P],
                                             rhs=g.w3_pair[:, :, :].rearrange("p a k -> p (a k)"), start=True, stop=True)
                        result_pe.done(step, "result")
                    if c2:
                        n, b = c2.n, c2.slot % 2
                        te.wait_ge(sum_dve.sem, sum_dve.after(n, "r1"))
                        for q in range(GROUP // 2):
                            step = te.transpose(turned[b][:, q * P:(q + 1) * P],
                                                p0[:, b, 2 * q:2 * q + 2, :].rearrange("p a d -> p (a d)"), g.ident[:, :])
                        turn_pe.done(step, "turn")
                stages(te, CH, 4, 5, body)

            @block.scalar
            def _(a):
                def body(c0, c1, c2, c3, c4, c5):
                    if c2:
                        n, b = c2.n, c2.slot % 2
                        a.wait_ge(turn_pe.sem, turn_pe.after(n, "turn"))
                        turn_act.done(a.activation(pt[:, b, :], turned[b][:, :], ACT.Copy), "pt")
                    if c1:
                        n, b = c1.n, c1.slot % 2
                        a.wait_ge(logs_dve.sem, logs_dve.after(n, "rise"))
                        ex_act.done(a.activation(logs[:, b, :, :], logs[:, b, :, :], ACT.Exp), "ex")
                    if c3:
                        norm1.square(a, c3.n, c3.slot)
                stages(a, CH, 4, 5, body)

            @block.gpsimd
            def _(gp):
                def body(c0, c1, c2, c3, c4, c5):
                    if c2:
                        n, h, b = c2.n, c2.slot, c2.slot % 2
                        gp.wait_ge(sum_dve.sem, sum_dve.after(n, "shares"))
                        own_pool.done(gp.tensor_tensor(p2[:, b, :, :], x3[:, h, :, 1:D + 1],
                                                       share[:, b, 2, :].unsqueeze(2).to_broadcast([P, GROUP, D]), ALU.mult), "own")
                    if c4:
                        n, h = c4.n, c4.slot
                        norm2.rstd(gp, n, h)
                        gp.wait_ge(rstd_pool.sem, rstd_pool.after(n, "rstd"))
                        gp.wait_ge(stored[h], c4.k * 16)
                        norm2.scaled(gp, out[:, h, :, :], h).then_inc(ready[h], 1)
                stages(gp, CH, 4, 5, body)
    sem.clear()


class Bag:
    pass


def gnn_kernel(nc, x, src, dst, edge_attr_16, L0_gnn_W, L0_gnn_c, L1_gnn_W1_1, L1_gnn_W2_1, L1_gnn_W1_2,
               L1_gnn_W2_2, L2_gnn_W, L2_gnn_att_src, L2_gnn_att_dst, L2_gnn_bias, L3_gnn_W, L3_gnn_a, out,
               table=None):
    def dram(name, rows, width, dt=F32):
        if table:
            return table(name, rows, width, dt)
        return nc.dram_tensor(name, (rows, width), dt).ap()

    g, w = Bag(), Bag()
    w.L0_W, w.L0_c, w.L2_W, w.L2_bias, w.L3_W, w.L3_a = L0_gnn_W, L0_gnn_c, L2_gnn_W, L2_gnn_bias, L3_gnn_W, L3_gnn_a
    w.L2_att_dst, w.L2_att_src = L2_gnn_att_dst, L2_gnn_att_src
    w.L1_W1_1, w.L1_W2_1, w.L1_W1_2, w.L1_W2_2 = L1_gnn_W1_1, L1_gnn_W2_1, L1_gnn_W1_2, L1_gnn_W2_2
    w.loads = 20
    g.mid0 = [dram(f"mid0_{s}", EP, 4, I32) for s in range(ORDERS)]
    g.mid1 = [dram(f"mid1_{s}", EP, 4, I32) for s in range(ORDERS)]
    g.sorted = [dram(f"sorted_{s}", EP + 2, 4, I32) for s in range(ORDERS)]
    g.same_row = [dram(f"same_row{s}", 1, EP) for s in range(ORDERS)]
    g.pen_row = [dram(f"pen_row{s}", 1, EP) for s in range(ORDERS)]
    g.Y, g.T0 = dram("Y", NP, D), dram("T0", NP, D + 2)
    g.X1, g.G1, g.H1, g.G2 = (dram(q, NP, D) for q in ("X1", "G1", "H1", "G2"))
    g.X2, g.B2, g.X3, g.S3 = dram("X2", NP, D + 8), dram("B2", NP, D), dram("X3", NP, D + 2), dram("S3", NP, 2)
    g.A0, g.A1, g.A2, g.A3 = dram("A0", NP, D + 2), dram("A1", NP, D + 1), dram("A2", NP, D + 1), dram("A3", NP, D)
    g.A4 = [dram(f"A4_{s}", NP, D + 2) for s in range(ORDERS)]
    g.zeroed_tables = [(g.A0, D + 2), (g.A1, D + 1), (g.A2, D + 1), (g.A3, D), (g.A4[0], D + 2), (g.A4[1], D + 2)]

    ctx = ExitStack()
    with ctx:
        def sb(name, shape, dt=F32):
            return ctx.enter_context(nc.sbuf_tensor(name, shape, dt))

        g.ident = sb("ident", [P, P])
        g.zeros_bf = sb("zeros_bf", [P, 512], BF16)
        g.zero_rows = sb("zero_rows", [P, GROUP * (D + 2)])
        g.half, g.minus_half = sb("half", [P, GROUP]), sb("minus_half", [P, GROUP])
        g.pick = sb("pick", [P, 2, 2, P])
        g.w0_pair, g.w2_pair = sb("w0_pair", [P, 2, D + 2]), sb("w2_pair", [P, 2, D + 8])
        g.a3_pair, g.w3_pair = sb("a3_pair", [P, 2, 2]), sb("w3_pair", [P, 2, D])
        g.w_heads = sb("w_heads", [P, 2, D])
        g.w_conv1, g.w_conv2 = sb("w_conv1", [P, D]), sb("w_conv2", [P, D])
        g.bias, g.k_row, g.k_cols = sb("bias", [P, D]), sb("k_row", [P, D]), sb("k_cols", [P, 2])
        g.c_cols = sb("c_cols", [P, 8])
        g.cs = {q: g.c_cols[:, i:i + 1] for i, q in enumerate(("c", "sqrt", "1/sqrt", "clip", "-2c", "c*c"))}
        g.rows = [sb(f"rows{s}", [P, EC, 3 * JT], I32) for s in range(ORDERS)]
        g.pen = [sb(f"pen{s}", [P, EC, JT]) for s in range(ORDERS)]
        g.contrib = [sb(f"contrib{s}", [P, EC, JT]) for s in range(ORDERS)]
        g.same = [sb(f"same{s}", [P, EC, JT]) for s in range(ORDERS)]
        g.node = {q: sb(f"node_{q}", [P, CH, GROUP]) for q in
                  "n2 sf y2 yk sy nh2 zeta s1 s2 rso rsi".split()}
        sem = Semaphores(nc)
        set_up(nc, g, w, sem)
        sort_edges(nc, g, src, dst, L3_gnn_a, edge_attr_16, sem)
        lay_out_edges(nc, g, sem)
        project(nc, g, x, sem)
        factors(nc, g, sem)
        place(nc, g, sem)
        attend_edges(nc, g, "e0", 0, "hyper", g.T0, g.T0, g.A0, sem)
        close_layer0(nc, g, x, sem)
        sum_edges(nc, g, "e1", g.G1, g.A1, sem)
        convolve(nc, g, False, sem)
        sum_edges(nc, g, "e2", g.G2, g.A2, sem)
        convolve(nc, g, True, sem)
        attend_edges(nc, g, "e3", 1, "heads", g.X2, g.X2, g.A3, sem)
        close_layer2(nc, g, sem)
        attend_edges(nc, g, "e4d", 1, "edge", g.S3, g.X3, g.A4[1], sem)
        attend_edges(nc, g, "e4s", 0, "edge", g.S3, g.X3, g.A4[0], sem)
        close_layer3(nc, g, out, sem)


_INS = ["x", "src", "dst", "edge_attr_16", "L0_gnn_W", "L0_gnn_c", "L1_gnn_W1_1", "L1_gnn_W2_1", "L1_gnn_W1_2",
        "L1_gnn_W2_2", "L2_gnn_W", "L2_gnn_att_src", "L2_gnn_att_dst", "L2_gnn_bias", "L3_gnn_W", "L3_gnn_a"]
_OUT = ((N, D), "float32")


def kernel(**inputs):
    import numpy as np
    import concourse.bacc as bacc
    from concourse.bass_utils import run_bass_kernel_spmd

    nc = bacc.Bacc("TRN2", target_bir_lowering=False, num_devices=1)
    arrays, args = {}, []
    for name in _INS:
        a = np.ascontiguousarray(inputs[name])
        arrays[f"in_{name}"] = a
        args.append(nc.dram_tensor(f"in_{name}", a.shape, mybir.dt.from_np(a.dtype), kind="ExternalInput").ap())
    result = nc.dram_tensor("out_rows", _OUT[0], mybir.dt.from_np(np.dtype(_OUT[1])), kind="ExternalOutput").ap()
    gnn_kernel(nc, *args, result)
    return run_bass_kernel_spmd(nc, [arrays], core_ids=[0]).results[0]["out_rows"]
```

```python
import math
from contextlib import ExitStack

import concourse.bass as bass
from concourse import mybir

F32 = mybir.dt.float32
I32 = mybir.dt.int32
BF16 = mybir.dt.bfloat16
F16 = mybir.dt.float16
ALU = mybir.AluOpType
ACT = mybir.ActivationFunctionType
AX = mybir.AxisListType

P = 128
D = 64
HEADS = 4
N = 100000
E = 50000
GROUP = 8
NODES = P * GROUP
CH = -(-N // NODES)
NP = CH * NODES
TAIL = (N - (CH - 1) * NODES) // GROUP
JT = 4
EDGES = P * JT
EC = -(-E // EDGES)
EP = EC * EDGES
TILES = EP // P
PAD_KEY = NP - 1
SKIP = 1 << 20
LOW = 256
HIGH = NP // LOW
LAST_E = E - (P - 1) * TILES
EPS, CLIP, LN_EPS, SLOPE = 1e-15, 0.98, 1e-5, 0.2
NEG = -1e30
ORDERS = 2

assert (N - (CH - 1) * NODES) % GROUP == 0 and EC == CH and HIGH <= 512


class Chunk:

    def __init__(self, i, r, unroll):
        self.n = i * unroll + r
        self.slot = r % unroll
        self.k = i + r // unroll


def stages(eng, count, unroll, skew, body, tail=0):
    def single(n):
        body(*[Chunk(0, n - s, unroll) if 0 <= n - s < count else None for s in range(skew + 1)])

    first = skew + unroll
    for n in range(first):
        single(n)
    loops = (count - first - tail) // unroll
    with eng.Fori(0, loops) as i:
        for u in range(unroll):
            body(*[Chunk(i, first + u - s, unroll) for s in range(skew + 1)])
    for n in range(first + loops * unroll, count + skew):
        single(n)


class Engine:

    def __init__(self, sem, names):
        self.sem, self.names, self.next = sem, names.split(), 0

    def done(self, instruction, name):
        assert self.names[self.next % len(self.names)] == name, (name, self.names[self.next % len(self.names)])
        self.next += 1
        instruction.then_inc(self.sem, 1)

    def after(self, n, name):
        return n * len(self.names) + self.names.index(name) + 1


class Semaphores:

    def __init__(self, nc):
        self.nc, self.held, self.n = nc, [], 0

    def __call__(self, name):
        s = self.nc.alloc_semaphore(name)
        self.held.append(s)
        return s

    def pair(self, name):
        return [self(f"{name}{h}") for h in range(2)]

    def quad(self, name):
        return [self(f"{name}{h}") for h in range(4)]

    def clear(self):
        self.nc.clear_and_free_semaphores(self.held)
        self.held = []
        self.nc.all_engine_barrier()


def lay_out_edges(nc, g, sem):
    for s in range(ORDERS):
        ctx = ExitStack()
        with ctx:
            def sb(name, shape, dt):
                return ctx.enter_context(nc.sbuf_tensor(name, shape, dt))

            rows = [sb(f"lay_rows{s}{q}", [EC, EDGES, 4], I32) for q in range(3)]
            key = [sb(f"lay_key{s}{q}", [EC, EDGES], F32) for q in range(3)]
            other = sb(f"lay_other{s}", [EC, EDGES], F32)
            contrib = sb(f"lay_contrib{s}", [EC, EDGES], F32)
            same = sb(f"lay_same{s}", [EC, EDGES], F32)
            more = sb(f"lay_more{s}", [EC, EDGES], F32)
            scat = sb(f"lay_scat{s}", [EC, EDGES], F32)
            pen = sb(f"lay_pen{s}", [EC, EDGES], F32)
            flat = [key[1], other, scat, pen, contrib, same]
            turned = [ctx.enter_context(nc.psum_tensor(f"lay_turned{s}{a}", [P, JT * EC], F32)) for a in range(6)]
            loaded, split, turn, stored = (sem(f"lay_{x}{s}") for x in ("loaded", "split", "turn", "stored"))
            with nc.Block() as block:
                @block.sync
                def _(sp):
                    for q in range(3):
                        sp.dma_start(rows[q][:, :, :].rearrange("p t k -> p (t k)"),
                                     g.sorted[s][q:q + EP, :].rearrange("(p t) k -> p (t k)", p=EC)).then_inc(loaded, 16)
                    sp.wait_ge(split, 3)
                    sp.dma_start(g.same_row[s][:, :].rearrange("a (p t) -> (a p) t", p=EC), same[:, :]).then_inc(stored, 16)
                    sp.dma_start(g.pen_row[s][:, :].rearrange("a (p t) -> (a p) t", p=EC), pen[:, :]).then_inc(stored, 16)
                    sp.wait_ge(stored, 32)

                @block.vector
                def _(v):
                    v.wait_ge(loaded, 48)
                    for q in range(3):
                        v.tensor_copy(key[q][:, :], rows[q][:, :, 0])
                    v.tensor_copy(other[:, :], rows[1][:, :, 1])
                    v.tensor_copy(contrib[:, :], rows[1][:, :, 2].bitcast(F32)).then_inc(split, 1)
                    v.wait_ge(split, 1)
                    v.tensor_tensor(same[:, :], key[1][:, :], key[0][:, :], ALU.is_equal)
                    v.tensor_tensor(more[:, :], key[1][:, :], key[2][:, :], ALU.is_equal).then_inc(split, 1)
                    v.wait_ge(split, 2)
                    v.tensor_scalar(pen[:, :], same[:, :], -1.0, -NEG, ALU.add, ALU.mult)
                    v.scalar_tensor_tensor(out=scat[:, :], in0=more[:, :], scalar=float(SKIP), in1=key[1][:, :],
                                           op0=ALU.mult, op1=ALU.add).then_inc(split, 1)
                    v.wait_ge(turn, 1)
                    for a in range(3):
                        v.tensor_copy(g.rows[s][:, :, a * JT:(a + 1) * JT],
                                      turned[a][:, :].rearrange("p (j c) -> p c j", j=JT))
                    for a, out in ((3, g.pen[s]), (4, g.contrib[s]), (5, g.same[s])):
                        last = v.tensor_copy(out[:, :, :], turned[a][:, :].rearrange("p (j c) -> p c j", j=JT))
                    last.then_inc(split, 1)

                @block.tensor
                def _(pe):
                    pe.wait_ge(split, 3)
                    for a in range(6):
                        for j in range(JT):
                            last = pe.transpose(turned[a][:, j * EC:(j + 1) * EC], flat[a][:, j * P:(j + 1) * P], g.ident[0:EC, 0:EC])
                    last.then_inc(turn, 1)
        sem.clear()


def sum_edges(nc, g, name, table, sums, sem):
    W = D + 1
    s = 1
    ctx = ExitStack()
    with ctx:
        def sb(label, shape, dt=F32):
            return ctx.enter_context(nc.sbuf_tensor(f"{name}_{label}", shape, dt))

        def ps(label, shape):
            return ctx.enter_context(nc.psum_tensor(f"{name}_{label}", shape, F32))

        from_rows = sb("from_rows", [P, 2, JT], I32)
        to_rows = sb("to_rows", [P, 2, JT], I32)
        got = sb("got", [P, 2, JT, W])
        same = sb("same_b", [W, 2, EDGES])
        run = sb("run", [W, 2, EDGES])
        out = sb("out", [P, 2, JT, W])
        turned = [ps(f"turned{h}", [W, EDGES]) for h in range(2)]
        back = [ps(f"back{h}", [P, JT * W]) for h in range(2)]
        from_ready, gathered, same_loaded, flipped, scanned, unflipped, out_ready, to_ready, filed = (
            sem.pair(f"{name}_{x}") for x in ("from_ready", "gathered", "same_loaded", "flipped", "scanned",
                                             "unflipped", "out_ready", "to_ready", "filed"))
        set_up = sem(f"{name}_set_up")
        with nc.Block() as block:
            @block.sync
            def _(sp):
                def body(c0, c1, c2):
                    if c0:
                        h, k = c0.slot, c0.k
                        sp.wait_ge(scanned[h], k)
                        sp.dma_start(same[:, h, :], g.same_row[s][:, bass.ds(c0.n * EDGES, EDGES)]
                                     .to_broadcast([W, EDGES])).then_inc(same_loaded[h], 16)
                stages(sp, EC, 2, 2, body)

            @block.vector
            def _(v):
                v.memset(got[:, :, :, D:W], 1.0)
                v.memset(run[:, 1, :], 0.0).then_inc(set_up, 1)
                v.wait_ge(set_up, 1)

                def body(c0, c1, c2):
                    if c0:
                        h, k = c0.slot, c0.k
                        v.wait_ge(gathered[h], k * 16 * JT)
                        v.tensor_copy(from_rows[:, h, :], g.rows[s][:, bass.ds(c0.n, 1), JT:2 * JT]
                                      .rearrange("p a j -> p (a j)")).then_inc(from_ready[h], 1)
                    if c1:
                        h, k = c1.slot, c1.k
                        v.wait_ge(filed[h], k * 16 * JT)
                        v.tensor_copy(to_rows[:, h, :], g.rows[s][:, bass.ds(c1.n, 1), 2 * JT:3 * JT]
                                      .rearrange("p a j -> p (a j)")).then_inc(to_ready[h], 1)
                        v.wait_ge(same_loaded[h], (k + 1) * 16)
                        v.wait_ge(flipped[h], k + 1)
                        v.wait_ge(unflipped[h], k)
                        v.wait_ge(scanned[1 - h], k + h)
                        v.tensor_tensor_scan(run[:, h, :], same[:, h, :], turned[h][:, :],
                                             run[:, 1 - h, EDGES - 1:EDGES], ALU.mult, ALU.add).then_inc(scanned[h], 1)
                stages(v, EC, 2, 2, body)

            @block.tensor
            def _(pe):
                pe.wait_ge(set_up, 1)

                def body(c0, c1, c2):
                    if c1:
                        h, k = c1.slot, c1.k
                        pe.wait_ge(gathered[h], (k + 1) * 16 * JT)
                        pe.wait_ge(scanned[h], k)
                        for j in range(JT):
                            last = pe.transpose(turned[h][:, j * P:(j + 1) * P], got[:, h, j, :], g.ident[:, :])
                        last.then_inc(flipped[h], 1)
                        pe.wait_ge(scanned[h], k + 1)
                        pe.wait_ge(out_ready[h], k)
                        for j in range(JT):
                            last = pe.transpose(back[h][:, j * W:(j + 1) * W], run[:, h, j * P:(j + 1) * P], g.ident[0:W, 0:W])
                        last.then_inc(unflipped[h], 1)
                stages(pe, EC, 2, 2, body)

            @block.scalar
            def _(a):
                def body(c0, c1, c2):
                    if c1:
                        h, k = c1.slot, c1.k
                        a.wait_ge(unflipped[h], k + 1)
                        a.wait_ge(filed[h], k * 16 * JT)
                        a.activation(out[:, h, :, :].rearrange("p j w -> p (j w)"), back[h][:, :],
                                     ACT.Copy).then_inc(out_ready[h], 1)
                stages(a, EC, 2, 2, body)

            @block.gpsimd
            def _(gp):
                gp.wait_ge(set_up, 1)

                def body(c0, c1, c2):
                    if c0:
                        h, k = c0.slot, c0.k
                        gp.wait_ge(from_ready[h], k + 1)
                        gp.wait_ge(flipped[h], k)
                        gp.nop(nofuse=True)
                        for j in range(JT):
                            gp.indirect_dma_start(out=got[:, h, j, 0:D], out_offset=None, in_=table[:, :],
                                                  in_offset=bass.IndirectOffsetOnAxis(ap=from_rows[:, h, j:j + 1], axis=0)
                                                  ).then_inc(gathered[h], 16)
                    if c2:
                        h, k = c2.slot, c2.k
                        gp.wait_ge(out_ready[h], k + 1)
                        gp.wait_ge(to_ready[h], k + 1)
                        gp.nop(nofuse=True)
                        for j in range(JT):
                            gp.indirect_dma_start(out=sums[:, :],
                                                  out_offset=bass.IndirectOffsetOnAxis(ap=to_rows[:, h, j:j + 1], axis=0),
                                                  in_=out[:, h, j, :], in_offset=None,
                                                  bounds_check=NP - 1, oob_is_err=False).then_inc(filed[h], 16)
                stages(gp, EC, 2, 2, body)
                for h in range(2):
                    gp.wait_ge(filed[h], EC // 2 * 16 * JT)
    sem.clear()


def chunk_rows(table, n, width):
    return table[bass.ds(n * NODES, NODES), :].rearrange("(p j) k -> p (j k)", p=P)


def flat(tile):
    return tile.rearrange("p j k -> p (j k)")


def set_up(nc, g, w, sem):
    ctx = ExitStack()
    with ctx:
        def sb(label, shape, dt=F32):
            return ctx.enter_context(nc.sbuf_tensor(f"su_{label}", shape, dt))

        ones = sb("ones", [D, P])
        w0 = sb("w0", [P, D])
        w_att = sb("w_att", [P, HEADS, D])
        att = sb("att", [P, 2, HEADS, D])
        prod = sb("prod", [P, 2, HEADS, D])
        summed = sb("summed", [P, 2, HEADS])
        mean = sb("mean", [P, D])
        w3 = sb("w3", [P, D])
        a3 = sb("a3", [P, 2, D])
        prod3 = sb("prod3", [P, 2, D])
        sum3 = sb("sum3", [P, 2])
        prod0 = sb("prod0", [P, 2, D])
        sum0 = sb("sum0", [P, 2])
        colsum = ctx.enter_context(nc.psum_tensor("su_colsum", [P, D], F32))
        const, loaded, pe_done, dve, pooled = (sem(f"su_{x}") for x in (
            "const", "loaded", "pe", "dve", "pooled"))
        with nc.Block() as block:
            @block.gpsimd
            def _(gp):
                gp.memset(g.ident[:, :], 0.0)
                gp.memset(g.zeros_bf[:, :], 0.0)
                gp.memset(g.zero_rows[:, :], 0.0)
                gp.memset(g.half[:, :], 0.5)
                gp.memset(g.minus_half[:, :], -0.5)
                gp.memset(ones[:, :], 1.0)
                gp.memset(g.w0_pair[:, :, :], 0.0)
                gp.memset(g.w2_pair[:, :, :], 0.0)
                gp.memset(g.a3_pair[:, :, :], 0.0)
                gp.memset(g.w3_pair[:, :, :], 0.0)
                gp.memset(g.pick[:, :, :, :], 0.0).then_inc(const, 1)
                gp.wait_ge(const, 1)
                gp.affine_select(out=g.ident[:, :], in_=g.ident[:, :], compare_op=ALU.not_equal, fill=1.0,
                                 base=0, pattern=[[-1, P]], channel_multiplier=1)
                picked = g.pick[:, :, :, :].rearrange("r w q (a d) -> r (w q a) d", d=D)
                gp.affine_select(out=picked, in_=picked, compare_op=ALU.not_equal, fill=1.0,
                                 base=0, pattern=[[-1, 8], [0, D]], channel_multiplier=1).then_inc(const, 1)
                gp.wait_ge(loaded, 16 * w.loads)
                gp.tensor_tensor(g.c_cols[:, 1:2], g.c_cols[:, 0:1], g.half[:, 0:1], ALU.pow).then_inc(pooled, 1)

            @block.sync
            def _(sp):
                n = 0

                def load(out, in_):
                    nonlocal n
                    n += 1
                    sp.dma_start(out, in_).then_inc(loaded, 16)

                for a in range(2):
                    half = slice(a * D, (a + 1) * D)
                    load(w0[half, :], w.L0_W[:, :])
                    load(w3[half, :], w.L3_W[:, :])
                    load(w_att[half, :, :], w.L2_W.rearrange("k (h d) -> k h d", h=HEADS))
                    for q in range(2):
                        load(g.w_heads[half, q, :], w.L2_W[:, (2 * q + a) * D:(2 * q + a + 1) * D])
                    load(g.w_conv1[half, :], (w.L1_W1_1, w.L1_W2_1)[a][:, :])
                    load(g.w_conv2[half, :], (w.L1_W1_2, w.L1_W2_2)[a][:, :])
                for a, x in enumerate((w.L2_att_dst, w.L2_att_src)):
                    load(att[:, a, :, :].rearrange("p h d -> p (h d)"), x.rearrange("a h d -> a (h d)").to_broadcast([P, HEADS * D]))
                load(a3[:, 0, :], w.L3_a[D:2 * D, :].rearrange("k a -> a k").to_broadcast([P, D]))
                load(a3[:, 1, :], w.L3_a[0:D, :].rearrange("k a -> a k").to_broadcast([P, D]))
                load(g.bias[:, :], w.L2_bias.rearrange("(a d) -> a d", a=1).to_broadcast([P, D]))
                load(g.c_cols[:, 0:1], w.L0_c.rearrange("(a d) -> a d", a=1).to_broadcast([P, 1]))
                assert n == w.loads, n

            @block.tensor
            def _(pe):
                pe.wait_ge(const, 2)
                pe.wait_ge(loaded, 16 * w.loads)
                pe.matmul(colsum[:, :], lhsT=ones[:, :], rhs=w0[0:D, :], start=True, stop=True).then_inc(pe_done, 1)

            @block.vector
            def _(v):
                n = 0

                def step(instruction):
                    nonlocal n
                    n += 1
                    instruction.then_inc(dve, 1)
                    v.wait_ge(dve, n)

                v.wait_ge(loaded, 16 * w.loads)
                v.wait_ge(const, 2)
                v.wait_ge(pe_done, 1)
                v.tensor_copy(g.k_row[:, :], colsum[:, :])
                step(v.tensor_copy(prod0[:, 1, :], w0[:, :]))
                step(v.tensor_tensor(prod0[:, 0, :], w0[:, :], g.k_row[:, :], ALU.mult))
                step(v.tensor_reduce(sum0[:, :], prod0[:, :, :], AX.X, ALU.add))
                for a in range(2):
                    half = slice(a * D, (a + 1) * D)
                    v.tensor_copy(g.w0_pair[half, a, 0:D], w0[half, :])
                    v.tensor_copy(g.w0_pair[half, a, D:D + 2], sum0[half, :])
                    v.tensor_copy(g.w3_pair[half, a, :], w3[half, :])
                step(v.tensor_reduce(g.k_cols[:, 0:1], g.k_row[:, :], AX.X, ALU.add))
                step(v.tensor_tensor(prod0[:, 0, :], g.k_row[:, :], g.k_row[:, :], ALU.mult))
                step(v.tensor_reduce(g.k_cols[:, 1:2], prod0[:, 0, :], AX.X, ALU.add))
                step(v.tensor_scalar(g.k_cols[:, 0:1], g.k_cols[:, 0:1], EPS, None, ALU.mult))
                step(v.tensor_scalar(g.k_cols[:, 1:2], g.k_cols[:, 1:2], EPS * EPS, None, ALU.mult))
                step(v.tensor_tensor(prod[:, :, :, :].rearrange("p a h d -> p a (h d)"), att[:, :, :, :].rearrange("p a h d -> p a (h d)"),
                                     w_att[:, :, :].rearrange("p h d -> p (h d)").unsqueeze(1).to_broadcast([P, 2, HEADS * D]), ALU.mult))
                step(v.tensor_reduce(summed[:, :, :], prod[:, :, :, :], AX.X, ALU.add))
                step(v.tensor_reduce(mean[:, :], w_att[:, :, :].rearrange("p h d -> p d h"), AX.X, ALU.add))
                step(v.tensor_scalar(mean[:, :], mean[:, :], 1.0 / HEADS, None, ALU.mult))
                step(v.tensor_scalar(g.w_heads[:, :, :], g.w_heads[:, :, :], 1.0 / HEADS, None, ALU.mult))
                step(v.tensor_tensor(prod3[:, :, :], a3[:, :, :], w3[:, :].unsqueeze(1).to_broadcast([P, 2, D]), ALU.mult))
                step(v.tensor_reduce(sum3[:, :], prod3[:, :, :], AX.X, ALU.add))
                for a in range(2):
                    half = slice(a * D, (a + 1) * D)
                    v.tensor_copy(g.w2_pair[half, a, 0:8], summed[half, :, :].rearrange("p a h -> p (a h)"))
                    v.tensor_copy(g.w2_pair[half, a, 8:], mean[half, :])
                    v.tensor_copy(g.a3_pair[half, a, :], sum3[half, :])
                c = g.cs
                v.wait_ge(pooled, 1)
                step(v.reciprocal(c["1/sqrt"], c["sqrt"]))
                step(v.tensor_scalar(c["clip"], c["1/sqrt"], CLIP, None, ALU.mult))
                step(v.tensor_scalar(c["-2c"], c["c"], -2.0, None, ALU.mult))
                step(v.tensor_tensor(c["c*c"], c["c"], c["c"], ALU.mult))
    sem.clear()


class Beside:

    def __init__(self, sync, vector, tensor, scalar, finish):
        self.sync, self.vector, self.tensor, self.scalar, self.finish = sync, vector, tensor, scalar, finish


def project(nc, g, x, sem, ctx):
    def sb(label, shape, dt=F32):
        return ctx.enter_context(nc.sbuf_tensor(f"pr_{label}", shape, dt))

    def ps(label, shape):
        return ctx.enter_context(nc.psum_tensor(f"pr_{label}", shape, F32))

    xin = sb("x", [P, 4, GROUP, D])
    f0 = sb("f0", [P, 2, GROUP, D])
    xt = sb("xt", [P, 2, GROUP // 2, P])
    y = sb("y", [P, 4, GROUP, D])
    squares = sb("squares", [P, 2, 2, GROUP, D])
    turned = [ps(f"turned{h}", [P, GROUP // 2 * P]) for h in range(2)]
    prod = [[ps(f"prod{h}{b}", [P, 2, 2, D + 2]) for b in range(2)] for h in range(2)]
    loaded, stored = sem.quad("pr_loaded"), sem.quad("pr_stored")
    turn_dve, turn_act, turn_pe = Engine(sem("pr_dve"), "f0 sum"), Engine(sem("pr_act"), "sqx xt"), Engine(sem("pr_pe"), "turn")
    prod_act, prod_pe = Engine(sem("pr_prod_act"), "y0 y1 sqy0 sqy1"), Engine(sem("pr_prod_pe"), "prod")
    def sync(sp, c0, c1, c2, c3):
        if c0:
            h, k = c0.slot, c0.k
            if not (isinstance(c0.n, int) and c0.n < 4):
                sp.wait_ge(turn_dve.sem, turn_dve.after(c0.n - 4, "f0"))
            if isinstance(c0.n, int) and c0.n == CH - 1:
                sp.dma_start(flat(xin[0:TAIL, h, :, :]), x[(CH - 1) * NODES:N, :]
                             .rearrange("(p j) k -> p (j k)", j=GROUP)).then_inc(loaded[h], 16)
            else:
                sp.dma_start(flat(xin[:, h, :, :]), chunk_rows(x, c0.n, D)).then_inc(loaded[h], 16)
        if c3:
            sp.wait_ge(prod_act.sem, prod_act.after(c3.n, "y1"))
            sp.dma_start(chunk_rows(g.Y, c3.n, D), flat(y[:, c3.slot, :, :])).then_inc(stored[c3.slot], 16)

    def finish(sp):
        for h in range(4):
            sp.wait_ge(stored[h], len(range(h, CH, 4)) * 16)

    def reduce(v, name, n, of):
        return v.tensor_reduce(g.node[name][:, bass.ds(n, 1), :].rearrange("p a j -> p (a j)"), of, AX.X, ALU.add)

    def vector(v, c0, c1, c2, c3):
        if c3:
            n, b = c3.n, c3.slot % 2
            v.wait_ge(prod_act.sem, prod_act.after(n, "sqy1"))
            for i in range(2):
                for which, name in enumerate(("yk", "sy")):
                    at = g.node[name][:, bass.ds(n, 1), 4 * i:4 * i + 4]
                    v.tensor_copy(at, prod[b][i][:, :, :, D + which].rearrange("p q a -> p (q a)").unsqueeze(1))
            reduce(v, "y2", n, squares[:, b, 1, :, :])
        if c1:
            n, h, b = c1.n, c1.slot, c1.slot % 2
            v.wait_ge(loaded[h], (c1.k + 1) * 16)
            turn_dve.done(v.tensor_scalar(f0[:, b, :, :], xin[:, h, :, :], EPS, None, ALU.add), "f0")
            v.wait_ge(turn_dve.sem, turn_dve.after(n, "f0"))
            turn_dve.done(reduce(v, "sf", n, f0[:, b, :, :]), "sum")
        if c2:
            n, b = c2.n, c2.slot % 2
            v.wait_ge(turn_act.sem, turn_act.after(n, "sqx"))
            reduce(v, "n2", n, squares[:, b, 0, :, :])

    def tensor(t, c0, c1, c2, c3):
        if c2:
            n, b = c2.n, c2.slot % 2
            t.wait_ge(turn_act.sem, turn_act.after(n, "xt"))
            for q in range(GROUP // 2):
                last = t.matmul(prod[b][q // 2][:, q % 2, :, :].rearrange("p a k -> p (a k)"),
                                lhsT=xt[:, b, q, :], rhs=g.w0_pair[:, :, :].rearrange("p a k -> p (a k)"),
                                start=True, stop=True)
            prod_pe.done(last, "prod")
        if c1:
            n, b = c1.n, c1.slot % 2
            t.wait_ge(turn_dve.sem, turn_dve.after(n, "f0"))
            for q in range(GROUP // 2):
                last = t.transpose(turned[b][:, q * P:(q + 1) * P],
                                   f0[:, b, 2 * q:2 * q + 2, :].rearrange("p a d -> p (a d)"), g.ident[:, :])
            turn_pe.done(last, "turn")

    def scalar(a, c0, c1, c2, c3):
        if c1:
            n, b = c1.n, c1.slot % 2
            a.wait_ge(turn_dve.sem, turn_dve.after(n, "f0"))
            turn_act.done(a.activation(squares[:, b, 0, :, :], f0[:, b, :, :], ACT.Square), "sqx")
            a.wait_ge(turn_pe.sem, turn_pe.after(n, "turn"))
            turn_act.done(a.activation(xt[:, b, :, :].rearrange("p q m -> p (q m)"), turned[b][:, :], ACT.Copy), "xt")
        if c2:
            n, h, b = c2.n, c2.slot, c2.slot % 2
            a.wait_ge(prod_pe.sem, prod_pe.after(n, "prod"))
            a.wait_ge(stored[h], c2.k * 16)
            for i in range(2):
                prod_act.done(a.activation(y[:, h, 4 * i:4 * i + 4, :], prod[b][i][:, :, :, 0:D]
                                           .rearrange("p q a k -> p (q a) k"), ACT.Copy), f"y{i}")
            for i in range(2):
                prod_act.done(a.activation(squares[:, b, 1, 4 * i:4 * i + 4, :], prod[b][i][:, :, :, 0:D]
                                           .rearrange("p q a k -> p (q a) k"), ACT.Square), f"sqy{i}")

    return Beside(sync, vector, tensor, scalar, finish)


def factors(nc, g, sem):
    ctx = ExitStack()
    with ctx:
        node, c = g.node, g.cs
        names = "n fs a pn pc yn sp b t t2 m u s sg".split()
        tile = {x: ctx.enter_context(nc.sbuf_tensor(f"fa_{x}", [P, CH * GROUP], F32)) for x in names}
        A = {x: tile[x][:, :] for x in names}
        for x in ("n2", "sf", "y2", "yk", "sy", "nh2", "zeta", "s1", "s2"):
            A[x] = node[x][:, :, :].rearrange("p c j -> p (c j)")
        to_act, from_act, dve = sem("fa_to_act"), sem("fa_from_act"), sem("fa_dve")
        asked = []

        with nc.Block() as block:
            @block.vector
            def _(v):
                n = 0

                def step(instruction):
                    nonlocal n
                    n += 1
                    instruction.then_inc(dve, 1)
                    v.wait_ge(dve, n)

                def ts(out, x, a, op, b=None, op2=None):
                    if op2 is None:
                        step(v.tensor_scalar(A[out], A[x], a, None, op))
                    else:
                        step(v.tensor_scalar(A[out], A[x], a, b, op, op2))

                def tt(out, x, y, op):
                    step(v.tensor_tensor(A[out], A[x], A[y], op))

                def stt(out, x, a, y, op, op2):
                    step(v.scalar_tensor_tensor(out=A[out], in0=A[x], scalar=a, in1=A[y], op0=op, op1=op2))

                def inv(out, x):
                    step(v.reciprocal(A[out], A[x]))

                def on_act(out, x, f, scale=1.0, bias=0.0):
                    asked.append((out, x, f, scale, bias))
                    v.sem_inc(to_act, 1)
                    v.wait_ge(from_act, len(asked))

                def clip_factor(out, norm, limit):
                    ts("t", norm, limit, ALU.max)
                    inv("t", "t")
                    ts(out, "t", limit, ALU.mult)

                def artanh(out, x):
                    tt("t", x, x, ALU.mult)
                    ts("t2", "t", 1 / 15, ALU.mult, 1 / 13, ALU.add)
                    for d in (11, 9, 7, 5, 3, 1):
                        tt("t2", "t2", "t", ALU.mult)
                        ts("t2", "t2", 1 / d, ALU.add)
                    tt("t2", "t2", x, ALU.mult)
                    on_act("t", x, ACT.Ln, 1.0, 1.0)
                    on_act("u", x, ACT.Ln, -1.0, 1.0)
                    tt("t", "t", "u", ALU.subtract)
                    ts("t", "t", 0.5, ALU.mult)
                    ts("m", x, 0.25, ALU.is_lt)
                    tt("t2", "t2", "m", ALU.mult)
                    ts("m", x, 0.25, ALU.is_ge)
                    tt("t", "t", "m", ALU.mult)
                    tt(out, "t", "t2", ALU.add)

                on_act("n", "n2", ACT.Sqrt)
                clip_factor("fs", "n", CLIP)
                tt("n", "n", "fs", ALU.mult)
                inv("s", "n")
                on_act("n", "n", ACT.Tanh)
                tt("a", "n", "s", ALU.mult)
                tt("a", "a", "fs", ALU.mult)
                tt("s", "a", "a", ALU.mult)
                tt("t", "s", "n2", ALU.mult)
                tt("u", "a", "sf", ALU.mult)
                stt("t", "u", 2 * EPS, "t", ALU.mult, ALU.add)
                ts("t", "t", D * EPS * EPS, ALU.add, 0.0, ALU.max)
                on_act("pn", "t", ACT.Sqrt)
                clip_factor("pc", "pn", CLIP)
                tt("pn", "pn", "pc", ALU.mult)
                tt("t", "s", "y2", ALU.mult)
                tt("u", "a", "yk", ALU.mult)
                stt("t", "u", 2 * EPS, "t", ALU.mult, ALU.add)
                ts("t", "t", g.k_cols[:, 1:2], ALU.add)
                ts("t", "t", 0.0, ALU.max)
                on_act("yn", "t", ACT.Sqrt)
                tt("sp", "a", "sy", ALU.mult)
                ts("sp", "sp", g.k_cols[:, 0:1], ALU.add)
                ts("s", "pn", c["sqrt"], ALU.mult, 0.9, ALU.min)
                artanh("b", "s")
                inv("s", "pn")
                tt("b", "b", "s", ALU.mult)
                tt("b", "b", "pc", ALU.mult)
                ts("b", "b", c["1/sqrt"], ALU.mult)
                tt("n", "b", "yn", ALU.mult)
                clip_factor("fs", "n", c["clip"])
                tt("n", "n", "fs", ALU.mult)
                inv("s", "n")
                on_act("n", "n", ACT.Tanh, "sqrt")
                tt("n", "n", "s", ALU.mult)
                tt("n", "n", "fs", ALU.mult)
                tt("n", "n", "b", ALU.mult)
                ts("sg", "n", c["1/sqrt"], ALU.mult)
                tt("s1", "sg", "a", ALU.mult)
                ts("s2", "sg", EPS, ALU.mult)
                tt("t", "sg", "yn", ALU.mult)
                tt("nh2", "t", "t", ALU.mult)
                tt("u", "sg", "sp", ALU.mult)
                stt("t", "u", 2 * EPS, "nh2", ALU.mult, ALU.add)
                ts("t", "t", D * EPS * EPS, ALU.add, 0.0, ALU.max)
                on_act("n", "t", ACT.Sqrt)
                clip_factor("fs", "n", CLIP)
                tt("n", "n", "fs", ALU.mult)
                ts("s", "n", c["sqrt"], ALU.mult, 0.9, ALU.min)
                artanh("b", "s")
                inv("s", "n")
                tt("b", "b", "s", ALU.mult)
                tt("zeta", "b", "fs", ALU.mult)

            @block.scalar
            def _(a):
                for i, (out, x, f, scale, bias) in enumerate(asked):
                    a.wait_ge(to_act, i + 1)
                    a.activation(A[out], A[x], f, bias=bias, scale=c["sqrt"] if scale == "sqrt" else scale).then_inc(from_act, 1)
    sem.clear()


def place(nc, g, sem, ctx):
    def sb(label, shape, dt=F32):
        return ctx.enter_context(nc.sbuf_tensor(f"pl_{label}", shape, dt))

    y = sb("y", [P, 4, GROUP, D])
    t1 = sb("t1", [P, 2, GROUP, D])
    t2 = sb("t2", [P, 2, GROUP, D])
    row = sb("row", [P, 4, GROUP, D + 2])
    loaded, stored, ready = (sem.quad(f"pl_{x}") for x in ("loaded", "stored", "ready"))
    made = Engine(sem("pl_dve"), "t1 t2")
    def sync(sp, c0, c1, c2, c3):
        if c0:
            sp.wait_ge(stored[c0.slot], c0.k * 16)
            sp.dma_start(flat(y[:, c0.slot, :, :]), chunk_rows(g.Y, c0.n, D)).then_inc(loaded[c0.slot], 16)
        if c2:
            sp.wait_ge(ready[c2.slot], c2.k + 1)
            sp.dma_start(chunk_rows(g.T0, c2.n, D + 2), flat(row[:, c2.slot, :, :])).then_inc(stored[c2.slot], 16)

    def finish(sp):
        for h in range(4):
            sp.wait_ge(stored[h], len(range(h, CH, 4)) * 16)

    def vector(v, c0, c1, c2, c3):
        if c1:
            n, h, b = c1.n, c1.slot, c1.slot % 2

            def per_node(name):
                return g.node[name][:, bass.ds(n, 1), :].rearrange("p a j -> p j a")

            v.wait_ge(loaded[h], (c1.k + 1) * 16)
            made.done(v.tensor_tensor(t1[:, b, :, :], y[:, h, :, :], per_node("s1").to_broadcast([P, GROUP, D]), ALU.mult), "t1")
            made.done(v.tensor_tensor(t2[:, b, :, :], g.k_row[:, :].unsqueeze(1).to_broadcast([P, GROUP, D]),
                                      per_node("s2").to_broadcast([P, GROUP, D]), ALU.mult), "t2")
            v.wait_ge(stored[h], c1.k * 16)
            v.tensor_copy(row[:, h, :, 0:1], per_node("nh2"))
            v.tensor_copy(row[:, h, :, 1:2], per_node("zeta"))
            v.wait_ge(made.sem, made.after(n, "t2"))
            v.tensor_tensor(row[:, h, :, 2:], t1[:, b, :, :], t2[:, b, :, :], ALU.add).then_inc(ready[h], 1)

    def nothing(engine, *chunks):
        pass

    return Beside(sync, vector, nothing, nothing, finish)


def sort_edges(nc, g, src, dst, l3_a, attr, x, sem):
    ctx = ExitStack()
    with ctx:
        def sb(name, shape, dt):
            return ctx.enter_context(nc.sbuf_tensor(name, shape, dt))

        hot = sb("sort_hot", [P, 8, 2 * LOW + 2 * HIGH], BF16)
        buckets = sb("sort_buckets", [P, 512], F16)
        base = sb("sort_base", [P, 2 * LOW + 2 * HIGH], F32)
        before = sb("sort_before", [P, P], BF16)
        notbefore = sb("sort_notbefore", [P, P], BF16)
        stage = sb("sort_stage", [P, 4, ORDERS, JT, 4], I32)
        half_i = sb("sort_half_i", [P, 4, ORDERS * JT], I32)
        half_d = sb("sort_half_d", [P, 4, ORDERS * JT], F32)
        place_f = sb("sort_place_f", [P, 4, ORDERS * JT], F32)
        place_i = sb("sort_place_i", [P, 4, ORDERS * JT], I32)
        junk = sb("sort_junk", [P, 2, 512], F32)
        ranks = [ctx.enter_context(nc.psum_tensor(f"sort_ranks{s}", [P, 512], F32)) for s in range(2)]

        def cols(s, high):
            at = 2 * LOW + s * HIGH if high else s * LOW
            return slice(at, at + (HIGH if high else LOW))

        mid0, mid1, final = g.mid0, g.mid1, g.sorted

        loaded, const, made, dve, counted = (sem(x) for x in (
            "sort_loaded", "sort_const", "sort_made", "sort_dve", "sort_counted"))
        hot_ready, hot_used, mid_stored = sem("sort_hot_ready"), sem("sort_hot_used"), sem("sort_mid_stored")
        hist = ExitStack()
        with hist:
            def first(name, shape, dt):
                return hist.enter_context(nc.sbuf_tensor(name, shape, dt))

            keys = first("sort_keys", [P, ORDERS, TILES], I32)
            digit_i = first("sort_digit_i", [P, TILES], I32)
            digits = first("sort_digits", [P, ORDERS, 2, TILES], F32)
            attrs = first("sort_attrs", [P, TILES, 16], F32)
            a_edge = first("sort_a_edge", [P, 16], F32)
            contrib = first("sort_contrib", [P, TILES], F32)
            record = first("sort_record", [P, ORDERS, TILES, 4], I32)
            ones_row = first("sort_ones_row", [P, 512], F32)
            total = first("sort_total", [P, 2 * LOW + 2 * HIGH], F32)
            upto = first("sort_upto", [P, 2 * LOW + 2 * HIGH], F32)
            ones_bf = first("sort_ones", [P, P], BF16)
            edge_row = first("sort_edge_row", [1, 8], I32)
            count_lo = hist.enter_context(nc.psum_tensor("sort_count_lo", [P, 512], F32))
            count_hi = [hist.enter_context(nc.psum_tensor(f"sort_count_hi{s}", [P, 512], F32)) for s in range(2)]
            with nc.Block() as block:
                @block.sync
                def _(sp):
                    sp.wait_ge(const, 3)
                    for s, key in enumerate((src, dst)):
                        whole = key[0:(P - 1) * TILES].rearrange("(p t) -> p t", t=TILES)
                        sp.dma_start(keys[0:P - 1, s, :], whole).then_inc(loaded, 16)
                        sp.dma_start(keys[P - 1:P, s, 0:LAST_E],
                                     key[(P - 1) * TILES:E].rearrange("(a t) -> a t", a=1)).then_inc(loaded, 16)
                    sp.dma_start(attrs[0:P - 1, :, :].rearrange("p t k -> p (t k)"),
                                 attr[0:(P - 1) * TILES, :].rearrange("(p t) k -> p (t k)", t=TILES)).then_inc(loaded, 16)
                    sp.dma_start(attrs[P - 1:P, 0:LAST_E, :].rearrange("p t k -> p (t k)"),
                                 attr[(P - 1) * TILES:E, :].rearrange("(a t) k -> a (t k)", a=1)).then_inc(loaded, 16)
                    sp.dma_start(a_edge[:, :], l3_a[2 * D:2 * D + 16, :].rearrange("k a -> a k").to_broadcast([P, 16])).then_inc(loaded, 16)
                    sp.wait_ge(made, 1)
                    for s in range(ORDERS):
                        sp.dma_start(mid0[s][:, :].rearrange("(p t) k -> p (t k)", p=P),
                                     record[:, s, :, :].rearrange("p t k -> p (t k)")).then_inc(mid_stored, 16)
                        sp.dma_start(final[s][0:1, :], edge_row[0:1, 0:4]).then_inc(mid_stored, 16)
                        sp.dma_start(final[s][EP + 1:EP + 2, :], edge_row[0:1, 4:8]).then_inc(mid_stored, 16)
                    sp.wait_ge(mid_stored, 16 * 6)

                @block.gpsimd
                def _(gp):
                    gp.memset(keys[:, :, :], PAD_KEY).then_inc(const, 1)
                    gp.memset(attrs[:, :, :], 0.0).then_inc(const, 1)
                    gp.memset(edge_row[:, :], -1).then_inc(const, 1)
                    gp.iota(buckets[:, :], pattern=[[1, 512]], base=0, channel_multiplier=0,
                            allow_small_or_imprecise_dtypes=True).then_inc(const, 1)
                    gp.memset(ones_bf[:, :], 1.0).then_inc(const, 1)
                    gp.memset(ones_row[:, :], 1.0).then_inc(const, 1)
                    gp.wait_ge(const, 6)
                    gp.affine_select(out=before[:, :], in_=ones_bf[:, :], compare_op=ALU.is_gt, fill=0.0,
                                     base=0, pattern=[[1, P]], channel_multiplier=-1).then_inc(const, 1)
                    gp.affine_select(out=notbefore[:, :], in_=ones_bf[:, :], compare_op=ALU.is_ge, fill=0.0,
                                     base=0, pattern=[[-1, P]], channel_multiplier=1).then_inc(const, 1)

                @block.vector
                def _(v):
                    n = 0
                    v.wait_ge(loaded, 16 * 7)
                    for s in range(ORDERS):
                        for high in range(2):
                            if high:
                                i = v.tensor_scalar(digit_i[:, :], keys[:, s, :], 8, None, ALU.arith_shift_right)
                            else:
                                i = v.tensor_scalar(digit_i[:, :], keys[:, s, :], LOW - 1, None, ALU.bitwise_and)
                            i.then_inc(dve, 1)
                            n += 1
                            v.wait_ge(dve, n)
                            v.tensor_copy(digits[:, s, high, :], digit_i[:, :]).then_inc(dve, 1)
                            n += 1
                            v.wait_ge(dve, n)
                    v.wait_ge(const, 8)
                    v.tensor_tensor(attrs[:, :, :], attrs[:, :, :],
                                    a_edge[:, :].unsqueeze(1).to_broadcast([P, TILES, 16]), ALU.mult).then_inc(dve, 1)
                    n += 1
                    v.wait_ge(dve, n)
                    v.tensor_reduce(contrib[:, :], attrs[:, :, :], AX.X, ALU.add).then_inc(dve, 1)
                    n += 1
                    v.wait_ge(dve, n)
                    for s in range(ORDERS):
                        v.tensor_copy(record[:, s, :, 0], keys[:, s, :])
                        v.tensor_copy(record[:, s, :, 1], keys[:, 1 - s, :])
                        v.tensor_copy(record[:, s, :, 3], keys[:, s, :])
                        last = v.tensor_copy(record[:, s, :, 2].bitcast(F32), contrib[:, :])
                        if s == 0:
                            last.then_inc(dve, 1)
                    n += 1
                    last.then_inc(made, 1)
                    def one_hot(t, k, first):
                        if not first:
                            v.wait_ge(hot_used, t - k)
                        for s in range(ORDERS):
                            for high in range(2):
                                c = cols(s, high)
                                last = v.tensor_scalar(hot[:, k, c], buckets[:, 0:c.stop - c.start],
                                                       digits[:, s, high, bass.ds(t, 1)], None, ALU.is_equal)
                        last.then_inc(hot_ready, 1)

                    for k in range(8):
                        one_hot(k, k, True)
                    with v.Fori(1, TILES // 8) as i:
                        for k in range(8):
                            one_hot(i * 8 + k, k, False)
                    v.wait_ge(counted, 1)
                    v.tensor_copy(total[:, 0:512], count_lo[:, :])
                    v.tensor_copy(total[:, cols(0, 1)], count_hi[0][:, 0:HIGH])
                    v.tensor_copy(total[:, cols(1, 1)], count_hi[1][:, 0:HIGH]).then_inc(dve, 1)
                    n += 1
                    v.wait_ge(dve, n)
                    for s in range(ORDERS):
                        for high in range(2):
                            c = cols(s, high)
                            last = v.tensor_tensor_scan(upto[:, c], ones_row[:, 0:c.stop - c.start], total[:, c],
                                                        0.0, ALU.mult, ALU.add)
                    last.then_inc(dve, 1)
                    n += 1
                    v.wait_ge(dve, n)
                    v.tensor_tensor(base[:, :], upto[:, :], total[:, :], ALU.subtract).then_inc(dve, 1)
                    n += 1
                    v.wait_ge(dve, n)
                    v.tensor_scalar(base[:, 2 * LOW:], base[:, 2 * LOW:], 1.0, None, ALU.add).then_inc(dve, 1)

                @block.tensor
                def _(pe):
                    pe.wait_ge(const, 8)
                    pe.matmul(count_lo[:, :], lhsT=g.zeros_bf[:, 0:P], rhs=g.zeros_bf[:, :], start=True, stop=False)
                    pe.matmul(count_hi[0][:, 0:HIGH], lhsT=g.zeros_bf[:, 0:P], rhs=g.zeros_bf[:, 0:HIGH], start=True, stop=False)
                    pe.matmul(count_hi[1][:, 0:HIGH], lhsT=g.zeros_bf[:, 0:P], rhs=g.zeros_bf[:, 0:HIGH], start=True, stop=False)
                    with pe.Fori(0, TILES // 8) as i:
                        for k in range(8):
                            pe.wait_ge(hot_ready, i * 8 + k + 1)
                            pe.matmul(count_lo[:, :], lhsT=ones_bf[:, :], rhs=hot[:, k, 0:512], start=False, stop=False)
                            pe.matmul(count_hi[0][:, 0:HIGH], lhsT=ones_bf[:, :], rhs=hot[:, k, cols(0, 1)], start=False, stop=False)
                            pe.matmul(count_hi[1][:, 0:HIGH], lhsT=ones_bf[:, :], rhs=hot[:, k, cols(1, 1)],
                                      start=False, stop=False).then_inc(hot_used, 1)
                    pe.matmul(count_lo[:, :], lhsT=g.zeros_bf[:, 0:P], rhs=g.zeros_bf[:, :], start=False, stop=True)
                    pe.matmul(count_hi[0][:, 0:HIGH], lhsT=g.zeros_bf[:, 0:P], rhs=g.zeros_bf[:, 0:HIGH], start=False, stop=True)
                    pe.matmul(count_hi[1][:, 0:HIGH], lhsT=g.zeros_bf[:, 0:P], rhs=g.zeros_bf[:, 0:HIGH],
                              start=False, stop=True).then_inc(counted, 1)

        for high in range(2):
            source, target = ((mid0, mid1), (mid1, final))[high]
            width = HIGH if high else LOW
            if high:
                factors(nc, g, sem)
            beside = ExitStack()
            other = place(nc, g, sem, beside) if high else project(nc, g, x, sem, beside)
            zeroed, cleared = g.zeroed_tables[high::2], sem(f"pass{high}_cleared")
            read, split, hot_made, ranked, placed, filed = (
                sem.quad(f"pass{high}_{x}") for x in
                ("read", "split", "hot_made", "ranked", "placed", "filed"))
            summed, taken = sem(f"pass{high}_summed"), sem(f"pass{high}_taken")
            PAIRS = ORDERS * JT

            def hot_rows(c, k):
                return hot[:, k, c.slot % 2 * HIGH:c.slot % 2 * HIGH + width]

            with beside:
                with nc.Block() as block:
                    @block.sync
                    def _(sp):
                        def body(c0, c1, c2, c3):
                            if c0:
                                h = c0.slot
                                sp.wait_ge(filed[h], c0.k * (16 * PAIRS))
                                for s in range(ORDERS):
                                    rows = source[s][bass.ds(c0.n * EDGES, EDGES), :]
                                    sp.dma_start(stage[:, h, s, :, :],
                                                 rows.rearrange("(t p) k -> p t k", p=P)).then_inc(read[h], 16)
                            other.sync(sp, c0, c1, c2, c3)
                        stages(sp, EC, 4, 3, body, tail=1)
                        other.finish(sp)

                    @block.vector
                    def _(v):
                        def body(c0, c1, c2, c3):
                            other.vector(v, c0, c1, c2, c3)
                            if c1:
                                h, i = c1.slot, c1.k
                                v.wait_ge(read[h], (i + 1) * 32)
                                keys_h = stage[:, h, :, :, 0].rearrange("p s t -> p (s t)")
                                if high:
                                    ins = v.tensor_scalar(half_i[:, h, :], keys_h, 8, None, ALU.arith_shift_right)
                                else:
                                    ins = v.tensor_scalar(half_i[:, h, :], keys_h, LOW - 1, None, ALU.bitwise_and)
                                ins.then_inc(split[h], 1)
                                v.wait_ge(split[h], i * 2 + 1)
                                v.tensor_copy(half_d[:, h, :], half_i[:, h, :]).then_inc(split[h], 1)
                                v.wait_ge(split[h], i * 2 + 2)
                            for k in range(PAIRS):
                                tile, s = k // 2, k % 2
                                if c2:
                                    h = c2.slot
                                    v.wait_ge(summed, c2.n * PAIRS + k + 1)
                                    v.tensor_tensor_reduce(
                                        out=junk[:, s, 0:width], in0=ranks[s][:, 0:width], in1=hot_rows(c2, k),
                                        scale=1.0, scalar=0.0, op0=ALU.mult, op1=ALU.add,
                                        accum_out=place_f[:, h, s * JT + tile:s * JT + tile + 1]).then_inc(ranked[h], 1)
                                if c1:
                                    h = c1.slot
                                    if k == 0 and not (isinstance(c1.n, int) and c1.n < 2):
                                        v.wait_ge(taken, (c1.n - 1) * PAIRS)
                                    v.tensor_scalar(hot_rows(c1, k), buckets[:, 0:width],
                                                    half_d[:, h, s * JT + tile:s * JT + tile + 1],
                                                    None, ALU.is_equal).then_inc(hot_made[h], 1)
                            if c2:
                                h = c2.slot
                                v.wait_ge(ranked[h], (c2.k + 1) * PAIRS)
                                v.tensor_copy(place_i[:, h, :], place_f[:, h, :]).then_inc(placed[h], 1)
                        stages(v, EC, 4, 3, body)

                    @block.tensor
                    def _(pe):
                        for s in range(ORDERS):
                            pe.matmul(ranks[s][:, 0:width], lhsT=g.ident[:, :], rhs=base[:, cols(s, high)],
                                      start=True, stop=False, skip_group_check=True)

                        def body(c0, c1, c2, c3):
                            def add(k):
                                pe.wait_ge(hot_made[c2.slot], c2.k * PAIRS + k + 1)
                                pe.matmul(ranks[k % 2][:, 0:width], lhsT=before[:, :], rhs=hot_rows(c2, k),
                                          start=False, stop=False, skip_group_check=True).then_inc(summed, 1)

                            def rest(k):
                                pe.wait_ge(ranked[c2.slot], c2.k * PAIRS + k + 1)
                                pe.matmul(ranks[k % 2][:, 0:width], lhsT=notbefore[:, :], rhs=hot_rows(c2, k),
                                          start=False, stop=False, skip_group_check=True).then_inc(taken, 1)

                            if c2:
                                add(0)
                                add(1)
                            other.tensor(pe, c0, c1, c2, c3)
                            if c2:
                                for k in range(PAIRS):
                                    rest(k)
                                    if k + 2 < PAIRS:
                                        add(k + 2)
                        stages(pe, EC, 4, 3, body)

                    @block.scalar
                    def _(a):
                        def body(c0, c1, c2, c3):
                            if c0:
                                a.wait_ge(read[c0.slot], (c0.k + 1) * 32)
                                for table, size in zeroed:
                                    a.dma_start(chunk_rows(table, c0.n, size), g.zero_rows[:, 0:GROUP * size]).then_inc(cleared, 16)
                            other.scalar(a, c0, c1, c2, c3)
                        stages(a, EC, 4, 3, body)
                        a.wait_ge(cleared, CH * 16 * len(zeroed))

                    @block.gpsimd
                    def _(gp):
                        def body(c0, c1, c2, c3):
                            if c2:
                                h = c2.slot
                                gp.wait_ge(placed[h], c2.k + 1)
                                gp.nop(nofuse=True)
                                for s in range(ORDERS):
                                    for t in range(JT):
                                        k = s * JT + t
                                        gp.indirect_dma_start(
                                            out=target[s][:, :],
                                            out_offset=bass.IndirectOffsetOnAxis(ap=place_i[:, h, k:k + 1], axis=0),
                                            in_=stage[:, h, s, t, :], in_offset=None).then_inc(filed[h], 16)
                        stages(gp, EC, 4, 3, body)
                        for h in range(4):
                            gp.wait_ge(filed[h], len(range(h, EC, 4)) * 16 * PAIRS)
    sem.clear()


def attend_edges(nc, g, name, s, kind, own, others, target, sem):
    H = HEADS if kind == "heads" else 1
    WOWN = {"hyper": D + 2, "heads": D + 8, "edge": 2}[kind]
    WOTHER = {"hyper": D + 2, "heads": D + 8, "edge": D + 2}[kind]
    WRUN = {"hyper": D + 2, "heads": P, "edge": D + 1}[kind]
    WOUT = D if kind == "heads" else D + 2
    Q = 2 if kind == "heads" else 1
    RING = 4
    ctx = ExitStack()
    with ctx:
        def sb(label, shape, dt=F32):
            return ctx.enter_context(nc.sbuf_tensor(f"{name}_{label}", shape, dt))

        def ps(label, shape):
            return ctx.enter_context(nc.psum_tensor(f"{name}_{label}", shape, F32))

        from_rows = sb("from_rows", [P, RING, 2 * JT], I32)
        to_rows = sb("to_rows", [P, RING, JT], I32)
        mine = sb("mine", [P, RING, JT, WOWN])
        other = sb("other", [P, RING, JT, WOTHER])
        pen = sb("pen_b", [H, RING, EDGES])
        score = sb("score", [P, JT, H])
        loop = sb("loop", [P, 2, JT, H])
        tmp = sb("tmp", [P, 12, JT, H])
        top = sb("top", [H, 2, EDGES + 1])
        cols = sb("cols", [P, 2, 2, JT, H])
        lows = sb("lows", [P, 2, 2, JT, H])
        ex = sb("ex", [P, 2, 2, JT, H])
        pay = sb("pay", [P, JT, Q * WRUN])
        decay = sb("decay", [P, Q, EDGES])
        run = sb("run", [P, 2, Q, EDGES])
        out = sb("out", [P, RING, JT, WOUT])
        score_row, top_col, pay_row, spread = ps("score_row", [H, EDGES]), ps("top_col", [P, 2 * JT * H + JT * H]), \
            ps("pay_row0", [P, EDGES]), [ps("spread0", [P, EDGES])]
        back = ps("back", [P, JT * WOUT])
        pay_rows = [pay_row]
        if kind == "hyper":
            big = sb("big", [P, 4, JT, D])
            log_h = sb("log_h", [P, 2, JT, D])
            decays = sb("decays", [P, JT, WRUN])
        if kind == "heads":
            pay_rows.append(ps("pay_row1", [P, EDGES]))
            spread.append(ps("spread1", [P, EDGES]))
            decay_row = ps("decay_row", [2 * H, EDGES])
            decay_row_s = sb("decay_row_s", [P, EDGES])
            weights = sb("weights", [H, 2, EDGES])
            wcol = sb("wcol", [P, JT, H])
            fin = sb("fin", [P, 2, JT, H])
            share = sb("share", [P, JT, 2, H])
            share_row = sb("share_row", [P, EDGES])
            twice = sb("twice", [P, JT, 2, D])
            own_row = sb("own_row", [P, 2, EDGES])
            z = sb("z", [P, 4, EDGES])
        cs = g.cs

        SKEW = 4 if kind == "heads" else 3
        dve, act, pe = Engine(sem(f"{name}_dve"), {
            "hyper": "prod dot a c1 c2 nn den rden t1 t2 ma ma2 rn2 low clip lndiff score "
                     "keep top cols fall fallen rise log",
            "edge": "s1 s2 score keep top cols fall fallen rise",
            "heads": "sadd score qadd loop keep top cols fall fallen rise"}[kind]), \
            Engine(sem(f"{name}_act"), "square root ln1 ln2 ex" if kind == "hyper" else "ex"), \
            Engine(sem(f"{name}_pe"), "score_row top_col")
        acc_dve = Engine(sem(f"{name}_acc_dve"), {
            "hyper": "pay payw decays decay1 run", "edge": "pay run",
            "heads": "pay weights run0 run1 wcol most f1 f2"}[kind])
        acc_act = Engine(sem(f"{name}_acc_act"), "twice decay_row decay0 decay1 own" if kind == "heads" else "decay out")
        acc_pe = Engine(sem(f"{name}_acc_pe"), "weight_row decay_row decay0 decay1 pay own wcol" if kind == "heads"
                        else "decay pay back")
        end_dve, end_act, end_pe = acc_dve, acc_act, acc_pe
        if kind == "heads":
            end_dve = Engine(sem(f"{name}_end_dve"), "g1 g2 g3 beta al0 alpha z0 z1 z2 z3")
            end_act = Engine(sem(f"{name}_end_act"), "exf share_row out")
            end_pe = Engine(sem(f"{name}_end_pe"), "share_row beta0 beta1 alpha0 alpha1 back")
        from_ready, gathered, pen_loaded, to_ready, filed = (
            sem.quad(f"{name}_{x}") for x in ("from_ready", "gathered", "pen_loaded", "to_ready", "filed"))
        set_up = sem(f"{name}_set_up")

        with nc.Block() as block:
            @block.sync
            def _(sp):
                def body(*c):
                    gather, attending, adding, end, scatter = c[0], c[1], c[2], c[-2], c[-1]
                    if gather:
                        n, h = gather.n, gather.slot
                        if not (isinstance(n, int) and n < RING):
                            sp.wait_ge(dve.sem, dve.after(n - RING, "top"))
                        sp.dma_start(pen[:, h, :], g.pen_row[s][:, bass.ds(n * EDGES, EDGES)]
                                     .to_broadcast([H, EDGES])).then_inc(pen_loaded[h], 16)
                stages(sp, EC, RING, SKEW, body)

            @block.gpsimd
            def _(gp):
                gp.wait_ge(set_up, 1)

                def body(*c):
                    gather, attending, adding, end, scatter = c[0], c[1], c[2], c[-2], c[-1]
                    if gather:
                        n, h, k = gather.n, gather.slot, gather.k
                        gp.wait_ge(from_ready[h], k + 1)
                        if not (isinstance(n, int) and n < RING):
                            gp.wait_ge(acc_dve.sem, acc_dve.after(n - RING, acc_dve.names[-1]))
                        gp.nop(nofuse=True)
                        for j in range(JT):
                            gp.indirect_dma_start(out=mine[:, h, j, :], out_offset=None, in_=own[:, :],
                                                  in_offset=bass.IndirectOffsetOnAxis(ap=from_rows[:, h, j:j + 1], axis=0)
                                                  ).then_inc(gathered[h], 16)
                            gp.indirect_dma_start(out=other[:, h, j, :], out_offset=None, in_=others[:, :],
                                                  in_offset=bass.IndirectOffsetOnAxis(ap=from_rows[:, h, JT + j:JT + j + 1], axis=0)
                                                  ).then_inc(gathered[h], 16)
                    if scatter:
                        h, k = scatter.slot, scatter.k
                        gp.wait_ge(end_act.sem, end_act.after(scatter.n, "out"))
                        gp.wait_ge(to_ready[h], k + 1)
                        gp.nop(nofuse=True)
                        for j in range(JT):
                            gp.indirect_dma_start(out=target[:, :],
                                                  out_offset=bass.IndirectOffsetOnAxis(ap=to_rows[:, h, j:j + 1], axis=0),
                                                  in_=out[:, h, j, :], in_offset=None,
                                                  bounds_check=NP - 1, oob_is_err=False).then_inc(filed[h], 16)
                stages(gp, EC, RING, SKEW, body)
                for h in range(RING):
                    gp.wait_ge(filed[h], len(range(h, EC, RING)) * 16 * JT)

            @block.vector
            def _(v):
                v.memset(top[:, 1, :], NEG)
                if kind == "hyper":
                    v.memset(pay[:, :, D + 1:D + 2], 1.0)
                if kind == "heads":
                    v.memset(weights[:, 1, :], 0.0)
                    v.memset(decay_row_s[:, :], 0.0)
                    v.memset(share_row[:, :], 0.0)
                v.memset(run[:, 1, :, :], 0.0).then_inc(set_up, 1)
                v.wait_ge(set_up, 1)

                def body(*c):
                    gather, attending, adding, end, scatter = c[0], c[1], c[2], c[-2], c[-1]
                    if gather:
                        h, k = gather.slot, gather.k
                        v.wait_ge(gathered[h], k * 32 * JT)
                        v.tensor_copy(from_rows[:, h, :], g.rows[s][:, bass.ds(gather.n, 1), 0:2 * JT]
                                      .rearrange("p a j -> p (a j)")).then_inc(from_ready[h], 1)
                    if adding:
                        pay_out(adding)
                    if end:
                        row_numbers(end)
                        if kind == "heads":
                            shares(end)
                    if attending:
                        scores(attending)
                    if adding:
                        running_sums(adding)
                    if attending:
                        if kind == "hyper":
                            distances(attending)
                        maximum(attending)
                    if end and kind == "heads":
                        scaled_runs(end)
                    if attending:
                        weigh(attending)
                    if end and kind == "heads":
                        scaled_own(end)
                    if adding and kind == "heads":
                        join_loop(adding)

                def row_numbers(c):
                    n, h, k, b = c.n, c.slot, c.k, c.slot % 2
                    v.wait_ge(filed[h], k * 16 * JT)
                    v.tensor_copy(to_rows[:, h, :], g.rows[s][:, bass.ds(n, 1), 2 * JT:3 * JT]
                                  .rearrange("p a j -> p (a j)")).then_inc(to_ready[h], 1)

                def scores(c):
                    n, h, k, b = c.n, c.slot, c.k, c.slot % 2

                    def need(engine, step):
                        v.wait_ge(engine.sem, engine.after(n, step))

                    v.wait_ge(gathered[h], (k + 1) * 32 * JT)
                    mi, ot = mine[:, h, :, :], other[:, h, :, :]
                    if kind == "hyper":
                        dve.done(v.tensor_tensor(big[:, 0, :, :], mi[:, :, 2:], ot[:, :, 2:], ALU.mult), "prod")
                        need(dve, "prod")
                        dve.done(v.tensor_reduce(tmp[:, 0, :, 0], big[:, 0, :, :], AX.X, ALU.add), "dot")
                        need(dve, "dot")
                        nu, nv = mi[:, :, 0], ot[:, :, 0]
                        dve.done(v.tensor_scalar(tmp[:, 1, :, 0], tmp[:, 0, :, 0], cs["-2c"], 1.0, ALU.mult, ALU.add), "a")
                        need(dve, "a")
                        dve.done(v.scalar_tensor_tensor(out=tmp[:, 2, :, 0], in0=nv, scalar=cs["c"], in1=tmp[:, 1, :, 0],
                                                        op0=ALU.mult, op1=ALU.add), "c1")
                        dve.done(v.tensor_scalar(tmp[:, 3, :, 0], nu, cs["c"], -1.0, ALU.mult, ALU.add), "c2")
                        dve.done(v.scalar_tensor_tensor(out=tmp[:, 4, :, 0], in0=nu, scalar=cs["c*c"], in1=nv,
                                                        op0=ALU.mult, op1=ALU.mult), "nn")
                        need(dve, "nn")
                        dve.done(v.tensor_tensor(tmp[:, 5, :, 0], tmp[:, 4, :, 0], tmp[:, 1, :, 0], ALU.add), "den")
                        need(dve, "den")
                        dve.done(v.reciprocal(tmp[:, 6, :, 0], tmp[:, 5, :, 0]), "rden")
                        dve.done(v.tensor_tensor(big[:, 1, :, :], mi[:, :, 2:], tmp[:, 2, :, :].to_broadcast([P, JT, D]), ALU.mult), "t1")
                        dve.done(v.tensor_tensor(big[:, 2, :, :], ot[:, :, 2:], tmp[:, 3, :, :].to_broadcast([P, JT, D]), ALU.mult), "t2")
                        need(dve, "t2")
                        dve.done(v.tensor_tensor(big[:, 1, :, :], big[:, 1, :, :], big[:, 2, :, :], ALU.add), "ma")
                        need(dve, "ma")
                        dve.done(v.tensor_tensor(big[:, 3, :, :], big[:, 1, :, :], tmp[:, 6, :, :].to_broadcast([P, JT, D]), ALU.mult), "ma2")
                    elif kind == "edge":
                        dve.done(v.tensor_tensor(tmp[:, 0, :, 0], ot[:, :, 0], mi[:, :, 0], ALU.add), "s1")
                        need(dve, "s1")
                        dve.done(v.tensor_tensor(tmp[:, 1, :, 0], tmp[:, 0, :, 0],
                                                 g.contrib[s][:, bass.ds(n, 1), :].rearrange("p a j -> p (a j)"), ALU.add), "s2")
                        need(dve, "s2")
                        dve.done(v.scalar_tensor_tensor(out=score[:, :, 0], in0=tmp[:, 1, :, 0], scalar=SLOPE, in1=tmp[:, 1, :, 0],
                                                        op0=ALU.mult, op1=ALU.max), "score")
                    else:
                        dve.done(v.tensor_tensor(tmp[:, 0, :, :], ot[:, :, 4:8], mi[:, :, 0:4], ALU.add), "sadd")
                        need(dve, "sadd")
                        dve.done(v.scalar_tensor_tensor(out=score[:, :, :], in0=tmp[:, 0, :, :], scalar=SLOPE, in1=tmp[:, 0, :, :],
                                                        op0=ALU.mult, op1=ALU.max), "score")
                        dve.done(v.tensor_tensor(tmp[:, 1, :, :], mi[:, :, 4:8], mi[:, :, 0:4], ALU.add), "qadd")
                        need(dve, "qadd")
                        dve.done(v.scalar_tensor_tensor(out=loop[:, b, :, :], in0=tmp[:, 1, :, :], scalar=SLOPE, in1=tmp[:, 1, :, :],
                                                        op0=ALU.mult, op1=ALU.max), "loop")

                def distances(c):
                    n, h, k, b = c.n, c.slot, c.k, c.slot % 2

                    def need(engine, step):
                        v.wait_ge(engine.sem, engine.after(n, step))

                    need(act, "square")
                    dve.done(v.tensor_reduce(tmp[:, 7, :, 0], big[:, 0, :, :], AX.X, ALU.add), "rn2")
                    need(dve, "rn2")
                    dve.done(v.tensor_scalar(tmp[:, 8, :, 0], tmp[:, 7, :, 0], cs["c"], 1e-16, ALU.mult, ALU.max), "low")
                    need(act, "root")
                    dve.done(v.tensor_scalar(tmp[:, 9, :, 0], tmp[:, 9, :, 0], CLIP, None, ALU.min), "clip")
                    need(act, "ln2")
                    dve.done(v.tensor_tensor(tmp[:, 0, :, 0], tmp[:, 11, :, 0], tmp[:, 10, :, 0], ALU.subtract), "lndiff")
                    need(dve, "lndiff")
                    dve.done(v.tensor_scalar(score[:, :, 0], tmp[:, 0, :, 0], cs["1/sqrt"], None, ALU.mult), "score")

                def maximum(c):
                    n, h, k, b = c.n, c.slot, c.k, c.slot % 2

                    def need(engine, step):
                        v.wait_ge(engine.sem, engine.after(n, step))

                    dve.done(v.tensor_copy(top[:, b, 0:1], top[:, 1 - b, EDGES:EDGES + 1]), "keep")
                    v.wait_ge(pen_loaded[h], (k + 1) * 16)
                    need(pe, "score_row")
                    dve.done(v.tensor_tensor_scan(top[:, b, 1:], pen[:, h, :], score_row[:, :],
                                                  top[:, 1 - b, EDGES:EDGES + 1], ALU.add, ALU.max), "top")

                def weigh(c):
                    n, h, k, b = c.n, c.slot, c.k, c.slot % 2
                    ot = other[:, h, :, :]

                    def need(engine, step):
                        v.wait_ge(engine.sem, engine.after(n, step))

                    need(pe, "top_col")
                    dve.done(v.tensor_copy(cols[:, b, :, :, :], top_col[:, 0:2 * JT * H]
                                           .rearrange("p (a j q) -> p a j q", a=2, j=JT)), "cols")
                    need(dve, "cols")
                    dve.done(v.tensor_tensor(lows[:, b, 0, :, :], cols[:, b, 1, :, :], cols[:, b, 0, :, :], ALU.subtract), "fall")
                    need(dve, "fall")
                    dve.done(v.tensor_tensor(lows[:, b, 0, :, :], lows[:, b, 0, :, :],
                                             g.pen[s][:, bass.ds(n, 1), :].rearrange("p a j -> p j a")
                                             .to_broadcast([P, JT, H]), ALU.min), "fallen")
                    dve.done(v.tensor_tensor(lows[:, b, 1, :, :], score[:, :, :], cols[:, b, 0, :, :], ALU.subtract), "rise")
                    if kind == "hyper":
                        dve.done(v.scalar_tensor_tensor(out=log_h[:, b, :, :], in0=ot[:, :, 2:], scalar=EPS,
                                                        in1=ot[:, :, 1:2].to_broadcast([P, JT, D]),
                                                        op0=ALU.add, op1=ALU.mult), "log")
                        need(dve, "log")

                def pay_out(c):
                    n, h, k, b = c.n, c.slot, c.k, c.slot % 2
                    ot = other[:, h, :, :]

                    def need(engine, step):
                        v.wait_ge(engine.sem, engine.after(n, step))

                    need(act, "ex")
                    if kind == "hyper":
                        acc_dve.done(v.tensor_tensor(pay[:, :, 0:D], log_h[:, b, :, :], ex[:, b, 1, :, :].to_broadcast([P, JT, D]), ALU.mult), "pay")
                        acc_dve.done(v.tensor_copy(pay[:, :, D:D + 1], ex[:, b, 1, :, :]), "payw")
                        acc_dve.done(v.tensor_copy(decays[:, :, 0:D + 1], ex[:, b, 0, :, :].to_broadcast([P, JT, D + 1])), "decays")
                        acc_dve.done(v.tensor_copy(decays[:, :, D + 1:D + 2], g.same[s][:, bass.ds(n, 1), :]
                                               .rearrange("p a j -> p j a")), "decay1")
                    elif kind == "edge":
                        acc_dve.done(v.tensor_tensor(pay[:, :, :], ot[:, :, 1:], ex[:, b, 1, :, :].to_broadcast([P, JT, D + 1]), ALU.mult), "pay")
                    else:
                        acc_dve.done(v.tensor_tensor(pay[:, :, :].rearrange("p j (q d) -> p j q d", d=D),
                                                 ot[:, :, 8:].unsqueeze(2).to_broadcast([P, JT, H, D]),
                                                 ex[:, b, 1, :, :].unsqueeze(3).to_broadcast([P, JT, H, D]), ALU.mult), "pay")

                def running_sums(c):
                    n, h, k, b = c.n, c.slot, c.k, c.slot % 2

                    def need(engine, step):
                        v.wait_ge(engine.sem, engine.after(n, step))

                    if kind != "heads":
                        need(acc_pe, "pay")
                        need(acc_act, "decay")
                        acc_dve.done(v.tensor_tensor_scan(run[0:WRUN, b, 0, :], decay[0:WRUN, 0, :], pay_rows[0][0:WRUN, :],
                                                      run[0:WRUN, 1 - b, 0, EDGES - 1:EDGES], ALU.mult, ALU.add), "run")
                        return
                    need(acc_act, "decay_row")
                    need(acc_pe, "decay_row")
                    acc_dve.done(v.tensor_tensor_scan(weights[:, b, :], decay_row_s[0:H, :], score_row[:, :],
                                                  weights[:, 1 - b, EDGES - 1:EDGES], ALU.mult, ALU.add), "weights")
                    need(acc_pe, "pay")
                    for q in range(2):
                        need(acc_act, f"decay{q}")
                        acc_dve.done(v.tensor_tensor_scan(run[:, b, q, :], decay[:, q, :], pay_rows[q][:, :],
                                                      run[:, 1 - b, q, EDGES - 1:EDGES], ALU.mult, ALU.add), f"run{q}")

                def join_loop(c):
                    n, h, k, b = c.n, c.slot, c.k, c.slot % 2

                    def need(engine, step):
                        v.wait_ge(engine.sem, engine.after(n, step))

                    need(acc_pe, "wcol")
                    acc_dve.done(v.tensor_copy(wcol[:, :, :], top_col[:, 2 * JT * H:].rearrange("p (j q) -> p j q", j=JT)), "wcol")
                    acc_dve.done(v.tensor_tensor(tmp[:, 2, :, :], cols[:, b, 0, :, :], loop[:, b, :, :], ALU.max), "most")
                    need(acc_dve, "most")
                    acc_dve.done(v.tensor_tensor(fin[:, 0, :, :], cols[:, b, 0, :, :], tmp[:, 2, :, :], ALU.subtract), "f1")
                    acc_dve.done(v.tensor_tensor(fin[:, 1, :, :], loop[:, b, :, :], tmp[:, 2, :, :], ALU.subtract), "f2")

                def shares(c):
                    n = c.n

                    def need(engine, step):
                        v.wait_ge(engine.sem, engine.after(n, step))

                    need(end_act, "exf")
                    end_dve.done(v.tensor_tensor(tmp[:, 3, :, :], wcol[:, :, :], fin[:, 0, :, :], ALU.mult), "g1")
                    need(end_dve, "g1")
                    end_dve.done(v.scalar_tensor_tensor(out=tmp[:, 4, :, :], in0=fin[:, 1, :, :], scalar=1e-16, in1=tmp[:, 3, :, :],
                                                        op0=ALU.add, op1=ALU.add), "g2")
                    need(end_dve, "g2")
                    end_dve.done(v.reciprocal(tmp[:, 5, :, :], tmp[:, 4, :, :]), "g3")
                    need(end_dve, "g3")
                    end_dve.done(v.tensor_tensor(share[:, :, 0, :], fin[:, 0, :, :], tmp[:, 5, :, :], ALU.mult), "beta")
                    end_dve.done(v.tensor_tensor(tmp[:, 6, :, :], fin[:, 1, :, :], tmp[:, 5, :, :], ALU.mult), "al0")
                    need(end_dve, "al0")
                    end_dve.done(v.tensor_scalar(share[:, :, 1, :], tmp[:, 6, :, :], -1.0, None, ALU.add), "alpha")

                def scaled_runs(c):
                    for q in range(2):
                        v.wait_ge(end_pe.sem, end_pe.after(c.n, f"beta{q}"))
                        end_dve.done(v.tensor_tensor(z[:, q, :], run[:, c.slot % 2, q, :], spread[1 - q][:, :], ALU.mult), f"z{q}")

                def scaled_own(c):
                    v.wait_ge(acc_act.sem, acc_act.after(c.n, "own"))
                    for q in range(2):
                        v.wait_ge(end_pe.sem, end_pe.after(c.n, f"alpha{q}"))
                        end_dve.done(v.tensor_tensor(z[:, 2 + q, :], own_row[:, c.slot % 2, :], spread[1 - q][:, :], ALU.mult), f"z{2 + q}")
                stages(v, EC, RING, SKEW, body)

            @block.scalar
            def _(a):
                a.wait_ge(set_up, 1)

                def body(*c):
                    gather, attending, adding, end, scatter = c[0], c[1], c[2], c[-2], c[-1]
                    if kind == "heads" and end:
                        a.wait_ge(acc_dve.sem, acc_dve.after(end.n, "f2"))
                        end_act.done(a.activation(fin[:, :, :, :], fin[:, :, :, :], ACT.Exp), "exf")
                    if kind == "heads" and adding:
                        a.wait_ge(gathered[adding.slot], (adding.k + 1) * 32 * JT)
                        acc_act.done(a.activation(twice[:, :, :, :], mine[:, adding.slot, :, 8:].unsqueeze(2)
                                                  .to_broadcast([P, JT, 2, D]), ACT.Copy), "twice")
                    if adding:
                        accumulate(adding)
                    if kind == "heads" and end:
                        a.wait_ge(end_pe.sem, end_pe.after(end.n, "share_row"))
                        end_act.done(a.activation(share_row[0:2 * H, :], decay_row[:, :], ACT.Copy), "share_row")
                    if attending:
                        attend(attending)
                    if end:
                        n, h, k = end.n, end.slot, end.k
                        a.wait_ge(end_pe.sem, end_pe.after(n, "back"))
                        a.wait_ge(filed[h], k * 16 * JT)
                        end_act.done(a.activation(out[:, h, :, :].rearrange("p j w -> p (j w)"), back[:, :], ACT.Copy), "out")

                def attend(c):
                    n, h, k, b = c.n, c.slot, c.k, c.slot % 2

                    def need(engine, step):
                        a.wait_ge(engine.sem, engine.after(n, step))

                    if kind == "hyper":
                        need(dve, "ma2")
                        act.done(a.activation(big[:, 0, :, :], big[:, 3, :, :], ACT.Square), "square")
                        need(dve, "low")
                        act.done(a.activation(tmp[:, 9, :, :], tmp[:, 8, :, :], ACT.Sqrt), "root")
                        need(dve, "clip")
                        act.done(a.activation(tmp[:, 10, :, :], tmp[:, 9, :, :], ACT.Ln, bias=1.0, scale=1.0), "ln1")
                        act.done(a.activation(tmp[:, 11, :, :], tmp[:, 9, :, :], ACT.Ln, bias=1.0, scale=-1.0), "ln2")
                    need(dve, "rise")
                    act.done(a.activation(ex[:, b, :, :, :], lows[:, b, :, :, :], ACT.Exp), "ex")

                def accumulate(c):
                    n = c.n

                    def need(engine, step):
                        a.wait_ge(engine.sem, engine.after(n, step))

                    if kind != "heads":
                        need(acc_pe, "decay")
                        acc_act.done(a.activation(decay[0:WRUN, 0, :], spread[0][0:WRUN, :], ACT.Copy), "decay")
                    else:
                        need(acc_pe, "decay_row")
                        acc_act.done(a.activation(decay_row_s[0:H, :], decay_row[0:H, :], ACT.Copy), "decay_row")
                        for q in range(2):
                            need(acc_pe, f"decay{q}")
                            acc_act.done(a.activation(decay[:, q, :], spread[q][:, :], ACT.Copy), f"decay{q}")
                        need(acc_pe, "own")
                        acc_act.done(a.activation(own_row[:, c.slot % 2, :], spread[0][:, :], ACT.Copy), "own")
                stages(a, EC, RING, SKEW, body)

            @block.tensor
            def _(t):
                t.wait_ge(set_up, 1)
                ident = g.ident

                def body(*c):
                    gather, attending, adding, end, scatter = c[0], c[1], c[2], c[-2], c[-1]
                    if adding:
                        if kind == "heads":
                            weight_rows(adding)
                            turn(adding)
                        else:
                            turn_and_back(adding)
                    if attending:
                        score_rows(attending)
                    if kind == "heads":
                        if end:
                            share_rows(end)
                        if adding:
                            turn_own(adding)
                    if attending:
                        maxima(attending)
                    if kind == "heads" and end:
                        spread_shares(end)
                        products(end)

                def mm(out, lhsT, rhs, start=True, stop=True):
                    return t.matmul(out, lhsT=lhsT, rhs=rhs, start=start, stop=stop)

                def tile(j):
                    return slice(j * P, (j + 1) * P)

                def need_of(c):
                    def need(engine, step):
                        t.wait_ge(engine.sem, engine.after(c.n, step))
                    return need

                def score_rows(c):
                    need_of(c)(dve, "score")
                    if kind == "heads" and not (isinstance(c.n, int) and c.n < 1):
                        t.wait_ge(acc_dve.sem, acc_dve.after(c.n - 1, "weights"))
                    for j in range(JT):
                        last = t.transpose(score_row[:, tile(j)], score[:, j, :], ident[:, :])
                    pe.done(last, "score_row")

                def maxima(c):
                    need_of(c)(dve, "top")
                    t.nop(nofuse=True)
                    for m in range(2):
                        for j in range(JT):
                            last = t.transpose(top_col[:, (m * JT + j) * H:(m * JT + j + 1) * H],
                                               top[:, c.slot % 2, 1 - m + j * P:1 - m + (j + 1) * P], ident[0:H, 0:H])
                    pe.done(last, "top_col")

                def turn_and_back(c):
                    b, need = c.slot % 2, need_of(c)
                    need(act, "ex")
                    if kind == "hyper":
                        need(acc_dve, "decay1")
                    for j in range(JT):
                        last = t.transpose(spread[0][0:WRUN, tile(j)], decays[:, j, :] if kind == "hyper"
                                  else ex[:, b, 0, j, :].to_broadcast([P, WRUN]), ident[:, :])
                    acc_pe.done(last, "decay")
                    need(acc_dve, "payw" if kind == "hyper" else "pay")
                    for j in range(JT):
                        last = t.transpose(pay_rows[0][0:WRUN, tile(j)], pay[:, j, :], ident[:, :])
                    acc_pe.done(last, "pay")
                    need(acc_dve, "run")
                    for j in range(JT):
                        last = t.transpose(back[:, j * WOUT:j * WOUT + WRUN], run[0:WRUN, b, 0, tile(j)], ident[0:WRUN, 0:WRUN])
                        if kind == "edge":
                            last = t.transpose(back[:, j * WOUT + WRUN:(j + 1) * WOUT],
                                      top[:, b, 1 + j * P:1 + (j + 1) * P], ident[0:1, 0:1])
                    acc_pe.done(last, "back")

                def broadcast(rows, what, q, to):
                    return mm(spread[to][:, :], g.pick[:, what, q, :], rows[:, :])

                def weight_rows(c):
                    need_of(c)(act, "ex")
                    for what, row in ((1, score_row), (0, decay_row)):
                        for j in range(JT):
                            last = t.transpose(row[0:H, tile(j)], ex[:, c.slot % 2, what, j, :], ident[:, :])
                        acc_pe.done(last, ("decay_row", "weight_row")[what])

                def turn(c):
                    b, need = c.slot % 2, need_of(c)
                    need(acc_act, "decay_row")
                    acc_pe.done(broadcast(decay_row_s, 0, 0, 0), "decay0")
                    acc_pe.done(broadcast(decay_row_s, 0, 1, 1), "decay1")
                    need(acc_dve, "pay")
                    for q in range(2):
                        for j in range(JT):
                            last = t.transpose(pay_rows[q][:, tile(j)], pay[:, j, q * P:(q + 1) * P], ident[:, :])
                    acc_pe.done(last, "pay")

                def turn_own(c):
                    b, need = c.slot % 2, need_of(c)
                    need(acc_act, "decay0")
                    for j in range(JT):
                        last = t.transpose(spread[0][:, tile(j)], twice[:, j, :, :].rearrange("p a d -> p (a d)"), ident[:, :])
                    acc_pe.done(last, "own")
                    need(acc_dve, "weights")
                    t.nop(nofuse=True)
                    for j in range(JT):
                        last = t.transpose(top_col[:, (2 * JT + j) * H:(2 * JT + j + 1) * H], weights[:, b, tile(j)], ident[0:H, 0:H])
                    acc_pe.done(last, "wcol")

                def share_rows(c):
                    need_of(c)(end_dve, "alpha")
                    for j in range(JT):
                        last = t.transpose(decay_row[:, tile(j)], share[:, j, :, :].rearrange("p a q -> p (a q)"), ident[:, :])
                    end_pe.done(last, "share_row")

                def spread_shares(c):
                    need = need_of(c)
                    need(end_act, "share_row")
                    end_pe.done(broadcast(share_row, 0, 0, 1), "beta0")
                    end_pe.done(broadcast(share_row, 0, 1, 0), "beta1")
                    need(end_dve, "z0")
                    end_pe.done(broadcast(share_row, 1, 0, 1), "alpha0")
                    need(end_dve, "z1")
                    end_pe.done(broadcast(share_row, 1, 1, 0), "alpha1")

                def products(c):
                    need_of(c)(end_dve, "z3")
                    for j in range(JT):
                        for m in range(4):
                            last = mm(back[:, j * D:(j + 1) * D], z[:, m, tile(j)], g.w_heads[:, m % 2, :],
                                      start=(m == 0), stop=(m == 3))
                    end_pe.done(last, "back")
                stages(t, EC, RING, SKEW, body)
    sem.clear()


LN1 = "total centre"
LN2 = "spread var"


class Norm:

    def __init__(self, g, x, squares, small, v_steps, a_steps, p_steps):
        self.g, self.x, self.squares, self.small = g, x, squares, small
        self.v, self.a, self.p = v_steps, a_steps, p_steps

    def total(self, v, n, b, before):
        steps, x, s = self.v, self.x[:, b, :, :], self.small[:, b]
        v.wait_ge(steps.sem, steps.after(n, before))
        steps.done(v.tensor_reduce(s[:, 0, :], x, AX.X, ALU.add), "total")

    def subtract(self, v, n, b):
        steps, x, s = self.v, self.x[:, b, :, :], self.small[:, b]
        v.wait_ge(steps.sem, steps.after(n, "total"))
        steps.done(v.scalar_tensor_tensor(out=x, in0=s[:, 0, :].unsqueeze(2).to_broadcast([P, GROUP, D]), scalar=-1.0 / D,
                                          in1=x, op0=ALU.mult, op1=ALU.add), "centre")

    def square(self, a, n, b):
        a.wait_ge(self.v.sem, self.v.after(n, "centre"))
        self.a.done(a.activation(self.squares[:, b, :, :], self.x[:, b, :, :], ACT.Square), "lnsq")

    def spread(self, v, n, b):
        steps, s = self.v, self.small[:, b]
        v.wait_ge(self.a.sem, self.a.after(n, "lnsq"))
        steps.done(v.tensor_reduce(s[:, 2, :], self.squares[:, b, :, :], AX.X, ALU.add), "spread")

    def variance(self, v, n, b):
        steps, s = self.v, self.small[:, b]
        v.wait_ge(steps.sem, steps.after(n, "spread"))
        steps.done(v.tensor_scalar(s[:, 3, :], s[:, 2, :], 1.0 / D, LN_EPS, ALU.mult, ALU.add), "var")

    def rstd(self, gp, n, b):
        gp.wait_ge(self.v.sem, self.v.after(n, "var"))
        self.p.done(gp.tensor_tensor(self.small[:, b, 4, :], self.small[:, b, 3, :], self.g.minus_half[:, :], ALU.pow), "rstd")

    def scaled(self, v, out, b):
        return v.tensor_tensor(out, self.x[:, b, :, :],
                               self.small[:, b, 4, :].unsqueeze(2).to_broadcast([P, GROUP, D]), ALU.mult)


def of_node(g, name, n):
    return g.node[name][:, bass.ds(n, 1), :].rearrange("p a j -> p j a")


def close_layer0(nc, g, x, sem):
    ctx = ExitStack()
    with ctx:
        def sb(label, shape, dt=F32):
            return ctx.enter_context(nc.sbuf_tensor(f"c0_{label}", shape, dt))

        xin, att = sb("x", [P, 4, GROUP, D]), sb("att", [P, 4, GROUP, D + 2])
        z1, z2, z3, y = (sb(q, [P, 4, GROUP, D]) for q in ("z1", "z2", "z3", "y"))
        squares = sb("squares", [P, 4, GROUP, D])
        small, t = sb("small", [P, 4, 5, GROUP]), sb("t", [P, 4, 14, GROUP])
        rso = sb("rso", [P, 4, GROUP])
        x1, g1 = sb("x1", [P, 4, GROUP, D]), sb("g1", [P, 4, GROUP, D])
        loaded, stored, ready = (sem.quad(f"c0_{q}") for q in ("loaded", "stored", "ready"))
        c = g.cs
        dve, ball = Engine(sem("c0_dve"), "den rden rc att dmax elu z"), Engine(sem("c0_ball"), "z2 zm zr zf zn zi")
        late, closing = Engine(sem("c0_late"), "s1 s2 s3 hp y " + LN1), Engine(sem("c0_closing"), LN2 + " rso")
        act, ball_act = Engine(sem("c0_act"), "low exp relu sq"), Engine(sem("c0_ball_act"), "tanh")
        degree_pool, root_pool = Engine(sem("c0_degree_pool"), "rso"), Engine(sem("c0_root_pool"), "zn0")
        lact, lgps = Engine(sem("c0_lact"), "lnsq"), Engine(sem("c0_lgps"), "rstd x1")
        norm1 = Norm(g, y, squares, small, late, lact, lgps)
        norm2 = Norm(g, y, squares, small, closing, lact, lgps)
        with nc.Block() as block:
            @block.sync
            def _(sp):
                def body(c0, c1, c2, c3, c4, c5):
                    if c0:
                        h, k = c0.slot, c0.k
                        if not (isinstance(c0.n, int) and c0.n < 4):
                            sp.wait_ge(late.sem, late.after(c0.n - 4, "y"))
                        if isinstance(c0.n, int) and c0.n == CH - 1:
                            sp.dma_start(flat(xin[0:TAIL, h, :, :]), x[(CH - 1) * NODES:N, :]
                                         .rearrange("(p j) k -> p (j k)", j=GROUP)).then_inc(loaded[h], 16)
                        else:
                            sp.dma_start(flat(xin[:, h, :, :]), chunk_rows(x, c0.n, D)).then_inc(loaded[h], 16)
                        sp.dma_start(flat(att[:, h, :, :]), chunk_rows(g.A0, c0.n, D + 2)).then_inc(loaded[h], 16)
                stages(sp, CH, 4, 5, body, tail=1)

            @block.vector
            def _(v):
                def tiles(ch):
                    b = ch.slot
                    return ch.n, ch.slot, b, [t[:, b, i, :] for i in range(14)]

                def per(a):
                    return a.unsqueeze(2).to_broadcast([P, GROUP, D])

                def body(c0, c1, c2, c3, c4, c5):
                    if c4:
                        norm2.spread(v, c4.n, c4.slot)
                    if c2:
                        n, h, b, q = tiles(c2)
                        v.wait_ge(act.sem, act.after(n, "sq"))
                        ball.done(v.tensor_reduce(q[4], z2[:, b, :, :], AX.X, ALU.add), "z2")
                    if c4:
                        norm2.variance(v, c4.n, c4.slot)
                    for piece in range(5):
                        if c1:
                            attention(c1, piece)
                        if c3:
                            on_ball(c3, piece)
                    if c4:
                        n, h, b, q = tiles(c4)
                        v.wait_ge(degree_pool.sem, degree_pool.after(n, "rso"))
                        closing.done(v.tensor_copy(of_node(g, "rso", n), rso[:, h, :].unsqueeze(2)), "rso")
                    if c3:
                        norm1.total(v, c3.n, c3.slot, "y")
                    if c1:
                        n, h, b, q = tiles(c1)
                        v.wait_ge(act.sem, act.after(n, "relu"))
                        dve.done(v.scalar_tensor_tensor(out=z1[:, b, :, :], in0=z2[:, b, :, :], scalar=-1.0, in1=z3[:, b, :, :],
                                                        op0=ALU.add, op1=ALU.add), "elu")
                    if c3:
                        norm1.subtract(v, c3.n, c3.slot)
                    if c1:
                        n, h, b, q = tiles(c1)
                        v.wait_ge(dve.sem, dve.after(n, "elu"))
                        dve.done(v.tensor_scalar(z1[:, b, :, :], z1[:, b, :, :], EPS, None, ALU.add), "z")
                    if c2:
                        factor(c2)

                def attention(ch, piece):
                    n, h, b, q = tiles(ch)
                    if piece == 0:
                        v.wait_ge(loaded[h], (ch.k + 1) * 32)
                        dve.done(v.tensor_scalar(q[0], att[:, h, :, D], 1e-16, None, ALU.add), "den")
                    elif piece == 1:
                        v.wait_ge(dve.sem, dve.after(n, "den"))
                        dve.done(v.reciprocal(q[1], q[0]), "rden")
                    elif piece == 2:
                        v.wait_ge(dve.sem, dve.after(n, "rden"))
                        dve.done(v.tensor_scalar(q[2], q[1], c["sqrt"], None, ALU.mult), "rc")
                    elif piece == 3:
                        v.wait_ge(dve.sem, dve.after(n, "rc"))
                        dve.done(v.tensor_tensor(z1[:, b, :, :], att[:, h, :, 0:D], per(q[2]), ALU.mult), "att")
                    elif piece == 4:
                        dve.done(v.tensor_scalar(q[3], att[:, h, :, D + 1], 1.0, None, ALU.max), "dmax")

                def on_ball(ch, piece):
                    n, h, b, q = tiles(ch)
                    if piece == 0:
                        v.wait_ge(ball.sem, ball.after(n, "zi"))
                        late.done(v.tensor_tensor(q[12], q[8], q[10], ALU.mult), "s1")
                    elif piece == 1:
                        v.wait_ge(ball_act.sem, ball_act.after(n, "tanh"))
                        v.wait_ge(late.sem, late.after(n, "s1"))
                        late.done(v.tensor_tensor(q[13], q[11], q[12], ALU.mult), "s2")
                    elif piece == 2:
                        v.wait_ge(late.sem, late.after(n, "s2"))
                        late.done(v.tensor_scalar(q[0], q[13], c["1/sqrt"], None, ALU.mult), "s3")
                    elif piece == 3:
                        v.wait_ge(late.sem, late.after(n, "s3"))
                        late.done(v.tensor_tensor(z3[:, b, :, :], z1[:, b, :, :], per(q[0]), ALU.mult), "hp")
                    elif piece == 4:
                        v.wait_ge(late.sem, late.after(n, "hp"))
                        late.done(v.tensor_tensor(y[:, b, :, :], z3[:, b, :, :], xin[:, h, :, :], ALU.add), "y")

                def factor(ch):
                    n, h, b, q = tiles(ch)
                    v.wait_ge(root_pool.sem, root_pool.after(n, "zn0"))
                    ball.done(v.tensor_scalar(q[6], q[5], c["clip"], None, ALU.max), "zm")
                    v.wait_ge(ball.sem, ball.after(n, "zm"))
                    ball.done(v.reciprocal(q[7], q[6]), "zr")
                    v.wait_ge(ball.sem, ball.after(n, "zr"))
                    ball.done(v.tensor_scalar(q[8], q[7], c["clip"], None, ALU.mult), "zf")
                    v.wait_ge(ball.sem, ball.after(n, "zf"))
                    ball.done(v.tensor_tensor(q[9], q[5], q[8], ALU.mult), "zn")
                    v.wait_ge(ball.sem, ball.after(n, "zn"))
                    ball.done(v.reciprocal(q[10], q[9]), "zi")
                stages(v, CH, 4, 5, body)

            @block.scalar
            def _(a):
                def body(c0, c1, c2, c3, c4, c5):
                    if c1:
                        n, b = c1.n, c1.slot
                        a.wait_ge(dve.sem, dve.after(n, "att"))
                        act.done(a.activation(z3[:, b, :, :], z1[:, b, :, :], ACT.Relu, scale=-1.0), "low")
                        a.wait_ge(act.sem, act.after(n, "low"))
                        act.done(a.activation(z2[:, b, :, :], z3[:, b, :, :], ACT.Exp, scale=-1.0), "exp")
                        a.wait_ge(act.sem, act.after(n, "exp"))
                        act.done(a.activation(z3[:, b, :, :], z1[:, b, :, :], ACT.Relu), "relu")
                    if c3:
                        norm1.square(a, c3.n, c3.slot)
                    if c1:
                        n, b = c1.n, c1.slot
                        a.wait_ge(dve.sem, dve.after(n, "z"))
                        act.done(a.activation(z2[:, b, :, :], z1[:, b, :, :], ACT.Square), "sq")
                    if c2:
                        n, b = c2.n, c2.slot
                        a.wait_ge(ball.sem, ball.after(n, "zn"))
                        ball_act.done(a.activation(t[:, b, 11, :], t[:, b, 9, :], ACT.Tanh, scale=c["sqrt"]), "tanh")
                    if c5:
                        n, h = c5.n, c5.slot
                        a.wait_ge(ready[h], c5.k + 1)
                        a.dma_start(chunk_rows(g.X1, n, D), flat(x1[:, h, :, :])).then_inc(stored[h], 16)
                        a.dma_start(chunk_rows(g.G1, n, D), flat(g1[:, h, :, :])).then_inc(stored[h], 16)
                stages(a, CH, 4, 5, body)
                for h in range(4):
                    a.wait_ge(stored[h], len(range(h, CH, 4)) * 32)

            @block.gpsimd
            def _(gp):
                def body(c0, c1, c2, c3, c4, c5):
                    if c4:
                        n, h, k = c4.n, c4.slot, c4.k
                        norm2.rstd(gp, n, h)
                        gp.wait_ge(lgps.sem, lgps.after(n, "rstd"))
                        gp.wait_ge(stored[h], k * 32)
                        lgps.done(norm2.scaled(gp, x1[:, h, :, :], h), "x1")
                        gp.wait_ge(lgps.sem, lgps.after(n, "x1"))
                        gp.tensor_tensor(g1[:, h, :, :], x1[:, h, :, :],
                                         rso[:, h, :].unsqueeze(2).to_broadcast([P, GROUP, D]), ALU.mult).then_inc(ready[h], 1)
                    if c2:
                        n, b = c2.n, c2.slot
                        gp.wait_ge(ball.sem, ball.after(n, "z2"))
                        root_pool.done(gp.tensor_tensor(t[:, b, 5, :], t[:, b, 4, :], g.half[:, :], ALU.pow), "zn0")
                    if c1:
                        n, b = c1.n, c1.slot
                        gp.wait_ge(dve.sem, dve.after(n, "dmax"))
                        degree_pool.done(gp.tensor_tensor(rso[:, b, :], t[:, b, 3, :], g.minus_half[:, :], ALU.pow), "rso")
                stages(gp, CH, 4, 5, body)
    sem.clear()


def convolve(nc, g, last, sem):
    name = "v2" if last else "v1"
    own, sums, weight = (g.H1, g.A2, g.w_conv2) if last else (g.X1, g.A1, g.w_conv1)
    LOADS = 48 if last else 32
    ctx = ExitStack()
    with ctx:
        def sb(label, shape, dt=F32):
            return ctx.enter_context(nc.sbuf_tensor(f"{name}_{label}", shape, dt))

        def ps(label, shape):
            return ctx.enter_context(nc.psum_tensor(f"{name}_{label}", shape, F32))

        x, a_in = sb("x", [P, 4, GROUP, D]), sb("a", [P, 4, GROUP, D + 1])
        s = sb("s", [P, 2, GROUP, D])
        both = sb("both", [P, 2, GROUP, 2 * D])
        both_t = sb("both_t", [P, 2, 2, 4 * P])
        turned = [ps(f"turned{i}", [P, 4 * P]) for i in range(2)]
        result = [ps(f"result{b}", [P, GROUP, D]) for b in range(2)]
        out = sb("out", [P, 4, GROUP, D])
        loaded, stored, ready = (sem.quad(f"{name}_{q}") for q in ("loaded", "stored", "ready"))
        sums_dve, turn_act = Engine(sem(f"{name}_sums"), "s u0 u1"), Engine(sem(f"{name}_turn_act"), "t0 t1")
        turn_pe, product_pe = Engine(sem(f"{name}_turn_pe"), "turn0 turn1"), Engine(sem(f"{name}_product_pe"), "result")
        if last:
            x1 = sb("x1", [P, 4, GROUP, D])
            y, x2, squares = (sb(q, [P, 2, GROUP, D]) for q in ("y", "x2", "squares"))
            small = sb("small", [P, 2, 5, GROUP])
            x2_t = sb("x2_t", [P, 4 * P])
            turned2 = ps("turned2", [P, 4 * P])
            heads = [ps(f"heads{i}", [P, 2, 2, D + 8]) for i in range(2)]
            out2 = sb("out2", [P, 4, GROUP, D + 8])
            centre_dve, centre_act = Engine(sem(f"{name}_centre"), "y " + LN1), Engine(sem(f"{name}_square"), "lnsq")
            norm_dve, rstd_pool = Engine(sem(f"{name}_norm"), LN2 + " x2"), Engine(sem(f"{name}_rstd"), "rstd")
            row_act, heads_pe = Engine(sem(f"{name}_row"), "row x2t"), Engine(sem(f"{name}_heads_pe"), "turn2 heads")
            close_dve = Engine(sem(f"{name}_close"), "b")
            norm1 = Norm(g, y, squares, small, centre_dve, centre_act, rstd_pool)
            norm2 = Norm(g, y, squares, small, norm_dve, centre_act, rstd_pool)
        else:
            degree, rsi = sb("degree", [P, 2, GROUP]), sb("rsi", [P, 4, GROUP])
            out2 = sb("out2", [P, 4, GROUP, D])
            degree_dve, relu_act = Engine(sem(f"{name}_degree"), "dm"), Engine(sem(f"{name}_relu"), "relu")
            rsi_pool = Engine(sem(f"{name}_rsi"), "rsi")

        SKEW = 5 if last else 4

        def roles(c):
            return (None, c[1], c[2], c[3], c[4]) if last else (c[1], c[2], c[3], None, None)

        with nc.Block() as block:
            @block.sync
            def _(sp):
                def body(*c):
                    if c[0]:
                        n, h = c[0].n, c[0].slot
                        if not (isinstance(n, int) and n < 4):
                            if last:
                                sp.wait_ge(centre_dve.sem, centre_dve.after(n - 4, "y"))
                            else:
                                sp.wait_ge(sums_dve.sem, sums_dve.after(n - 4, "u1"))
                        sp.dma_start(flat(x[:, h, :, :]), chunk_rows(own, n, D)).then_inc(loaded[h], 16)
                        sp.dma_start(flat(a_in[:, h, :, :]), chunk_rows(sums, n, D + 1)).then_inc(loaded[h], 16)
                        if last:
                            sp.dma_start(flat(x1[:, h, :, :]), chunk_rows(g.X1, n, D)).then_inc(loaded[h], 16)
                stages(sp, CH, 4, SKEW, body)

            @block.vector
            def _(v):
                def body(*c):
                    for_degree, for_sums, for_products, for_norm, for_heads = roles(c)
                    if for_degree:
                        n, h, b = for_degree.n, for_degree.slot, for_degree.slot % 2
                        v.wait_ge(loaded[h], (for_degree.k + 1) * LOADS)
                        degree_dve.done(v.tensor_scalar(degree[:, b, :], a_in[:, h, :, D], 1.0, None, ALU.max), "dm")
                    if for_sums:
                        n, h, b = for_sums.n, for_sums.slot, for_sums.slot % 2
                        if last:
                            v.wait_ge(loaded[h], (for_sums.k + 1) * LOADS)
                            factor = of_node(g, "rsi", n)
                        else:
                            v.wait_ge(rsi_pool.sem, rsi_pool.after(n, "rsi"))
                            v.tensor_copy(of_node(g, "rsi", n), rsi[:, h, :].unsqueeze(2))
                            factor = rsi[:, h, :].unsqueeze(2)
                        sums_dve.done(v.tensor_tensor(s[:, b, :, :], a_in[:, h, :, 0:D], factor.to_broadcast([P, GROUP, D]), ALU.mult), "s")
                    if for_norm:
                        norm2.spread(v, for_norm.n, for_norm.slot % 2)
                    if for_sums:
                        n, h, b = for_sums.n, for_sums.slot, for_sums.slot % 2
                        v.wait_ge(sums_dve.sem, sums_dve.after(n, "s"))
                        if not (isinstance(n, int) and n < 2):
                            v.wait_ge(turn_pe.sem, turn_pe.after(n - 2, "turn1"))
                        sums_dve.done(v.tensor_tensor(both[:, b, :, 0:D], s[:, b, :, :], x[:, h, :, :], ALU.add), "u0")
                    if for_norm:
                        norm2.variance(v, for_norm.n, for_norm.slot % 2)
                    if for_sums:
                        n, h, b = for_sums.n, for_sums.slot, for_sums.slot % 2
                        sums_dve.done(v.tensor_tensor(both[:, b, :, D:], s[:, b, :, :], x[:, h, :, :], ALU.mult), "u1")
                    if for_products and last:
                        n, h, b = for_products.n, for_products.slot, for_products.slot % 2
                        v.wait_ge(product_pe.sem, product_pe.after(n, "result"))
                        centre_dve.done(v.tensor_tensor(y[:, b, :, :], result[b][:, :, :], x1[:, h, :, :], ALU.add), "y")
                    if for_heads:
                        n, h, b = for_heads.n, for_heads.slot, for_heads.slot % 2
                        v.wait_ge(heads_pe.sem, heads_pe.after(n, "heads"))
                        for i in range(2):
                            part = heads[i][:, :, :, :].rearrange("p q a k -> p (q a) k")
                            v.tensor_copy(out2[:, h, 4 * i:4 * i + 4, 0:8], part[:, :, 0:8])
                            step = v.tensor_tensor(x2[:, b, 4 * i:4 * i + 4, :], x2[:, b, 4 * i:4 * i + 4, :], part[:, :, 8:], ALU.add)
                        close_dve.done(step, "b")
                    if for_products and last:
                        norm1.total(v, for_products.n, for_products.slot % 2, "y")
                    if for_norm:
                        n, b = for_norm.n, for_norm.slot % 2
                        v.wait_ge(rstd_pool.sem, rstd_pool.after(n, "rstd"))
                        norm_dve.done(norm2.scaled(v, x2[:, b, :, :], b), "x2")
                    if for_products and last:
                        norm1.subtract(v, for_products.n, for_products.slot % 2)
                stages(v, CH, 4, SKEW, body)

            @block.tensor
            def _(te):
                def body(*c):
                    _, for_sums, for_products, for_norm, for_heads = roles(c)
                    if for_products:
                        n, b = for_products.n, for_products.slot % 2
                        te.wait_ge(turn_act.sem, turn_act.after(n, "t0"))
                        if not last and not (isinstance(n, int) and n < 2):
                            te.wait_ge(relu_act.sem, relu_act.after(n - 2, "relu"))
                        for j in range(GROUP):
                            if j == 4:
                                te.wait_ge(turn_act.sem, turn_act.after(n, "t1"))
                            step = te.matmul(result[b][:, j, :], lhsT=both_t[:, b, j // 4, (j % 4) * P:(j % 4 + 1) * P],
                                             rhs=weight[:, :], start=True, stop=True)
                        product_pe.done(step, "result")
                    if for_heads:
                        n = for_heads.n
                        te.wait_ge(row_act.sem, row_act.after(n, "x2t"))
                        if not (isinstance(n, int) and n < 1):
                            te.wait_ge(close_dve.sem, close_dve.after(n - 1, "b"))
                        for q in range(GROUP // 2):
                            step = te.matmul(heads[q // 2][:, q % 2, :, :].rearrange("p a k -> p (a k)"),
                                             lhsT=x2_t[:, q * P:(q + 1) * P],
                                             rhs=g.w2_pair[:, :, :].rearrange("p a k -> p (a k)"), start=True, stop=True)
                        heads_pe.done(step, "heads")
                    if for_sums:
                        n, b = for_sums.n, for_sums.slot % 2
                        te.wait_ge(sums_dve.sem, sums_dve.after(n, "u1"))
                        for j in range(GROUP):
                            step = te.transpose(turned[j // 4][:, (j % 4) * P:(j % 4 + 1) * P], both[:, b, j, :], g.ident[:, :])
                            if j % 4 == 3:
                                turn_pe.done(step, f"turn{j // 4}")
                    if for_norm:
                        n, b = for_norm.n, for_norm.slot % 2
                        te.wait_ge(norm_dve.sem, norm_dve.after(n, "x2"))
                        for q in range(GROUP // 2):
                            step = te.transpose(turned2[:, q * P:(q + 1) * P],
                                                x2[:, b, 2 * q:2 * q + 2, :].rearrange("p a d -> p (a d)"), g.ident[:, :])
                        heads_pe.done(step, "turn2")
                stages(te, CH, 4, SKEW, body)

            @block.scalar
            def _(a):
                def body(*c):
                    _, for_sums, for_products, for_norm, _ = roles(c)
                    if for_products and not last:
                        n, h, b = for_products.n, for_products.slot, for_products.slot % 2
                        a.wait_ge(product_pe.sem, product_pe.after(n, "result"))
                        a.wait_ge(stored[h], for_products.k * 32)
                        relu_act.done(a.activation(out[:, h, :, :], result[b][:, :, :], ACT.Relu), "relu")
                    if for_sums:
                        n, b = for_sums.n, for_sums.slot % 2
                        for i in range(2):
                            a.wait_ge(turn_pe.sem, turn_pe.after(n, f"turn{i}"))
                            turn_act.done(a.activation(both_t[:, b, i, :], turned[i][:, :], ACT.Copy), f"t{i}")
                    if for_norm:
                        n, h, b = for_norm.n, for_norm.slot, for_norm.slot % 2
                        a.wait_ge(norm_dve.sem, norm_dve.after(n, "x2"))
                        a.wait_ge(stored[h], for_norm.k * 32)
                        row_act.done(a.activation(out2[:, h, :, 8:], x2[:, b, :, :], ACT.Copy), "row")
                    if for_products and last:
                        norm1.square(a, for_products.n, for_products.slot % 2)
                    if for_norm:
                        n = for_norm.n
                        a.wait_ge(heads_pe.sem, heads_pe.after(n, "turn2"))
                        row_act.done(a.activation(x2_t[:, :], turned2[:, :], ACT.Copy), "x2t")
                    if c[-1]:
                        n, h = c[-1].n, c[-1].slot
                        a.wait_ge(ready[h], c[-1].k + 1)
                        first, second = (g.B2, g.X2) if last else (g.H1, g.G2)
                        a.dma_start(chunk_rows(first, n, D), flat(out[:, h, :, :])).then_inc(stored[h], 16)
                        a.dma_start(chunk_rows(second, n, D + 8 if last else D), flat(out2[:, h, :, :])).then_inc(stored[h], 16)
                stages(a, CH, 4, SKEW, body)
                for h in range(4):
                    a.wait_ge(stored[h], len(range(h, CH, 4)) * 32)

            @block.gpsimd
            def _(gp):
                def body(*c):
                    for_degree, _, for_products, for_norm, for_heads = roles(c)
                    if for_degree:
                        n, h, b = for_degree.n, for_degree.slot, for_degree.slot % 2
                        gp.wait_ge(degree_dve.sem, degree_dve.after(n, "dm"))
                        rsi_pool.done(gp.tensor_tensor(rsi[:, h, :], degree[:, b, :], g.minus_half[:, :], ALU.pow), "rsi")
                    if for_products and not last:
                        n, h, b = for_products.n, for_products.slot, for_products.slot % 2
                        gp.wait_ge(relu_act.sem, relu_act.after(n, "relu"))
                        gp.tensor_tensor(out2[:, h, :, :], out[:, h, :, :],
                                         of_node(g, "rso", n).to_broadcast([P, GROUP, D]), ALU.mult).then_inc(ready[h], 1)
                    if for_norm:
                        norm2.rstd(gp, for_norm.n, for_norm.slot % 2)
                    if for_heads:
                        n, h, b = for_heads.n, for_heads.slot, for_heads.slot % 2
                        gp.wait_ge(close_dve.sem, close_dve.after(n, "b"))
                        gp.wait_ge(stored[h], for_heads.k * 32)
                        gp.tensor_tensor(out[:, h, :, :], x2[:, b, :, :],
                                         g.bias[:, :].unsqueeze(1).to_broadcast([P, GROUP, D]), ALU.add).then_inc(ready[h], 1)
                stages(gp, CH, 4, SKEW, body)
    sem.clear()


def close_layer2(nc, g, sem):
    ctx = ExitStack()
    with ctx:
        def sb(label, shape, dt=F32):
            return ctx.enter_context(nc.sbuf_tensor(f"c2_{label}", shape, dt))

        def ps(label, shape):
            return ctx.enter_context(nc.psum_tensor(f"c2_{label}", shape, F32))

        base, more = sb("base", [P, 4, GROUP, D]), sb("more", [P, 4, GROUP, D])
        y, x3, squares = (sb(q, [P, 4, GROUP, D]) for q in ("y", "x3", "squares"))
        small = sb("small", [P, 4, 5, GROUP])
        x3_t = sb("x3_t", [P, 4 * P])
        turned = ps("turned", [P, 4 * P])
        scores = ps("scores", [P, GROUP, 2])
        row, pair = sb("row", [P, 4, GROUP, D + 2]), sb("pair", [P, 4, GROUP, 2])
        loaded, stored, ready = (sem.quad(f"c2_{q}") for q in ("loaded", "stored", "ready"))
        centre_dve, square_act = Engine(sem("c2_centre"), "y " + LN1), Engine(sem("c2_square"), "lnsq")
        norm_dve, scaled_dve, rstd_pool = Engine(sem("c2_norm"), LN2), Engine(sem("c2_scaled"), "x3"), Engine(sem("c2_rstd"), "rstd")
        row_act, scores_pe = Engine(sem("c2_row"), "row x3t"), Engine(sem("c2_scores_pe"), "turn scores")
        close_dve = Engine(sem("c2_close"), "pair")
        norm1 = Norm(g, y, squares, small, centre_dve, square_act, rstd_pool)
        norm2 = Norm(g, y, squares, small, norm_dve, square_act, rstd_pool)
        ones_set = sem("c2_ones")
        with nc.Block() as block:
            @block.sync
            def _(sp):
                def body(c0, c1, c2, c3, c4, c5):
                    if c0:
                        n, h = c0.n, c0.slot
                        if not (isinstance(n, int) and n < 4):
                            sp.wait_ge(centre_dve.sem, centre_dve.after(n - 4, "y"))
                        sp.dma_start(flat(base[:, h, :, :]), chunk_rows(g.B2, n, D)).then_inc(loaded[h], 16)
                        sp.dma_start(flat(more[:, h, :, :]), chunk_rows(g.A3, n, D)).then_inc(loaded[h], 16)
                stages(sp, CH, 4, 5, body)

            @block.vector
            def _(v):
                v.memset(row[:, :, :, D + 1:], 1.0).then_inc(ones_set, 1)
                v.wait_ge(ones_set, 1)

                def body(c0, c1, c2, c3, c4, c5):
                    if c3:
                        n, b = c3.n, c3.slot
                        v.wait_ge(rstd_pool.sem, rstd_pool.after(n, "rstd"))
                        scaled_dve.done(norm2.scaled(v, x3[:, b, :, :], b), "x3")
                    if c1:
                        n, h, b = c1.n, c1.slot, c1.slot
                        v.wait_ge(loaded[h], (c1.k + 1) * 32)
                        centre_dve.done(v.tensor_tensor(y[:, b, :, :], base[:, h, :, :], more[:, h, :, :], ALU.add), "y")
                    if c2:
                        norm2.spread(v, c2.n, c2.slot)
                    if c1:
                        norm1.total(v, c1.n, c1.slot, "y")
                    if c2:
                        norm2.variance(v, c2.n, c2.slot)
                    if c4:
                        n, h = c4.n, c4.slot
                        v.wait_ge(scores_pe.sem, scores_pe.after(n, "scores"))
                        v.wait_ge(stored[h], c4.k * 32)
                        v.tensor_copy(row[:, h, :, 0:1], scores[:, :, 1:2])
                        close_dve.done(v.tensor_copy(pair[:, h, :, :], scores[:, :, :]), "pair")
                    if c1:
                        norm1.subtract(v, c1.n, c1.slot)
                    if c4:
                        v.wait_ge(close_dve.sem, close_dve.after(c4.n, "pair"))
                        v.sem_inc(ready[c4.slot], 1)
                stages(v, CH, 4, 5, body)

            @block.tensor
            def _(te):
                def body(c0, c1, c2, c3, c4, c5):
                    if c3:
                        n, b = c3.n, c3.slot
                        te.wait_ge(scaled_dve.sem, scaled_dve.after(n, "x3"))
                        for q in range(GROUP // 2):
                            step = te.transpose(turned[:, q * P:(q + 1) * P],
                                                x3[:, b, 2 * q:2 * q + 2, :].rearrange("p a d -> p (a d)"), g.ident[:, :])
                        scores_pe.done(step, "turn")
                        te.wait_ge(row_act.sem, row_act.after(n, "x3t"))
                        if not (isinstance(n, int) and n < 1):
                            te.wait_ge(close_dve.sem, close_dve.after(n - 1, "pair"))
                        for q in range(GROUP // 2):
                            step = te.matmul(scores[:, 2 * q:2 * q + 2, :].rearrange("p a k -> p (a k)"),
                                             lhsT=x3_t[:, q * P:(q + 1) * P],
                                             rhs=g.a3_pair[:, :, :].rearrange("p a k -> p (a k)"), start=True, stop=True)
                        scores_pe.done(step, "scores")
                stages(te, CH, 4, 5, body)

            @block.scalar
            def _(a):
                a.wait_ge(ones_set, 1)

                def body(c0, c1, c2, c3, c4, c5):
                    if c1:
                        norm1.square(a, c1.n, c1.slot)
                    if c3:
                        n, h, b = c3.n, c3.slot, c3.slot
                        a.wait_ge(scaled_dve.sem, scaled_dve.after(n, "x3"))
                        a.wait_ge(stored[h], c3.k * 32)
                        row_act.done(a.activation(row[:, h, :, 1:D + 1], x3[:, b, :, :], ACT.Copy), "row")
                        a.wait_ge(scores_pe.sem, scores_pe.after(n, "turn"))
                        row_act.done(a.activation(x3_t[:, :], turned[:, :], ACT.Copy), "x3t")
                    if c5:
                        n, h = c5.n, c5.slot
                        a.wait_ge(ready[h], c5.k + 1)
                        a.dma_start(chunk_rows(g.X3, n, D + 2), flat(row[:, h, :, :])).then_inc(stored[h], 16)
                        a.dma_start(chunk_rows(g.S3, n, 2), flat(pair[:, h, :, :])).then_inc(stored[h], 16)
                stages(a, CH, 4, 5, body)
                for h in range(4):
                    a.wait_ge(stored[h], len(range(h, CH, 4)) * 32)

            @block.gpsimd
            def _(gp):
                def body(c0, c1, c2, c3, c4, c5):
                    if c2:
                        norm2.rstd(gp, c2.n, c2.slot)
                stages(gp, CH, 4, 5, body)
    sem.clear()


def close_layer3(nc, g, out_rows, sem):
    ctx = ExitStack()
    with ctx:
        def sb(label, shape, dt=F32):
            return ctx.enter_context(nc.sbuf_tensor(f"c3_{label}", shape, dt))

        def ps(label, shape):
            return ctx.enter_context(nc.psum_tensor(f"c3_{label}", shape, F32))

        x3, pair = sb("x3", [P, 4, GROUP, D + 2]), sb("pair", [P, 4, GROUP, 2])
        part = sb("part", [P, 4, 2, GROUP, D + 2])
        t = sb("t", [P, 2, 16, GROUP])
        logs = sb("logs", [P, 2, 3, GROUP])
        share = sb("share", [P, 2, 3, GROUP])
        p0, p1, p2 = (sb(q, [P, 2, GROUP, D]) for q in ("p0", "p1", "p2"))
        y, squares = (sb(q, [P, 4, GROUP, D]) for q in ("y", "squares"))
        small = sb("small", [P, 4, 5, GROUP])
        pt = sb("pt", [P, 2, 4 * P])
        turned = [ps(f"turned{i}", [P, 4 * P]) for i in range(2)]
        result = [ps(f"result{i}", [P, GROUP, D]) for i in range(2)]
        out = sb("out", [P, 4, GROUP, D])
        loaded, stored, ready = (sem.quad(f"c3_{q}") for q in ("loaded", "stored", "ready"))
        logs_dve, ex_act = Engine(sem("c3_logs"), "l0 has loop none m0 m1 top0 top rise"), Engine(sem("c3_ex"), "ex")
        sum_dve, own_pool = Engine(sem("c3_sum"), "w0 d0 d1 d2 shares q0 q1 q2 r1"), Engine(sem("c3_own"), "own")
        turn_pe, turn_act = Engine(sem("c3_turn_pe"), "turn"), Engine(sem("c3_turn_act"), "pt")
        result_pe, square_act = Engine(sem("c3_result_pe"), "result"), Engine(sem("c3_square"), "lnsq")
        centre_dve, norm_dve = Engine(sem("c3_centre"), "y " + LN1), Engine(sem("c3_norm"), LN2)
        rstd_pool = Engine(sem("c3_rstd"), "rstd")
        norm1 = Norm(g, y, squares, small, centre_dve, square_act, rstd_pool)
        norm2 = Norm(g, y, squares, small, norm_dve, square_act, rstd_pool)
        with nc.Block() as block:
            @block.sync
            def _(sp):
                def body(c0, c1, c2, c3, c4, c5):
                    if c0:
                        n, h = c0.n, c0.slot
                        if not (isinstance(n, int) and n < 4):
                            sp.wait_ge(centre_dve.sem, centre_dve.after(n - 4, "y"))
                        sp.dma_start(flat(x3[:, h, :, :]), chunk_rows(g.X3, n, D + 2)).then_inc(loaded[h], 16)
                        sp.dma_start(flat(pair[:, h, :, :]), chunk_rows(g.S3, n, 2)).then_inc(loaded[h], 16)
                        sp.dma_start(flat(part[:, h, 0, :, :]), chunk_rows(g.A4[1], n, D + 2)).then_inc(loaded[h], 16)
                        sp.dma_start(flat(part[:, h, 1, :, :]), chunk_rows(g.A4[0], n, D + 2)).then_inc(loaded[h], 16)
                stages(sp, CH, 4, 5, body)

            @block.vector
            def _(v):
                def scores(ch, piece):
                    n, h, b = ch.n, ch.slot, ch.slot % 2
                    q = [t[:, b, i, :] for i in range(16)]
                    both = part[:, h, :, :, :]

                    def need(name):
                        v.wait_ge(logs_dve.sem, logs_dve.after(n, name))

                    if piece == 0:
                        v.wait_ge(loaded[h], (ch.k + 1) * 64)
                        logs_dve.done(v.tensor_tensor(q[0], pair[:, h, :, 0], pair[:, h, :, 1], ALU.add), "l0")
                        logs_dve.done(v.tensor_scalar(t[:, b, 2:4, :], both[:, :, :, D], 0.0, None, ALU.is_gt), "has")
                    elif piece == 1:
                        need("l0")
                        logs_dve.done(v.scalar_tensor_tensor(out=logs[:, b, 2, :], in0=q[0], scalar=SLOPE, in1=q[0], op0=ALU.mult, op1=ALU.max), "loop")
                        need("has")
                        logs_dve.done(v.tensor_scalar(t[:, b, 4:6, :], t[:, b, 2:4, :], -1.0, -NEG, ALU.add, ALU.mult), "none")
                        logs_dve.done(v.tensor_tensor(t[:, b, 6:8, :], both[:, :, :, D + 1], t[:, b, 2:4, :], ALU.mult), "m0")
                    elif piece == 2:
                        need("m0")
                        logs_dve.done(v.tensor_tensor(logs[:, b, 0:2, :], t[:, b, 6:8, :], t[:, b, 4:6, :], ALU.add), "m1")
                    elif piece == 3:
                        need("m1")
                        logs_dve.done(v.tensor_tensor(q[8], logs[:, b, 0, :], logs[:, b, 1, :], ALU.max), "top0")
                    elif piece == 4:
                        need("top0")
                        logs_dve.done(v.tensor_tensor(q[9], q[8], logs[:, b, 2, :], ALU.max), "top")
                    elif piece == 5:
                        need("top")
                        logs_dve.done(v.tensor_tensor(logs[:, b, :, :], logs[:, b, :, :], q[9].unsqueeze(1).to_broadcast([P, 3, GROUP]), ALU.subtract), "rise")

                def sums(ch, piece):
                    n, h, b = ch.n, ch.slot, ch.slot % 2
                    q = [t[:, b, i, :] for i in range(16)]
                    both = part[:, h, :, :, :]

                    def need(name):
                        v.wait_ge(sum_dve.sem, sum_dve.after(n, name))

                    def of(i):
                        return share[:, b, i, :].unsqueeze(2).to_broadcast([P, GROUP, D])

                    if piece == 0:
                        v.wait_ge(ex_act.sem, ex_act.after(n, "ex"))
                        sum_dve.done(v.tensor_tensor(t[:, b, 10:12, :], both[:, :, :, D], logs[:, b, 0:2, :], ALU.mult), "w0")
                    elif piece == 1:
                        need("w0")
                        sum_dve.done(v.tensor_tensor(q[12], q[10], q[11], ALU.add), "d0")
                    elif piece == 2:
                        need("d0")
                        sum_dve.done(v.tensor_tensor(q[13], q[12], logs[:, b, 2, :], ALU.add), "d1")
                    elif piece == 3:
                        need("d1")
                        sum_dve.done(v.reciprocal(q[14], q[13]), "d2")
                    elif piece == 4:
                        need("d2")
                        sum_dve.done(v.tensor_tensor(share[:, b, :, :], logs[:, b, :, :], q[14].unsqueeze(1).to_broadcast([P, 3, GROUP]), ALU.mult), "shares")
                    elif piece == 5:
                        need("shares")
                        sum_dve.done(v.tensor_tensor(p0[:, b, :, :], both[:, 0, :, 0:D], of(0), ALU.mult), "q0")
                        sum_dve.done(v.tensor_tensor(p1[:, b, :, :], both[:, 1, :, 0:D], of(1), ALU.mult), "q1")
                    elif piece == 6:
                        need("q1")
                        sum_dve.done(v.tensor_tensor(p0[:, b, :, :], p0[:, b, :, :], p1[:, b, :, :], ALU.add), "q2")
                    elif piece == 7:
                        need("q2")
                        v.wait_ge(own_pool.sem, own_pool.after(n, "own"))
                        sum_dve.done(v.tensor_tensor(p0[:, b, :, :], p0[:, b, :, :], p2[:, b, :, :], ALU.add), "r1")

                def body(c0, c1, c2, c3, c4, c5):
                    for piece in range(6):
                        if c2:
                            sums(c2, piece)
                        if c1:
                            scores(c1, piece)
                    if c3:
                        v.wait_ge(result_pe.sem, result_pe.after(c3.n, "result"))
                        centre_dve.done(v.tensor_tensor(y[:, c3.slot, :, :], result[c3.slot % 2][:, :, :], x3[:, c3.slot, :, 1:D + 1], ALU.add), "y")
                    if c2:
                        sums(c2, 6)
                    if c4:
                        norm2.spread(v, c4.n, c4.slot)
                    if c3:
                        norm1.total(v, c3.n, c3.slot, "y")
                    if c2:
                        sums(c2, 7)
                    if c4:
                        norm2.variance(v, c4.n, c4.slot)
                    if c3:
                        norm1.subtract(v, c3.n, c3.slot)
                stages(v, CH, 4, 5, body)

            @block.tensor
            def _(te):
                def body(c0, c1, c2, c3, c4, c5):
                    if c3:
                        n, b = c3.n, c3.slot % 2
                        te.wait_ge(turn_act.sem, turn_act.after(n, "pt"))
                        for q in range(GROUP // 2):
                            step = te.matmul(result[b][:, 2 * q:2 * q + 2, :].rearrange("p a k -> p (a k)"),
                                             lhsT=pt[:, b, q * P:(q + 1) * P],
                                             rhs=g.w3_pair[:, :, :].rearrange("p a k -> p (a k)"), start=True, stop=True)
                        result_pe.done(step, "result")
                    if c2:
                        n, b = c2.n, c2.slot % 2
                        te.wait_ge(sum_dve.sem, sum_dve.after(n, "r1"))
                        for q in range(GROUP // 2):
                            step = te.transpose(turned[b][:, q * P:(q + 1) * P],
                                                p0[:, b, 2 * q:2 * q + 2, :].rearrange("p a d -> p (a d)"), g.ident[:, :])
                        turn_pe.done(step, "turn")
                stages(te, CH, 4, 5, body)

            @block.scalar
            def _(a):
                def body(c0, c1, c2, c3, c4, c5):
                    if c2:
                        n, b = c2.n, c2.slot % 2
                        a.wait_ge(turn_pe.sem, turn_pe.after(n, "turn"))
                        turn_act.done(a.activation(pt[:, b, :], turned[b][:, :], ACT.Copy), "pt")
                    if c1:
                        n, b = c1.n, c1.slot % 2
                        a.wait_ge(logs_dve.sem, logs_dve.after(n, "rise"))
                        ex_act.done(a.activation(logs[:, b, :, :], logs[:, b, :, :], ACT.Exp), "ex")
                    if c3:
                        norm1.square(a, c3.n, c3.slot)
                    if c5:
                        n, h = c5.n, c5.slot
                        a.wait_ge(ready[h], c5.k + 1)
                        if isinstance(n, int) and n == CH - 1:
                            a.dma_start(out_rows[(CH - 1) * NODES:N, :].rearrange("(p j) k -> p (j k)", j=GROUP),
                                         flat(out[0:TAIL, h, :, :])).then_inc(stored[h], 16)
                        else:
                            a.dma_start(chunk_rows(out_rows, n, D), flat(out[:, h, :, :])).then_inc(stored[h], 16)
                stages(a, CH, 4, 5, body)
                for h in range(4):
                    a.wait_ge(stored[h], len(range(h, CH, 4)) * 16)

            @block.gpsimd
            def _(gp):
                def body(c0, c1, c2, c3, c4, c5):
                    if c2:
                        n, h, b = c2.n, c2.slot, c2.slot % 2
                        gp.wait_ge(sum_dve.sem, sum_dve.after(n, "shares"))
                        own_pool.done(gp.tensor_tensor(p2[:, b, :, :], x3[:, h, :, 1:D + 1],
                                                       share[:, b, 2, :].unsqueeze(2).to_broadcast([P, GROUP, D]), ALU.mult), "own")
                    if c4:
                        n, h = c4.n, c4.slot
                        norm2.rstd(gp, n, h)
                        gp.wait_ge(rstd_pool.sem, rstd_pool.after(n, "rstd"))
                        gp.wait_ge(stored[h], c4.k * 16)
                        norm2.scaled(gp, out[:, h, :, :], h).then_inc(ready[h], 1)
                stages(gp, CH, 4, 5, body)
    sem.clear()


class Bag:
    pass


def gnn_kernel(nc, x, src, dst, edge_attr_16, L0_gnn_W, L0_gnn_c, L1_gnn_W1_1, L1_gnn_W2_1, L1_gnn_W1_2,
               L1_gnn_W2_2, L2_gnn_W, L2_gnn_att_src, L2_gnn_att_dst, L2_gnn_bias, L3_gnn_W, L3_gnn_a, out,
               table=None):
    def dram(name, rows, width, dt=F32):
        if table:
            return table(name, rows, width, dt)
        return nc.dram_tensor(name, (rows, width), dt).ap()

    g, w = Bag(), Bag()
    w.L0_W, w.L0_c, w.L2_W, w.L2_bias, w.L3_W, w.L3_a = L0_gnn_W, L0_gnn_c, L2_gnn_W, L2_gnn_bias, L3_gnn_W, L3_gnn_a
    w.L2_att_dst, w.L2_att_src = L2_gnn_att_dst, L2_gnn_att_src
    w.L1_W1_1, w.L1_W2_1, w.L1_W1_2, w.L1_W2_2 = L1_gnn_W1_1, L1_gnn_W2_1, L1_gnn_W1_2, L1_gnn_W2_2
    w.loads = 20
    g.mid0 = [dram(f"mid0_{s}", EP, 4, I32) for s in range(ORDERS)]
    g.mid1 = [dram(f"mid1_{s}", EP, 4, I32) for s in range(ORDERS)]
    g.sorted = [dram(f"sorted_{s}", EP + 2, 4, I32) for s in range(ORDERS)]
    g.same_row = [dram(f"same_row{s}", 1, EP) for s in range(ORDERS)]
    g.pen_row = [dram(f"pen_row{s}", 1, EP) for s in range(ORDERS)]
    g.Y, g.T0 = dram("Y", NP, D), dram("T0", NP, D + 2)
    g.X1, g.G1, g.H1, g.G2 = (dram(q, NP, D) for q in ("X1", "G1", "H1", "G2"))
    g.X2, g.B2, g.X3, g.S3 = dram("X2", NP, D + 8), dram("B2", NP, D), dram("X3", NP, D + 2), dram("S3", NP, 2)
    g.A0, g.A1, g.A2, g.A3 = dram("A0", NP, D + 2), dram("A1", NP, D + 1), dram("A2", NP, D + 1), dram("A3", NP, D)
    g.A4 = [dram(f"A4_{s}", NP, D + 2) for s in range(ORDERS)]
    g.zeroed_tables = [(g.A0, D + 2), (g.A1, D + 1), (g.A2, D + 1), (g.A3, D), (g.A4[0], D + 2), (g.A4[1], D + 2)]

    ctx = ExitStack()
    with ctx:
        def sb(name, shape, dt=F32):
            return ctx.enter_context(nc.sbuf_tensor(name, shape, dt))

        g.ident = sb("ident", [P, P])
        g.zeros_bf = sb("zeros_bf", [P, 512], BF16)
        g.zero_rows = sb("zero_rows", [P, GROUP * (D + 2)])
        g.half, g.minus_half = sb("half", [P, GROUP]), sb("minus_half", [P, GROUP])
        g.pick = sb("pick", [P, 2, 2, P])
        g.w0_pair, g.w2_pair = sb("w0_pair", [P, 2, D + 2]), sb("w2_pair", [P, 2, D + 8])
        g.a3_pair, g.w3_pair = sb("a3_pair", [P, 2, 2]), sb("w3_pair", [P, 2, D])
        g.w_heads = sb("w_heads", [P, 2, D])
        g.w_conv1, g.w_conv2 = sb("w_conv1", [P, D]), sb("w_conv2", [P, D])
        g.bias, g.k_row, g.k_cols = sb("bias", [P, D]), sb("k_row", [P, D]), sb("k_cols", [P, 2])
        g.c_cols = sb("c_cols", [P, 8])
        g.cs = {q: g.c_cols[:, i:i + 1] for i, q in enumerate(("c", "sqrt", "1/sqrt", "clip", "-2c", "c*c"))}
        g.rows = [sb(f"rows{s}", [P, EC, 3 * JT], I32) for s in range(ORDERS)]
        g.pen = [sb(f"pen{s}", [P, EC, JT]) for s in range(ORDERS)]
        g.contrib = [sb(f"contrib{s}", [P, EC, JT]) for s in range(ORDERS)]
        g.same = [sb(f"same{s}", [P, EC, JT]) for s in range(ORDERS)]
        g.node = {q: sb(f"node_{q}", [P, CH, GROUP]) for q in
                  "n2 sf y2 yk sy nh2 zeta s1 s2 rso rsi".split()}
        sem = Semaphores(nc)
        set_up(nc, g, w, sem)
        sort_edges(nc, g, src, dst, L3_gnn_a, edge_attr_16, x, sem)
        lay_out_edges(nc, g, sem)
        attend_edges(nc, g, "e0", 0, "hyper", g.T0, g.T0, g.A0, sem)
        close_layer0(nc, g, x, sem)
        sum_edges(nc, g, "e1", g.G1, g.A1, sem)
        convolve(nc, g, False, sem)
        sum_edges(nc, g, "e2", g.G2, g.A2, sem)
        convolve(nc, g, True, sem)
        attend_edges(nc, g, "e3", 1, "heads", g.X2, g.X2, g.A3, sem)
        close_layer2(nc, g, sem)
        attend_edges(nc, g, "e4d", 1, "edge", g.S3, g.X3, g.A4[1], sem)
        attend_edges(nc, g, "e4s", 0, "edge", g.S3, g.X3, g.A4[0], sem)
        close_layer3(nc, g, out, sem)


_INS = ["x", "src", "dst", "edge_attr_16", "L0_gnn_W", "L0_gnn_c", "L1_gnn_W1_1", "L1_gnn_W2_1", "L1_gnn_W1_2",
        "L1_gnn_W2_2", "L2_gnn_W", "L2_gnn_att_src", "L2_gnn_att_dst", "L2_gnn_bias", "L3_gnn_W", "L3_gnn_a"]
_OUT = ((N, D), "float32")


def kernel(**inputs):
    import numpy as np
    import concourse.bacc as bacc
    from concourse.bass_utils import run_bass_kernel_spmd

    nc = bacc.Bacc("TRN2", target_bir_lowering=False, num_devices=1)
    arrays, args = {}, []
    for name in _INS:
        a = np.ascontiguousarray(inputs[name])
        arrays[f"in_{name}"] = a
        args.append(nc.dram_tensor(f"in_{name}", a.shape, mybir.dt.from_np(a.dtype), kind="ExternalInput").ap())
    result = nc.dram_tensor("out_rows", _OUT[0], mybir.dt.from_np(np.dtype(_OUT[1])), kind="ExternalOutput").ap()
    gnn_kernel(nc, *args, result)
    return run_bass_kernel_spmd(nc, [arrays], core_ids=[0]).results[0]["out_rows"]
```
